# Optimizing a Trainium2 kernel written in Bass

```python
import numpy as np
import jax
import jax.numpy as jnp

def _softmax(x, axis=-1):
    return jax.nn.softmax(x, axis=axis)

def _gelu(x):
    return jax.nn.gelu(x, approximate=True)

def _silu(x):
    return jax.nn.silu(x)

def _sigmoid(x):
    return jax.nn.sigmoid(x)

def _layernorm(x, axis=-1, eps=1e-05):
    m = jnp.mean(x, axis=axis, keepdims=True)
    v = jnp.var(x, axis=axis, keepdims=True)
    return (x - m) / jnp.sqrt(v + eps)

def _scatter_add(tgt, idx, src, axis=0):
    return tgt.at[idx].add(src)

def _segment_sum(src, seg, n):
    return jax.ops.segment_sum(src, seg, n)
kernel_name = 'mk_gps_d2_gnn_r8_979acf'

def setup_inputs(seed: int=0):
    np.random.seed(seed)
    _w = jnp.asarray

    def _rec_inputs():
        import jax
        import jax.numpy as jnp
        _gk = jax.random.key(seed)
        x = -0.0003713 + 1 * jax.random.normal(jax.random.fold_in(_gk, 1), (6250, 256), jnp.float32)
        src = jax.random.randint(jax.random.fold_in(_gk, 2), (100000,), 0, 6250, jnp.int32)
        dst = jnp.minimum((6250 * jax.random.uniform(jax.random.fold_in(_gk, 3), (100000,)) ** 2.0).astype(jnp.int32), 49999)
        _o = jnp.argsort(dst, stable=True)
        src = src[_o]
        dst = dst[_o]
        edge_weight = jax.random.uniform(jax.random.fold_in(_gk, 12), (100000,), jnp.float32, 0.0, 0.999998)
        return (x, src, dst, edge_weight)
    x, src, dst, edge_weight = _rec_inputs()

    def _L0_gnn_setup():
        import jax, jax.numpy as jnp
        import numpy as np
        N_NODES = 6250
        N_EDGES = 125000
        D = 256

        def gcn_conv(x, src, dst, ew, W, b, n):
            x = x @ W
            loop = jnp.arange(n)
            src_l = jnp.concatenate([src, loop])
            dst_l = jnp.concatenate([dst, loop])
            ew_l = jnp.concatenate([ew, jnp.ones((n,), ew.dtype)])
            deg = jax.ops.segment_sum(ew_l, dst_l, num_segments=n)
            dinv = jnp.where(deg > 0, jax.lax.rsqrt(deg), 0.0).astype(x.dtype)
            norm = dinv[src_l] * ew_l * dinv[dst_l]
            out = jax.ops.segment_sum(norm[:, None] * x[src_l], dst_l, num_segments=n)
            return out + b
        key = jax.random.key(seed)
        k = jax.random.split(key, 8)
        glorot = 1.0 / np.sqrt(D)
        return {'x': jax.random.normal(k[0], (N_NODES, D), jnp.float32), 'edge_index': jax.random.randint(k[1], (2, N_EDGES), 0, N_NODES, jnp.int64), 'edge_weight': jax.random.uniform(k[2], (N_EDGES,), jnp.float32), 'W1': jax.random.normal(k[3], (D, D), jnp.float32) * glorot, 'b1': jnp.zeros((D,), jnp.float32), 'W2': jax.random.normal(k[4], (D, D), jnp.float32) * glorot, 'b2': jnp.zeros((D,), jnp.float32)}
    _L0_gnn_all = _L0_gnn_setup()
    _L0_gnn_in = {k: v for k, v in _L0_gnn_all.items() if k in ('W1', 'b1', 'W2', 'b2')}
    del _L0_gnn_all

    def _L0_mix_setup():
        import jax, jax.numpy as jnp
        import numpy as np
        HEADS = 8
        DIM_HEAD = 64
        EPS = 1e-05

        def _inst_norm_lastdim(t):
            mu = jnp.mean(t, axis=-1, keepdims=True)
            var = jnp.mean(jnp.square(t - mu), axis=-1, keepdims=True)
            return (t - mu) * jax.lax.rsqrt(var + EPS)
        key = jax.random.key(seed)
        k1, k2, k3, k4 = jax.random.split(key, 4)
        b, n, dim = (4, 1024, 256)
        inner = HEADS * DIM_HEAD
        x = jax.random.normal(k1, (b, n, dim), dtype=jnp.float32)
        Wqkv = jax.random.normal(k2, (3 * inner, dim), dtype=jnp.float32) * (1.0 / np.sqrt(dim))
        Wout = jax.random.normal(k3, (dim, inner), dtype=jnp.float32) * (1.0 / np.sqrt(inner))
        bout = jax.random.normal(k4, (dim,), dtype=jnp.float32) * 0.01
        return {'x': x, 'Wqkv': Wqkv, 'Wout': Wout, 'bout': bout}
    _L0_mix_all = _L0_mix_setup()
    _L0_mix_in = {k: v for k, v in _L0_mix_all.items() if k in ('Wqkv', 'Wout', 'bout')}
    del _L0_mix_all

    def _L0_ffn_setup():
        import math
        import jax, jax.numpy as jnp
        import numpy as np
        CAPACITY_FACTOR = 1.25
        key = jax.random.key(seed)
        ks = jax.random.split(key, 5)
        B, L, D, F, E = (8, 1024, 256, 1024, 8)
        h = jax.random.normal(ks[0], (B, L, D), dtype=jnp.float32)
        gate_w = jax.random.normal(ks[1], (D, E), dtype=jnp.float32) * 0.02
        gate_b = jnp.zeros((E,), dtype=jnp.float32)
        w1 = jax.random.normal(ks[2], (E, D, F), dtype=jnp.float32) * (1.0 / math.sqrt(D))
        b1 = jnp.zeros((E, F), dtype=jnp.float32)
        w2 = jax.random.normal(ks[3], (E, F, D), dtype=jnp.float32) * (1.0 / math.sqrt(F))
        b2 = jnp.zeros((E, D), dtype=jnp.float32)
        return {'h': h, 'gate_w': gate_w, 'gate_b': gate_b, 'w1': w1, 'b1': b1, 'w2': w2, 'b2': b2}
    _L0_ffn_all = _L0_ffn_setup()
    _L0_ffn_in = {k: v for k, v in _L0_ffn_all.items() if k in ('gate_w', 'gate_b', 'w1', 'b1', 'w2', 'b2')}
    del _L0_ffn_all

    def _L1_gnn_setup():
        import jax, jax.numpy as jnp
        import numpy as np
        N, E = (6250, 100000)
        IN, HID, HEADS, OUT = (256, 64, 4, 256)
        FIRST_OUT = HID * HEADS

        def gat_conv(x, src, dst, W, a_src, a_dst, b, concat):
            n = x.shape[0]
            H, C = a_src.shape
            h = (x @ W).reshape(n, H, C)
            es = jnp.einsum('nhc,hc->nh', h, a_src)[src]
            ed = jnp.einsum('nhc,hc->nh', h, a_dst)[dst]
            e = jax.nn.leaky_relu(es + ed, negative_slope=0.2)
            m = jax.ops.segment_max(e, dst, num_segments=n)
            p = jnp.exp(e - m[dst])
            z = jax.ops.segment_sum(p, dst, num_segments=n)
            alpha = p / z[dst]
            out = jax.ops.segment_sum(h[src] * alpha[:, :, None], dst, num_segments=n)
            out = out.reshape(n, H * C) if concat else out.mean(axis=1)
            return out + b

        def batchnorm(x, gamma, beta, eps=1e-05):
            mu = x.mean(axis=0)
            var = ((x - mu) ** 2).mean(axis=0)
            return gamma * (x - mu) / jnp.sqrt(var + eps) + beta
        key = jax.random.key(seed)
        ks = jax.random.split(key, 10)
        s = 0.05
        return {'x': jax.random.normal(ks[0], (N, IN), jnp.float32), 'edge_index': jax.random.randint(ks[1], (2, E), 0, N, dtype=jnp.int64), 'W0': jax.random.normal(ks[2], (IN, HEADS * HID), jnp.float32) * s, 'a_src0': jax.random.normal(ks[3], (HEADS, HID), jnp.float32) * s, 'a_dst0': jax.random.normal(ks[4], (HEADS, HID), jnp.float32) * s, 'b0': jnp.zeros((HEADS * HID,), jnp.float32), 'gamma0': jnp.ones((FIRST_OUT,), jnp.float32), 'beta0': jnp.zeros((FIRST_OUT,), jnp.float32), 'W1': jax.random.normal(ks[5], (FIRST_OUT, OUT), jnp.float32) * s, 'a_src1': jax.random.normal(ks[6], (1, OUT), jnp.float32) * s, 'a_dst1': jax.random.normal(ks[7], (1, OUT), jnp.float32) * s, 'b1': jnp.zeros((OUT,), jnp.float32)}
    _L1_gnn_all = _L1_gnn_setup()
    _L1_gnn_in = {k: v for k, v in _L1_gnn_all.items() if k in ('W0', 'a_src0', 'a_dst0', 'b0', 'gamma0', 'beta0', 'W1', 'a_src1', 'a_dst1', 'b1')}
    del _L1_gnn_all

    def _L1_mix_setup():
        import jax, jax.numpy as jnp
        import numpy as np
        DIM = 256
        HEADS = 4
        DIM_HEAD = 32
        NUM_MEM = 4
        HIDDEN = HEADS * DIM_HEAD
        SCALE = DIM_HEAD ** (-0.5)

        def rmsnorm(x, g):
            n = jnp.linalg.norm(x, axis=-1, keepdims=True)
            return x / jnp.maximum(n, 1e-12) * g * x.shape[-1] ** 0.5
        key = jax.random.key(seed)
        ks = jax.random.split(key, 8)
        B, N = (4, 2048)
        return {'x': jax.random.normal(ks[0], (B, N, DIM), jnp.float32), 't': jax.random.normal(ks[1], (B,), jnp.float32), 'w_qkv': jax.random.normal(ks[2], (DIM, 3 * HIDDEN), jnp.float32) * 0.02, 'mem_kv': jax.random.normal(ks[3], (2, HEADS, DIM_HEAD, NUM_MEM), jnp.float32), 'w_out': jax.random.normal(ks[4], (HIDDEN, DIM), jnp.float32) * 0.02, 'b_out': jnp.zeros((DIM,), jnp.float32), 'g_out': jnp.ones((DIM,), jnp.float32), 'g_pre': jnp.ones((DIM,), jnp.float32)}
    _L1_mix_all = _L1_mix_setup()
    _L1_mix_in = {k: v for k, v in _L1_mix_all.items() if k in ('t', 'w_qkv', 'mem_kv', 'w_out', 'b_out', 'g_out', 'g_pre')}
    del _L1_mix_all

    def _L1_ffn_setup():
        import jax, jax.numpy as jnp
        import numpy as np
        C = 256
        HID = 1024
        E = 8
        TEMP = 1.0
        key = jax.random.key(seed)
        ks = jax.random.split(key, 7)
        x = jax.random.normal(ks[0], (8, 2048, C), dtype=jnp.float32)
        W1 = jax.random.normal(ks[1], (C, HID), dtype=jnp.float32) * 0.02
        b1 = jnp.zeros((HID,), dtype=jnp.float32)
        Wg = jax.random.normal(ks[2], (HID, E), dtype=jnp.float32) * 0.02
        bg = jnp.zeros((E,), dtype=jnp.float32)
        Wd = jax.random.normal(ks[3], (E, HID, C), dtype=jnp.float32) * 0.02
        bd = jnp.zeros((E, C), dtype=jnp.float32)
        return {'x': x, 'W1': W1, 'b1': b1, 'Wg': Wg, 'bg': bg, 'Wd': Wd, 'bd': bd}
    _L1_ffn_all = _L1_ffn_setup()
    _L1_ffn_in = {k: v for k, v in _L1_ffn_all.items() if k in ('W1', 'b1', 'Wg', 'bg', 'Wd', 'bd')}
    del _L1_ffn_all
    return {'x': x, 'src': src, 'dst': dst, 'edge_weight': edge_weight, 'L0_gnn_W1': _L0_gnn_in['W1'], 'L0_gnn_b1': _L0_gnn_in['b1'], 'L0_gnn_W2': _L0_gnn_in['W2'], 'L0_gnn_b2': _L0_gnn_in['b2'], 'L0_mix_Wqkv': _L0_mix_in['Wqkv'], 'L0_mix_Wout': _L0_mix_in['Wout'], 'L0_mix_bout': _L0_mix_in['bout'], 'L0_ffn_gate_w': _L0_ffn_in['gate_w'], 'L0_ffn_gate_b': _L0_ffn_in['gate_b'], 'L0_ffn_w1': _L0_ffn_in['w1'], 'L0_ffn_b1': _L0_ffn_in['b1'], 'L0_ffn_w2': _L0_ffn_in['w2'], 'L0_ffn_b2': _L0_ffn_in['b2'], 'L1_gnn_W0': _L1_gnn_in['W0'], 'L1_gnn_a_src0': _L1_gnn_in['a_src0'], 'L1_gnn_a_dst0': _L1_gnn_in['a_dst0'], 'L1_gnn_b0': _L1_gnn_in['b0'], 'L1_gnn_gamma0': _L1_gnn_in['gamma0'], 'L1_gnn_beta0': _L1_gnn_in['beta0'], 'L1_gnn_W1': _L1_gnn_in['W1'], 'L1_gnn_a_src1': _L1_gnn_in['a_src1'], 'L1_gnn_a_dst1': _L1_gnn_in['a_dst1'], 'L1_gnn_b1': _L1_gnn_in['b1'], 'L1_mix_t': _L1_mix_in['t'], 'L1_mix_w_qkv': _L1_mix_in['w_qkv'], 'L1_mix_mem_kv': _L1_mix_in['mem_kv'], 'L1_mix_w_out': _L1_mix_in['w_out'], 'L1_mix_b_out': _L1_mix_in['b_out'], 'L1_mix_g_out': _L1_mix_in['g_out'], 'L1_mix_g_pre': _L1_mix_in['g_pre'], 'L1_ffn_W1': _L1_ffn_in['W1'], 'L1_ffn_b1': _L1_ffn_in['b1'], 'L1_ffn_Wg': _L1_ffn_in['Wg'], 'L1_ffn_bg': _L1_ffn_in['bg'], 'L1_ffn_Wd': _L1_ffn_in['Wd'], 'L1_ffn_bd': _L1_ffn_in['bd']}

def reference(x, src, dst, edge_weight, L0_gnn_W1, L0_gnn_b1, L0_gnn_W2, L0_gnn_b2, L0_mix_Wqkv, L0_mix_Wout, L0_mix_bout, L0_ffn_gate_w, L0_ffn_gate_b, L0_ffn_w1, L0_ffn_b1, L0_ffn_w2, L0_ffn_b2, L1_gnn_W0, L1_gnn_a_src0, L1_gnn_a_dst0, L1_gnn_b0, L1_gnn_gamma0, L1_gnn_beta0, L1_gnn_W1, L1_gnn_a_src1, L1_gnn_a_dst1, L1_gnn_b1, L1_mix_t, L1_mix_w_qkv, L1_mix_mem_kv, L1_mix_w_out, L1_mix_b_out, L1_mix_g_out, L1_mix_g_pre, L1_ffn_W1, L1_ffn_b1, L1_ffn_Wg, L1_ffn_bg, L1_ffn_Wd, L1_ffn_bd):
    import jax
    import jax.numpy as jnp

    def _L0_gnn_ref(x, edge_index, edge_weight, W1, b1, W2, b2):
        import jax, jax.numpy as jnp
        import numpy as np
        N_NODES = 6250
        N_EDGES = 125000
        D = 256

        def gcn_conv(x, src, dst, ew, W, b, n):
            x = x @ W
            loop = jnp.arange(n)
            src_l = jnp.concatenate([src, loop])
            dst_l = jnp.concatenate([dst, loop])
            ew_l = jnp.concatenate([ew, jnp.ones((n,), ew.dtype)])
            deg = jax.ops.segment_sum(ew_l, dst_l, num_segments=n)
            dinv = jnp.where(deg > 0, jax.lax.rsqrt(deg), 0.0).astype(x.dtype)
            norm = dinv[src_l] * ew_l * dinv[dst_l]
            out = jax.ops.segment_sum(norm[:, None] * x[src_l], dst_l, num_segments=n)
            return out + b
        n = x.shape[0]
        src, dst = (edge_index[0], edge_index[1])
        h = gcn_conv(x, src, dst, edge_weight, W1, b1, n)
        h = jax.nn.relu(h)
        out = gcn_conv(h, src, dst, edge_weight, W2, b2, n)
        return out

    def _L0_mix_ref(x, Wqkv, Wout, bout):
        import jax, jax.numpy as jnp
        import numpy as np
        HEADS = 8
        DIM_HEAD = 64
        EPS = 1e-05

        def _inst_norm_lastdim(t):
            mu = jnp.mean(t, axis=-1, keepdims=True)
            var = jnp.mean(jnp.square(t - mu), axis=-1, keepdims=True)
            return (t - mu) * jax.lax.rsqrt(var + EPS)
        b, n, dim = x.shape
        qkv = jnp.einsum('bnc,fc->bnf', x, Wqkv)
        q, k, v = jnp.split(qkv, 3, axis=-1)

        def to_heads(t):
            return t.reshape(b, n, HEADS, DIM_HEAD).transpose(0, 2, 1, 3)
        q, k, v = (to_heads(q), to_heads(k), to_heads(v))
        k = _inst_norm_lastdim(k)
        v = _inst_norm_lastdim(v)
        dots = jnp.einsum('bhnd,bhne->bhde', k, v)
        out = jnp.einsum('bhnd,bhde->bhne', q, dots) / n
        out = out.transpose(0, 2, 1, 3).reshape(b, n, HEADS * DIM_HEAD)
        return jnp.einsum('bnf,cf->bnc', out, Wout) + bout

    def _L0_ffn_ref(h, gate_w, gate_b, w1, b1, w2, b2):
        import math
        import jax, jax.numpy as jnp
        import numpy as np
        CAPACITY_FACTOR = 1.25
        B, L, D = h.shape
        E = gate_w.shape[1]
        T = B * L
        C = max(1, math.ceil(CAPACITY_FACTOR * T / E))
        x = h.reshape(T, D)
        logits = x @ gate_w + gate_b
        probs = jax.nn.softmax(logits, axis=-1)
        idx = jnp.argmax(probs, axis=-1)
        prb = jnp.take_along_axis(probs, idx[:, None], axis=1)[:, 0]
        one_hot = jax.nn.one_hot(idx, E, dtype=jnp.float32)
        pos = (jnp.cumsum(one_hot, axis=0) * one_hot).sum(-1).astype(jnp.int32) - 1
        kept = pos < C
        pos_safe = jnp.where(kept, pos, C)
        buf = jnp.zeros((E, C, D), dtype=h.dtype).at[idx, pos_safe].set(x, mode='drop')
        hmid = jax.nn.relu(jnp.einsum('ecd,edf->ecf', buf, w1) + b1[:, None, :])
        ybuf = jnp.einsum('ecf,efd->ecd', hmid, w2) + b2[:, None, :]
        pos_g = jnp.minimum(pos, C - 1)
        y_tok = ybuf[idx, pos_g] * (prb * kept)[:, None]
        y = y_tok.reshape(B, L, D)
        y = jnp.nan_to_num(y, nan=0.0, posinf=10000.0, neginf=-10000.0)
        return y

    def _L1_gnn_ref(x, edge_index, W0, a_src0, a_dst0, b0, gamma0, beta0, W1, a_src1, a_dst1, b1):
        import jax, jax.numpy as jnp
        import numpy as np
        N, E = (6250, 100000)
        IN, HID, HEADS, OUT = (256, 64, 4, 256)
        FIRST_OUT = HID * HEADS

        def gat_conv(x, src, dst, W, a_src, a_dst, b, concat):
            n = x.shape[0]
            H, C = a_src.shape
            h = (x @ W).reshape(n, H, C)
            es = jnp.einsum('nhc,hc->nh', h, a_src)[src]
            ed = jnp.einsum('nhc,hc->nh', h, a_dst)[dst]
            e = jax.nn.leaky_relu(es + ed, negative_slope=0.2)
            m = jax.ops.segment_max(e, dst, num_segments=n)
            p = jnp.exp(e - m[dst])
            z = jax.ops.segment_sum(p, dst, num_segments=n)
            alpha = p / z[dst]
            out = jax.ops.segment_sum(h[src] * alpha[:, :, None], dst, num_segments=n)
            out = out.reshape(n, H * C) if concat else out.mean(axis=1)
            return out + b

        def batchnorm(x, gamma, beta, eps=1e-05):
            mu = x.mean(axis=0)
            var = ((x - mu) ** 2).mean(axis=0)
            return gamma * (x - mu) / jnp.sqrt(var + eps) + beta
        n = x.shape[0]
        loops = jnp.arange(n, dtype=edge_index.dtype)
        src = jnp.concatenate([edge_index[0], loops])
        dst = jnp.concatenate([edge_index[1], loops])
        h = gat_conv(x, src, dst, W0, a_src0, a_dst0, b0, concat=True)
        h = batchnorm(h, gamma0, beta0)
        h = jax.nn.elu(h)
        h = gat_conv(h, src, dst, W1, a_src1, a_dst1, b1, concat=False)
        norm = jnp.maximum(jnp.linalg.norm(h, axis=-1, keepdims=True), 1e-12)
        return h / norm

    def _L1_mix_ref(x, t, w_qkv, mem_kv, w_out, b_out, g_out, g_pre):
        import jax, jax.numpy as jnp
        import numpy as np
        DIM = 256
        HEADS = 4
        DIM_HEAD = 32
        NUM_MEM = 4
        HIDDEN = HEADS * DIM_HEAD
        SCALE = DIM_HEAD ** (-0.5)

        def rmsnorm(x, g):
            n = jnp.linalg.norm(x, axis=-1, keepdims=True)
            return x / jnp.maximum(n, 1e-12) * g * x.shape[-1] ** 0.5
        b, n, c = x.shape
        xn = rmsnorm(x, g_pre)
        qkv = xn @ w_qkv
        q, k, v = jnp.split(qkv, 3, axis=-1)

        def to_heads(z):
            return z.reshape(b, n, HEADS, DIM_HEAD).transpose(0, 2, 3, 1)
        q, k, v = map(to_heads, (q, k, v))
        mk = jnp.broadcast_to(mem_kv[0], (b, HEADS, DIM_HEAD, NUM_MEM))
        mv = jnp.broadcast_to(mem_kv[1], (b, HEADS, DIM_HEAD, NUM_MEM))
        k = jnp.concatenate([mk, k], axis=-1)
        v = jnp.concatenate([mv, v], axis=-1)
        q = jax.nn.softmax(q, axis=-2) * SCALE
        k = jax.nn.softmax(k, axis=-1)
        context = jnp.einsum('bhdn,bhen->bhde', k, v)
        out = jnp.einsum('bhde,bhdn->bhen', context, q)
        out = out.transpose(0, 3, 1, 2).reshape(b, n, HIDDEN)
        out = rmsnorm(out @ w_out + b_out, g_out)
        return out + x

    def _L1_ffn_ref(x, W1, b1, Wg, bg, Wd, bd):
        import jax, jax.numpy as jnp
        import numpy as np
        C = 256
        HID = 1024
        E = 8
        TEMP = 1.0
        orig_shape = x.shape
        xf = x.reshape(-1, orig_shape[-1])
        H = jax.nn.gelu(xf @ W1 + b1, approximate=False)
        probs = jax.nn.softmax((H @ Wg + bg) / TEMP, axis=-1)
        assign = jnp.argmax(probs, axis=-1)
        out = jnp.zeros_like(xf)
        for e in range(Wd.shape[0]):
            y = H @ Wd[e] + bd[e]
            sel = (assign == e)[:, None]
            out = out + jnp.where(sel, probs[:, e:e + 1] * y, 0.0)
        return out.reshape(orig_shape)
    edge_index = jnp.stack([src, dst])
    xn = _layernorm(x, axis=-1)
    x = x + _L0_gnn_ref(xn, edge_index, edge_weight, L0_gnn_W1, L0_gnn_b1, L0_gnn_W2, L0_gnn_b2) + _L0_mix_ref(xn[None], L0_mix_Wqkv, L0_mix_Wout, L0_mix_bout)[0]
    x = x + _L0_ffn_ref(_layernorm(x, axis=-1)[None], L0_ffn_gate_w, L0_ffn_gate_b, L0_ffn_w1, L0_ffn_b1, L0_ffn_w2, L0_ffn_b2)[0]
    xn = _layernorm(x, axis=-1)
    x = x + _L1_gnn_ref(xn, edge_index, L1_gnn_W0, L1_gnn_a_src0, L1_gnn_a_dst0, L1_gnn_b0, L1_gnn_gamma0, L1_gnn_beta0, L1_gnn_W1, L1_gnn_a_src1, L1_gnn_a_dst1, L1_gnn_b1) + _L1_mix_ref(xn[None], L1_mix_t, L1_mix_w_qkv, L1_mix_mem_kv, L1_mix_w_out, L1_mix_b_out, L1_mix_g_out, L1_mix_g_pre)[0]
    x = x + _L1_ffn_ref(_layernorm(x, axis=-1)[None], L1_ffn_W1, L1_ffn_b1, L1_ffn_Wg, L1_ffn_bg, L1_ffn_Wd, L1_ffn_bd)[0]
    return x

_drawn_inputs = setup_inputs


def setup_inputs(seed=0):
    import zlib

    import numpy as np

    out = dict(_drawn_inputs(seed))
    spreads = {'L0_gnn_b1': (0.0, 0.1),
     'L0_gnn_b2': (0.0, 0.1),
     'L0_ffn_gate_b': (0.0, 0.1),
     'L0_ffn_b1': (0.0, 0.793),
     'L0_ffn_b2': (0.0, 0.565),
     'L1_gnn_b0': (0.0, 0.8),
     'L1_gnn_gamma0': (1.0, 0.6),
     'L1_gnn_beta0': (0.0, 0.8),
     'L1_gnn_b1': (0.0, 0.8),
     'L1_mix_b_out': (0.0, 0.1),
     'L1_mix_g_out': (1.0, 0.2),
     'L1_mix_g_pre': (1.0, 0.6),
     'L1_ffn_b1': (0.0, 0.8),
     'L1_ffn_bg': (0.0, 0.8),
     'L1_ffn_bd': (0.0, 0.8)}
    factors = {'L0_mix_bout': 5.013,
     'L1_gnn_W0': 2.99,
     'L1_gnn_a_src0': 8.0,
     'L1_gnn_a_dst0': 8.0,
     'L1_gnn_a_src1': 7.259,
     'L1_gnn_a_dst1': 8.0,
     'L1_mix_w_qkv': 5.435,
     'L1_mix_mem_kv': 8.0,
     'L1_mix_w_out': 5.425,
     'L1_ffn_W1': 6.115,
     'L1_ffn_Wg': 6.554,
     'L1_ffn_Wd': 7.683}
    for name, (base, spread) in spreads.items():
        noise = np.random.default_rng([zlib.crc32(name.encode()), seed]).standard_normal(out[name].shape)
        drawn = base * np.exp(spread * noise) if base else spread * noise
        out[name] = jnp.asarray(drawn.astype(out[name].dtype))
    for name, factor in factors.items():
        out[name] = (out[name] * factor).astype(out[name].dtype)
    return out
```

```python
import numpy as np
from contextlib import ExitStack
import concourse.bass as bass
from concourse import mybir

f32 = mybir.dt.float32
i32 = mybir.dt.int32
bf16 = mybir.dt.bfloat16
ALU = mybir.AluOpType
ACT = mybir.ActivationFunctionType
AX = mybir.AxisListType

P = 128
NODES = 6250
D = 256
NB = -(-NODES // P)
NPAD = NB * P
LASTROWS = NODES - (NB - 1) * P
EDGES = 100000
ET = -(-EDGES // P)
EG = -(-ET // P)
STEPS = ET + NB - 1
SG = -(-STEPS // P)
SPAD = SG * P
CG = 7
NG = NB // CG


class Kept:

    def __init__(self, nc, ctx):
        sb = lambda n, s, t=f32: ctx.enter_context(nc.sbuf_tensor(n, s, t))
        self.ident = sb("ident", [P, P])
        self.before = sb("before", [P, P])
        self.ones = sb("ones", [P, P])
        self.iota = sb("iota", [P, P])
        self.row_start = sb("row_start", [P, NB], i32)
        self.row_count = sb("row_count", [P, NB], i32)
        self.dinv = sb("dinv", [P, NB])
        self.src_idx = sb("src_idx", [P, SPAD], i32)
        self.lane = sb("lane", [P, SPAD])
        self.weight = sb("weight", [P, SPAD])
        self.step_blk = sb("step_blk", [P, SPAD], i32)
        self.tile_idx = sb("tile_idx", [P, SG], i32)


def bc(ap, shape):
    return ap.to_broadcast(shape)


def allocators(nc, ctx, stage):
    sems = []

    def clear():
        nc.clear_and_free_semaphores(sems)
        nc.all_engine_barrier()

    def sem(n):
        sems.append(nc.alloc_semaphore(name=f"{stage}_{n}"))
        return sems[-1]

    ctx.callback(clear)
    sb = lambda n, s, t=f32: ctx.enter_context(nc.sbuf_tensor(f"{stage}_{n}", s, t))
    ps = lambda n, s, t=f32: ctx.enter_context(nc.psum_tensor(f"{stage}_{n}", s, t))
    return sb, ps, sem


def stage_prepare(nc, k, src_rows, dst_rows, w_rows):
    T = 17
    assert ET % (2 * T) == 0
    with ExitStack() as ctx:
        sb, ps, sem = allocators(nc, ctx, "prep")
        iota_i = sb("iota_i", [P, P], i32)
        iota_sf = sb("iota_sf", [P, SPAD])
        iota_si = sb("iota_si", [P, SPAD], i32)
        tile_i = sb("tile_i", [P, EG], i32)
        tile_f = sb("tile_f", [P, EG])
        dst_r = sb("dst_r", [P, EG, P], i32)
        w_r = sb("w_r", [P, EG, P])
        dst_rf = sb("dst_rf", [P, EG, P])
        last_i = sb("last_i", [P, EG], i32)
        last_f = sb("last_f", [P, EG])
        key = sb("key", [P, EG])
        dst_t = sb("dst_t", [P, EG * P], i32)
        blk_ti = sb("blk_ti", [P, EG * P], i32)
        lane_ti = sb("lane_ti", [P, EG * P], i32)
        blk_t = sb("blk_t", [P, EG * P])
        lane_t = sb("lane_t", [P, EG * P])
        w_t = sb("w_t", [P, EG * P])
        lane_hot = sb("lane_hot", [P, 2, T, P])
        blk_hot = sb("blk_hot", [P, 2, T, 2, NB])
        cmp = sb("cmp", [P, 2, SPAD])
        counts = sb("counts", [P, 2 * NB])
        deg = sb("deg", [P, NB])
        pos = sb("pos", [P, NB])
        rdeg = sb("rdeg", [P, NB])
        totals = sb("totals", [P, NB])
        base = sb("base", [P, NB])
        zero = sb("zero", [P, NB])
        start_f = sb("start_f", [P, NB])
        step_tile = sb("step_tile", [P, SPAD])
        step_blk = sb("step_blk", [P, SPAD])
        diag = sb("diag", [P, SG, P])
        tile_col = sb("tile_col", [P, SG])
        got_src = sb("got_src", [P, SG, P], i32)
        got_dst = sb("got_dst", [P, SG, P], i32)
        got_w = sb("got_w", [P, SG, P])
        got_srcf = sb("got_srcf", [P, SG, P])
        got_dstf = sb("got_dstf", [P, SG, P])
        psA = ps("psA", [P, 2, 512])
        psB = ps("psB", [P, 2, 512])
        psC = ps("psC", [P, 512])
        psD = ps("psD", [P, 2, 512])
        loaded = sem("loaded")
        pool_done = sem("pool_done")
        v = sem("v_prep")
        turned = sem("turned")
        hot = sem("hot")
        hot_a = sem("hot_a")
        hot_prep = sem("hot_prep")
        counted = sem("counted")
        totalled = sem("totalled")
        compared = sem("compared")
        stepped = sem("stepped")
        gathered = sem("gathered")
        turned2 = sem("turned2")

        with nc.Block() as block:
            @block.sync
            def _(sp):
                sp.dma_start(dst_r[:, :, :], dst_rows.rearrange("(g r) l -> r g l", r=P)).then_inc(loaded, 16)
                sp.dma_start(w_r[:, :, :], w_rows.rearrange("(g r) l -> r g l", r=P)).then_inc(loaded, 16)

            @block.gpsimd
            def _(pool):
                nc.gpsimd.iota(iota_i[:, :], pattern=[[1, P]], base=0, channel_multiplier=0).then_inc(pool_done, 1)
                nc.gpsimd.iota(iota_si[:, :], pattern=[[1, SPAD]], base=0, channel_multiplier=0).then_inc(pool_done, 1)
                nc.gpsimd.iota(tile_i[:, :], pattern=[[P, EG]], base=0, channel_multiplier=1).then_inc(pool_done, 1)
                nc.gpsimd.memset(k.ones[:, :], 1.0).then_inc(pool_done, 1)
                nc.gpsimd.memset(k.ident[:, :], 0.0).then_inc(pool_done, 1)
                pool.wait_ge(pool_done, 5)
                nc.gpsimd.affine_select(out=k.ident[:, :], in_=k.ident[:, :], compare_op=ALU.not_equal, fill=1.0,
                                        base=0, pattern=[[-1, P]], channel_multiplier=1).then_inc(pool_done, 1)
                nc.gpsimd.affine_select(out=k.before[:, :], in_=k.ones[:, :], compare_op=ALU.is_gt, fill=0.0,
                                        base=0, pattern=[[1, P]], channel_multiplier=-1).then_inc(pool_done, 1)
                pool.wait_ge(stepped, 1)
                for g in range(SG):
                    idx = bass.IndirectOffsetOnAxis(ap=k.tile_idx[:, g:g + 1], axis=0)
                    for to, rows in ((got_src, src_rows), (got_dst, dst_rows), (got_w, w_rows)):
                        nc.gpsimd.indirect_dma_start(out=to[:, g, :], out_offset=None, in_=rows,
                                                     in_offset=idx).then_inc(gathered, 16)
                pool.wait_ge(gathered, 16 * 3 * SG)

            @block.tensor
            def _(pe):
                pe.wait_ge(pool_done, 7)
                pe.wait_ge(loaded, 32)
                pe.wait_ge(v, 4)
                for g in range(EG):
                    nc.tensor.transpose(psA[:, g // 4, g % 4 * P:(g % 4 + 1) * P], dst_rf[:, g, :], k.ident[:, :])
                    last = nc.tensor.transpose(psB[:, g // 4, g % 4 * P:(g % 4 + 1) * P], w_r[:, g, :], k.ident[:, :])
                last.then_inc(turned, 1)
                pe.wait_ge(v, 8)
                nc.tensor.matmul(psC[:, 0:2 * NB], k.ident[:, :], counts[:, :], start=True, stop=False)
                with nc.tensor.Fori(0, ET // T // 2) as i:
                    for h in range(2):
                        pe.wait_ge(hot, 2 * i + h + 1)
                        for t in range(T):
                            last = nc.tensor.matmul(psC[:, 0:2 * NB], lane_hot[:, h, t, :],
                                                    blk_hot[:, h, t, :, :].rearrange("p a b -> p (a b)"),
                                                    start=False, stop=False)
                        last.then_inc(counted, 1)
                nc.tensor.matmul(psC[:, 0:2 * NB], k.ident[:, :], counts[:, :], start=False, stop=True).then_inc(counted, 1)
                pe.wait_ge(v, 9)
                nc.tensor.matmul(psA[:, 0, 0:NB], k.before[:, :], counts[:, 0:NB], start=True, stop=True)
                nc.tensor.matmul(psA[:, 1, 0:NB], k.ones[:, :], counts[:, 0:NB], start=True, stop=True).then_inc(totalled, 1)
                for g in range(EG):
                    pe.wait_ge(compared, g + 1)
                    for h in range(2):
                        last = nc.tensor.matmul(psD[:, h, 0:SPAD // 2], k.ones[:, :],
                                                cmp[:, g % 2, h * (SPAD // 2):(h + 1) * (SPAD // 2)],
                                                start=(g == 0), stop=(g == EG - 1))
                    last.then_inc(totalled, 1)
                pe.wait_ge(turned2, 1)
                for g in range(SG):
                    nc.tensor.transpose(psA[:, g // 4, g % 4 * P:(g % 4 + 1) * P], got_srcf[:, g, :], k.ident[:, :])
                    nc.tensor.transpose(psB[:, g // 4, g % 4 * P:(g % 4 + 1) * P], got_dstf[:, g, :], k.ident[:, :])
                    last = nc.tensor.transpose(psD[:, g // 4, g % 4 * P:(g % 4 + 1) * P], got_w[:, g, :], k.ident[:, :])
                last.then_inc(turned2, 1)

            @block.vector
            def _(dve):
                dve.wait_ge(pool_done, 3)
                dve.wait_ge(loaded, 32)
                nc.vector.tensor_copy(k.iota[:, :], iota_i[:, :]).then_inc(v, 1)
                nc.vector.tensor_copy(iota_sf[:, :], iota_si[:, :]).then_inc(v, 1)
                nc.vector.tensor_copy(tile_f[:, :], tile_i[:, :]).then_inc(v, 1)
                nc.vector.tensor_copy(dst_rf[:, :, :], dst_r[:, :, :]).then_inc(v, 1)
                nc.vector.tensor_single_scalar(last_i[:, :], dst_r[:, :, P - 1], 7, op=ALU.arith_shift_right).then_inc(v, 1)
                nc.vector.memset(counts[:, :], 0.0).then_inc(v, 1)
                dve.wait_ge(v, 5)
                nc.vector.tensor_copy(last_f[:, :], last_i[:, :]).then_inc(v, 1)
                dve.wait_ge(v, 7)
                nc.vector.tensor_tensor(key[:, :], last_f[:, :], tile_f[:, :], ALU.add).then_inc(v, 1)
                dve.wait_ge(turned, 1)
                for h in range(2):
                    w = 512 if h == 0 else EG * P - 512
                    nc.vector.tensor_copy(dst_t[:, h * 512:h * 512 + w], psA[:, h, 0:w]).then_inc(hot_prep, 1)
                    nc.vector.tensor_copy(w_t[:, h * 512:h * 512 + w], psB[:, h, 0:w]).then_inc(hot_prep, 1)
                dve.wait_ge(hot_prep, 4)
                nc.vector.tensor_single_scalar(blk_ti[:, :], dst_t[:, :], 7, op=ALU.arith_shift_right).then_inc(hot_prep, 1)
                nc.vector.tensor_single_scalar(lane_ti[:, :], dst_t[:, :], P - 1, op=ALU.bitwise_and).then_inc(hot_prep, 1)
                dve.wait_ge(hot_prep, 6)
                nc.vector.tensor_copy(blk_t[:, :], blk_ti[:, :]).then_inc(hot_prep, 1)
                nc.vector.tensor_copy(lane_t[:, :], lane_ti[:, :]).then_inc(hot_prep, 1)
                dve.wait_ge(hot_prep, 8)

                def make_hot(t0, h):
                    nc.vector.tensor_tensor(lane_hot[:, h, :, :], k.iota[:, :].unsqueeze(1).to_broadcast([P, T, P]),
                                            lane_t[:, bass.ds(t0, T)].unsqueeze(2).to_broadcast([P, T, P]), ALU.is_equal).then_inc(hot_a, 1)
                    nc.vector.tensor_tensor(blk_hot[:, h, :, 0, :], k.iota[:, 0:NB].unsqueeze(1).to_broadcast([P, T, NB]),
                                            blk_t[:, bass.ds(t0, T)].unsqueeze(2).to_broadcast([P, T, NB]), ALU.is_equal).then_inc(hot_a, 1)

                def weigh_hot(t0, h):
                    nc.vector.tensor_tensor(blk_hot[:, h, :, 1, :], blk_hot[:, h, :, 0, :],
                                            w_t[:, bass.ds(t0, T)].unsqueeze(2).to_broadcast([P, T, NB]), ALU.mult).then_inc(hot, 1)

                make_hot(0, 0)
                make_hot(T, 1)
                dve.wait_ge(hot_a, 2)
                weigh_hot(0, 0)
                dve.wait_ge(hot_a, 4)
                weigh_hot(T, 1)
                with nc.vector.Fori(1, ET // T // 2) as i:
                    for h in range(2):
                        dve.wait_ge(counted, 2 * i + h - 1)
                        make_hot((2 * i + h) * T, h)
                        dve.wait_ge(hot_a, 4 * i + 2 * h + 2)
                        weigh_hot((2 * i + h) * T, h)
                dve.wait_ge(counted, ET // T + 1)
                nc.vector.tensor_copy(counts[:, :], psC[:, 0:2 * NB]).then_inc(v, 1)
                dve.wait_ge(v, 9)
                nc.vector.tensor_scalar(deg[:, :], counts[:, NB:2 * NB], 1.0, None, ALU.add).then_inc(v, 1)
                nc.vector.memset(zero[:, :], 0.0).then_inc(v, 1)
                dve.wait_ge(v, 11)
                nc.vector.tensor_scalar(pos[:, :], deg[:, :], 0.0, None, ALU.is_gt).then_inc(v, 1)
                nc.vector.tensor_scalar(deg[:, :], deg[:, :], 1e-30, None, ALU.max).then_inc(v, 1)
                dve.wait_ge(v, 13)
                nc.vector.reciprocal(rdeg[:, :], deg[:, :]).then_inc(v, 1)
                dve.wait_ge(totalled, 1)
                nc.vector.tensor_copy(totals[:, :], psA[:, 1, 0:NB]).then_inc(v, 1)
                dve.wait_ge(v, 15)
                nc.vector.tensor_tensor_scan(base[:, :], totals[:, :], zero[:, :], 0.0, ALU.add, ALU.add).then_inc(v, 1)
                dve.wait_ge(v, 16)
                nc.vector.tensor_tensor(base[:, :], base[:, :], totals[:, :], ALU.subtract).then_inc(v, 1)
                dve.wait_ge(v, 17)
                nc.vector.tensor_tensor(start_f[:, :], base[:, :], psA[:, 0, 0:NB], ALU.add).then_inc(v, 1)
                dve.wait_ge(v, 18)
                nc.vector.tensor_copy(k.row_start[:, :], start_f[:, :]).then_inc(v, 1)
                nc.vector.tensor_copy(k.row_count[:, :], counts[:, 0:NB]).then_inc(v, 1)
                for g in range(EG):
                    if g >= 2:
                        dve.wait_ge(totalled, g)
                    nc.vector.tensor_scalar(cmp[:, g % 2, :], iota_sf[:, :], key[:, g:g + 1], None, ALU.is_gt).then_inc(compared, 1)
                dve.wait_ge(totalled, EG + 1)
                for h in range(2):
                    nc.vector.tensor_copy(step_tile[:, h * (SPAD // 2):(h + 1) * (SPAD // 2)], psD[:, h, 0:SPAD // 2]).then_inc(v, 1)
                dve.wait_ge(v, 22)
                nc.vector.tensor_tensor(step_blk[:, :], iota_sf[:, :], step_tile[:, :], ALU.subtract).then_inc(v, 1)
                nc.vector.tensor_tensor(diag[:, :, :], step_tile[:, :].rearrange("p (g l) -> p g l", l=P),
                                        k.ident[:, :].unsqueeze(1).to_broadcast([P, SG, P]), ALU.mult).then_inc(v, 1)
                dve.wait_ge(v, 24)
                nc.vector.tensor_reduce(tile_col[:, :], diag[:, :, :], AX.X, ALU.add).then_inc(v, 1)
                nc.vector.tensor_copy(k.step_blk[:, :], step_blk[:, :]).then_inc(v, 1)
                dve.wait_ge(v, 25)
                nc.vector.tensor_copy(k.tile_idx[:, :], tile_col[:, :]).then_inc(stepped, 1)
                dve.wait_ge(gathered, 16 * 3 * SG)
                nc.vector.tensor_copy(got_srcf[:, :, :], got_src[:, :, :]).then_inc(v, 1)
                nc.vector.tensor_copy(got_dstf[:, :, :], got_dst[:, :, :]).then_inc(turned2, 1)
                dve.wait_ge(turned2, 2)
                for h in range(2):
                    w = 512 if h == 0 else SPAD - 512
                    c = slice(h * 512, h * 512 + w)
                    nc.vector.tensor_copy(k.src_idx[:, c], psA[:, h, 0:w]).then_inc(v, 1)
                    nc.vector.scalar_tensor_tensor(out=k.lane[:, c], in0=step_blk[:, c], scalar=-float(P), in1=psB[:, h, 0:w],
                                                   op0=ALU.mult, op1=ALU.add).then_inc(v, 1)
                    nc.vector.tensor_copy(k.weight[:, c], psD[:, h, 0:w]).then_inc(v, 1)

            @block.scalar
            def _(act):
                act.wait_ge(v, 14)
                nc.scalar.activation(rdeg[:, :], rdeg[:, :], ACT.Sqrt).then_inc(turned, 1)

        with nc.Block() as block:
            @block.vector
            def _(dve):
                nc.vector.tensor_tensor(k.dinv[:, :], rdeg[:, :], pos[:, :], ALU.mult).then_inc(v, 1)


HALF = 8
PASSES = -(-STEPS // (2 * HALF))
BANKS = 4
assert PASSES * 2 * HALF <= SPAD


def stage_aggregate(nc, k, name, table, acc, width, weights, heads=0, side=None):
    with ExitStack() as ctx:
        sb, ps, sem = allocators(nc, ctx, name)
        rows = sb("rows", [P, 2, HALF, width])
        scaled = sb("scaled", [P, 2, HALF, width]) if heads else rows
        hot = sb("hot", [P, 2, HALF, P])
        idx = sb("idx", [P, 2, HALF], i32)
        part = [ps(f"part{j}", [P, 512]) for j in range(BANKS)]
        gathered = [sem(f"gathered{j}") for j in range(2 * HALF)]
        idx_ready = sem("idx_ready")
        hot_ready = sem("hot_ready")
        scaled_ready = sem("scaled_ready")
        multiplied = sem("multiplied")
        added = sem("added")
        slot_free = sem("slot_free")
        row_seen = sem("row_seen")
        ones_ready = sem("ones_ready")
        state = side.open(nc, k, ctx) if side else None
        SIDE = NB if side else 0

        with nc.Block() as block:
            @block.sync
            def _(sp):
                if side:
                    side.sync(sp, state)

            @block.gpsimd
            def _(pool):
                if width > D and not heads:
                    nc.gpsimd.memset(rows[:, :, :, D:width], 1.0).then_inc(ones_ready, 1)

                def gather(i, first):
                    for h in range(2):
                        pool.wait_ge(idx_ready, 2 * i + h + 1)
                        pool.sem_inc(slot_free, 1)
                        for j in range(HALF):
                            if not first:
                                pool.wait_ge(multiplied, 2 * HALF * (i - 1) + HALF * h + j + 1)
                                pool.sem_inc(slot_free, 1)
                            nc.gpsimd.indirect_dma_start(
                                out=rows[:, h, j, 0:D], out_offset=None, in_=table,
                                in_offset=bass.IndirectOffsetOnAxis(ap=idx[:, h, j:j + 1], axis=0),
                            ).then_inc(gathered[h * HALF + j], 16)

                gather(0, True)
                with nc.gpsimd.Fori(1, PASSES) as i:
                    gather(i, False)

            @block.scalar
            def _(act):
                if side:
                    side.act_start(act, state)

                def scale_rows(i):
                    for h in range(2):
                        for j in range(HALF):
                            act.wait_ge(gathered[h * HALF + j], 16 * (i + 1))
                            act.sem_inc(row_seen, 1)
                            for q in range(heads):
                                c = slice(q * (D // heads), (q + 1) * (D // heads))
                                nc.scalar.activation(
                                    scaled[:, h, j, c], rows[:, h, j, c], ACT.Copy,
                                    scale=weights[:, bass.ds((2 * HALF * i + HALF * h + j) * heads + q, 1)],
                                ).then_inc(scaled_ready, 1)

                with nc.scalar.Fori(0, PASSES) if not SIDE else nc.scalar.Fori(0, SIDE) as i:
                    if heads:
                        scale_rows(i)
                    if side:
                        side.act(act, state, i)
                if side:
                    if heads:
                        with nc.scalar.Fori(SIDE, PASSES) as i:
                            scale_rows(i)
                    side.act_end(act, state)

            @block.tensor
            def _(pe):
                if side:
                    side.pe_start(pe, state)
                if width > D and not heads:
                    pe.wait_ge(ones_ready, 1)

                def products(i, first):
                    for h in range(2):
                        pe.wait_ge(hot_ready, 2 * i + h + 1)
                        for j in range(HALF):
                            s = 2 * HALF * i + HALF * h + j
                            if heads:
                                pe.wait_ge(scaled_ready, heads * s + heads)
                            else:
                                pe.wait_ge(gathered[h * HALF + j], 16 * (i + 1))
                            if not first or h * HALF + j >= BANKS:
                                pe.wait_ge(added, s - BANKS + 1)
                            nc.tensor.matmul(part[j % BANKS][:, 0:width], hot[:, h, j, :], scaled[:, h, j, :],
                                             start=True, stop=True).then_inc(multiplied, 1)

                products(0, True)
                if side:
                    side.pe(pe, state, 0)
                with nc.tensor.Fori(1, SIDE or PASSES) as i:
                    products(i, False)
                    if side:
                        side.pe(pe, state, i)
                if side:
                    with nc.tensor.Fori(SIDE, PASSES) as i:
                        products(i, False)
                    side.pe_end(pe, state)

            @block.vector
            def _(dve):
                if side:
                    side.dve_start(dve, state)

                def make_hot(n, h):
                    s = HALF * n
                    nc.vector.tensor_copy(idx[:, h, :], k.src_idx[:, bass.ds(s, HALF)]).then_inc(idx_ready, 1)
                    if heads:
                        nc.vector.tensor_copy(
                            scaled[:, h, :, D:D + heads],
                            weights[:, bass.ds(s * heads, HALF * heads)].rearrange("p (j q) -> p j q", q=heads))
                    for j in range(HALF):
                        last = nc.vector.tensor_scalar(
                            hot[:, h, j, :], k.iota[:, :], k.lane[:, bass.ds(s + j, 1)],
                            None if heads else weights[:, bass.ds(s + j, 1)],
                            ALU.is_equal, *(() if heads else (ALU.mult,)))
                    last.then_inc(hot_ready, 1)

                def add_parts(n, h):
                    s = HALF * n
                    _, blocks = nc.values_load_multi_w_load_instructions(
                        k.step_blk[0:1, bass.ds(s, HALF)], engines=(mybir.EngineType.DVE,), min_val=0, max_val=NB - 1,
                        skip_runtime_bounds_check_because="a step's block lies in the blocks of its edge tile")
                    for j in range(HALF):
                        dve.wait_ge(multiplied, s + j + 1)
                        dve.wait_ge(added, s + j)
                        a = acc[:, bass.ds(blocks[j], 1), 0:width]
                        nc.vector.tensor_tensor(a, a, part[j % BANKS][:, 0:width].unsqueeze(1), ALU.add).then_inc(added, 1)

                make_hot(0, 0)
                make_hot(1, 1)

                def one_pass(i, with_side):
                    for h in range(2):
                        add_parts(2 * i + h, h)
                        make_hot(2 * i + h + 2, h)
                        if with_side:
                            side.dve(dve, state, i - 1, h)

                one_pass(0, False)
                if side:
                    with nc.vector.Fori(1, SIDE + 1) as i:
                        one_pass(i, True)
                with nc.vector.Fori(SIDE + 1, PASSES - 1) as i:
                    one_pass(i, False)
                for h in range(2):
                    add_parts(2 * (PASSES - 1) + h, h)
                if side:
                    side.dve_end(dve, state)


def sharpen_inverse_root(nc, dve, v, at, s, y, t):
    nc.vector.tensor_tensor(t, y, y, ALU.mult).then_inc(v, 1)
    dve.wait_ge(v, at + 1)
    nc.vector.tensor_tensor(t, t, s, ALU.mult).then_inc(v, 1)
    dve.wait_ge(v, at + 2)
    nc.vector.tensor_scalar(t, t, -0.5, 1.5, ALU.mult, ALU.add).then_inc(v, 1)
    dve.wait_ge(v, at + 3)
    nc.vector.tensor_tensor(y, y, t, ALU.mult).then_inc(v, 1)
    dve.wait_ge(v, at + 4)


def stage_layernorm(nc, k, name, x, xn, x_dram=None):
    with ExitStack() as ctx:
        sb, ps, sem = allocators(nc, ctx, name)
        stats = sb("stats", [P, NB, 6])
        mean = sb("mean", [P, NB])
        apart = sb("apart", [P, NB])
        var = sb("var", [P, NB])
        dev = sb("dev", [P, NB])
        rstd = sb("rstd", [P, NB])
        loaded = [sem(f"loaded{g}") for g in range(NG)]
        summed = sem("summed")
        v = sem("v")
        root = sem("root")
        with nc.Block() as block:
            @block.sync
            def _(sp):
                if x_dram is not None:
                    for g in range(NG):
                        b = slice(g * CG, (g + 1) * CG)
                        sp.dma_start(x[:, b, 0:D], x_dram.rearrange("(b l) d -> l b d", l=P)[:, b, :]).then_inc(loaded[g], 16)

            @block.vector
            def _(dve):
                if x_dram is not None:
                    for g in range(NG):
                        dve.wait_ge(loaded[g], 16)
                with nc.vector.Fori(0, NG) as g:
                    for j in range(CG):
                        nc.vector.bn_stats(stats[:, bass.ds(g * CG + j, 1), :], x[:, bass.ds(g * CG + j, 1), 0:D]).then_inc(summed, 1)
                dve.wait_ge(summed, NB)
                even, odd = stats[:, :, 1], stats[:, :, 4]
                nc.vector.tensor_tensor(mean[:, :], even, odd, ALU.add).then_inc(v, 1)
                nc.vector.tensor_tensor(apart[:, :], even, odd, ALU.subtract).then_inc(v, 1)
                nc.vector.tensor_tensor(var[:, :], stats[:, :, 2], stats[:, :, 5], ALU.add).then_inc(v, 1)
                dve.wait_ge(v, 3)
                nc.vector.tensor_scalar(mean[:, :], mean[:, :], 0.5, None, ALU.mult).then_inc(v, 1)
                nc.vector.tensor_tensor(apart[:, :], apart[:, :], apart[:, :], ALU.mult).then_inc(v, 1)
                nc.vector.tensor_scalar(var[:, :], var[:, :], 1.0 / D, 1e-5, ALU.mult, ALU.add).then_inc(v, 1)
                dve.wait_ge(v, 6)
                nc.vector.scalar_tensor_tensor(out=var[:, :], in0=apart[:, :], scalar=0.25, in1=var[:, :],
                                               op0=ALU.mult, op1=ALU.add).then_inc(v, 1)
                dve.wait_ge(root, 1)
                nc.vector.reciprocal(rstd[:, :], dev[:, :]).then_inc(v, 1)
                dve.wait_ge(v, 8)
                sharpen_inverse_root(nc, dve, v, 8, var[:, :], rstd[:, :], apart[:, :])
                with nc.vector.Fori(0, NG) as g:
                    for j in range(CG):
                        n = g * CG + j
                        nc.vector.tensor_scalar(xn[:, bass.ds(n, 1), :], x[:, bass.ds(n, 1), 0:D],
                                                mean[:, bass.ds(n, 1)], rstd[:, bass.ds(n, 1)],
                                                ALU.subtract, ALU.mult)

            @block.scalar
            def _(act):
                act.wait_ge(v, 7)
                nc.scalar.activation(dev[:, :], var[:, :], ACT.Sqrt).then_inc(root, 1)


def stage_scale_store(nc, k, name, x, scale, acc, table):
    with ExitStack() as ctx:
        sb, ps, sem = allocators(nc, ctx, name)
        v = sem("v")
        stored = sem("stored")
        t = table.rearrange("(b l) d -> l b d", l=P)
        with nc.Block() as block:
            @block.vector
            def _(dve):
                with nc.vector.Fori(0, NG) as g:
                    for j in range(CG):
                        n = g * CG + j
                        nc.vector.tensor_scalar(acc[:, bass.ds(n, 1), 0:D], x[:, bass.ds(n, 1), 0:D],
                                                scale[:, bass.ds(n, 1)], None, ALU.mult).then_inc(v, 1)

            @block.sync
            def _(sp):
                for g in range(NG):
                    b = slice(g * CG, (g + 1) * CG)
                    sp.wait_ge(v, (g + 1) * CG)
                    sp.dma_start(t[:, b, :], acc[:, b, 0:D]).then_inc(stored, 16)
                sp.wait_ge(stored, 16 * NG)


HEADS0, DH0 = 8, 64
INNER0 = HEADS0 * DH0


class Mix0Side:

    def __init__(self, xn, wkv_t):
        self.xn, self.wkv_t = xn, wkv_t

    def open(self, nc, k, ctx):
        self.nc, self.k = nc, k
        sb, ps, sem = allocators(nc, ctx, "mix0")
        self.w = sb("w", [P, 2, 2 * INNER0])
        self.mean = sb("mean", [P, 2, 2 * HEADS0])
        self.xt = sb("xt", [P, D])
        self.staged = sb("staged", [P, D])
        self.stage_ready = sem("stage_ready")
        self.sq = sb("sq", [P, 2 * HEADS0, DH0])
        self.kc = sb("kc", [P, INNER0])
        self.vs = sb("vs", [P, INNER0])
        self.var = sb("var", [P, 2 * HEADS0])
        self.dev = sb("dev", [P, HEADS0])
        self.pt = ps("pt", [P, 512])
        self.kv = ps("kv", [P, 2, 512])
        self.dots = ps("dots", [P, 512])
        self.loaded, self.centred, self.zeroed, self.turned = sem("loaded"), sem("centred"), sem("zeroed"), sem("turned")
        self.copied, self.projected, self.squared, self.varied = sem("copied"), sem("projected"), sem("squared"), sem("varied")
        self.rooted, self.weighed, self.scaled, self.dotted = sem("rooted"), sem("weighed"), sem("scaled"), sem("dotted")
        self.closed, self.cleared = sem("closed"), sem("cleared")
        return self

    def sync(self, sp, s):
        sp.dma_start(s.w[:, :, :], s.wkv_t.rearrange("(c p) f -> p c f", p=P)).then_inc(s.loaded, 16)
        sp.sem_inc(s.turned, 1)
        with self.nc.sync.Fori(0, NB) as i:
            sp.wait_ge(s.turned, i + 1)
            sp.dma_start(s.staged[:, :], s.xn[:, bass.ds(i, 1), :].rearrange("p a d -> p (a d)")).then_inc(s.stage_ready, 16)

    def dve_start(self, dve, s):
        v = self.nc.vector
        v.memset(s.xt[:, :], 0.0).then_inc(s.zeroed, 1)
        v.memset(s.kc[:, :], 0.0).then_inc(s.zeroed, 1)
        v.memset(s.vs[:, :], 0.0).then_inc(s.zeroed, 1)
        dve.wait_ge(s.loaded, 16)
        w = s.w[:, :, :].rearrange("p c (h d) -> p (c h) d", d=DH0)
        mean = s.mean[:, :, :].rearrange("p c h -> p (c h)")
        v.tensor_reduce(mean, w, AX.X, ALU.add).then_inc(s.centred, 1)
        dve.wait_ge(s.centred, 1)
        v.tensor_scalar(mean, mean, -1.0 / DH0, None, ALU.mult).then_inc(s.centred, 1)
        dve.wait_ge(s.centred, 2)
        v.tensor_tensor(w, w, mean.unsqueeze(2).to_broadcast([P, 4 * HEADS0, DH0]), ALU.add).then_inc(s.centred, 1)

    def pe_start(self, pe, s):
        t = self.nc.tensor
        pe.wait_ge(s.zeroed, 3)
        pe.wait_ge(s.centred, 3)
        t.matmul(s.dots[:, :], self.k.ident[:, :], s.kc[:, :], start=True, stop=False)

    def products(self, pe, s):
        for g in range(HEADS0 // 2):
            c = slice(g * P, (g + 1) * P)
            last = self.nc.tensor.matmul(s.dots[:, c], s.vs[:, c], s.kc[:, c], start=False, stop=False)
        last.then_inc(s.dotted, 1)

    def project(self, pe, s):
        for h in range(2):
            for c in range(2):
                last = self.nc.tensor.matmul(s.kv[:, h, :], s.xt[:, c * P:(c + 1) * P], s.w[:, c, h * 512:(h + 1) * 512],
                                             start=(c == 0), stop=(c == 1))
        last.then_inc(s.projected, 1)

    def pe(self, pe, s, i):
        first = isinstance(i, int)
        if not first:
            pe.wait_ge(s.scaled, i)
            pe.wait_ge(s.squared, 2 * i)
            pe.wait_ge(s.copied, i)
        self.products(pe, s)
        self.project(pe, s)
        pe.wait_ge(s.stage_ready, 16 * i + 16)
        for c in range(2):
            last = self.nc.tensor.transpose(s.pt[:, c * P:(c + 1) * P], s.staged[:, c * P:(c + 1) * P], self.k.ident[:, :])
        last.then_inc(s.turned, 1)

    def pe_end(self, pe, s):
        for n in range(2):
            pe.wait_ge(s.scaled, NB + n)
            pe.wait_ge(s.squared, 2 * (NB + n))
            pe.wait_ge(s.copied, NB)
            self.products(pe, s)
            if n == 0:
                self.project(pe, s)
        pe.wait_ge(s.cleared, 1)
        self.nc.tensor.matmul(s.dots[:, :], self.k.ident[:, :], s.kc[:, :], start=False, stop=True).then_inc(s.closed, 1)

    def act_start(self, act, s):
        act.wait_ge(s.zeroed, 3)

    def evacuate(self, act, s, i):
        a = self.nc.scalar
        act.wait_ge(s.projected, i + 1)
        a.activation(s.sq[:, :, :].rearrange("p h d -> p (h d)"), s.kv[:, :, :].rearrange("p a n -> p (a n)"),
                     ACT.Square).then_inc(s.squared, 1)
        a.activation(s.kc[:, :], s.kv[:, 0, :], ACT.Copy).then_inc(s.squared, 1)
        act.wait_ge(s.varied, 3 * i + 3)
        a.activation(s.dev[:, :], s.dev[:, :], ACT.Sqrt).then_inc(s.rooted, 1)

    def act(self, act, s, i):
        act.wait_ge(s.turned, i + 2)
        self.nc.scalar.activation(s.xt[:, :], s.pt[:, 0:D], ACT.Copy).then_inc(s.copied, 1)
        self.evacuate(act, s, i)

    def act_end(self, act, s):
        self.evacuate(act, s, NB)

    def vary(self, dve, s, i):
        v = self.nc.vector
        dve.wait_ge(s.squared, 2 * i + 1)
        v.tensor_reduce(s.var[:, :], s.sq[:, :, :], AX.X, ALU.add).then_inc(s.varied, 1)
        dve.wait_ge(s.varied, 3 * i + 1)
        v.tensor_scalar(s.var[:, :], s.var[:, :], 1.0 / DH0, 1e-5, ALU.mult, ALU.add).then_inc(s.varied, 1)
        dve.wait_ge(s.varied, 3 * i + 2)
        v.tensor_tensor(s.dev[:, :], s.var[:, 0:HEADS0], s.var[:, HEADS0:], ALU.mult).then_inc(s.varied, 1)

    def scale(self, dve, s, i):
        v = self.nc.vector
        dve.wait_ge(s.rooted, i + 1)
        v.reciprocal(s.dev[:, :], s.dev[:, :]).then_inc(s.weighed, 1)
        dve.wait_ge(s.weighed, i + 1)
        v.tensor_tensor(s.vs[:, :].rearrange("p (h d) -> p h d", d=DH0), s.kv[:, 1, :].rearrange("p (h d) -> p h d", d=DH0),
                        s.dev[:, :].unsqueeze(2).to_broadcast([P, HEADS0, DH0]), ALU.mult).then_inc(s.scaled, 1)

    def dve(self, dve, s, i, h):
        if h == 0:
            self.vary(dve, s, i)
        else:
            self.scale(dve, s, i)

    def dve_end(self, dve, s):
        self.vary(dve, s, NB)
        self.scale(dve, s, NB)
        v = self.nc.vector
        dve.wait_ge(s.dotted, NB + 2)
        v.memset(s.kc[:, :], 0.0).then_inc(s.cleared, 1)
        dve.wait_ge(s.closed, 1)
        for g in range(HEADS0 // 2):
            for a in range(2):
                r, c = slice(a * DH0, (a + 1) * DH0), g * P + a * DH0
                v.tensor_scalar(self.k.dots[r, g, a * DH0:(a + 1) * DH0], s.dots[r, c:c + DH0], 1.0 / NODES, None, ALU.mult)


def stage_mix0_fold(nc, k, wq, wout_t):
    with ExitStack() as ctx:
        sb, ps, sem = allocators(nc, ctx, "fold0")
        wq_sb = sb("wq", [P, 4, D])
        wo_sb = sb("wo", [P, 4, D])
        a1 = sb("a1", [P, 4, D])
        pa = ps("pa", [P, 4, D])
        pm = ps("pm", [P, 2, D])
        loaded, made, copied, folded = sem("loaded"), sem("made"), sem("copied"), sem("folded")
        with nc.Block() as block:
            @block.sync
            def _(sp):
                sp.dma_start(wq_sb[:, :, :], wq.rearrange("(g p) c -> p g c", p=P)).then_inc(loaded, 16)
                sp.dma_start(wo_sb[:, :, :], wout_t.rearrange("(g p) c -> p g c", p=P)).then_inc(loaded, 16)

            @block.tensor
            def _(pe):
                pe.wait_ge(loaded, 32)
                for g in range(4):
                    nc.tensor.matmul(pa[:, g, :], k.dots[:, g, :], wo_sb[:, g, :], start=True, stop=True).then_inc(made, 1)
                pe.wait_ge(copied, 1)
                for c in range(2):
                    for g in range(4):
                        last = nc.tensor.matmul(pm[:, c, :], wq_sb[:, g, c * P:(c + 1) * P], a1[:, g, :],
                                                start=(g == 0), stop=(g == 3))
                last.then_inc(folded, 1)

            @block.vector
            def _(dve):
                dve.wait_ge(made, 4)
                nc.vector.tensor_copy(a1[:, :, :], pa[:, :, :]).then_inc(copied, 1)
                dve.wait_ge(folded, 1)
                nc.vector.tensor_copy(k.mix[:, :, :], pm[:, :, :])


def half_index(n, h):
    return (n - h) // 2 + 1


def stage_gcn_dense(nc, k, name, acc, w, bias, table=None, xn=None, x_in=None, bias2=None):
    last_layer = table is None
    with ExitStack() as ctx:
        sb, ps, sem = allocators(nc, ctx, name)
        terms = 2 if last_layer else 1
        w_sb = sb("w", [P, 2, D])
        b_sb = sb("b", [P, 2, D])
        xt = sb("xt", [P, 2, terms * D])
        staged = sb("staged", [P, 2, terms, D])
        xin = sb("xin", [P, 2, D])
        pt = ps("pt", [P, 2, 512])
        po = ps("po", [P, 2, 512])
        loaded, biased, turned, copied = sem("loaded"), sem("biased"), sem("turned"), sem("copied")
        multiplied, done, stored = sem("multiplied"), sem("done"), sem("stored")
        scaled, summed = sem("scaled"), sem("summed")
        xloaded = [sem("xloaded0"), sem("xloaded1")]
        rows = lambda ap: ap.rearrange("(b l) d -> l b d", l=P)

        def paired(engine, one):
            with engine.Fori(0, NB // 2) as i:
                for h in range(2):
                    one(2 * i + h, h)
            one(NB - 1, 0)

        with nc.Block() as block:
            @block.sync
            def _(sp):
                sp.dma_start(w_sb[:, :, :], w.rearrange("(c p) n -> p c n", p=P)).then_inc(loaded, 16)
                sp.dma_start(b_sb[:, 0, :], bias.rearrange("(a n) -> a n", a=1).to_broadcast([P, D])).then_inc(loaded, 16)
                if last_layer:
                    sp.dma_start(b_sb[:, 1, :], bias2.rearrange("(a n) -> a n", a=1).to_broadcast([P, D])).then_inc(loaded, 16)

                    def load(n, h):
                        sp.wait_ge(done, n + 1)
                        sp.wait_ge(turned, n + 1)
                        sp.dma_start(staged[:, h, 1, :], xn[:, bass.ds(n, 1), :].rearrange("p a d -> p (a d)")).then_inc(xloaded[h], 16)
                        sp.dma_start(xin[:, h:h + 1, :], rows(x_in)[:, bass.ds(n, 1), :]).then_inc(xloaded[h], 16)
                    paired(nc.sync, load)
                if not last_layer:
                    for g in range(NG):
                        b = slice(g * CG, (g + 1) * CG)
                        sp.wait_ge(done, (g + 1) * CG + 2)
                        sp.dma_start(rows(table)[:, b, :], acc[:, b, 0:D]).then_inc(stored, 16)
                    sp.wait_ge(stored, 16 * NG)

            @block.tensor
            def _(pe):
                pe.sem_inc(multiplied, 2)
                pe.sem_inc(turned, 2)
                pe.wait_ge(loaded, 32 + 16 * last_layer)

                def turn(n, h):
                    pe.wait_ge(copied, n + 1)
                    pe.wait_ge(scaled, n + 1)
                    if last_layer:
                        pe.wait_ge(xloaded[h], 32 * half_index(n, h))
                    for t in range(terms):
                        for c in range(2):
                            last = nc.tensor.transpose(pt[:, h, t * D + c * P:t * D + (c + 1) * P],
                                                       staged[:, h, t, c * P:(c + 1) * P], k.ident[:, :])
                    last.then_inc(turned, 1)

                def multiply(n, h):
                    pe.wait_ge(copied, n + 3)
                    pe.wait_ge(done, n + 1)
                    for t in range(terms):
                        for c in range(2):
                            rhs = w_sb[:, c, :] if t == 0 else k.mix[:, c, :]
                            last = nc.tensor.matmul(po[:, h, 0:D], xt[:, h, t * D + c * P:t * D + (c + 1) * P], rhs,
                                                    start=(t + c == 0), stop=(t == terms - 1 and c == 1))
                    last.then_inc(multiplied, 1)

                turn(0, 0)
                with nc.tensor.Fori(0, NB // 2) as i:
                    turn(2 * i + 1, 1)
                    multiply(2 * i, 0)
                    turn(2 * i + 2, 0)
                    multiply(2 * i + 1, 1)
                multiply(NB - 1, 0)

            @block.scalar
            def _(act):
                act.sem_inc(copied, 2)

                def copy(n, h):
                    act.wait_ge(turned, n + 3)
                    act.wait_ge(multiplied, n + 1)
                    nc.scalar.activation(xt[:, h, :], pt[:, h, 0:terms * D], ACT.Copy).then_inc(copied, 1)
                paired(nc.scalar, copy)

            @block.vector
            def _(dve):
                dve.sem_inc(done, 2)
                dve.wait_ge(loaded, 32 + 16 * last_layer)
                if last_layer:
                    nc.vector.tensor_tensor(b_sb[:, 0, :], b_sb[:, 0, :], b_sb[:, 1, :], ALU.add).then_inc(biased, 1)
                    dve.wait_ge(biased, 1)

                def scale(n, h):
                    dve.wait_ge(turned, n + 1)
                    nc.vector.tensor_scalar(staged[:, h, 0:1, :], acc[:, bass.ds(n, 1), 0:D], k.dinv[:, bass.ds(n, 1)],
                                            None, ALU.mult).then_inc(scaled, 1)

                def finish(n, h):
                    a = acc[:, bass.ds(n, 1), 0:D]
                    dinv = k.dinv[:, bass.ds(n, 1)]
                    out = po[:, h:h + 1, 0:D]
                    dve.wait_ge(multiplied, n + 3)
                    if last_layer:
                        dve.wait_ge(xloaded[h], 32 * half_index(n, h))
                        nc.vector.tensor_tensor(a, out, xin[:, h:h + 1, :], ALU.add).then_inc(summed, 1)
                        dve.wait_ge(summed, n + 1)
                        nc.vector.tensor_tensor(a, a, b_sb[:, 0:1, :], ALU.add).then_inc(done, 1)
                    else:
                        nc.vector.tensor_tensor(a, out, b_sb[:, 0:1, :], ALU.add).then_inc(summed, 1)
                        dve.wait_ge(summed, n + 1)
                        nc.vector.tensor_scalar(a, a, 0.0, dinv, ALU.max, ALU.mult).then_inc(done, 1)

                scale(0, 0)
                with nc.vector.Fori(0, NB // 2) as i:
                    scale(2 * i + 1, 1)
                    finish(2 * i, 0)
                    scale(2 * i + 2, 0)
                    finish(2 * i + 1, 1)
                finish(NB - 1, 0)


EXPERTS = 8
HID = 1024
FC = HID // P
CAP = -(-(5 * NODES) // (4 * EXPERTS))
CAPPAD = -(-CAP // P) * P
TT = CAPPAD // P
OUTSIDE = 1 << 20
FMAX = 3.4028234e38


def paired(engine, one):
    with engine.Fori(0, NB // 2) as i:
        for h in range(2):
            one(2 * i + h, h)
    one(NB - 1, 0)


def in_blocks(ap):
    return ap.rearrange("(b l) d -> l b d", l=P)


def on_all(ap):
    return ap.rearrange("(a n) -> a n", a=1).to_broadcast([P, ap.shape[0]])


def stage_gate(nc, k, xn, gate_w, gate_b, logits):
    with ExitStack() as ctx:
        sb, ps, sem = allocators(nc, ctx, "gate")
        w_sb = sb("w", [P, 2, EXPERTS])
        b_sb = sb("b", [P, EXPERTS])
        staged = sb("staged", [P, 2, D])
        xt = sb("xt", [P, 2, D])
        pt = ps("pt", [P, 2, 512])
        po = ps("po", [P, 2, 512])
        loaded, turned, copied = sem("loaded"), sem("turned"), sem("copied")
        multiplied, done = sem("multiplied"), sem("done")
        xloaded = [sem("xloaded0"), sem("xloaded1")]
        with nc.Block() as block:
            @block.sync
            def _(sp):
                sp.dma_start(w_sb[:, :, :], gate_w.rearrange("(c p) n -> p c n", p=P)).then_inc(loaded, 16)
                sp.dma_start(b_sb[:, :], on_all(gate_b)).then_inc(loaded, 16)

                def load(n, h):
                    sp.wait_ge(turned, n + 1)
                    sp.dma_start(staged[:, h, :], xn[:, bass.ds(n, 1), :].rearrange("p a d -> p (a d)")).then_inc(xloaded[h], 16)
                paired(nc.sync, load)

            @block.tensor
            def _(pe):
                pe.sem_inc(turned, 2)
                pe.sem_inc(multiplied, 2)
                pe.wait_ge(loaded, 32)

                def turn(n, h):
                    pe.wait_ge(copied, n + 1)
                    pe.wait_ge(xloaded[h], 16 * half_index(n, h))
                    for c in range(2):
                        last = nc.tensor.transpose(pt[:, h, c * P:(c + 1) * P], staged[:, h, c * P:(c + 1) * P], k.ident[:, :])
                    last.then_inc(turned, 1)

                def multiply(n, h):
                    pe.wait_ge(copied, n + 3)
                    pe.wait_ge(done, n + 1)
                    for c in range(2):
                        last = nc.tensor.matmul(po[:, h, 0:EXPERTS], xt[:, h, c * P:(c + 1) * P], w_sb[:, c, :],
                                                start=(c == 0), stop=(c == 1))
                    last.then_inc(multiplied, 1)

                turn(0, 0)
                with nc.tensor.Fori(0, NB // 2) as i:
                    turn(2 * i + 1, 1)
                    multiply(2 * i, 0)
                    turn(2 * i + 2, 0)
                    multiply(2 * i + 1, 1)
                multiply(NB - 1, 0)

            @block.scalar
            def _(act):
                act.sem_inc(copied, 2)

                def copy(n, h):
                    act.wait_ge(turned, n + 3)
                    act.wait_ge(multiplied, n + 1)
                    nc.scalar.activation(xt[:, h, :], pt[:, h, 0:D], ACT.Copy).then_inc(copied, 1)
                paired(nc.scalar, copy)

            @block.vector
            def _(dve):
                dve.sem_inc(done, 2)
                dve.wait_ge(loaded, 32)

                def finish(n, h):
                    dve.wait_ge(multiplied, n + 3)
                    nc.vector.tensor_tensor(logits[:, bass.ds(n, 1), :], po[:, h:h + 1, 0:EXPERTS], b_sb[:, :].unsqueeze(1),
                                            ALU.add).then_inc(done, 1)
                paired(nc.vector, finish)


def stage_route(nc, k, name, logits, prob, to_slot, from_slot, capacity=None, block_expert=None):
    SLOTS = EXPERTS * NB
    with ExitStack() as ctx:
        sb, ps, sem = allocators(nc, ctx, name)
        best = sb("best", [P, NB])
        hot = sb("hot", [P, NB, EXPERTS])
        exps = sb("exps", [P, NB, EXPERTS])
        code = sb("code", [P, EXPERTS])
        codes = sb("codes", [P, NB, EXPERTS])
        first = sb("first", [P, NB])
        tot = sb("tot", [P, NB, EXPERTS])
        run = sb("run", [P, NB, EXPERTS])
        zero = sb("zero", [P, NB])
        pos = sb("pos", [P, NB])
        slot = sb("slot", [P, NB])
        kept = sb("kept", [P, NB])
        away = sb("away", [P, NB])
        last_slot = sb("last_slot", [P, NB])
        size = sb("size", [P, EXPERTS])
        size_i = sb("size_i", [P, EXPERTS], i32)
        ends = sb("ends", [P, EXPERTS])
        below = sb("below", [P, P])
        owner = sb("owner", [P, P])
        p_in = ps("p_in", [P, 512])
        p_tot = ps("p_tot", [P, 512])
        v, exped, counted = sem("v"), sem("exped"), sem("counted")
        flat = lambda t: t[:, :, :].rearrange("p b e -> p (b e)")
        wide = lambda t: t[:, :].unsqueeze(2).to_broadcast([P, NB, EXPERTS])
        with nc.Block() as block:
            @block.tensor
            def _(pe):
                pe.wait_ge(v, 8)
                nc.tensor.matmul(p_in[:, 0:SLOTS], k.before[:, :], flat(hot), start=True, stop=True)
                nc.tensor.matmul(p_tot[:, 0:SLOTS], k.ones[:, :], flat(hot), start=True, stop=True).then_inc(counted, 1)

            @block.scalar
            def _(act):
                act.wait_ge(v, 3)
                nc.scalar.activation(flat(exps), flat(exps), ACT.Exp).then_inc(exped, 1)

            @block.vector
            def _(dve):
                nc.vector.tensor_reduce(best[:, :], logits[:, :, :], AX.X, ALU.max).then_inc(v, 1)
                nc.vector.tensor_scalar(code[:, :], k.iota[:, 0:EXPERTS], -float(EXPERTS), None, ALU.add).then_inc(v, 1)
                dve.wait_ge(v, 2)
                nc.vector.tensor_tensor(exps[:, :, :], logits[:, :, :], wide(best), ALU.subtract).then_inc(v, 1)
                nc.vector.tensor_tensor(hot[:, :, :], logits[:, :, :], wide(best), ALU.is_equal).then_inc(v, 1)
                dve.wait_ge(v, 4)
                nc.vector.tensor_tensor(codes[:, :, :], hot[:, :, :], code[:, :].unsqueeze(1).to_broadcast([P, NB, EXPERTS]),
                                        ALU.mult).then_inc(v, 1)
                dve.wait_ge(v, 5)
                nc.vector.tensor_reduce(first[:, :], codes[:, :, :], AX.X, ALU.min).then_inc(v, 1)
                dve.wait_ge(v, 6)
                nc.vector.tensor_tensor(hot[:, :, :], code[:, :].unsqueeze(1).to_broadcast([P, NB, EXPERTS]), wide(first),
                                        ALU.is_equal).then_inc(v, 1)
                nc.vector.memset(zero[:, :], 0.0).then_inc(v, 1)
                dve.wait_ge(exped, 1)
                nc.vector.tensor_reduce(prob[:, :], exps[:, :, :], AX.X, ALU.add).then_inc(v, 1)
                dve.wait_ge(v, 9)
                nc.vector.reciprocal(prob[:, :], prob[:, :]).then_inc(v, 1)
                dve.wait_ge(counted, 1)
                nc.vector.tensor_copy(flat(tot), p_tot[:, 0:SLOTS]).then_inc(v, 1)
                dve.wait_ge(v, 11)
                for e in range(EXPERTS):
                    nc.vector.tensor_tensor_scan(run[:, :, e], tot[:, :, e], zero[:, :], 0.0, ALU.add, ALU.add).then_inc(v, 1)
                dve.wait_ge(v, 19)
                nc.vector.tensor_copy(size[:, :], run[:, NB - 1, :]).then_inc(v, 1)
                dve.wait_ge(v, 20)
                nc.vector.tensor_tensor(run[:, :, :], run[:, :, :], tot[:, :, :], ALU.subtract).then_inc(v, 1)
                dve.wait_ge(v, 21)
                nc.vector.tensor_tensor(flat(run), flat(run), p_in[:, 0:SLOTS], ALU.add).then_inc(v, 1)
                if capacity is None:
                    nc.vector.tensor_scalar(size[:, :], size[:, :], float(P - 1), None, ALU.add).then_inc(v, 1)
                    dve.wait_ge(v, 23)
                    nc.vector.tensor_copy(size_i[:, :], size[:, :]).then_inc(v, 1)
                    dve.wait_ge(v, 24)
                    nc.vector.tensor_single_scalar(size_i[:, :], size_i[:, :], 7, op=ALU.arith_shift_right).then_inc(v, 1)
                    dve.wait_ge(v, 25)
                    nc.vector.tensor_copy(size[:, :], size_i[:, :]).then_inc(v, 1)
                    dve.wait_ge(v, 26)
                    nc.vector.tensor_tensor_scan(ends[:, :], size[:, :], zero[:, 0:EXPERTS], 0.0, ALU.add, ALU.add).then_inc(v, 1)
                    dve.wait_ge(v, 27)
                    nc.vector.memset(owner[:, :], 0.0).then_inc(v, 1)
                    for e in range(EXPERTS - 1):
                        dve.wait_ge(v, 28 + 2 * e)
                        nc.vector.tensor_scalar(below[:, :], k.iota[:, :], ends[:, e:e + 1], None, ALU.is_ge).then_inc(v, 1)
                        dve.wait_ge(v, 29 + 2 * e)
                        nc.vector.tensor_tensor(owner[:, :], owner[:, :], below[:, :], ALU.add).then_inc(v, 1)
                    dve.wait_ge(v, 42)
                    nc.vector.tensor_copy(block_expert[:, :], owner[0:1, :]).then_inc(v, 1)
                    nc.vector.tensor_tensor(ends[:, :], ends[:, :], size[:, :], ALU.subtract).then_inc(v, 1)
                    dve.wait_ge(v, 44)
                    nc.vector.tensor_scalar(ends[:, :], ends[:, :], float(P), None, ALU.mult).then_inc(v, 1)
                    dve.wait_ge(v, 45)
                    nc.vector.tensor_tensor(run[:, :, :], run[:, :, :], ends[:, :].unsqueeze(1).to_broadcast([P, NB, EXPERTS]),
                                            ALU.add).then_inc(v, 1)
                    at = 46
                else:
                    at = 22
                dve.wait_ge(v, at)
                nc.vector.tensor_tensor(run[:, :, :], run[:, :, :], hot[:, :, :], ALU.mult).then_inc(v, 1)
                dve.wait_ge(v, at + 1)
                nc.vector.tensor_reduce(pos[:, :], run[:, :, :], AX.X, ALU.add).then_inc(v, 1)
                dve.wait_ge(v, at + 2)
                if capacity is None:
                    nc.vector.tensor_copy(to_slot[:, :], pos[:, :]).then_inc(v, 1)
                    nc.vector.tensor_copy(from_slot[:, :], pos[:, :]).then_inc(v, 1)
                else:
                    nc.vector.tensor_scalar(kept[:, :], pos[:, :], float(capacity), None, ALU.is_lt).then_inc(v, 1)
                    nc.vector.tensor_scalar(slot[:, :], first[:, :], float(EXPERTS), float(CAPPAD), ALU.add, ALU.mult).then_inc(v, 1)
                    nc.vector.tensor_scalar(last_slot[:, :], pos[:, :], float(capacity - 1), None, ALU.min).then_inc(v, 1)
                    dve.wait_ge(v, at + 5)
                    nc.vector.tensor_tensor(last_slot[:, :], last_slot[:, :], slot[:, :], ALU.add).then_inc(v, 1)
                    nc.vector.tensor_tensor(slot[:, :], slot[:, :], pos[:, :], ALU.add).then_inc(v, 1)
                    nc.vector.tensor_tensor(prob[:, :], prob[:, :], kept[:, :], ALU.mult).then_inc(v, 1)
                    nc.vector.tensor_scalar(away[:, :], kept[:, :], -float(OUTSIDE), float(OUTSIDE), ALU.mult, ALU.add).then_inc(v, 1)
                    dve.wait_ge(v, at + 9)
                    nc.vector.tensor_copy(from_slot[:, :], last_slot[:, :]).then_inc(v, 1)
                    nc.vector.tensor_tensor(slot[:, :], slot[:, :], away[:, :], ALU.add).then_inc(v, 1)
                    dve.wait_ge(v, at + 11)
                    nc.vector.tensor_copy(to_slot[:, :], slot[:, :]).then_inc(v, 1)


def stage_dispatch(nc, k, name, xn, to_slot, slots):
    with ExitStack() as ctx:
        sb, ps, sem = allocators(nc, ctx, name)
        sent = sem("sent")
        with nc.Block() as block:
            @block.gpsimd
            def _(pool):
                for b in range(NB):
                    nc.gpsimd.indirect_dma_start(
                        out=slots, out_offset=bass.IndirectOffsetOnAxis(ap=to_slot[:, b:b + 1], axis=0),
                        in_=xn[:, b, :], in_offset=None, bounds_check=EXPERTS * CAPPAD - 1, oob_is_err=False,
                    ).then_inc(sent, 16)
                pool.wait_ge(sent, 16 * NB)


def stage_experts0(nc, k, slots, w1, b1, w2, b2, out, scratch):
    HT = TT // 2
    HW = HT * P
    with ExitStack() as ctx:
        sb, ps, sem = allocators(nc, ctx, "experts0")
        w1_sb = sb("w1", [P, 2, 2, HID])
        w2_sb = sb("w2", [P, 2, FC, D])
        b1_sb = sb("b1", [P, 2, FC])
        b2_sb = sb("b2", [P, 2, D])
        x_sb = sb("x", [P, 2, TT, D])
        xt = sb("xt", [P, 2, TT * P])
        ht = scratch[:, 0:FC * TT * P // D, :].rearrange("p b d -> p (b d)").rearrange("p (f n) -> p f n", f=FC)
        y_sb = sb("y", [P, 2, TT, D])
        pt = ps("pt", [P, 2, 512])
        ph = [ps(f"ph{j}", [P, 512]) for j in range(4)]
        py = [ps(f"py{j}", [P, 512]) for j in range(2)]
        loaded = [sem("loaded0"), sem("loaded1")]
        stored = [sem("stored0"), sem("stored1")]
        turned, copied = sem("turned"), sem("copied")
        h_made, relued = sem("h_made"), sem("relued")
        y_made, evacuated, y_free = sem("y_made"), sem("evacuated"), sem("y_free")
        with nc.Block() as block:
            @block.sync
            def _(sp):
                sp.sem_inc(y_free, 2)

                def load(e, h):
                    d = bass.ds(e, 1)
                    sp.dma_start(x_sb[:, h, :, :], slots.rearrange("(e t l) d -> l e t d", l=P, t=TT)[:, d, :, :]
                                 .rearrange("l a t d -> l (a t) d")).then_inc(loaded[h], 16)
                    sp.dma_start(w1_sb[:, h, :, :], w1[d, :, :].rearrange("a (c p) f -> p (a c) f", p=P)).then_inc(loaded[h], 16)
                    sp.dma_start(w2_sb[:, h, :, :], w2[d, :, :].rearrange("a (c p) n -> p (a c) n", p=P)).then_inc(loaded[h], 16)
                    sp.dma_start(b2_sb[:, h, :], b2[d, :].to_broadcast([P, D])).then_inc(loaded[h], 16)
                    sp.dma_start(b1_sb[:, h, :], b1[d, :, :].rearrange("a p f -> p (a f)")).then_inc(loaded[h], 16)

                def store(e, h):
                    sp.wait_ge(evacuated, TT * (e + 1) + 2)
                    sp.dma_start(out.rearrange("(e t l) d -> l e t d", l=P, t=TT)[:, bass.ds(e, 1), :, :]
                                 .rearrange("l a t d -> l (a t) d"), y_sb[:, h, :, :]).then_inc(stored[h], 16)

                load(0, 0)
                load(1, 1)
                with nc.sync.Fori(0, EXPERTS // 2 - 1) as i:
                    for h in range(2):
                        e = 2 * i + h
                        store(e, h)
                        load(e + 2, h)
                        sp.wait_ge(stored[h], 16 * (i + 1))
                        sp.sem_inc(y_free, 1)
                for h in range(2):
                    store(EXPERTS - 2 + h, h)
                for h in range(2):
                    sp.wait_ge(stored[h], 16 * (EXPERTS // 2))

            @block.tensor
            def _(pe):
                with nc.tensor.Fori(0, EXPERTS // 2) as i:
                    for h in range(2):
                        e = 2 * i + h
                        pe.wait_ge(loaded[h], 80 * (i + 1))
                        for t in range(TT):
                            pe.wait_ge(copied, TT * e + t + 1)
                            for c in range(2):
                                last = nc.tensor.transpose(pt[:, t % 2, c * P:(c + 1) * P], x_sb[:, h, t, c * P:(c + 1) * P],
                                                           k.ident[:, :])
                            last.then_inc(turned, 1)
                        for half in range(2):
                            pe.wait_ge(copied, TT * e + HT * (half + 1) + 2)
                            for f in range(FC):
                                pe.wait_ge(relued, 2 * FC * e + FC * half + f + 1)
                                for c in range(2):
                                    last = nc.tensor.matmul(ph[f % 4][:, 0:HW], w1_sb[:, h, c, f * P:(f + 1) * P],
                                                            xt[:, c, half * HW:(half + 1) * HW], start=(c == 0), stop=(c == 1))
                                last.then_inc(h_made, 1)
                        for t in range(TT):
                            if t % HT == 0:
                                pe.wait_ge(relued, 2 * FC * e + FC * (t // HT + 1) + 4)
                            pe.wait_ge(evacuated, TT * e + t + 1)
                            for f in range(FC):
                                last = nc.tensor.matmul(py[t % 2][:, 0:D], ht[:, f, t * P:(t + 1) * P], w2_sb[:, h, f, :],
                                                        start=(f == 0), stop=(f == FC - 1))
                            last.then_inc(y_made, 1)

            @block.scalar
            def _(act):
                act.sem_inc(relued, 4)
                with nc.scalar.Fori(0, EXPERTS // 2) as i:
                    for h in range(2):
                        e = 2 * i + h
                        act.wait_ge(loaded[h], 80 * (i + 1))
                        for half in range(2):
                            for f in range(FC):
                                act.wait_ge(h_made, 2 * FC * e + FC * half + f + 1)
                                nc.scalar.activation(ht[:, f, half * HW:(half + 1) * HW], ph[f % 4][:, 0:HW], ACT.Relu,
                                                     bias=b1_sb[:, h, f:f + 1]).then_inc(relued, 1)

            @block.vector
            def _(dve):
                dve.sem_inc(copied, 2)
                dve.sem_inc(evacuated, 2)
                with nc.vector.Fori(0, EXPERTS // 2) as i:
                    for h in range(2):
                        e = 2 * i + h
                        for t in range(TT):
                            dve.wait_ge(turned, TT * e + t + 1)
                            nc.vector.tensor_copy(xt[:, :, t * P:(t + 1) * P], pt[:, t % 2, 0:D].rearrange("p (c n) -> p c n", c=2)).then_inc(copied, 1)
                        dve.wait_ge(y_free, e + 1)
                        dve.wait_ge(loaded[h], 80 * (i + 1))
                        for t in range(TT):
                            dve.wait_ge(y_made, TT * e + t + 1)
                            nc.vector.tensor_tensor(y_sb[:, h, t, :], py[t % 2][:, 0:D], b2_sb[:, h, :], ALU.add).then_inc(evacuated, 1)


def stage_combine(nc, k, name, rows, from_slot, x, prob, guard, x_out=None):
    R = 4
    with ExitStack() as ctx:
        sb, ps, sem = allocators(nc, ctx, name)
        got = sb("got", [P, R, D])
        bad = sb("bad", [P, 2, D], i32)
        most = sb("most", [P, D])
        least = sb("least", [P, D])
        nought = sb("nought", [P, D])
        gathered = [sem(f"gathered{j}") for j in range(R)]
        done, v, stored, turn = sem("done"), sem("v"), sem("stored"), sem("turn")
        FULL = NB // R

        with nc.Block() as block:
            @block.gpsimd
            def _(pool):
                for b in range(NB):
                    if b >= R:
                        pool.wait_ge(done, b - R + 1)
                    nc.gpsimd.indirect_dma_start(out=got[:, b % R, :], out_offset=None, in_=rows,
                                                 in_offset=bass.IndirectOffsetOnAxis(ap=from_slot[:, b:b + 1], axis=0),
                                                 ).then_inc(gathered[b % R], 16)

            @block.vector
            def _(dve):
                if guard:
                    nc.vector.memset(most[:, :], 10000.0).then_inc(v, 1)
                    nc.vector.memset(least[:, :], -10000.0).then_inc(v, 1)
                    nc.vector.memset(nought[:, :], 0.0).then_inc(v, 1)

                def combine(b, j, use):
                    g = got[:, j, :]
                    a = x[:, bass.ds(b, 1), 0:D]
                    dve.wait_ge(gathered[j], 16 * use)
                    if not guard:
                        nc.vector.scalar_tensor_tensor(out=a, in0=got[:, j:j + 1, :], scalar=prob[:, bass.ds(b, 1)], in1=a,
                                                       op0=ALU.mult, op1=ALU.add).then_inc(done, 1)
                        return
                    w = 3 + 9 * b
                    dve.wait_ge(v, w)
                    nc.vector.tensor_scalar(g, g, prob[:, bass.ds(b, 1)], None, ALU.mult).then_inc(v, 1)
                    dve.wait_ge(v, w + 1)
                    nc.vector.tensor_scalar(bad[:, 0, :], g, FMAX, None, ALU.is_gt).then_inc(v, 1)
                    nc.vector.tensor_scalar(bad[:, 1, :], g, -FMAX, None, ALU.is_lt).then_inc(v, 1)
                    dve.wait_ge(v, w + 3)
                    dve.sem_inc(turn, 1)
                    nc.vector.copy_predicated(g, bad[:, 0, :], most[:, :]).then_inc(v, 1)
                    dve.wait_ge(v, w + 4)
                    dve.sem_inc(turn, 1)
                    nc.vector.copy_predicated(g, bad[:, 1, :], least[:, :]).then_inc(v, 1)
                    dve.wait_ge(v, w + 5)
                    nc.vector.tensor_tensor(bad[:, 0, :], g, g, ALU.not_equal).then_inc(v, 1)
                    dve.wait_ge(v, w + 6)
                    dve.sem_inc(turn, 1)
                    nc.vector.copy_predicated(g, bad[:, 0, :], nought[:, :]).then_inc(v, 1)
                    dve.wait_ge(v, w + 7)
                    nc.vector.tensor_tensor(a, a, got[:, j:j + 1, :], ALU.add).then_inc(v, 1)
                    dve.wait_ge(v, w + 8)
                    dve.sem_inc(v, 1)
                    dve.sem_inc(done, 1)

                with nc.vector.Fori(0, FULL) as i:
                    for j in range(R):
                        combine(R * i + j, j, i + 1)
                for b in range(FULL * R, NB):
                    combine(b, b % R, FULL + 1)

            @block.sync
            def _(sp):
                if x_out is not None:
                    for g in range(NG):
                        b = slice(g * CG, (g + 1) * CG)
                        sp.wait_ge(done, (g + 1) * CG)
                        sp.dma_start(in_blocks(x_out)[:, b, :], x[:, b, 0:D]).then_inc(stored, 16)
                    sp.wait_ge(stored, 16 * NG)


ECOLS = ET
EPAD = ECOLS * P
EROWS = EG * P
LOW = -1e30


class Tally:

    def __init__(self):
        self.n = 0

    def one(self):
        self.n += 1
        return 1


def stage_gat_project(nc, k, name, xn, w, w_t, a_src, a_dst, heads, acc, esd, table, es_table):
    C = D // heads
    W2 = D + 2 * heads
    with ExitStack() as ctx:
        sb, ps, sem = allocators(nc, ctx, name)
        w_sb = sb("w", [P, 2, W2])
        wt_sb = sb("wt", [P, 2, D])
        a_sb = sb("a", [P, 2, 2 * heads])
        staged = sb("staged", [P, 2, D])
        xt = sb("xt", [P, 2, D])
        pt = ps("pt", [P, 2, 512])
        po = ps("po", [P, 2, 512])
        loaded, zeroed, folded, ready = sem("loaded"), sem("zeroed"), sem("folded"), sem("ready")
        turned, copied, multiplied, done, stored = sem("turned"), sem("copied"), sem("multiplied"), sem("done"), sem("stored")
        xloaded = [sem("xloaded0"), sem("xloaded1")]
        with nc.Block() as block:
            @block.sync
            def _(sp):
                sp.dma_start(w_sb[:, :, 0:D], w.rearrange("(c p) n -> p c n", p=P)).then_inc(loaded, 16)
                sp.dma_start(wt_sb[:, :, :], w_t.rearrange("(c p) n -> p c n", p=P)).then_inc(loaded, 16)
                sp.wait_ge(zeroed, 1)
                for s, a in enumerate((a_src, a_dst)):
                    for q in range(heads):
                        for r in range(q * C, (q + 1) * C, min(C, P)):
                            n = min(C, P)
                            sp.dma_start(a_sb[r % P:r % P + n, r // P, s * heads + q:s * heads + q + 1],
                                         a[q, r - q * C:r - q * C + n].rearrange("(n a) -> n a", a=1)).then_inc(loaded, 16)

                def load(n, h):
                    sp.wait_ge(turned, n + 1)
                    sp.dma_start(staged[:, h, :], xn[:, bass.ds(n, 1), :].rearrange("p a d -> p (a d)")).then_inc(xloaded[h], 16)
                paired(nc.sync, load)
                for g in range(NG):
                    b = slice(g * CG, (g + 1) * CG)
                    sp.wait_ge(done, 2 * (g + 1) * CG + 2)
                    sp.dma_start(in_blocks(table)[:, b, :], acc[:, b, 0:D]).then_inc(stored, 16)
                sp.dma_start(in_blocks(es_table), esd[:, :, :]).then_inc(stored, 16)
                sp.wait_ge(stored, 16 * (NG + 1))
            pieces = 2 * heads * (C // min(C, P))

            @block.tensor
            def _(pe):
                pe.sem_inc(turned, 2)
                pe.sem_inc(multiplied, 2)
                pe.wait_ge(loaded, 16 * (2 + pieces))
                for m in range(2):
                    for c in range(2):
                        last = nc.tensor.matmul(po[:, m, 0:2 * heads], wt_sb[:, c, m * P:(m + 1) * P], a_sb[:, c, :],
                                                start=(c == 0), stop=(c == 1))
                last.then_inc(folded, 1)
                pe.wait_ge(ready, 1)

                def turn(n, h):
                    pe.wait_ge(copied, n + 1)
                    pe.wait_ge(xloaded[h], 16 * half_index(n, h))
                    for c in range(2):
                        last = nc.tensor.transpose(pt[:, h, c * P:(c + 1) * P], staged[:, h, c * P:(c + 1) * P], k.ident[:, :])
                    last.then_inc(turned, 1)

                def multiply(n, h):
                    pe.wait_ge(copied, n + 3)
                    pe.wait_ge(done, 2 * n + 1)
                    for c in range(2):
                        last = nc.tensor.matmul(po[:, h, 0:W2], xt[:, h, c * P:(c + 1) * P], w_sb[:, c, :],
                                                start=(c == 0), stop=(c == 1))
                    last.then_inc(multiplied, 1)

                turn(0, 0)
                with nc.tensor.Fori(0, NB // 2) as i:
                    turn(2 * i + 1, 1)
                    multiply(2 * i, 0)
                    turn(2 * i + 2, 0)
                    multiply(2 * i + 1, 1)
                multiply(NB - 1, 0)

            @block.scalar
            def _(act):
                act.sem_inc(copied, 2)

                def copy(n, h):
                    act.wait_ge(turned, n + 3)
                    act.wait_ge(multiplied, n + 1)
                    nc.scalar.activation(xt[:, h, :], pt[:, h, 0:D], ACT.Copy).then_inc(copied, 1)
                paired(nc.scalar, copy)

            @block.vector
            def _(dve):
                nc.vector.memset(a_sb[:, :, :], 0.0).then_inc(zeroed, 1)
                dve.wait_ge(folded, 1)
                nc.vector.tensor_copy(w_sb[:, :, D:W2], po[:, :, 0:2 * heads]).then_inc(ready, 1)
                dve.sem_inc(done, 2)

                def finish(n, h):
                    dve.wait_ge(multiplied, n + 3)
                    nc.vector.tensor_copy(acc[:, bass.ds(n, 1), 0:D], po[:, h:h + 1, 0:D]).then_inc(done, 1)
                    nc.vector.tensor_copy(esd[:, bass.ds(n, 1), :], po[:, h:h + 1, D:W2]).then_inc(done, 1)
                paired(nc.vector, finish)


def stage_gat_weights(nc, k, name, heads, es_table, esd, src_flat, dst_flat, prev_flat, run_dram, node_dram, p_dram, weights, p_self):
    H = heads
    T = 17
    HALVES = ECOLS // T
    assert HALVES * T == ECOLS and HALVES % 2 == 0
    with ExitStack() as ctx:
        sb, ps, sem = allocators(nc, ctx, name)
        src_c = sb("src_c", [P, ECOLS], i32)
        dst_c = sb("dst_c", [P, ECOLS], i32)
        prev_c = sb("prev_c", [P, ECOLS], i32)
        idx = sb("idx", [P, 2, T], i32)
        got = sb("got", [P, 2, T, 2 * H])
        es = sb("es", [P, ECOLS, H])
        same = sb("same", [P, ECOLS])
        pen = sb("pen", [P, ECOLS])
        run = sb("run", [P, ECOLS, 2 * H])
        node = sb("node", [P, NB, 2 * H])
        nodes = sb("nodes", [P, ECOLS, 2 * H])
        top = nodes[:, :, :].rearrange("p i h -> p (i h)")[:, 0:ECOLS * H].rearrange("p (i h) -> p i h", h=H)
        ends = sb("ends", [P, 3 * H + 2])
        ends_t = sb("ends_t", [3 * H + 2, P])
        whole = sb("whole", [P, 1])
        end_idx = sb("end_idx", [P, NB], i32)
        start_idx = sb("start_idx", [P, NB], i32)
        cnt = sb("cnt", [P, NB])
        beg = sb("beg", [P, NB])
        none = sb("none", [P, NB])
        tmp = sb("tmp", [P, NB])
        seg = sb("seg", [P, NB, H])
        rows = sb("rows", [2 * H, 4, P])
        carry = sb("carry", [P, 2 * H])
        tiles = sb("tiles", [P, SG, P * H])
        pt = ps("pt", [P, 512])
        pw = ps("pw", [P, 2, 512])

        loaded, idx_ready, taken, free = sem("loaded"), sem("idx_ready"), sem("taken"), sem("free")
        gat = [sem("gat0"), sem("gat1")]
        with nc.Block() as block:
            @block.sync
            def _(sp):
                sp.dma_start(src_c[:, :], src_flat[0:EPAD].rearrange("(q i) -> q i", q=P)).then_inc(loaded, 16)
                sp.dma_start(dst_c[:, :], dst_flat[0:EPAD].rearrange("(q i) -> q i", q=P)).then_inc(loaded, 16)
                sp.dma_start(prev_c[:, :], prev_flat[0:EPAD].rearrange("(q i) -> q i", q=P)).then_inc(loaded, 16)

            @block.gpsimd
            def _(pool):
                with nc.gpsimd.Fori(0, HALVES // 2) as i:
                    for h in range(2):
                        pool.wait_ge(idx_ready, 2 * i + h + 1)
                        pool.sem_inc(free, 1)
                        for j in range(T):
                            nc.gpsimd.indirect_dma_start(
                                out=got[:, h, j, :], out_offset=None, in_=es_table,
                                in_offset=bass.IndirectOffsetOnAxis(ap=idx[:, h, j:j + 1], axis=0)).then_inc(gat[h], 16)

            @block.vector
            def _(dve):
                dve.wait_ge(loaded, 48)

                def give(n, h):
                    nc.vector.tensor_copy(idx[:, h, :], src_c[:, bass.ds(n * T, T)]).then_inc(idx_ready, 1)

                def take(n, h):
                    dve.wait_ge(gat[h], 16 * T * half_index(n, h))
                    nc.vector.tensor_copy(es[:, bass.ds(n * T, T), :], got[:, h, :, 0:H]).then_inc(taken, 1)

                give(0, 0)
                give(1, 1)
                with nc.vector.Fori(0, HALVES // 2 - 1) as i:
                    for h in range(2):
                        take(2 * i + h, h)
                        give(2 * i + h + 2, h)
                take(HALVES - 2, 0)
                take(HALVES - 1, 1)

        v2, turned2, stored2, seg2 = sem("v2"), sem("turned2"), sem("stored2"), sem("seg2")
        c = Tally()
        with nc.Block() as block:
            @block.vector
            def _(dve):
                nc.vector.tensor_tensor(same[:, :], dst_c[:, :], prev_c[:, :], ALU.is_equal).then_inc(v2, c.one())
                dve.wait_ge(v2, c.n)
                nc.vector.tensor_scalar(pen[:, :], same[:, :], -LOW, LOW, ALU.mult, ALU.add).then_inc(v2, c.one())
                nc.vector.tensor_reduce(ends[:, H:H + 1], same[:, :], AX.X, ALU.min).then_inc(v2, c.one())
                dve.wait_ge(v2, c.n)
                nc.vector.tensor_copy(whole[:, :], ends[:, H:H + 1]).then_inc(v2, c.one())
                for q in range(H):
                    nc.vector.tensor_tensor_scan(top[:, :, q], pen[:, :], es[:, :, q], LOW, ALU.add, ALU.max).then_inc(v2, c.one())
                dve.wait_ge(v2, c.n)
                nc.vector.tensor_copy(ends[:, 0:H], top[:, ECOLS - 1, :]).then_inc(v2, c.one())
                dve.wait_ge(turned2, 2)
                nc.vector.tensor_copy(ends_t[0:H + 1, :], pt[0:H + 1, 0:P]).then_inc(v2, c.one())
                dve.wait_ge(turned2, 2)
                nc.vector.tensor_copy(rows[0:H, 0, :], pt[0:H, P:2 * P]).then_inc(v2, c.one())
                dve.wait_ge(v2, c.n)
                nc.vector.tensor_scalar(rows[0:H, 1, :], rows[0:H, 0, :], -LOW, LOW, ALU.mult, ALU.add).then_inc(v2, c.one())
                nc.vector.memset(rows[0:H, 3, :], LOW).then_inc(v2, c.one())
                dve.wait_ge(v2, c.n)
                nc.vector.tensor_tensor_scan(rows[0:H, 2, :], rows[0:H, 1, :], ends_t[0:H, :], LOW, ALU.add, ALU.max).then_inc(v2, c.one())
                dve.wait_ge(v2, c.n)
                nc.vector.tensor_copy(rows[0:H, 3, 1:P], rows[0:H, 2, 0:P - 1]).then_inc(v2, c.one())
                dve.wait_ge(turned2, 3)
                nc.vector.tensor_copy(carry[:, 0:H], pt[:, 2 * P:2 * P + H]).then_inc(v2, c.one())
                dve.wait_ge(v2, c.n)
                for q in range(H):
                    nc.vector.tensor_tensor_scan(top[:, :, q], pen[:, :], es[:, :, q], carry[:, q:q + 1], ALU.add, ALU.max).then_inc(v2, c.one())
                nc.vector.tensor_copy(cnt[:, :], k.row_count[:, :]).then_inc(v2, c.one())
                nc.vector.tensor_copy(beg[:, :], k.row_start[:, :]).then_inc(v2, c.one())
                dve.wait_ge(v2, c.n)
                nc.vector.tensor_scalar(none[:, :], cnt[:, :], 0.5, None, ALU.is_lt).then_inc(v2, c.one())
                nc.vector.tensor_tensor(tmp[:, :], beg[:, :], cnt[:, :], ALU.add).then_inc(v2, c.one())
                dve.wait_ge(v2, c.n)
                nc.vector.tensor_scalar(tmp[:, :], tmp[:, :], -1.0, 0.0, ALU.add, ALU.max).then_inc(v2, c.one())
                nc.vector.scalar_tensor_tensor(out=beg[:, :], in0=none[:, :], scalar=float(OUTSIDE), in1=beg[:, :],
                                               op0=ALU.mult, op1=ALU.add).then_inc(v2, c.one())
                dve.wait_ge(v2, c.n)
                nc.vector.tensor_copy(end_idx[:, :], tmp[:, :]).then_inc(v2, c.one())
                nc.vector.tensor_copy(start_idx[:, :], beg[:, :]).then_inc(v2, c.one())

            @block.tensor
            def _(pe):
                pe.wait_ge(v2, 4 + H + 1)
                nc.tensor.transpose(pt[0:H + 1, 0:P], ends[:, 0:H + 1], k.ident[:, :]).then_inc(turned2, 1)
                nc.tensor.matmul(pt[0:H, P:2 * P], whole[:, :].to_broadcast([P, H]), k.ident[:, :], start=True, stop=True).then_inc(turned2, 1)
                pe.wait_ge(v2, 4 + H + 1 + 6)
                nc.tensor.transpose(pt[:, 2 * P:2 * P + H], rows[0:H, 3, :], k.ident[0:H, 0:H]).then_inc(turned2, 1)

            @block.sync
            def _(sp):
                sp.wait_ge(v2, 4 + H + 1 + 7 + H)
                sp.dma_start(run_dram.rearrange("(q i) h -> q i h", q=P), top[:, :, :]).then_inc(stored2, 16)

            @block.gpsimd
            def _(pool):
                pool.wait_ge(v2, 4 + H + 1 + 7 + H + 8)
                pool.wait_ge(stored2, 16)
                for b in range(NB):
                    nc.gpsimd.indirect_dma_start(out=seg[:, b, :], out_offset=None, in_=run_dram,
                                                 in_offset=bass.IndirectOffsetOnAxis(ap=end_idx[:, b:b + 1], axis=0)).then_inc(seg2, 16)
                pool.wait_ge(seg2, 16 * NB)

        v3, exp3, sent3, back3 = sem("v3"), sem("exp3"), sem("sent3"), sem("back3")
        c3 = Tally()
        wide = lambda t: t[:, :].unsqueeze(2).to_broadcast([P, NB, H])
        with nc.Block() as block:
            @block.vector
            def _(dve):
                for q in range(H):
                    nc.vector.scalar_tensor_tensor(out=seg[:, :, q], in0=none[:, :], scalar=2 * LOW, in1=seg[:, :, q],
                                                   op0=ALU.mult, op1=ALU.add).then_inc(v3, c3.one())
                nc.vector.tensor_tensor(p_self[:, :, :], esd[:, :, 0:H], esd[:, :, H:2 * H], ALU.add).then_inc(v3, c3.one())
                nc.vector.tensor_copy(node[:, :, 0:H], esd[:, :, H:2 * H]).then_inc(v3, c3.one())
                dve.wait_ge(v3, c3.n)
                nc.vector.tensor_tensor(seg[:, :, :], seg[:, :, :], esd[:, :, 0:H], ALU.max).then_inc(v3, c3.one())
                nc.vector.scalar_tensor_tensor(out=p_self[:, :, :], in0=p_self[:, :, :], scalar=0.2, in1=p_self[:, :, :],
                                               op0=ALU.mult, op1=ALU.max).then_inc(v3, c3.one())
                dve.wait_ge(v3, c3.n)
                nc.vector.tensor_tensor(seg[:, :, :], seg[:, :, :], esd[:, :, H:2 * H], ALU.add).then_inc(v3, c3.one())
                dve.wait_ge(v3, c3.n)
                nc.vector.scalar_tensor_tensor(out=node[:, :, H:2 * H], in0=seg[:, :, :], scalar=0.2, in1=seg[:, :, :],
                                               op0=ALU.mult, op1=ALU.max).then_inc(v3, c3.one())
                dve.wait_ge(v3, c3.n)
                nc.vector.tensor_tensor(p_self[:, :, :], p_self[:, :, :], node[:, :, H:2 * H], ALU.subtract).then_inc(v3, c3.one())

            @block.scalar
            def _(act):
                act.wait_ge(v3, H + 7)
                nc.scalar.activation(p_self[:, :, :], p_self[:, :, :], ACT.Exp).then_inc(exp3, 1)

            @block.gpsimd
            def _(pool):
                pool.wait_ge(v3, H + 6)
                for b in range(NB):
                    nc.gpsimd.indirect_dma_start(
                        out=node_dram[:, 0:2 * H], out_offset=bass.IndirectOffsetOnAxis(ap=start_idx[:, b:b + 1], axis=0),
                        in_=node[:, b, :], in_offset=None, bounds_check=EPAD - 1, oob_is_err=False).then_inc(sent3, 16)

            @block.sync
            def _(sp):
                sp.wait_ge(sent3, 16 * NB)
                sp.dma_start(nodes[:, :, :], node_dram.rearrange("(q i) h -> q i h", q=P)).then_inc(back3, 16)
                sp.wait_ge(back3, 16)

        v4, turned4, exp4, stored4 = sem("v4"), sem("turned4"), sem("exp4"), sem("stored4")
        c4 = Tally()
        with nc.Block() as block:
            @block.vector
            def _(dve):
                for q in range(2 * H):
                    nc.vector.tensor_tensor_scan(run[:, :, q], same[:, :], nodes[:, :, q], 0.0, ALU.mult, ALU.add).then_inc(v4, c4.one())
                dve.wait_ge(v4, c4.n)
                nc.vector.tensor_copy(ends[:, 0:2 * H], run[:, ECOLS - 1, :]).then_inc(v4, c4.one())
                dve.wait_ge(turned4, 2)
                nc.vector.tensor_copy(ends_t[0:2 * H, :], pt[0:2 * H, 0:P]).then_inc(v4, c4.one())
                nc.vector.tensor_copy(rows[0:2 * H, 0, :], pt[0:2 * H, P:2 * P]).then_inc(v4, c4.one())
                nc.vector.memset(rows[0:2 * H, 3, :], 0.0).then_inc(v4, c4.one())
                dve.wait_ge(v4, c4.n)
                nc.vector.tensor_tensor_scan(rows[0:2 * H, 2, :], rows[0:2 * H, 0, :], ends_t[0:2 * H, :], 0.0, ALU.mult, ALU.add).then_inc(v4, c4.one())
                dve.wait_ge(v4, c4.n)
                nc.vector.tensor_copy(rows[0:2 * H, 3, 1:P], rows[0:2 * H, 2, 0:P - 1]).then_inc(v4, c4.one())
                dve.wait_ge(turned4, 3)
                nc.vector.tensor_copy(carry[:, :], pt[:, 2 * P:2 * P + 2 * H]).then_inc(v4, c4.one())
                dve.wait_ge(v4, c4.n)
                for q in range(2 * H):
                    nc.vector.tensor_tensor_scan(run[:, :, q], same[:, :], nodes[:, :, q], carry[:, q:q + 1], ALU.mult, ALU.add).then_inc(v4, c4.one())
                dve.wait_ge(v4, c4.n)
                nc.vector.tensor_tensor(es[:, :, :], es[:, :, :], run[:, :, 0:H], ALU.add).then_inc(v4, c4.one())
                dve.wait_ge(v4, c4.n)
                nc.vector.scalar_tensor_tensor(out=es[:, :, :], in0=es[:, :, :], scalar=0.2, in1=es[:, :, :],
                                               op0=ALU.mult, op1=ALU.max).then_inc(v4, c4.one())
                dve.wait_ge(v4, c4.n)
                nc.vector.tensor_tensor(es[:, :, :], es[:, :, :], run[:, :, H:2 * H], ALU.subtract).then_inc(v4, c4.one())

            @block.tensor
            def _(pe):
                pe.wait_ge(v4, 2 * H + 1)
                nc.tensor.transpose(pt[0:2 * H, 0:P], ends[:, 0:2 * H], k.ident[:, :]).then_inc(turned4, 1)
                nc.tensor.matmul(pt[0:2 * H, P:2 * P], whole[:, :].to_broadcast([P, 2 * H]), k.ident[:, :], start=True, stop=True).then_inc(turned4, 1)
                pe.wait_ge(v4, 2 * H + 1 + 5)
                nc.tensor.transpose(pt[:, 2 * P:2 * P + 2 * H], rows[0:2 * H, 3, :], k.ident[0:2 * H, 0:2 * H]).then_inc(turned4, 1)

            @block.scalar
            def _(act):
                act.wait_ge(v4, 4 * H + 10)
                nc.scalar.activation(es[:, :, :], es[:, :, :], ACT.Exp).then_inc(exp4, 1)

            @block.sync
            def _(sp):
                sp.wait_ge(exp4, 1)
                sp.dma_start(p_dram[0:EPAD, :].rearrange("(q i) h -> q i h", q=P), es[:, :, :]).then_inc(stored4, 16)
                sp.wait_ge(stored4, 16)

        got5, turned5, v5 = sem("got5"), sem("turned5"), sem("v5")
        by_tile = p_dram.rearrange("(t l) h -> t (l h)", l=P)
        w3 = weights[:, :].rearrange("p (s h) -> p s h", h=H)
        with nc.Block() as block:
            @block.gpsimd
            def _(pool):
                for g in range(SG):
                    nc.gpsimd.indirect_dma_start(out=tiles[:, g, :], out_offset=None, in_=by_tile,
                                                 in_offset=bass.IndirectOffsetOnAxis(ap=k.tile_idx[:, g:g + 1], axis=0)).then_inc(got5, 16)

            @block.tensor
            def _(pe):
                pe.wait_ge(got5, 16 * SG)
                for n in range(SG * H):
                    g, q = n // H, n % H
                    if n >= 2:
                        pe.wait_ge(v5, n - 1)
                    nc.tensor.transpose(pw[:, n % 2, 0:P], tiles[:, g, :].rearrange("s (l h) -> s l h", h=H)[:, :, q], k.ident[:, :]).then_inc(turned5, 1)

            @block.vector
            def _(dve):
                for n in range(SG * H):
                    g, q = n // H, n % H
                    dve.wait_ge(turned5, n + 1)
                    nc.vector.tensor_copy(w3[:, g * P:(g + 1) * P, q], pw[:, n % 2, 0:P]).then_inc(v5, 1)


def stage_gat_self(nc, k, name, heads, acc, p_self):
    C = D // heads
    with ExitStack() as ctx:
        sb, ps, sem = allocators(nc, ctx, name)
        with nc.Block() as block:
            @block.vector
            def _(dve):
                nc.vector.tensor_copy(acc[:, :, D:D + heads], p_self[:, :, :])
                with nc.vector.Fori(0, NB) as n:
                    a = acc[:, bass.ds(n, 1), 0:D].rearrange("p a (h c) -> p (a h) c", c=C)
                    nc.vector.tensor_tensor(a, a, p_self[:, bass.ds(n, 1), :].rearrange("p a h -> p (a h)").unsqueeze(2)
                                            .to_broadcast([P, heads, C]), ALU.mult)


HEADS1, DH1 = 4, 32
INNER1 = HEADS1 * DH1
MEM = 4
assert INNER1 == P


def sum_squares(nc, dve, v, c, x, sq, ss):
    for g in range(NG):
        b = slice(g * CG, (g + 1) * CG)
        if c.n:
            dve.wait_ge(v, c.n)
        nc.vector.tensor_tensor(sq[:, :, :], x[:, b, 0:D], x[:, b, 0:D], ALU.mult).then_inc(v, c.one())
        dve.wait_ge(v, c.n)
        nc.vector.tensor_reduce(ss[:, b], sq[:, :, :], AX.X, ALU.add).then_inc(v, c.one())


def inverse_norm(nc, dve, v, c, rooted, ss, dev, rn, t):
    dve.wait_ge(v, c.n)
    nc.vector.tensor_scalar(ss[:, :], ss[:, :], 1e-24, None, ALU.max).then_inc(v, c.one())
    at = c.n
    dve.wait_ge(rooted, 1)
    nc.vector.reciprocal(rn[:, :], dev[:, :]).then_inc(v, c.one())
    dve.wait_ge(v, c.n)
    sharpen_inverse_root(nc, dve, v, c.n, ss[:, :], rn[:, :], t[:, :])
    c.n += 4
    return at


def stage_mix1(nc, k, xn, acc, w_qkv, g_pre, mem_k, mem_k_t, mem_v_t, w_out, b_out, g_out, x_out):
    with ExitStack() as ctx:
        sb, ps, sem = allocators(nc, ctx, "mix1")
        kv = sb("kv", [P, NB, D + 1])
        q = sb("q", [P, NB, INNER1])
        w_sb = sb("w", [P, 2, 3 * INNER1])
        gp = sb("gp", [P, 2])
        wo = sb("wo", [P, D])
        bo = sb("bo", [P, D])
        go = sb("go", [P, D])
        mk = sb("mk", [P, MEM])
        mkt = sb("mkt", [MEM, INNER1])
        mvt = sb("mvt", [MEM, INNER1 + 1])
        sq = q[:, 0:2 * CG, :].rearrange("p (g b) c -> p g (b c)", b=D // INNER1)
        ss = sb("ss", [P, NB])
        dev = sb("dev", [P, NB])
        rn = sb("rn", [P, NB])
        t = sb("t", [P, NB])
        staged = sb("staged", [P, 2, D])
        xt = sb("xt", [P, 2, D])
        top = sb("top", [P, INNER1])
        most = sb("most", [P, 2])
        low = sb("low", [P, 1])
        diag = sb("diag", [P, P])
        tops = sb("tops", [P, INNER1])
        qm = sb("qm", [P, NB * HEADS1])
        rz = sb("rz", [P, 1])
        att = sb("att", [P, P])
        att_t = sb("att_t", [P, P])
        mix = sb("mix", [P, D])
        pt = ps("pt", [P, 2, 512])
        po = ps("po", [P, 2, 512])
        pc = ps("pc", [P, 512])
        real = k.before[:, LASTROWS:LASTROWS + 1]
        heads = lambda a: a.rearrange("p b (h d) -> p (b h) d", d=DH1)

        loaded, v0, root0 = sem("loaded"), sem("v0"), sem("root0")
        c0 = Tally()
        at0 = []
        with nc.Block() as block:
            @block.sync
            def _(sp):
                for to, src in ((w_sb[:, :, :], w_qkv.rearrange("(c p) n -> p c n", p=P)), (gp[:, :], g_pre), (wo[:, :], w_out),
                                (bo[:, :], on_all(b_out)), (go[:, :], on_all(g_out)), (mk[:, :], mem_k), (mkt[:, :], mem_k_t),
                                (mvt[:, 0:INNER1], mem_v_t)):
                    sp.dma_start(to, src).then_inc(loaded, 16)

            @block.vector
            def _(dve):
                sum_squares(nc, dve, v0, c0, xn, sq, ss)
                at0.append(inverse_norm(nc, dve, v0, c0, root0, ss, dev, rn, t))
                nc.vector.memset(kv[:, :, D:D + 1], 1.0)
                nc.vector.memset(mvt[:, INNER1:], 1.0)
                dve.wait_ge(loaded, 16 * 8)
                for c in range(2):
                    nc.vector.tensor_scalar(w_sb[:, c, :], w_sb[:, c, :], gp[:, c:c + 1], float(D) ** 0.5, ALU.mult, ALU.mult)
                nc.vector.tensor_scalar(go[:, :], go[:, :], float(D) ** 0.5, None, ALU.mult)

            @block.scalar
            def _(act):
                act.wait_ge(v0, at0[0])
                nc.scalar.activation(dev[:, :], ss[:, :], ACT.Sqrt).then_inc(root0, 1)

        turned, copied, multiplied, scaled, kept_q = (sem(n) for n in ("turned", "copied", "multiplied", "scaled", "kept_q"))
        with nc.Block() as block:
            @block.tensor
            def _(pe):
                pe.sem_inc(turned, 2)
                pe.sem_inc(multiplied, 2)

                def turn(n, h):
                    pe.wait_ge(copied, n + 1)
                    pe.wait_ge(scaled, n + 1)
                    for c in range(2):
                        last = nc.tensor.transpose(pt[:, h, c * P:(c + 1) * P], staged[:, h, c * P:(c + 1) * P], k.ident[:, :])
                    last.then_inc(turned, 1)

                def multiply(n, h):
                    pe.wait_ge(copied, n + 3)
                    pe.wait_ge(kept_q, n + 1)
                    for c in range(2):
                        last = nc.tensor.matmul(po[:, h, 0:3 * INNER1], xt[:, h, c * P:(c + 1) * P], w_sb[:, c, :],
                                                start=(c == 0), stop=(c == 1))
                    last.then_inc(multiplied, 1)

                turn(0, 0)
                with nc.tensor.Fori(0, NB // 2) as i:
                    turn(2 * i + 1, 1)
                    multiply(2 * i, 0)
                    turn(2 * i + 2, 0)
                    multiply(2 * i + 1, 1)
                multiply(NB - 1, 0)

            @block.scalar
            def _(act):
                act.sem_inc(copied, 2)

                def copy(n, h):
                    act.wait_ge(turned, n + 3)
                    act.wait_ge(multiplied, n + 1)
                    nc.scalar.activation(xt[:, h, :], pt[:, h, 0:D], ACT.Copy).then_inc(copied, 1)
                paired(nc.scalar, copy)

            @block.vector
            def _(dve):
                dve.sem_inc(kept_q, 2)

                def scale(n, h):
                    dve.wait_ge(turned, n + 1)
                    nc.vector.tensor_scalar(staged[:, h:h + 1, :], xn[:, bass.ds(n, 1), :], rn[:, bass.ds(n, 1)],
                                            None, ALU.mult).then_inc(scaled, 1)

                def finish(n, h):
                    dve.wait_ge(multiplied, n + 3)
                    nc.vector.tensor_copy(kv[:, bass.ds(n, 1), 0:D], po[:, h:h + 1, INNER1:3 * INNER1])
                    nc.vector.tensor_copy(q[:, bass.ds(n, 1), :], po[:, h:h + 1, 0:INNER1]).then_inc(kept_q, 1)

                scale(0, 0)
                with nc.vector.Fori(0, NB // 2) as i:
                    scale(2 * i + 1, 1)
                    finish(2 * i, 0)
                    scale(2 * i + 2, 0)
                    finish(2 * i + 1, 1)
                finish(NB - 1, 0)

        v1, turned1, exp1 = sem("v1"), sem("turned1"), sem("exp1")
        c1 = Tally()
        with nc.Block() as block:
            @block.vector
            def _(dve):
                nc.vector.tensor_scalar(low[:, :], real, -LOW, LOW, ALU.mult, ALU.add).then_inc(v1, c1.one())
                dve.wait_ge(v1, c1.n)
                last = kv[:, NB - 1, 0:INNER1]
                nc.vector.tensor_scalar(last, last, real, low[:, :], ALU.mult, ALU.add).then_inc(v1, c1.one())
                dve.wait_ge(v1, c1.n)
                nc.vector.tensor_reduce(top[:, :], kv[:, :, 0:INNER1].rearrange("p b c -> p c b"), AX.X, ALU.max).then_inc(v1, c1.one())
                nc.vector.tensor_reduce(most[:, 1:2], mk[:, :], AX.X, ALU.max).then_inc(v1, c1.one())
                nc.vector.tensor_reduce(qm[:, :], heads(q[:, :, :]), AX.X, ALU.max).then_inc(v1, c1.one())
                dve.wait_ge(v1, c1.n)
                nc.vector.tensor_tensor(heads(q[:, :, :]), heads(q[:, :, :]), qm[:, :].unsqueeze(2).to_broadcast([P, NB * HEADS1, DH1]),
                                        ALU.subtract).then_inc(v1, c1.one())
                dve.wait_ge(turned1, 1)
                nc.vector.tensor_reduce(most[:, 0:1], pt[:, 0, 0:P], AX.X, ALU.max).then_inc(v1, c1.one())
                dve.wait_ge(v1, c1.n)
                nc.vector.tensor_tensor(most[:, 0:1], most[:, 0:1], most[:, 1:2], ALU.max).then_inc(v1, c1.one())
                dve.wait_ge(v1, c1.n)
                nc.vector.tensor_scalar(diag[:, :], k.ident[:, :], most[:, 0:1], None, ALU.mult).then_inc(v1, c1.one())
                dve.wait_ge(turned1, 2)
                nc.vector.tensor_copy(tops[:, :], pt[:, 1, 0:P]).then_inc(v1, c1.one())
                dve.wait_ge(v1, c1.n)
                nc.vector.tensor_tensor(mkt[:, :], mkt[:, :], tops[0:MEM, :], ALU.subtract).then_inc(v1, c1.one())
                nc.vector.tensor_tensor(kv[:, :, 0:INNER1], kv[:, :, 0:INNER1], tops[:, :].unsqueeze(1).to_broadcast([P, NB, INNER1]),
                                        ALU.subtract).then_inc(v1, c1.one())
                dve.wait_ge(exp1, 1)
                nc.vector.tensor_reduce(qm[:, :], heads(q[:, :, :]), AX.X, ALU.add).then_inc(v1, c1.one())
                dve.wait_ge(v1, c1.n)
                nc.vector.reciprocal(qm[:, :], qm[:, :])

            @block.tensor
            def _(pe):
                pe.wait_ge(v1, 3)
                nc.tensor.transpose(pt[:, 0, 0:P], top[:, :], k.ident[:, :]).then_inc(turned1, 1)
                pe.wait_ge(v1, 9)
                nc.tensor.matmul(pt[:, 1, 0:P], k.ones[:, :], diag[:, :], start=True, stop=True).then_inc(turned1, 1)

            @block.scalar
            def _(act):
                act.wait_ge(v1, 6)
                nc.scalar.activation(q[:, :, :], q[:, :, :], ACT.Exp).then_inc(exp1, 1)
                act.wait_ge(v1, 11)
                nc.scalar.activation(mkt[:, :], mkt[:, :], ACT.Exp).then_inc(exp1, 1)

        e_ready, e_used, seen2 = sem("e_ready"), sem("e_used"), sem("seen2")
        with nc.Block() as block:
            @block.scalar
            def _(act):
                def exponentiate(n, h):
                    act.wait_ge(e_used, n + 1)
                    act.sem_inc(seen2, 1)
                    nc.scalar.activation(xt[:, h:h + 1, 0:INNER1], kv[:, bass.ds(n, 1), 0:INNER1], ACT.Exp).then_inc(e_ready, 1)
                paired(nc.scalar, exponentiate)

            @block.tensor
            def _(pe):
                pe.sem_inc(e_used, 2)
                nc.tensor.matmul(pc[:, 0:INNER1 + 1], mkt[:, :], mvt[:, :], start=True, stop=False)

                def multiply(n, h):
                    pe.wait_ge(e_ready, n + 1)
                    nc.tensor.matmul(pc[:, 0:INNER1 + 1], xt[:, h, 0:INNER1], kv[:, bass.ds(n, 1), INNER1:D + 1].rearrange("p a d -> p (a d)"),
                                     start=False, stop=isinstance(n, int)).then_inc(e_used, 1)
                paired(nc.tensor, multiply)

        v2, made2 = sem("v2"), sem("made2")
        with nc.Block() as block:
            @block.vector
            def _(dve):
                nc.vector.memset(att[:, :], 0.0).then_inc(v2, 1)
                nc.vector.reciprocal(rz[:, :], pc[:, INNER1:INNER1 + 1]).then_inc(v2, 1)
                dve.wait_ge(v2, 2)
                nc.vector.tensor_scalar(rz[:, :], rz[:, :], DH1 ** -0.5, None, ALU.mult).then_inc(v2, 1)
                dve.wait_ge(v2, 3)
                for h in range(HEADS1):
                    s = slice(h * DH1, (h + 1) * DH1)
                    nc.vector.tensor_scalar(att[s, s], pc[s, s], rz[s, :], None, ALU.mult).then_inc(v2, 1)
                dve.wait_ge(made2, 1)
                nc.vector.tensor_copy(att_t[:, :], pt[:, 0, 0:P]).then_inc(v2, 1)
                dve.wait_ge(made2, 2)
                nc.vector.tensor_copy(mix[:, :], po[:, 0, 0:D])

            @block.tensor
            def _(pe):
                pe.wait_ge(v2, 3 + HEADS1)
                nc.tensor.transpose(pt[:, 0, 0:P], att[:, :], k.ident[:, :]).then_inc(made2, 1)
                pe.wait_ge(v2, 4 + HEADS1)
                nc.tensor.matmul(po[:, 0, 0:D], att_t[:, :], wo[:, :], start=True, stop=True).then_inc(made2, 1)

        turned3, copied3, multiplied3, done3, scaled3 = (sem(n) for n in ("turned3", "copied3", "multiplied3", "done3", "scaled3"))
        with nc.Block() as block:
            @block.tensor
            def _(pe):
                pe.sem_inc(turned3, 2)
                pe.sem_inc(multiplied3, 2)

                def turn(n, h):
                    pe.wait_ge(copied3, n + 1)
                    pe.wait_ge(scaled3, n + 1)
                    nc.tensor.transpose(pt[:, h, 0:P], staged[:, h, 0:P], k.ident[:, :]).then_inc(turned3, 1)

                def multiply(n, h):
                    pe.wait_ge(copied3, n + 3)
                    pe.wait_ge(done3, n + 1)
                    nc.tensor.matmul(po[:, h, 0:D], xt[:, h, 0:P], mix[:, :], start=True, stop=True).then_inc(multiplied3, 1)

                turn(0, 0)
                with nc.tensor.Fori(0, NB // 2) as i:
                    turn(2 * i + 1, 1)
                    multiply(2 * i, 0)
                    turn(2 * i + 2, 0)
                    multiply(2 * i + 1, 1)
                multiply(NB - 1, 0)

            @block.scalar
            def _(act):
                act.sem_inc(copied3, 2)

                def copy(n, h):
                    act.wait_ge(turned3, n + 3)
                    act.wait_ge(multiplied3, n + 1)
                    nc.scalar.activation(xt[:, h, 0:P], pt[:, h, 0:P], ACT.Copy).then_inc(copied3, 1)
                paired(nc.scalar, copy)

            @block.vector
            def _(dve):
                dve.sem_inc(done3, 2)

                def scale(n, h):
                    dve.wait_ge(turned3, n + 1)
                    nc.vector.tensor_tensor(staged[:, h, 0:P].rearrange("p (h d) -> p h d", d=DH1),
                                            q[:, bass.ds(n, 1), :].rearrange("p a (h d) -> p (a h) d", d=DH1),
                                            qm[:, bass.ds(n * HEADS1, HEADS1)].unsqueeze(2).to_broadcast([P, HEADS1, DH1]),
                                            ALU.mult).then_inc(scaled3, 1)

                def finish(n, h):
                    dve.wait_ge(multiplied3, n + 3)
                    nc.vector.tensor_tensor(kv[:, bass.ds(n, 1), 0:D], po[:, h:h + 1, 0:D], bo[:, :].unsqueeze(1), ALU.add).then_inc(done3, 1)

                scale(0, 0)
                with nc.vector.Fori(0, NB // 2) as i:
                    scale(2 * i + 1, 1)
                    finish(2 * i, 0)
                    scale(2 * i + 2, 0)
                    finish(2 * i + 1, 1)
                finish(NB - 1, 0)

        v4, root4, added4, stored4 = sem("v4"), sem("root4"), sem("added4"), sem("stored4")
        c4 = Tally()
        at4 = []
        with nc.Block() as block:
            @block.vector
            def _(dve):
                sum_squares(nc, dve, v4, c4, kv, sq, ss)
                at4.append(inverse_norm(nc, dve, v4, c4, root4, ss, dev, rn, t))
                for b in range(NB):
                    nc.vector.scalar_tensor_tensor(out=kv[:, b, 0:D], in0=kv[:, b, 0:D], scalar=rn[:, b:b + 1], in1=go[:, :],
                                                   op0=ALU.mult, op1=ALU.mult).then_inc(v4, c4.one())
                for g in range(NG):
                    b = slice(g * CG, (g + 1) * CG)
                    nc.vector.tensor_tensor(acc[:, b, 0:D], acc[:, b, 0:D], xn[:, b, :], ALU.add).then_inc(v4, c4.one())
                for g in range(NG):
                    b = slice(g * CG, (g + 1) * CG)
                    dve.wait_ge(v4, c4.n)
                    nc.vector.tensor_tensor(acc[:, b, 0:D], acc[:, b, 0:D], kv[:, b, 0:D], ALU.add).then_inc(added4, 1)

            @block.scalar
            def _(act):
                act.wait_ge(v4, at4[0])
                nc.scalar.activation(dev[:, :], ss[:, :], ACT.Sqrt).then_inc(root4, 1)

            @block.sync
            def _(sp):
                for g in range(NG):
                    b = slice(g * CG, (g + 1) * CG)
                    sp.wait_ge(added4, g + 1)
                    sp.dma_start(in_blocks(x_out)[:, b, :], acc[:, b, 0:D]).then_inc(stored4, 16)
                sp.wait_ge(stored4, 16 * NG)


def divide_sums(nc, dve, v, c, acc, rz, bias, heads):
    nc.vector.reciprocal(rz[:, :, :], acc[:, :, D:D + heads]).then_inc(v, c.one())
    dve.wait_ge(v, c.n)
    for q in range(heads):
        s = slice(q * (D // heads), (q + 1) * (D // heads))
        nc.vector.tensor_tensor(acc[:, :, s], acc[:, :, s], rz[:, :, q:q + 1].to_broadcast([P, NB, D // heads]), ALU.mult).then_inc(v, c.one())
    dve.wait_ge(v, c.n)
    nc.vector.tensor_tensor(acc[:, :, 0:D], acc[:, :, 0:D], bias[:, :].unsqueeze(1).to_broadcast([P, NB, D]), ALU.add).then_inc(v, c.one())
    dve.wait_ge(v, c.n)


def stage_gat_norm(nc, k, acc, xn, bias, gamma, beta):
    with ExitStack() as ctx:
        sb, ps, sem = allocators(nc, ctx, "gnorm")
        rz = sb("rz", [P, NB, HEADS1])
        bi, ga, be = sb("bi", [P, D]), sb("ga", [P, D]), sb("be", [P, D])
        part = sb("part", [P, D])
        mean = sb("mean", [P, D])
        var, dev, rstd, t = sb("var", [P, D]), sb("dev", [P, D]), sb("rstd", [P, D]), sb("t", [P, D])
        pm = ps("pm", [P, 2, 512])
        loaded, v, squared, summed, rooted, exped = (sem(n) for n in ("loaded", "v", "squared", "summed", "rooted", "exped"))
        real = k.before[:, LASTROWS:LASTROWS + 1]
        c = Tally()
        at = {}
        a = acc[:, :, 0:D]
        wide = lambda r: r[:, :].unsqueeze(1).to_broadcast([P, NB, D])
        with nc.Block() as block:
            @block.sync
            def _(sp):
                for to, src in ((bi, bias), (ga, gamma), (be, beta)):
                    sp.dma_start(to[:, :], on_all(src)).then_inc(loaded, 16)

            @block.vector
            def _(dve):
                dve.wait_ge(loaded, 48)
                divide_sums(nc, dve, v, c, acc, rz, bi, HEADS1)

                def clear_padding():
                    nc.vector.tensor_scalar(acc[:, NB - 1, 0:D], acc[:, NB - 1, 0:D], real, None, ALU.mult).then_inc(v, c.one())
                    dve.wait_ge(v, c.n)
                clear_padding()
                nc.vector.tensor_reduce(part[:, :], a.rearrange("p b d -> p d b"), AX.X, ALU.add).then_inc(v, c.one())
                at["sum"] = c.n
                dve.wait_ge(summed, 1)
                nc.vector.tensor_scalar(mean[:, :], pm[:, 0, 0:D], 1.0 / NODES, None, ALU.mult).then_inc(v, c.one())
                dve.wait_ge(v, c.n)
                nc.vector.tensor_tensor(a, a, wide(mean), ALU.subtract).then_inc(v, c.one())
                dve.wait_ge(v, c.n)
                clear_padding()
                at["square"] = c.n
                dve.wait_ge(squared, 1)
                nc.vector.tensor_reduce(part[:, :], xn[:, :, :].rearrange("p b d -> p d b"), AX.X, ALU.add).then_inc(v, c.one())
                at["sum2"] = c.n
                dve.wait_ge(summed, 2)
                nc.vector.tensor_scalar(var[:, :], pm[:, 1, 0:D], 1.0 / NODES, 1e-5, ALU.mult, ALU.add).then_inc(v, c.one())
                at["root"] = c.n
                dve.wait_ge(rooted, 1)
                nc.vector.reciprocal(rstd[:, :], dev[:, :]).then_inc(v, c.one())
                dve.wait_ge(v, c.n)
                sharpen_inverse_root(nc, dve, v, c.n, var[:, :], rstd[:, :], t[:, :])
                c.n += 4
                nc.vector.tensor_tensor(rstd[:, :], rstd[:, :], ga[:, :], ALU.mult).then_inc(v, c.one())
                dve.wait_ge(v, c.n)
                nc.vector.tensor_tensor(a, a, wide(rstd), ALU.mult).then_inc(v, c.one())
                dve.wait_ge(v, c.n)
                nc.vector.tensor_tensor(a, a, wide(be), ALU.add).then_inc(v, c.one())
                dve.wait_ge(v, c.n)
                nc.vector.tensor_scalar(xn[:, :, :], a, 0.0, None, ALU.min).then_inc(v, c.one())
                at["exp"] = c.n
                nc.vector.tensor_scalar(a, a, 0.0, None, ALU.max).then_inc(v, c.one())
                dve.wait_ge(v, c.n)
                dve.wait_ge(exped, 1)
                nc.vector.scalar_tensor_tensor(out=xn[:, :, :], in0=xn[:, :, :], scalar=-1.0, in1=a, op0=ALU.add, op1=ALU.add)

            @block.tensor
            def _(pe):
                pe.wait_ge(v, at["sum"])
                nc.tensor.matmul(pm[:, 0, 0:D], k.ones[:, :], part[:, :], start=True, stop=True).then_inc(summed, 1)
                pe.wait_ge(v, at["sum2"])
                nc.tensor.matmul(pm[:, 1, 0:D], k.ones[:, :], part[:, :], start=True, stop=True).then_inc(summed, 1)

            @block.scalar
            def _(act):
                act.wait_ge(v, at["square"])
                nc.scalar.activation(xn[:, :, :], a, ACT.Square).then_inc(squared, 1)
                act.wait_ge(v, at["root"])
                nc.scalar.activation(dev[:, :], var[:, :], ACT.Sqrt).then_inc(rooted, 1)
                act.wait_ge(v, at["exp"])
                nc.scalar.activation(xn[:, :, :], xn[:, :, :], ACT.Exp).then_inc(exped, 1)


def stage_gat_out(nc, k, acc, bias, x_in, xin):
    with ExitStack() as ctx:
        sb, ps, sem = allocators(nc, ctx, "gout")
        rz = sb("rz", [P, NB, 1])
        bi = sb("bi", [P, D])
        sq = sb("sq", [P, CG, D])
        ss, dev, rn, t = sb("ss", [P, NB]), sb("dev", [P, NB]), sb("rn", [P, NB]), sb("t", [P, NB])
        loaded, v, rooted = sem("loaded"), sem("v"), sem("rooted")
        c = Tally()
        at = []
        with nc.Block() as block:
            @block.sync
            def _(sp):
                sp.dma_start(bi[:, :], on_all(bias)).then_inc(loaded, 16)
                sp.dma_start(xin[:, :, :], in_blocks(x_in)).then_inc(loaded, 16)

            @block.vector
            def _(dve):
                dve.wait_ge(loaded, 32)
                divide_sums(nc, dve, v, c, acc, rz, bi, 1)
                sum_squares(nc, dve, v, c, acc, sq, ss)
                at.append(inverse_norm(nc, dve, v, c, rooted, ss, dev, rn, t))
                for b in range(NB):
                    nc.vector.scalar_tensor_tensor(out=acc[:, b, 0:D], in0=acc[:, b, 0:D], scalar=rn[:, b:b + 1], in1=xin[:, b, :],
                                                   op0=ALU.mult, op1=ALU.add)

            @block.scalar
            def _(act):
                act.wait_ge(v, at[0])
                nc.scalar.activation(dev[:, :], ss[:, :], ACT.Sqrt).then_inc(rooted, 1)


GB = 7
HALFTOK = GB * P // 2
SLOT_BLOCKS = NB + EXPERTS - 1
SLOT_GROUPS = -(-SLOT_BLOCKS // GB)
assert SLOT_GROUPS * GB * P <= EXPERTS * CAPPAD


def in_pairs(engine, count, one):
    with engine.Fori(0, count // 2) as i:
        for h in range(2):
            one(2 * i + h, h)
    if count % 2:
        one(count - 1, 0)


def stage_ffn1(nc, k, name, groups, rows, w1, b1, wg=None, bg=None, logits=None,
               wd=None, bd=None, block_expert=None, out=None):
    WIDTH = EXPERTS if wg is not None else D
    with ExitStack() as ctx:
        sb, ps, sem = allocators(nc, ctx, name)
        w1_sb = sb("w1", [P, 2, HID])
        b1_sb = sb("b1", [P, FC])
        x_sb = sb("x", [P, 2, GB, D])
        xt = sb("xt", [P, 2, GB * P])
        ht = sb("ht", [P, FC, GB * P])
        if wg is not None:
            wg_sb = sb("wg", [P, FC, EXPERTS])
            bg_sb = sb("bg", [P, EXPERTS])
        else:
            wd_sb = sb("wd", [P, EXPERTS, FC * D])
            bd_sb = sb("bd", [P, EXPERTS, D])
            y_sb = sb("y", [P, GB, D])
        pt = ps("pt", [P, 2, 512])
        ph = [ps(f"ph{j}", [P, 512]) for j in range(4)]
        py = [ps(f"py{j}", [P, 512]) for j in range(2)]
        wloaded = sem("wloaded")
        dloaded = sem("dloaded")
        loaded = [sem("loaded0"), sem("loaded1")]
        stored = sem("stored")
        turned = sem("turned")
        copied = sem("copied")
        h_made = sem("h_made")
        active = sem("active")
        y_made = sem("y_made")
        evacuated = sem("evacuated")
        y_free = sem("y_free")
        DLOADS = 2 if wg is not None else 1 + EXPERTS

        with nc.Block() as block:
            @block.sync
            def _(sp):
                sp.dma_start(w1_sb[:, :, :], w1.rearrange("(c p) n -> p c n", p=P)).then_inc(wloaded, 16)
                sp.dma_start(b1_sb[:, :], b1).then_inc(wloaded, 16)

                def load(n, h):
                    sp.wait_ge(turned, GB * n + GB)
                    sp.dma_start(x_sb[:, h, :, :], rows[:, bass.ds(GB * n, GB), :]).then_inc(loaded[h], 16)
                in_pairs(nc.sync, groups, load)

            @block.gpsimd
            def _(pool):
                if wg is not None:
                    pool.dma_start(wg_sb[:, :, :], wg.rearrange("(f p) e -> p f e", p=P)).then_inc(dloaded, 16)
                    pool.dma_start(bg_sb[:, :], on_all(bg)).then_inc(dloaded, 16)
                    return
                pool.dma_start(bd_sb[:, :, :], bd.rearrange("e (a n) -> a e n", a=1).to_broadcast([P, EXPERTS, D])).then_inc(dloaded, 16)
                for e in range(EXPERTS):
                    pool.dma_start(wd_sb[:, e, :].rearrange("p (f n) -> p f n", n=D),
                                   wd[e].rearrange("(f p) n -> p f n", p=P)).then_inc(dloaded, 16)

                pool.sem_inc(y_free, 1)

                def store(n, h):
                    pool.wait_ge(evacuated, GB * n + GB + 2)
                    pool.dma_start(out[:, bass.ds(GB * n, GB), :], y_sb[:, :, :]).then_inc(stored, 16)
                    pool.wait_ge(stored, 16 * n + 16)
                    pool.sem_inc(y_free, 1)
                in_pairs(nc.gpsimd, groups, store)

            @block.tensor
            def _(pe):
                pe.sem_inc(turned, 2 * GB)
                pe.wait_ge(wloaded, 32)
                pe.wait_ge(dloaded, 16 * DLOADS)

                def group(n, h):
                    pe.wait_ge(loaded[h], 16 * half_index(n, h))
                    for t in range(GB):
                        pe.wait_ge(copied, GB * n + t + 1)
                        for c in range(2):
                            last = nc.tensor.transpose(pt[:, (t + h) % 2, c * P:(c + 1) * P],
                                                       x_sb[:, h, t, c * P:(c + 1) * P], k.ident[:, :])
                        last.then_inc(turned, 1)
                    if wd is not None:
                        _, experts = nc.values_load_multi_w_load_instructions(
                            block_expert[0:1, bass.ds(GB * n, GB)], engines=(mybir.EngineType.PE,), min_val=0, max_val=EXPERTS - 1,
                            skip_runtime_bounds_check_because="a block's expert counts experts before the last")
                    for half in range(2):
                        pe.wait_ge(copied, GB * n + (GB + 1) // 2 * (1 - half) + GB * half + 2)
                        for f in range(FC):
                            pe.wait_ge(active, 2 * FC * n + FC * half + f + 1)
                            for c in range(2):
                                last = nc.tensor.matmul(ph[f % 4][:, 0:HALFTOK], w1_sb[:, c, f * P:(f + 1) * P],
                                                        xt[:, c, half * HALFTOK:(half + 1) * HALFTOK], start=(c == 0), stop=(c == 1))
                            last.then_inc(h_made, 1)
                    for t in range(GB):
                        if t == 0:
                            pe.wait_ge(active, 2 * FC * n + FC + 4)
                        if t == GB // 2:
                            pe.wait_ge(active, 2 * FC * n + 2 * FC + 4)
                        pe.wait_ge(evacuated, GB * n + t + 1)
                        for f in range(FC):
                            rhs = wg_sb[:, f, :] if wg is not None else \
                                wd_sb[:, bass.ds(experts[t], 1), f * D:(f + 1) * D].rearrange("p a d -> p (a d)")
                            last = nc.tensor.matmul(py[(t + h) % 2][:, 0:WIDTH], ht[:, f, t * P:(t + 1) * P], rhs,
                                                    start=(f == 0), stop=(f == FC - 1))
                        last.then_inc(y_made, 1)
                in_pairs(nc.tensor, groups, group)

            @block.scalar
            def _(act):
                act.sem_inc(active, 4)
                act.wait_ge(wloaded, 32)

                def activate(n, h):
                    for half in range(2):
                        for f in range(FC):
                            act.wait_ge(h_made, 2 * FC * n + FC * half + f + 1)
                            nc.scalar.activation(ht[:, f, half * HALFTOK:(half + 1) * HALFTOK], ph[f % 4][:, 0:HALFTOK], ACT.Gelu,
                                                 bias=b1_sb[:, f:f + 1]).then_inc(active, 1)
                in_pairs(nc.scalar, groups, activate)

            @block.vector
            def _(dve):
                dve.sem_inc(copied, 2)
                dve.sem_inc(evacuated, 2)
                dve.wait_ge(dloaded, 16 * DLOADS)

                def group(n, h):
                    if wd is not None:
                        _, experts = nc.values_load_multi_w_load_instructions(
                            block_expert[0:1, bass.ds(GB * n, GB)], engines=(mybir.EngineType.DVE,), min_val=0, max_val=EXPERTS - 1,
                            skip_runtime_bounds_check_because="a block's expert counts experts before the last")
                    for t in range(GB):
                        dve.wait_ge(turned, GB * n + 2 * GB + t + 1)
                        nc.vector.tensor_copy(xt[:, :, t * P:(t + 1) * P],
                                              pt[:, (t + h) % 2, 0:D].rearrange("p (c n) -> p c n", c=2)).then_inc(copied, 1)
                    if wd is not None:
                        dve.wait_ge(y_free, n + 1)
                    for t in range(GB):
                        dve.wait_ge(y_made, GB * n + t + 1)
                        y = py[(t + h) % 2]
                        if wd is not None:
                            nc.vector.tensor_tensor(y_sb[:, t:t + 1, :], y[:, 0:D].unsqueeze(1), bd_sb[:, bass.ds(experts[t], 1), :],
                                                    ALU.add).then_inc(evacuated, 1)
                        else:
                            nc.vector.tensor_tensor(logits[:, bass.ds(GB * n + t, 1), :], y[:, 0:EXPERTS].unsqueeze(1),
                                                    bg_sb[:, :].unsqueeze(1), ALU.add).then_inc(evacuated, 1)
                in_pairs(nc.vector, groups, group)


def stage_clear(nc, k, tables):
    WIDE = max(t.shape[0] * t.shape[1] // P for t in tables)
    with ExitStack() as ctx:
        sb, ps, sem = allocators(nc, ctx, "clear")
        zeros = sb("zeros", [P, WIDE])
        zeroed, stored = sem("zeroed"), sem("stored")
        with nc.Block() as block:
            @block.vector
            def _(dve):
                nc.vector.memset(zeros[:, :], 0.0).then_inc(zeroed, 1)
                nc.vector.memset(k.dots[:, :, :], 0.0)

            @block.sync
            def _(sp):
                sp.wait_ge(zeroed, 1)
                for t in tables:
                    sp.dma_start(t.rearrange("(p a) d -> p (a d)", p=P), zeros[:, 0:t.shape[0] * t.shape[1] // P]).then_inc(stored, 16)
                sp.wait_ge(stored, 16 * len(tables))


def gps_two_layers(nc, a, out):
    dram = lambda n, s: nc.dram_tensor(n, s, f32).ap()
    table = [dram(f"table{j}", [NPAD, D]) for j in range(4)]
    slots = dram("slots", [EXPERTS * CAPPAD, D])
    expert_out = dram("expert_out", [EXPERTS * CAPPAD, D])
    x2 = dram("x2", [NPAD, D])
    gat = [(dram(f"es{j}", [NPAD, 2 * h]), dram(f"run{j}", [EPAD, h]), dram(f"node{j}", [EPAD, 2 * h]), dram(f"p{j}", [EROWS * P, h]))
           for j, h in enumerate((HEADS1, 1))]
    edge_rows = lambda flat: flat.rearrange("(r l) -> r l", l=P)

    with ExitStack() as ctx:
        sb = lambda c, n, s, t=f32: c.enter_context(nc.sbuf_tensor(n, s, t))
        k = Kept(nc, ctx)
        stage_prepare(nc, k, edge_rows(a["src"]), edge_rows(a["dst"]), edge_rows(a["edge_weight"]))
        acc = sb(ctx, "acc", [P, NB, D + HEADS1])
        esd = [sb(ctx, f"esd{j}", [P, NB, 2 * h]) for j, h in enumerate((HEADS1, 1))]

        with ExitStack() as c:
            xn = sb(c, "xn", [P, NB, D])
            with ExitStack() as c0:
                k.dots = sb(c0, "dots", [P, 4, P])
                k.mix = sb(c0, "mix", [P, 2, D])
                with ExitStack() as cc:
                    stage_clear(nc, k, [slots[e * CAPPAD:(e + 1) * CAPPAD, :] for e in range(EXPERTS)] +
                                [g[2] for g in gat] + [g[3][EPAD:, :] for g in gat])
                stage_layernorm(nc, k, "norm0", acc, xn, a["x"])
                stage_scale_store(nc, k, "self0", xn, k.dinv, acc, table[0])
                stage_aggregate(nc, k, "conv0", table[0], acc, D, k.weight, side=Mix0Side(xn, a["L0_mix_Wqkv_t"][:, INNER0:3 * INNER0]))
                stage_mix0_fold(nc, k, a["L0_mix_Wqkv"][0:INNER0, :], a["L0_mix_Wout_t"])
                stage_gcn_dense(nc, k, "dense0", acc, a["L0_gnn_W1"], a["L0_gnn_b1"], table=table[1])
                stage_aggregate(nc, k, "conv1", table[1], acc, D, k.weight)
                stage_gcn_dense(nc, k, "dense1", acc, a["L0_gnn_W2"], a["L0_gnn_b2"], xn=xn, x_in=a["x"], bias2=a["L0_mix_bout"])
            with ExitStack() as c1:
                logits = sb(c1, "logits0", [P, NB, EXPERTS])
                prob = sb(c1, "prob0", [P, NB])
                to_slot, from_slot = sb(c1, "to_slot0", [P, NB], i32), sb(c1, "from_slot0", [P, NB], i32)
                stage_layernorm(nc, k, "norm1", acc, xn)
                stage_gate(nc, k, xn, a["L0_ffn_gate_w"], a["L0_ffn_gate_b"], logits)
                stage_route(nc, k, "route0", logits, prob, to_slot, from_slot, capacity=CAP)
                stage_dispatch(nc, k, "send0", xn, to_slot, slots)
                stage_experts0(nc, k, slots, a["L0_ffn_w1"], a["L0_ffn_b1"], a["L0_ffn_w2"], a["L0_ffn_b2"], expert_out, xn)
                stage_combine(nc, k, "combine0", expert_out, from_slot, acc, prob, True)
            stage_layernorm(nc, k, "norm2", acc, xn)
            stage_mix1(nc, k, xn, acc, a["L1_mix_w_qkv"], a["L1_mix_g_pre"], a["mem_k"], a["mem_k_t"], a["mem_v_t"],
                       a["L1_mix_w_out"], a["L1_mix_b_out"], a["L1_mix_g_out"], x2)
            stage_gat_project(nc, k, "project0", xn, a["L1_gnn_W0"], a["L1_gnn_W0_t"], a["L1_gnn_a_src0"], a["L1_gnn_a_dst0"],
                              HEADS1, acc, esd[0], table[2], gat[0][0])

        def attend(j, heads):
            with ExitStack() as c:
                weights = sb(c, f"weights{j}", [P, SPAD * heads])
                p_self = sb(c, f"p_self{j}", [P, NB, heads])
                stage_gat_weights(nc, k, f"soft{j}", heads, gat[j][0], esd[j], a["src"], a["dst"], a["last_dst"], *gat[j][1:], weights, p_self)
                stage_gat_self(nc, k, f"own{j}", heads, acc, p_self)
                stage_aggregate(nc, k, f"attend{j}", table[2 + j], acc, D + heads, weights, heads=heads if heads > 1 else 0)
        attend(0, HEADS1)
        with ExitStack() as c:
            xn = sb(c, "h1", [P, NB, D])
            stage_gat_norm(nc, k, acc, xn, a["L1_gnn_b0"], a["L1_gnn_gamma0"], a["L1_gnn_beta0"])
            stage_gat_project(nc, k, "project1", xn, a["L1_gnn_W1"], a["L1_gnn_W1_t"], a["L1_gnn_a_src1"], a["L1_gnn_a_dst1"],
                              1, acc, esd[1], table[3], gat[1][0])
        attend(1, 1)

        prob = sb(ctx, "prob1", [P, NB])
        from_slot = sb(ctx, "from_slot1", [P, NB], i32)
        block_expert = sb(ctx, "block_expert", [1, P], i32)
        with ExitStack() as c:
            xn = sb(c, "xn1", [P, NB, D])
            logits = sb(c, "logits1", [P, NB, EXPERTS])
            to_slot = sb(c, "to_slot1", [P, NB], i32)
            stage_gat_out(nc, k, acc, a["L1_gnn_b1"], x2, xn)
            stage_layernorm(nc, k, "norm3", acc, xn)
            stage_ffn1(nc, k, "gate1", NG, xn, a["L1_ffn_W1"], a["L1_ffn_b1"], wg=a["L1_ffn_Wg"], bg=a["L1_ffn_bg"], logits=logits)
            stage_route(nc, k, "route1", logits, prob, to_slot, from_slot, block_expert=block_expert)
            stage_dispatch(nc, k, "send1", xn, to_slot, slots)
        stage_ffn1(nc, k, "experts1", SLOT_GROUPS, in_blocks(slots), a["L1_ffn_W1"], a["L1_ffn_b1"],
                   wd=a["L1_ffn_Wd"], bd=a["L1_ffn_bd"], block_expert=block_expert, out=in_blocks(expert_out))
        stage_combine(nc, k, "combine1", expert_out, from_slot, acc, prob, False, x_out=out)


def kernel(**inputs):
    import concourse.bacc as _bacc
    from concourse.bass_utils import run_bass_kernel_spmd as _run

    arr = {n: np.ascontiguousarray(v) for n, v in inputs.items() if n != "L1_mix_t"}
    turned = lambda v: np.ascontiguousarray(v.T)
    mem = arr.pop("L1_mix_mem_kv")
    dst = arr.pop("dst").astype(np.int32, copy=False)
    src = arr.pop("src").astype(np.int32, copy=False)
    tail = EROWS * P - EDGES
    arr["x"] = np.concatenate([arr["x"], np.zeros((NPAD - NODES, D), arr["x"].dtype)])
    arr["src"] = np.concatenate([src, np.zeros(tail, np.int32)])
    arr["dst"] = np.concatenate([dst, np.full(tail, NODES, np.int32)])
    arr["last_dst"] = np.concatenate([np.full(1, -1, np.int32), arr["dst"][:-1]])
    arr["edge_weight"] = np.concatenate([arr["edge_weight"], np.zeros(tail, arr["edge_weight"].dtype)])
    for n in ("L0_mix_Wqkv", "L1_gnn_W0", "L1_gnn_W1"):
        arr[n + "_t"] = turned(arr[n])
    arr["L0_mix_Wout_t"] = turned(arr.pop("L0_mix_Wout"))
    arr["L0_ffn_b1"] = np.ascontiguousarray(arr["L0_ffn_b1"].reshape(EXPERTS, FC, P).transpose(0, 2, 1))
    arr["L1_ffn_b1"] = turned(arr["L1_ffn_b1"].reshape(FC, P))
    arr["L1_mix_g_pre"] = turned(arr["L1_mix_g_pre"].reshape(2, P))
    arr["mem_k"] = np.ascontiguousarray(mem[0].reshape(INNER1, MEM))
    arr["mem_k_t"] = turned(arr["mem_k"])
    arr["mem_v_t"] = turned(mem[1].reshape(INNER1, MEM))

    nc = _bacc.Bacc("TRN2", target_bir_lowering=False, num_devices=1)
    aps = {n: nc.dram_tensor("in_" + n, v.shape, mybir.dt.from_np(v.dtype), kind="ExternalInput").ap() for n, v in arr.items()}
    out = nc.dram_tensor("out", (NPAD, D), f32, kind="ExternalOutput").ap()
    gps_two_layers(nc, aps, out)
    r = _run(nc, [{"in_" + n: v for n, v in arr.items()}], core_ids=[0])
    return r.results[0]["out"][:NODES]
```

```python
import numpy as np
from contextlib import ExitStack
import concourse.bass as bass
from concourse import mybir

f32 = mybir.dt.float32
i32 = mybir.dt.int32
bf16 = mybir.dt.bfloat16
ALU = mybir.AluOpType
ACT = mybir.ActivationFunctionType
AX = mybir.AxisListType

P = 128
NODES = 6250
D = 256
NB = -(-NODES // P)
NPAD = NB * P
LASTROWS = NODES - (NB - 1) * P
EDGES = 100000
ET = -(-EDGES // P)
EG = -(-ET // P)
STEPS = ET + NB - 1
SG = -(-STEPS // P)
SPAD = SG * P
CG = 7
NG = NB // CG


class Kept:

    def __init__(self, nc, ctx):
        sb = lambda n, s, t=f32: ctx.enter_context(nc.sbuf_tensor(n, s, t))
        self.ident = sb("ident", [P, P])
        self.before = sb("before", [P, P])
        self.ones = sb("ones", [P, P])
        self.iota = sb("iota", [P, P])
        self.row_start = sb("row_start", [P, NB], i32)
        self.row_count = sb("row_count", [P, NB], i32)
        self.dinv = sb("dinv", [P, NB])
        self.src_idx = sb("src_idx", [P, SPAD], i32)
        self.lane = sb("lane", [P, SPAD])
        self.weight = sb("weight", [P, SPAD])
        self.step_blk = sb("step_blk", [P, SPAD], i32)
        self.tile_idx = sb("tile_idx", [P, SG], i32)


def bc(ap, shape):
    return ap.to_broadcast(shape)


def allocators(nc, ctx, stage):
    sems = []

    def clear():
        nc.clear_and_free_semaphores(sems)
        nc.all_engine_barrier()

    def sem(n):
        sems.append(nc.alloc_semaphore(name=f"{stage}_{n}"))
        return sems[-1]

    ctx.callback(clear)
    sb = lambda n, s, t=f32: ctx.enter_context(nc.sbuf_tensor(f"{stage}_{n}", s, t))
    ps = lambda n, s, t=f32: ctx.enter_context(nc.psum_tensor(f"{stage}_{n}", s, t))
    return sb, ps, sem


def stage_prepare(nc, k, src_rows, dst_rows, w_rows):
    T = 17
    assert ET % (2 * T) == 0
    with ExitStack() as ctx:
        sb, ps, sem = allocators(nc, ctx, "prep")
        iota_i = sb("iota_i", [P, P], i32)
        iota_sf = sb("iota_sf", [P, SPAD])
        iota_si = sb("iota_si", [P, SPAD], i32)
        tile_i = sb("tile_i", [P, EG], i32)
        tile_f = sb("tile_f", [P, EG])
        dst_r = sb("dst_r", [P, EG, P], i32)
        w_r = sb("w_r", [P, EG, P])
        dst_rf = sb("dst_rf", [P, EG, P])
        last_i = sb("last_i", [P, EG], i32)
        last_f = sb("last_f", [P, EG])
        key = sb("key", [P, EG])
        dst_t = sb("dst_t", [P, EG * P], i32)
        blk_ti = sb("blk_ti", [P, EG * P], i32)
        lane_ti = sb("lane_ti", [P, EG * P], i32)
        blk_t = sb("blk_t", [P, EG * P])
        lane_t = sb("lane_t", [P, EG * P])
        w_t = sb("w_t", [P, EG * P])
        lane_hot = sb("lane_hot", [P, 2, T, P])
        blk_hot = sb("blk_hot", [P, 2, T, 2, NB])
        cmp = sb("cmp", [P, 2, SPAD])
        counts = sb("counts", [P, 2 * NB])
        deg = sb("deg", [P, NB])
        pos = sb("pos", [P, NB])
        rdeg = sb("rdeg", [P, NB])
        totals = sb("totals", [P, NB])
        base = sb("base", [P, NB])
        zero = sb("zero", [P, NB])
        start_f = sb("start_f", [P, NB])
        step_tile = sb("step_tile", [P, SPAD])
        step_blk = sb("step_blk", [P, SPAD])
        diag = sb("diag", [P, SG, P])
        tile_col = sb("tile_col", [P, SG])
        got_src = sb("got_src", [P, SG, P], i32)
        got_dst = sb("got_dst", [P, SG, P], i32)
        got_w = sb("got_w", [P, SG, P])
        got_srcf = sb("got_srcf", [P, SG, P])
        got_dstf = sb("got_dstf", [P, SG, P])
        psA = ps("psA", [P, 2, 512])
        psB = ps("psB", [P, 2, 512])
        psC = ps("psC", [P, 512])
        psD = ps("psD", [P, 2, 512])
        loaded = sem("loaded")
        pool_done = sem("pool_done")
        v = sem("v_prep")
        turned = sem("turned")
        hot = sem("hot")
        hot_a = sem("hot_a")
        hot_prep = sem("hot_prep")
        counted = sem("counted")
        totalled = sem("totalled")
        compared = sem("compared")
        stepped = sem("stepped")
        gathered = sem("gathered")
        turned2 = sem("turned2")

        with nc.Block() as block:
            @block.sync
            def _(sp):
                sp.dma_start(dst_r[:, :, :], dst_rows.rearrange("(g r) l -> r g l", r=P)).then_inc(loaded, 16)
                sp.dma_start(w_r[:, :, :], w_rows.rearrange("(g r) l -> r g l", r=P)).then_inc(loaded, 16)

            @block.gpsimd
            def _(pool):
                nc.gpsimd.iota(iota_i[:, :], pattern=[[1, P]], base=0, channel_multiplier=0).then_inc(pool_done, 1)
                nc.gpsimd.iota(iota_si[:, :], pattern=[[1, SPAD]], base=0, channel_multiplier=0).then_inc(pool_done, 1)
                nc.gpsimd.iota(tile_i[:, :], pattern=[[P, EG]], base=0, channel_multiplier=1).then_inc(pool_done, 1)
                nc.gpsimd.memset(k.ones[:, :], 1.0).then_inc(pool_done, 1)
                nc.gpsimd.memset(k.ident[:, :], 0.0).then_inc(pool_done, 1)
                pool.wait_ge(pool_done, 5)
                nc.gpsimd.affine_select(out=k.ident[:, :], in_=k.ident[:, :], compare_op=ALU.not_equal, fill=1.0,
                                        base=0, pattern=[[-1, P]], channel_multiplier=1).then_inc(pool_done, 1)
                nc.gpsimd.affine_select(out=k.before[:, :], in_=k.ones[:, :], compare_op=ALU.is_gt, fill=0.0,
                                        base=0, pattern=[[1, P]], channel_multiplier=-1).then_inc(pool_done, 1)
                pool.wait_ge(stepped, 1)
                for g in range(SG):
                    idx = bass.IndirectOffsetOnAxis(ap=k.tile_idx[:, g:g + 1], axis=0)
                    for to, rows in ((got_src, src_rows), (got_dst, dst_rows), (got_w, w_rows)):
                        nc.gpsimd.indirect_dma_start(out=to[:, g, :], out_offset=None, in_=rows,
                                                     in_offset=idx).then_inc(gathered, 16)
                pool.wait_ge(gathered, 16 * 3 * SG)

            @block.tensor
            def _(pe):
                pe.wait_ge(pool_done, 7)
                pe.wait_ge(loaded, 32)
                pe.wait_ge(v, 4)
                for g in range(EG):
                    nc.tensor.transpose(psA[:, g // 4, g % 4 * P:(g % 4 + 1) * P], dst_rf[:, g, :], k.ident[:, :])
                    last = nc.tensor.transpose(psB[:, g // 4, g % 4 * P:(g % 4 + 1) * P], w_r[:, g, :], k.ident[:, :])
                last.then_inc(turned, 1)
                pe.wait_ge(v, 8)
                nc.tensor.matmul(psC[:, 0:2 * NB], k.ident[:, :], counts[:, :], start=True, stop=False)
                with nc.tensor.Fori(0, ET // T // 2) as i:
                    for h in range(2):
                        pe.wait_ge(hot, 2 * i + h + 1)
                        for t in range(T):
                            last = nc.tensor.matmul(psC[:, 0:2 * NB], lane_hot[:, h, t, :],
                                                    blk_hot[:, h, t, :, :].rearrange("p a b -> p (a b)"),
                                                    start=False, stop=False)
                        last.then_inc(counted, 1)
                nc.tensor.matmul(psC[:, 0:2 * NB], k.ident[:, :], counts[:, :], start=False, stop=True).then_inc(counted, 1)
                pe.wait_ge(v, 9)
                nc.tensor.matmul(psA[:, 0, 0:NB], k.before[:, :], counts[:, 0:NB], start=True, stop=True)
                nc.tensor.matmul(psA[:, 1, 0:NB], k.ones[:, :], counts[:, 0:NB], start=True, stop=True).then_inc(totalled, 1)
                for g in range(EG):
                    pe.wait_ge(compared, g + 1)
                    for h in range(2):
                        last = nc.tensor.matmul(psD[:, h, 0:SPAD // 2], k.ones[:, :],
                                                cmp[:, g % 2, h * (SPAD // 2):(h + 1) * (SPAD // 2)],
                                                start=(g == 0), stop=(g == EG - 1))
                    last.then_inc(totalled, 1)
                pe.wait_ge(turned2, 1)
                for g in range(SG):
                    nc.tensor.transpose(psA[:, g // 4, g % 4 * P:(g % 4 + 1) * P], got_srcf[:, g, :], k.ident[:, :])
                    nc.tensor.transpose(psB[:, g // 4, g % 4 * P:(g % 4 + 1) * P], got_dstf[:, g, :], k.ident[:, :])
                    last = nc.tensor.transpose(psD[:, g // 4, g % 4 * P:(g % 4 + 1) * P], got_w[:, g, :], k.ident[:, :])
                last.then_inc(turned2, 1)

            @block.vector
            def _(dve):
                dve.wait_ge(pool_done, 3)
                dve.wait_ge(loaded, 32)
                nc.vector.tensor_copy(k.iota[:, :], iota_i[:, :]).then_inc(v, 1)
                nc.vector.tensor_copy(iota_sf[:, :], iota_si[:, :]).then_inc(v, 1)
                nc.vector.tensor_copy(tile_f[:, :], tile_i[:, :]).then_inc(v, 1)
                nc.vector.tensor_copy(dst_rf[:, :, :], dst_r[:, :, :]).then_inc(v, 1)
                nc.vector.tensor_single_scalar(last_i[:, :], dst_r[:, :, P - 1], 7, op=ALU.arith_shift_right).then_inc(v, 1)
                nc.vector.memset(counts[:, :], 0.0).then_inc(v, 1)
                dve.wait_ge(v, 5)
                nc.vector.tensor_copy(last_f[:, :], last_i[:, :]).then_inc(v, 1)
                dve.wait_ge(v, 7)
                nc.vector.tensor_tensor(key[:, :], last_f[:, :], tile_f[:, :], ALU.add).then_inc(v, 1)
                dve.wait_ge(turned, 1)
                for h in range(2):
                    w = 512 if h == 0 else EG * P - 512
                    nc.vector.tensor_copy(dst_t[:, h * 512:h * 512 + w], psA[:, h, 0:w]).then_inc(hot_prep, 1)
                    nc.vector.tensor_copy(w_t[:, h * 512:h * 512 + w], psB[:, h, 0:w]).then_inc(hot_prep, 1)
                dve.wait_ge(hot_prep, 4)
                nc.vector.tensor_single_scalar(blk_ti[:, :], dst_t[:, :], 7, op=ALU.arith_shift_right).then_inc(hot_prep, 1)
                nc.vector.tensor_single_scalar(lane_ti[:, :], dst_t[:, :], P - 1, op=ALU.bitwise_and).then_inc(hot_prep, 1)
                dve.wait_ge(hot_prep, 6)
                nc.vector.tensor_copy(blk_t[:, :], blk_ti[:, :]).then_inc(hot_prep, 1)
                nc.vector.tensor_copy(lane_t[:, :], lane_ti[:, :]).then_inc(hot_prep, 1)
                dve.wait_ge(hot_prep, 8)

                def make_hot(t0, h):
                    nc.vector.tensor_tensor(lane_hot[:, h, :, :], k.iota[:, :].unsqueeze(1).to_broadcast([P, T, P]),
                                            lane_t[:, bass.ds(t0, T)].unsqueeze(2).to_broadcast([P, T, P]), ALU.is_equal).then_inc(hot_a, 1)
                    nc.vector.tensor_tensor(blk_hot[:, h, :, 0, :], k.iota[:, 0:NB].unsqueeze(1).to_broadcast([P, T, NB]),
                                            blk_t[:, bass.ds(t0, T)].unsqueeze(2).to_broadcast([P, T, NB]), ALU.is_equal).then_inc(hot_a, 1)

                def weigh_hot(t0, h):
                    nc.vector.tensor_tensor(blk_hot[:, h, :, 1, :], blk_hot[:, h, :, 0, :],
                                            w_t[:, bass.ds(t0, T)].unsqueeze(2).to_broadcast([P, T, NB]), ALU.mult).then_inc(hot, 1)

                make_hot(0, 0)
                make_hot(T, 1)
                dve.wait_ge(hot_a, 2)
                weigh_hot(0, 0)
                dve.wait_ge(hot_a, 4)
                weigh_hot(T, 1)
                with nc.vector.Fori(1, ET // T // 2) as i:
                    for h in range(2):
                        dve.wait_ge(counted, 2 * i + h - 1)
                        make_hot((2 * i + h) * T, h)
                        dve.wait_ge(hot_a, 4 * i + 2 * h + 2)
                        weigh_hot((2 * i + h) * T, h)
                dve.wait_ge(counted, ET // T + 1)
                nc.vector.tensor_copy(counts[:, :], psC[:, 0:2 * NB]).then_inc(v, 1)
                dve.wait_ge(v, 9)
                nc.vector.tensor_scalar(deg[:, :], counts[:, NB:2 * NB], 1.0, None, ALU.add).then_inc(v, 1)
                nc.vector.memset(zero[:, :], 0.0).then_inc(v, 1)
                dve.wait_ge(v, 11)
                nc.vector.tensor_scalar(pos[:, :], deg[:, :], 0.0, None, ALU.is_gt).then_inc(v, 1)
                nc.vector.tensor_scalar(deg[:, :], deg[:, :], 1e-30, None, ALU.max).then_inc(v, 1)
                dve.wait_ge(v, 13)
                nc.vector.reciprocal(rdeg[:, :], deg[:, :]).then_inc(v, 1)
                dve.wait_ge(totalled, 1)
                nc.vector.tensor_copy(totals[:, :], psA[:, 1, 0:NB]).then_inc(v, 1)
                dve.wait_ge(v, 15)
                nc.vector.tensor_tensor_scan(base[:, :], totals[:, :], zero[:, :], 0.0, ALU.add, ALU.add).then_inc(v, 1)
                dve.wait_ge(v, 16)
                nc.vector.tensor_tensor(base[:, :], base[:, :], totals[:, :], ALU.subtract).then_inc(v, 1)
                dve.wait_ge(v, 17)
                nc.vector.tensor_tensor(start_f[:, :], base[:, :], psA[:, 0, 0:NB], ALU.add).then_inc(v, 1)
                dve.wait_ge(v, 18)
                nc.vector.tensor_copy(k.row_start[:, :], start_f[:, :]).then_inc(v, 1)
                nc.vector.tensor_copy(k.row_count[:, :], counts[:, 0:NB]).then_inc(v, 1)
                for g in range(EG):
                    if g >= 2:
                        dve.wait_ge(totalled, g)
                    nc.vector.tensor_scalar(cmp[:, g % 2, :], iota_sf[:, :], key[:, g:g + 1], None, ALU.is_gt).then_inc(compared, 1)
                dve.wait_ge(totalled, EG + 1)
                for h in range(2):
                    nc.vector.tensor_copy(step_tile[:, h * (SPAD // 2):(h + 1) * (SPAD // 2)], psD[:, h, 0:SPAD // 2]).then_inc(v, 1)
                dve.wait_ge(v, 22)
                nc.vector.tensor_tensor(step_blk[:, :], iota_sf[:, :], step_tile[:, :], ALU.subtract).then_inc(v, 1)
                nc.vector.tensor_tensor(diag[:, :, :], step_tile[:, :].rearrange("p (g l) -> p g l", l=P),
                                        k.ident[:, :].unsqueeze(1).to_broadcast([P, SG, P]), ALU.mult).then_inc(v, 1)
                dve.wait_ge(v, 24)
                nc.vector.tensor_reduce(tile_col[:, :], diag[:, :, :], AX.X, ALU.add).then_inc(v, 1)
                nc.vector.tensor_copy(k.step_blk[:, :], step_blk[:, :]).then_inc(v, 1)
                dve.wait_ge(v, 25)
                nc.vector.tensor_copy(k.tile_idx[:, :], tile_col[:, :]).then_inc(stepped, 1)
                dve.wait_ge(gathered, 16 * 3 * SG)
                nc.vector.tensor_copy(got_srcf[:, :, :], got_src[:, :, :]).then_inc(v, 1)
                nc.vector.tensor_copy(got_dstf[:, :, :], got_dst[:, :, :]).then_inc(turned2, 1)
                dve.wait_ge(turned2, 2)
                for h in range(2):
                    w = 512 if h == 0 else SPAD - 512
                    c = slice(h * 512, h * 512 + w)
                    nc.vector.tensor_copy(k.src_idx[:, c], psA[:, h, 0:w]).then_inc(v, 1)
                    nc.vector.scalar_tensor_tensor(out=k.lane[:, c], in0=step_blk[:, c], scalar=-float(P), in1=psB[:, h, 0:w],
                                                   op0=ALU.mult, op1=ALU.add).then_inc(v, 1)
                    nc.vector.tensor_copy(k.weight[:, c], psD[:, h, 0:w]).then_inc(v, 1)

            @block.scalar
            def _(act):
                act.wait_ge(v, 14)
                nc.scalar.activation(rdeg[:, :], rdeg[:, :], ACT.Sqrt).then_inc(turned, 1)

        with nc.Block() as block:
            @block.vector
            def _(dve):
                nc.vector.tensor_tensor(k.dinv[:, :], rdeg[:, :], pos[:, :], ALU.mult).then_inc(v, 1)


HALF = 8
PASSES = -(-STEPS // (2 * HALF))
BANKS = 4
assert PASSES * 2 * HALF <= SPAD


def stage_aggregate(nc, k, name, table, acc, width, weights, heads=0, side=None):
    with ExitStack() as ctx:
        sb, ps, sem = allocators(nc, ctx, name)
        rows = sb("rows", [P, 2, HALF, width])
        scaled = sb("scaled", [P, 2, HALF, width]) if heads else rows
        hot = sb("hot", [P, 2, HALF, P])
        idx = sb("idx", [P, 2, HALF], i32)
        part = [ps(f"part{j}", [P, 512]) for j in range(BANKS)]
        gathered = [sem(f"gathered{j}") for j in range(2 * HALF)]
        idx_ready = sem("idx_ready")
        hot_ready = sem("hot_ready")
        scaled_ready = sem("scaled_ready")
        multiplied = sem("multiplied")
        added = sem("added")
        slot_free = sem("slot_free")
        row_seen = sem("row_seen")
        ones_ready = sem("ones_ready")
        state = side.open(nc, k, ctx) if side else None
        SIDE = NB if side else 0

        with nc.Block() as block:
            @block.sync
            def _(sp):
                if side:
                    side.sync(sp, state)

            @block.gpsimd
            def _(pool):
                if width > D and not heads:
                    nc.gpsimd.memset(rows[:, :, :, D:width], 1.0).then_inc(ones_ready, 1)

                def gather(i, first):
                    for h in range(2):
                        pool.wait_ge(idx_ready, 2 * i + h + 1)
                        pool.sem_inc(slot_free, 1)
                        for j in range(HALF):
                            if not first:
                                pool.wait_ge(multiplied, 2 * HALF * (i - 1) + HALF * h + j + 1)
                                pool.sem_inc(slot_free, 1)
                            nc.gpsimd.indirect_dma_start(
                                out=rows[:, h, j, 0:D], out_offset=None, in_=table,
                                in_offset=bass.IndirectOffsetOnAxis(ap=idx[:, h, j:j + 1], axis=0),
                            ).then_inc(gathered[h * HALF + j], 16)

                gather(0, True)
                with nc.gpsimd.Fori(1, PASSES) as i:
                    gather(i, False)

            @block.scalar
            def _(act):
                if side:
                    side.act_start(act, state)

                def scale_rows(i):
                    for h in range(2):
                        for j in range(HALF):
                            act.wait_ge(gathered[h * HALF + j], 16 * (i + 1))
                            act.sem_inc(row_seen, 1)
                            for q in range(heads):
                                c = slice(q * (D // heads), (q + 1) * (D // heads))
                                nc.scalar.activation(
                                    scaled[:, h, j, c], rows[:, h, j, c], ACT.Copy,
                                    scale=weights[:, bass.ds((2 * HALF * i + HALF * h + j) * heads + q, 1)],
                                ).then_inc(scaled_ready, 1)

                with nc.scalar.Fori(0, PASSES) if not SIDE else nc.scalar.Fori(0, SIDE) as i:
                    if heads:
                        scale_rows(i)
                    if side:
                        side.act(act, state, i)
                if side:
                    if heads:
                        with nc.scalar.Fori(SIDE, PASSES) as i:
                            scale_rows(i)
                    side.act_end(act, state)

            @block.tensor
            def _(pe):
                if side:
                    side.pe_start(pe, state)
                if width > D and not heads:
                    pe.wait_ge(ones_ready, 1)

                def products(i, first, with_side):
                    for h in range(2):
                        pe.wait_ge(hot_ready, 2 * i + h + 1)
                        for j in range(HALF):
                            s = 2 * HALF * i + HALF * h + j
                            if heads:
                                pe.wait_ge(scaled_ready, heads * s + heads)
                            else:
                                pe.wait_ge(gathered[h * HALF + j], 16 * (i + 1))
                            if not first or h * HALF + j >= BANKS:
                                pe.wait_ge(added, s - BANKS + 1)
                            nc.tensor.matmul(part[j % BANKS][:, 0:width], hot[:, h, j, :], scaled[:, h, j, :],
                                             start=True, stop=True).then_inc(multiplied, 1)
                        if with_side:
                            side.pe(pe, state, i, h)

                products(0, True, side)
                with nc.tensor.Fori(1, SIDE or PASSES) as i:
                    products(i, False, side)
                if side:
                    with nc.tensor.Fori(SIDE, PASSES) as i:
                        products(i, False, False)
                    side.pe_end(pe, state)

            @block.vector
            def _(dve):
                if side:
                    side.dve_start(dve, state)

                def make_hot(n, h):
                    s = HALF * n
                    nc.vector.tensor_copy(idx[:, h, :], k.src_idx[:, bass.ds(s, HALF)]).then_inc(idx_ready, 1)
                    if heads:
                        nc.vector.tensor_copy(
                            scaled[:, h, :, D:D + heads],
                            weights[:, bass.ds(s * heads, HALF * heads)].rearrange("p (j q) -> p j q", q=heads))
                    for j in range(HALF):
                        last = nc.vector.tensor_scalar(
                            hot[:, h, j, :], k.iota[:, :], k.lane[:, bass.ds(s + j, 1)],
                            None if heads else weights[:, bass.ds(s + j, 1)],
                            ALU.is_equal, *(() if heads else (ALU.mult,)))
                    last.then_inc(hot_ready, 1)

                def add_parts(n, h):
                    s = HALF * n
                    _, blocks = nc.values_load_multi_w_load_instructions(
                        k.step_blk[0:1, bass.ds(s, HALF)], engines=(mybir.EngineType.DVE,), min_val=0, max_val=NB - 1,
                        skip_runtime_bounds_check_because="a step's block lies in the blocks of its edge tile")
                    for j in range(HALF):
                        dve.wait_ge(multiplied, s + j + 1)
                        dve.wait_ge(added, s + j)
                        a = acc[:, bass.ds(blocks[j], 1), 0:width]
                        nc.vector.tensor_tensor(a, a, part[j % BANKS][:, 0:width].unsqueeze(1), ALU.add).then_inc(added, 1)

                make_hot(0, 0)
                make_hot(1, 1)

                def one_pass(i, with_side):
                    for h in range(2):
                        add_parts(2 * i + h, h)
                        if with_side and h:
                            side.vary(dve, state, i)
                        make_hot(2 * i + h + 2, h)
                        if with_side and h:
                            side.scale(dve, state, i)

                one_pass(0, side)
                if side:
                    with nc.vector.Fori(1, SIDE) as i:
                        one_pass(i, True)
                with nc.vector.Fori(SIDE or 1, PASSES - 1) as i:
                    one_pass(i, False)
                for h in range(2):
                    add_parts(2 * (PASSES - 1) + h, h)
                if side:
                    side.dve_end(dve, state)


def sharpen_inverse_root(nc, dve, v, at, s, y, t):
    nc.vector.tensor_tensor(t, y, y, ALU.mult).then_inc(v, 1)
    dve.wait_ge(v, at + 1)
    nc.vector.tensor_tensor(t, t, s, ALU.mult).then_inc(v, 1)
    dve.wait_ge(v, at + 2)
    nc.vector.tensor_scalar(t, t, -0.5, 1.5, ALU.mult, ALU.add).then_inc(v, 1)
    dve.wait_ge(v, at + 3)
    nc.vector.tensor_tensor(y, y, t, ALU.mult).then_inc(v, 1)
    dve.wait_ge(v, at + 4)


def stage_layernorm(nc, k, name, x, xn, x_dram=None):
    with ExitStack() as ctx:
        sb, ps, sem = allocators(nc, ctx, name)
        stats = sb("stats", [P, NB, 6])
        mean = sb("mean", [P, NB])
        apart = sb("apart", [P, NB])
        var = sb("var", [P, NB])
        dev = sb("dev", [P, NB])
        rstd = sb("rstd", [P, NB])
        loaded = [sem(f"loaded{g}") for g in range(NG)]
        summed = sem("summed")
        v = sem("v")
        root = sem("root")
        with nc.Block() as block:
            @block.sync
            def _(sp):
                if x_dram is not None:
                    for g in range(NG):
                        b = slice(g * CG, (g + 1) * CG)
                        sp.dma_start(x[:, b, 0:D], x_dram.rearrange("(b l) d -> l b d", l=P)[:, b, :]).then_inc(loaded[g], 16)

            @block.vector
            def _(dve):
                if x_dram is not None:
                    for g in range(NG):
                        dve.wait_ge(loaded[g], 16)
                with nc.vector.Fori(0, NG) as g:
                    for j in range(CG):
                        nc.vector.bn_stats(stats[:, bass.ds(g * CG + j, 1), :], x[:, bass.ds(g * CG + j, 1), 0:D]).then_inc(summed, 1)
                dve.wait_ge(summed, NB)
                even, odd = stats[:, :, 1], stats[:, :, 4]
                nc.vector.tensor_tensor(mean[:, :], even, odd, ALU.add).then_inc(v, 1)
                nc.vector.tensor_tensor(apart[:, :], even, odd, ALU.subtract).then_inc(v, 1)
                nc.vector.tensor_tensor(var[:, :], stats[:, :, 2], stats[:, :, 5], ALU.add).then_inc(v, 1)
                dve.wait_ge(v, 3)
                nc.vector.tensor_scalar(mean[:, :], mean[:, :], 0.5, None, ALU.mult).then_inc(v, 1)
                nc.vector.tensor_tensor(apart[:, :], apart[:, :], apart[:, :], ALU.mult).then_inc(v, 1)
                nc.vector.tensor_scalar(var[:, :], var[:, :], 1.0 / D, 1e-5, ALU.mult, ALU.add).then_inc(v, 1)
                dve.wait_ge(v, 6)
                nc.vector.scalar_tensor_tensor(out=var[:, :], in0=apart[:, :], scalar=0.25, in1=var[:, :],
                                               op0=ALU.mult, op1=ALU.add).then_inc(v, 1)
                dve.wait_ge(root, 1)
                nc.vector.reciprocal(rstd[:, :], dev[:, :]).then_inc(v, 1)
                dve.wait_ge(v, 8)
                sharpen_inverse_root(nc, dve, v, 8, var[:, :], rstd[:, :], apart[:, :])
                with nc.vector.Fori(0, NG) as g:
                    for j in range(CG):
                        n = g * CG + j
                        nc.vector.tensor_scalar(xn[:, bass.ds(n, 1), :], x[:, bass.ds(n, 1), 0:D],
                                                mean[:, bass.ds(n, 1)], rstd[:, bass.ds(n, 1)],
                                                ALU.subtract, ALU.mult)

            @block.scalar
            def _(act):
                act.wait_ge(v, 7)
                nc.scalar.activation(dev[:, :], var[:, :], ACT.Sqrt).then_inc(root, 1)


def stage_scale_store(nc, k, name, x, scale, acc, table):
    with ExitStack() as ctx:
        sb, ps, sem = allocators(nc, ctx, name)
        v = sem("v")
        stored = sem("stored")
        t = table.rearrange("(b l) d -> l b d", l=P)
        with nc.Block() as block:
            @block.vector
            def _(dve):
                with nc.vector.Fori(0, NG) as g:
                    for j in range(CG):
                        n = g * CG + j
                        nc.vector.tensor_scalar(acc[:, bass.ds(n, 1), 0:D], x[:, bass.ds(n, 1), 0:D],
                                                scale[:, bass.ds(n, 1)], None, ALU.mult).then_inc(v, 1)

            @block.sync
            def _(sp):
                for g in range(NG):
                    b = slice(g * CG, (g + 1) * CG)
                    sp.wait_ge(v, (g + 1) * CG)
                    sp.dma_start(t[:, b, :], acc[:, b, 0:D]).then_inc(stored, 16)
                sp.wait_ge(stored, 16 * NG)


HEADS0, DH0 = 8, 64
INNER0 = HEADS0 * DH0


class Mix0Side:

    def __init__(self, xn, wkv_t):
        self.xn, self.wkv_t = xn, wkv_t

    def open(self, nc, k, ctx):
        self.nc, self.k = nc, k
        sb, ps, sem = allocators(nc, ctx, "mix0")
        self.w = sb("w", [P, 2, 2 * INNER0])
        self.mean = sb("mean", [P, 2, 2 * HEADS0])
        self.xt = sb("xt", [P, D])
        self.staged = sb("staged", [P, D])
        self.stage_ready = sem("stage_ready")
        self.sq = sb("sq", [P, 2 * HEADS0, DH0])
        self.kc = sb("kc", [P, INNER0])
        self.vs = sb("vs", [P, INNER0])
        self.var = sb("var", [P, 2 * HEADS0])
        self.dev = sb("dev", [P, HEADS0])
        self.pt = ps("pt", [P, 512])
        self.kv = ps("kv", [P, 2, 512])
        self.dots = ps("dots", [P, 512])
        self.loaded, self.centred, self.zeroed, self.turned = sem("loaded"), sem("centred"), sem("zeroed"), sem("turned")
        self.copied, self.projected, self.squared, self.varied = sem("copied"), sem("projected"), sem("squared"), sem("varied")
        self.rooted, self.weighed, self.scaled, self.dotted = sem("rooted"), sem("weighed"), sem("scaled"), sem("dotted")
        self.closed, self.cleared = sem("closed"), sem("cleared")
        return self

    def sync(self, sp, s):
        sp.dma_start(s.w[:, :, :], s.wkv_t.rearrange("(c p) f -> p c f", p=P)).then_inc(s.loaded, 16)
        sp.sem_inc(s.turned, 1)
        with self.nc.sync.Fori(0, NB) as i:
            sp.wait_ge(s.turned, i + 1)
            sp.dma_start(s.staged[:, :], s.xn[:, bass.ds(i, 1), :].rearrange("p a d -> p (a d)")).then_inc(s.stage_ready, 16)

    def dve_start(self, dve, s):
        v = self.nc.vector
        v.memset(s.xt[:, :], 0.0).then_inc(s.zeroed, 1)
        v.memset(s.kc[:, :], 0.0).then_inc(s.zeroed, 1)
        v.memset(s.vs[:, :], 0.0).then_inc(s.zeroed, 1)
        dve.wait_ge(s.loaded, 16)
        w = s.w[:, :, :].rearrange("p c (h d) -> p (c h) d", d=DH0)
        mean = s.mean[:, :, :].rearrange("p c h -> p (c h)")
        v.tensor_reduce(mean, w, AX.X, ALU.add).then_inc(s.centred, 1)
        dve.wait_ge(s.centred, 1)
        v.tensor_scalar(mean, mean, -1.0 / DH0, None, ALU.mult).then_inc(s.centred, 1)
        dve.wait_ge(s.centred, 2)
        v.tensor_tensor(w, w, mean.unsqueeze(2).to_broadcast([P, 4 * HEADS0, DH0]), ALU.add).then_inc(s.centred, 1)

    def pe_start(self, pe, s):
        t = self.nc.tensor
        pe.wait_ge(s.zeroed, 3)
        pe.wait_ge(s.centred, 3)
        t.matmul(s.dots[:, :], self.k.ident[:, :], s.kc[:, :], start=True, stop=False)

    def products(self, pe, s):
        for g in range(HEADS0 // 2):
            c = slice(g * P, (g + 1) * P)
            last = self.nc.tensor.matmul(s.dots[:, c], s.vs[:, c], s.kc[:, c], start=False, stop=False)
        last.then_inc(s.dotted, 1)

    def project(self, pe, s):
        for h in range(2):
            for c in range(2):
                last = self.nc.tensor.matmul(s.kv[:, h, :], s.xt[:, c * P:(c + 1) * P], s.w[:, c, h * 512:(h + 1) * 512],
                                             start=(c == 0), stop=(c == 1))
        last.then_inc(s.projected, 1)

    def pe(self, pe, s, i, h):
        first = isinstance(i, int)
        if h == 0:
            if not first:
                pe.wait_ge(s.scaled, i)
                pe.wait_ge(s.squared, 2 * i)
                pe.wait_ge(s.copied, i)
            self.products(pe, s)
            self.project(pe, s)
            return
        pe.wait_ge(s.stage_ready, 16 * i + 16)
        for c in range(2):
            last = self.nc.tensor.transpose(s.pt[:, c * P:(c + 1) * P], s.staged[:, c * P:(c + 1) * P], self.k.ident[:, :])
        last.then_inc(s.turned, 1)

    def pe_end(self, pe, s):
        for n in range(2):
            pe.wait_ge(s.scaled, NB + n)
            pe.wait_ge(s.squared, 2 * (NB + n))
            pe.wait_ge(s.copied, NB)
            self.products(pe, s)
            if n == 0:
                self.project(pe, s)
        pe.wait_ge(s.cleared, 1)
        self.nc.tensor.matmul(s.dots[:, :], self.k.ident[:, :], s.kc[:, :], start=False, stop=True).then_inc(s.closed, 1)

    def act_start(self, act, s):
        act.wait_ge(s.zeroed, 3)

    def evacuate(self, act, s, i):
        a = self.nc.scalar
        act.wait_ge(s.projected, i + 1)
        a.activation(s.sq[:, :, :].rearrange("p h d -> p (h d)"), s.kv[:, :, :].rearrange("p a n -> p (a n)"),
                     ACT.Square).then_inc(s.squared, 1)
        a.activation(s.kc[:, :], s.kv[:, 0, :], ACT.Copy).then_inc(s.squared, 1)
        act.wait_ge(s.varied, 3 * i + 3)
        a.activation(s.dev[:, :], s.dev[:, :], ACT.Sqrt).then_inc(s.rooted, 1)

    def act(self, act, s, i):
        self.evacuate(act, s, i)
        act.wait_ge(s.turned, i + 2)
        self.nc.scalar.activation(s.xt[:, :], s.pt[:, 0:D], ACT.Copy).then_inc(s.copied, 1)

    def act_end(self, act, s):
        self.evacuate(act, s, NB)

    def vary(self, dve, s, i):
        v = self.nc.vector
        dve.wait_ge(s.squared, 2 * i + 1)
        v.tensor_reduce(s.var[:, :], s.sq[:, :, :], AX.X, ALU.add).then_inc(s.varied, 1)
        dve.wait_ge(s.varied, 3 * i + 1)
        v.tensor_scalar(s.var[:, :], s.var[:, :], 1.0 / DH0, 1e-5, ALU.mult, ALU.add).then_inc(s.varied, 1)
        dve.wait_ge(s.varied, 3 * i + 2)
        v.tensor_tensor(s.dev[:, :], s.var[:, 0:HEADS0], s.var[:, HEADS0:], ALU.mult).then_inc(s.varied, 1)

    def scale(self, dve, s, i):
        v = self.nc.vector
        dve.wait_ge(s.rooted, i + 1)
        v.reciprocal(s.dev[:, :], s.dev[:, :]).then_inc(s.weighed, 1)
        dve.wait_ge(s.weighed, i + 1)
        v.tensor_tensor(s.vs[:, :].rearrange("p (h d) -> p h d", d=DH0), s.kv[:, 1, :].rearrange("p (h d) -> p h d", d=DH0),
                        s.dev[:, :].unsqueeze(2).to_broadcast([P, HEADS0, DH0]), ALU.mult).then_inc(s.scaled, 1)

    def dve_end(self, dve, s):
        self.vary(dve, s, NB)
        self.scale(dve, s, NB)
        v = self.nc.vector
        dve.wait_ge(s.dotted, NB + 2)
        v.memset(s.kc[:, :], 0.0).then_inc(s.cleared, 1)
        dve.wait_ge(s.closed, 1)
        for g in range(HEADS0 // 2):
            for a in range(2):
                r, c = slice(a * DH0, (a + 1) * DH0), g * P + a * DH0
                v.tensor_scalar(self.k.dots[r, g, a * DH0:(a + 1) * DH0], s.dots[r, c:c + DH0], 1.0 / NODES, None, ALU.mult)


def stage_mix0_fold(nc, k, wq, wout_t):
    with ExitStack() as ctx:
        sb, ps, sem = allocators(nc, ctx, "fold0")
        wq_sb = sb("wq", [P, 4, D])
        wo_sb = sb("wo", [P, 4, D])
        a1 = sb("a1", [P, 4, D])
        pa = ps("pa", [P, 4, D])
        pm = ps("pm", [P, 2, D])
        loaded, made, copied, folded = sem("loaded"), sem("made"), sem("copied"), sem("folded")
        with nc.Block() as block:
            @block.sync
            def _(sp):
                sp.dma_start(wq_sb[:, :, :], wq.rearrange("(g p) c -> p g c", p=P)).then_inc(loaded, 16)
                sp.dma_start(wo_sb[:, :, :], wout_t.rearrange("(g p) c -> p g c", p=P)).then_inc(loaded, 16)

            @block.tensor
            def _(pe):
                pe.wait_ge(loaded, 32)
                for g in range(4):
                    nc.tensor.matmul(pa[:, g, :], k.dots[:, g, :], wo_sb[:, g, :], start=True, stop=True).then_inc(made, 1)
                pe.wait_ge(copied, 1)
                for c in range(2):
                    for g in range(4):
                        last = nc.tensor.matmul(pm[:, c, :], wq_sb[:, g, c * P:(c + 1) * P], a1[:, g, :],
                                                start=(g == 0), stop=(g == 3))
                last.then_inc(folded, 1)

            @block.vector
            def _(dve):
                dve.wait_ge(made, 4)
                nc.vector.tensor_copy(a1[:, :, :], pa[:, :, :]).then_inc(copied, 1)
                dve.wait_ge(folded, 1)
                nc.vector.tensor_copy(k.mix[:, :, :], pm[:, :, :])


RING = 4


def led(engine, lead, ahead, one):
    for n in range(lead):
        ahead(n, n % RING)
    full = (NB - lead) // RING
    with engine.Fori(0, full) as i:
        for h in range(RING):
            if lead:
                ahead(RING * i + h + lead, (h + lead) % RING)
            one(RING * i + h, h)
    for n in range(full * RING, NB):
        if lead and n + lead < NB:
            ahead(n + lead, (n + lead) % RING)
        one(n, n % RING)


def project_rows(nc, k, name, chunks, rhs, width, finish, load=None, loads=0, scale=None, columns=None, store=None):
    columns = columns or chunks * P
    with ExitStack() as ctx:
        sb, ps, sem = allocators(nc, ctx, name)
        staged = sb("staged", [P, RING, columns])
        extra = sb("extra", [P, RING, D]) if loads > 1 or (loads and scale) else None
        xt = sb("xt", [P, RING, chunks * P])
        pt = ps("pt", [P, RING, 512])
        po = ps("po", [P, RING, 512])
        loaded = [sem(f"loaded{h}") for h in range(RING)]
        scaled = sem("scaled")
        step = sem("step")
        turned, copied, multiplied, done = sem("turned"), sem("copied"), sem("multiplied"), sem("done")
        uses = lambda n, h: (n - h) // RING + 1

        with nc.Block() as block:
            @block.sync
            def _(sp):
                if load:
                    def bring(n, h):
                        sp.wait_ge(turned, n + 1)
                        if extra is not None:
                            sp.wait_ge(done, n + 1)
                        for dma in load(sp, n, staged[:, h, :], extra[:, h:h + 1, :] if extra is not None else None):
                            dma.then_inc(loaded[h], 16)
                    led(nc.sync, 0, None, bring)
                if store:
                    store(sp, done)

            @block.tensor
            def _(pe):
                pe.sem_inc(turned, RING)
                pe.sem_inc(multiplied, RING)

                def turn(n, h):
                    pe.wait_ge(copied, n + 1)
                    if load:
                        pe.wait_ge(loaded[h], 16 * loads * uses(n, h))
                    if scale:
                        pe.wait_ge(scaled, n + 1)
                    for c in range(chunks):
                        last = nc.tensor.transpose(pt[:, h, c * P:(c + 1) * P], staged[:, h, c * P:(c + 1) * P], k.ident[:, :])
                    last.then_inc(turned, 1)

                def multiply(n, h):
                    pe.wait_ge(copied, n + RING + 1)
                    pe.wait_ge(done, n + 1)
                    for c in range(chunks):
                        last = nc.tensor.matmul(po[:, h, 0:width], xt[:, h, c * P:(c + 1) * P], rhs(c),
                                                start=(c == 0), stop=(c == chunks - 1))
                    last.then_inc(multiplied, 1)
                led(nc.tensor, 2, turn, multiply)

            @block.scalar
            def _(act):
                act.sem_inc(copied, RING)

                def copy(n, h):
                    act.wait_ge(turned, n + RING + 1)
                    act.wait_ge(multiplied, n + 1)
                    nc.scalar.activation(xt[:, h, :], pt[:, h, 0:chunks * P], ACT.Copy).then_inc(copied, 1)
                led(nc.scalar, 0, None, copy)

            @block.vector
            def _(dve):
                dve.sem_inc(done, RING)

                def make(n, h):
                    dve.wait_ge(turned, n + 1)
                    scale(n, staged[:, h, :]).then_inc(scaled, 1)

                def end(n, h):
                    dve.wait_ge(multiplied, n + RING + 1)
                    if extra is not None:
                        dve.wait_ge(loaded[h], 16 * loads * uses(n, h))
                    finish(dve, n, po[:, h:h + 1, 0:width], extra[:, h:h + 1, :] if extra is not None else None, step).then_inc(done, 1)
                if scale:
                    led(nc.vector, 3, make, end)
                else:
                    led(nc.vector, 0, None, end)


def in_blocks(ap):
    return ap.rearrange("(b l) d -> l b d", l=P)


def on_all(ap):
    return ap.rearrange("(a n) -> a n", a=1).to_broadcast([P, ap.shape[0]])


def block_rows(t, n):
    return t[:, bass.ds(n, 1), 0:D].rearrange("p a d -> p (a d)")


def load_weights(nc, ctx, name, loads):
    sem = allocators(nc, ctx, name)[2]
    loaded = sem("loaded")
    with nc.Block() as block:
        @block.sync
        def _(sp):
            for to, source in loads:
                sp.dma_start(to, source).then_inc(loaded, 16)
            sp.wait_ge(loaded, 16 * len(loads))


def stage_gcn_dense(nc, k, name, acc, w, bias, table=None, xn=None, x_in=None, bias2=None):
    with ExitStack() as ctx:
        sb, _, sem = allocators(nc, ctx, name + "_out")
        w_sb = sb("w", [P, 2, D])
        b_sb = sb("b", [P, 2, D])
        stored = sem("stored")
        load_weights(nc, ctx, name + "w", [(w_sb[:, :, :], w.rearrange("(c p) n -> p c n", p=P)), (b_sb[:, 0, :], on_all(bias))] +
                     ([] if table is not None else [(b_sb[:, 1, :], on_all(bias2))]))

        def scale(n, staged):
            return nc.vector.tensor_scalar(staged[:, 0:D].unsqueeze(1), acc[:, bass.ds(n, 1), 0:D], k.dinv[:, bass.ds(n, 1)], None, ALU.mult)

        if table is not None:
            def finish(dve, n, out, extra, step):
                a = acc[:, bass.ds(n, 1), 0:D]
                nc.vector.tensor_tensor(a, out, b_sb[:, 0:1, :], ALU.add).then_inc(step, 1)
                dve.wait_ge(step, n + 1)
                return nc.vector.tensor_scalar(a, a, 0.0, k.dinv[:, bass.ds(n, 1)], ALU.max, ALU.mult)

            def store(sp, done):
                for g in range(NG):
                    b = slice(g * CG, (g + 1) * CG)
                    sp.wait_ge(done, (g + 1) * CG + RING)
                    sp.dma_start(in_blocks(table)[:, b, :], acc[:, b, 0:D]).then_inc(stored, 16)
                sp.wait_ge(stored, 16 * NG)
            project_rows(nc, k, name, 2, lambda c: w_sb[:, c, :], D, finish, scale=scale, store=store)
            return

        def load(sp, n, staged, extra):
            return [sp.dma_start(staged[:, D:2 * D], block_rows(xn, n)),
                    sp.dma_start(extra, in_blocks(x_in)[:, bass.ds(n, 1), :])]

        def finish(dve, n, out, extra, step):
            a = acc[:, bass.ds(n, 1), 0:D]
            nc.vector.tensor_tensor(a, out, extra, ALU.add).then_inc(step, 1)
            dve.wait_ge(step, 3 * n + 1)
            nc.vector.tensor_tensor(a, a, b_sb[:, 0:1, :], ALU.add).then_inc(step, 1)
            dve.wait_ge(step, 3 * n + 2)
            dve.sem_inc(step, 1)
            return nc.vector.tensor_tensor(a, a, b_sb[:, 1:2, :], ALU.add)
        project_rows(nc, k, name, 4, lambda c: w_sb[:, c, :] if c < 2 else k.mix[:, c - 2, :], D, finish, load=load, loads=2, scale=scale)


EXPERTS = 8
HID = 1024
FC = HID // P
CAP = -(-(5 * NODES) // (4 * EXPERTS))
CAPPAD = -(-CAP // P) * P
TT = CAPPAD // P
OUTSIDE = 1 << 20
FMAX = 3.4028234e38


def half_index(n, h):
    return (n - h) // 2 + 1


def paired(engine, one):
    with engine.Fori(0, NB // 2) as i:
        for h in range(2):
            one(2 * i + h, h)
    one(NB - 1, 0)


def in_pairs(engine, count, one):
    with engine.Fori(0, count // 2) as i:
        for h in range(2):
            one(2 * i + h, h)
    if count % 2:
        one(count - 1, 0)


def stage_gate(nc, k, xn, gate_w, gate_b, logits):
    with ExitStack() as ctx:
        w_sb = ctx.enter_context(nc.sbuf_tensor("gate_w", [P, 2, EXPERTS], f32))
        b_sb = ctx.enter_context(nc.sbuf_tensor("gate_b", [P, EXPERTS], f32))
        load_weights(nc, ctx, "gatew", [(w_sb[:, :, :], gate_w.rearrange("(c p) n -> p c n", p=P)), (b_sb[:, :], on_all(gate_b))])
        project_rows(nc, k, "gate", 2, lambda c: w_sb[:, c, :], EXPERTS,
                     lambda dve, n, out, extra, step: nc.vector.tensor_tensor(logits[:, bass.ds(n, 1), :], out, b_sb[:, :].unsqueeze(1), ALU.add),
                     load=lambda sp, n, staged, extra: [sp.dma_start(staged, block_rows(xn, n))], loads=1)


def stage_route(nc, k, name, logits, prob, to_slot, from_slot, capacity=None, block_expert=None):
    SLOTS = EXPERTS * NB
    with ExitStack() as ctx:
        sb, ps, sem = allocators(nc, ctx, name)
        best = sb("best", [P, NB])
        hot = sb("hot", [P, NB, EXPERTS])
        exps = sb("exps", [P, NB, EXPERTS])
        code = sb("code", [P, EXPERTS])
        codes = sb("codes", [P, NB, EXPERTS])
        first = sb("first", [P, NB])
        tot = sb("tot", [P, NB, EXPERTS])
        run = sb("run", [P, NB, EXPERTS])
        zero = sb("zero", [P, NB])
        pos = sb("pos", [P, NB])
        slot = sb("slot", [P, NB])
        kept = sb("kept", [P, NB])
        away = sb("away", [P, NB])
        last_slot = sb("last_slot", [P, NB])
        size = sb("size", [P, EXPERTS])
        size_i = sb("size_i", [P, EXPERTS], i32)
        ends = sb("ends", [P, EXPERTS])
        below = sb("below", [P, P])
        owner = sb("owner", [P, P])
        p_in = ps("p_in", [P, 512])
        p_tot = ps("p_tot", [P, 512])
        v, exped, counted = sem("v"), sem("exped"), sem("counted")
        flat = lambda t: t[:, :, :].rearrange("p b e -> p (b e)")
        wide = lambda t: t[:, :].unsqueeze(2).to_broadcast([P, NB, EXPERTS])
        with nc.Block() as block:
            @block.tensor
            def _(pe):
                pe.wait_ge(v, 8)
                nc.tensor.matmul(p_in[:, 0:SLOTS], k.before[:, :], flat(hot), start=True, stop=True)
                nc.tensor.matmul(p_tot[:, 0:SLOTS], k.ones[:, :], flat(hot), start=True, stop=True).then_inc(counted, 1)

            @block.scalar
            def _(act):
                act.wait_ge(v, 3)
                nc.scalar.activation(flat(exps), flat(exps), ACT.Exp).then_inc(exped, 1)

            @block.vector
            def _(dve):
                nc.vector.tensor_reduce(best[:, :], logits[:, :, :], AX.X, ALU.max).then_inc(v, 1)
                nc.vector.tensor_scalar(code[:, :], k.iota[:, 0:EXPERTS], -float(EXPERTS), None, ALU.add).then_inc(v, 1)
                dve.wait_ge(v, 2)
                nc.vector.tensor_tensor(exps[:, :, :], logits[:, :, :], wide(best), ALU.subtract).then_inc(v, 1)
                nc.vector.tensor_tensor(hot[:, :, :], logits[:, :, :], wide(best), ALU.is_equal).then_inc(v, 1)
                dve.wait_ge(v, 4)
                nc.vector.tensor_tensor(codes[:, :, :], hot[:, :, :], code[:, :].unsqueeze(1).to_broadcast([P, NB, EXPERTS]),
                                        ALU.mult).then_inc(v, 1)
                dve.wait_ge(v, 5)
                nc.vector.tensor_reduce(first[:, :], codes[:, :, :], AX.X, ALU.min).then_inc(v, 1)
                dve.wait_ge(v, 6)
                nc.vector.tensor_tensor(hot[:, :, :], code[:, :].unsqueeze(1).to_broadcast([P, NB, EXPERTS]), wide(first),
                                        ALU.is_equal).then_inc(v, 1)
                nc.vector.memset(zero[:, :], 0.0).then_inc(v, 1)
                dve.wait_ge(exped, 1)
                nc.vector.tensor_reduce(prob[:, :], exps[:, :, :], AX.X, ALU.add).then_inc(v, 1)
                dve.wait_ge(v, 9)
                nc.vector.reciprocal(prob[:, :], prob[:, :]).then_inc(v, 1)
                dve.wait_ge(counted, 1)
                nc.vector.tensor_copy(flat(tot), p_tot[:, 0:SLOTS]).then_inc(v, 1)
                dve.wait_ge(v, 11)
                for e in range(EXPERTS):
                    nc.vector.tensor_tensor_scan(run[:, :, e], tot[:, :, e], zero[:, :], 0.0, ALU.add, ALU.add).then_inc(v, 1)
                dve.wait_ge(v, 19)
                nc.vector.tensor_copy(size[:, :], run[:, NB - 1, :]).then_inc(v, 1)
                dve.wait_ge(v, 20)
                nc.vector.tensor_tensor(run[:, :, :], run[:, :, :], tot[:, :, :], ALU.subtract).then_inc(v, 1)
                dve.wait_ge(v, 21)
                nc.vector.tensor_tensor(flat(run), flat(run), p_in[:, 0:SLOTS], ALU.add).then_inc(v, 1)
                if capacity is None:
                    nc.vector.tensor_scalar(size[:, :], size[:, :], float(P - 1), None, ALU.add).then_inc(v, 1)
                    dve.wait_ge(v, 23)
                    nc.vector.tensor_copy(size_i[:, :], size[:, :]).then_inc(v, 1)
                    dve.wait_ge(v, 24)
                    nc.vector.tensor_single_scalar(size_i[:, :], size_i[:, :], 7, op=ALU.arith_shift_right).then_inc(v, 1)
                    dve.wait_ge(v, 25)
                    nc.vector.tensor_copy(size[:, :], size_i[:, :]).then_inc(v, 1)
                    dve.wait_ge(v, 26)
                    nc.vector.tensor_tensor_scan(ends[:, :], size[:, :], zero[:, 0:EXPERTS], 0.0, ALU.add, ALU.add).then_inc(v, 1)
                    dve.wait_ge(v, 27)
                    nc.vector.memset(owner[:, :], 0.0).then_inc(v, 1)
                    for e in range(EXPERTS - 1):
                        dve.wait_ge(v, 28 + 2 * e)
                        nc.vector.tensor_scalar(below[:, :], k.iota[:, :], ends[:, e:e + 1], None, ALU.is_ge).then_inc(v, 1)
                        dve.wait_ge(v, 29 + 2 * e)
                        nc.vector.tensor_tensor(owner[:, :], owner[:, :], below[:, :], ALU.add).then_inc(v, 1)
                    dve.wait_ge(v, 42)
                    nc.vector.tensor_copy(block_expert[:, :], owner[0:1, :]).then_inc(v, 1)
                    nc.vector.tensor_tensor(ends[:, :], ends[:, :], size[:, :], ALU.subtract).then_inc(v, 1)
                    dve.wait_ge(v, 44)
                    nc.vector.tensor_scalar(ends[:, :], ends[:, :], float(P), None, ALU.mult).then_inc(v, 1)
                    dve.wait_ge(v, 45)
                    nc.vector.tensor_tensor(run[:, :, :], run[:, :, :], ends[:, :].unsqueeze(1).to_broadcast([P, NB, EXPERTS]),
                                            ALU.add).then_inc(v, 1)
                    at = 46
                else:
                    at = 22
                dve.wait_ge(v, at)
                nc.vector.tensor_tensor(run[:, :, :], run[:, :, :], hot[:, :, :], ALU.mult).then_inc(v, 1)
                dve.wait_ge(v, at + 1)
                nc.vector.tensor_reduce(pos[:, :], run[:, :, :], AX.X, ALU.add).then_inc(v, 1)
                dve.wait_ge(v, at + 2)
                if capacity is None:
                    nc.vector.tensor_copy(to_slot[:, :], pos[:, :]).then_inc(v, 1)
                    nc.vector.tensor_copy(from_slot[:, :], pos[:, :]).then_inc(v, 1)
                else:
                    nc.vector.tensor_scalar(kept[:, :], pos[:, :], float(capacity), None, ALU.is_lt).then_inc(v, 1)
                    nc.vector.tensor_scalar(slot[:, :], first[:, :], float(EXPERTS), float(CAPPAD), ALU.add, ALU.mult).then_inc(v, 1)
                    nc.vector.tensor_scalar(last_slot[:, :], pos[:, :], float(capacity - 1), None, ALU.min).then_inc(v, 1)
                    dve.wait_ge(v, at + 5)
                    nc.vector.tensor_tensor(last_slot[:, :], last_slot[:, :], slot[:, :], ALU.add).then_inc(v, 1)
                    nc.vector.tensor_tensor(slot[:, :], slot[:, :], pos[:, :], ALU.add).then_inc(v, 1)
                    nc.vector.tensor_tensor(prob[:, :], prob[:, :], kept[:, :], ALU.mult).then_inc(v, 1)
                    nc.vector.tensor_scalar(away[:, :], kept[:, :], -float(OUTSIDE), float(OUTSIDE), ALU.mult, ALU.add).then_inc(v, 1)
                    dve.wait_ge(v, at + 9)
                    nc.vector.tensor_copy(from_slot[:, :], last_slot[:, :]).then_inc(v, 1)
                    nc.vector.tensor_tensor(slot[:, :], slot[:, :], away[:, :], ALU.add).then_inc(v, 1)
                    dve.wait_ge(v, at + 11)
                    nc.vector.tensor_copy(to_slot[:, :], slot[:, :]).then_inc(v, 1)


def stage_dispatch(nc, k, name, xn, to_slot, slots):
    with ExitStack() as ctx:
        sb, ps, sem = allocators(nc, ctx, name)
        sent = sem("sent")
        with nc.Block() as block:
            @block.gpsimd
            def _(pool):
                for b in range(NB):
                    nc.gpsimd.indirect_dma_start(
                        out=slots, out_offset=bass.IndirectOffsetOnAxis(ap=to_slot[:, b:b + 1], axis=0),
                        in_=xn[:, b, :], in_offset=None, bounds_check=EXPERTS * CAPPAD - 1, oob_is_err=False,
                    ).then_inc(sent, 16)
                pool.wait_ge(sent, 16 * NB)


def stage_experts0(nc, k, slots, w1, b1, w2, b2, out, scratch):
    HT = TT // 2
    HW = HT * P
    with ExitStack() as ctx:
        sb, ps, sem = allocators(nc, ctx, "experts0")
        w1_sb = sb("w1", [P, 2, 2, HID])
        w2_sb = sb("w2", [P, 2, FC, D])
        b1_sb = sb("b1", [P, 2, FC])
        b2_sb = sb("b2", [P, 2, D])
        x_sb = sb("x", [P, 2, TT, D])
        xt = sb("xt", [P, 2, TT * P])
        ht = scratch[:, 0:FC * TT * P // D, :].rearrange("p b d -> p (b d)").rearrange("p (f n) -> p f n", f=FC)
        y_sb = sb("y", [P, 2, TT, D])
        pt = ps("pt", [P, 2, 512])
        ph = [ps(f"ph{j}", [P, 512]) for j in range(4)]
        py = [ps(f"py{j}", [P, 512]) for j in range(2)]
        loaded = [sem("loaded0"), sem("loaded1")]
        stored = [sem("stored0"), sem("stored1")]
        turned, copied = sem("turned"), sem("copied")
        h_made, relued = sem("h_made"), sem("relued")
        y_made, evacuated, y_free = sem("y_made"), sem("evacuated"), sem("y_free")
        with nc.Block() as block:
            @block.sync
            def _(sp):
                sp.sem_inc(y_free, 2)

                def load(e, h):
                    d = bass.ds(e, 1)
                    sp.dma_start(x_sb[:, h, :, :], slots.rearrange("(e t l) d -> l e t d", l=P, t=TT)[:, d, :, :]
                                 .rearrange("l a t d -> l (a t) d")).then_inc(loaded[h], 16)
                    sp.dma_start(w1_sb[:, h, :, :], w1[d, :, :].rearrange("a (c p) f -> p (a c) f", p=P)).then_inc(loaded[h], 16)
                    sp.dma_start(w2_sb[:, h, :, :], w2[d, :, :].rearrange("a (c p) n -> p (a c) n", p=P)).then_inc(loaded[h], 16)
                    sp.dma_start(b2_sb[:, h, :], b2[d, :].to_broadcast([P, D])).then_inc(loaded[h], 16)
                    sp.dma_start(b1_sb[:, h, :], b1[d, :, :].rearrange("a p f -> p (a f)")).then_inc(loaded[h], 16)

                def store(e, h):
                    sp.wait_ge(evacuated, TT * (e + 1) + 2)
                    sp.dma_start(out.rearrange("(e t l) d -> l e t d", l=P, t=TT)[:, bass.ds(e, 1), :, :]
                                 .rearrange("l a t d -> l (a t) d"), y_sb[:, h, :, :]).then_inc(stored[h], 16)

                load(0, 0)
                load(1, 1)
                with nc.sync.Fori(0, EXPERTS // 2 - 1) as i:
                    for h in range(2):
                        e = 2 * i + h
                        store(e, h)
                        load(e + 2, h)
                        sp.wait_ge(stored[h], 16 * (i + 1))
                        sp.sem_inc(y_free, 1)
                for h in range(2):
                    store(EXPERTS - 2 + h, h)
                for h in range(2):
                    sp.wait_ge(stored[h], 16 * (EXPERTS // 2))

            @block.tensor
            def _(pe):
                with nc.tensor.Fori(0, EXPERTS // 2) as i:
                    for h in range(2):
                        e = 2 * i + h
                        pe.wait_ge(loaded[h], 80 * (i + 1))
                        for t in range(TT):
                            pe.wait_ge(copied, TT * e + t + 1)
                            for c in range(2):
                                last = nc.tensor.transpose(pt[:, t % 2, c * P:(c + 1) * P], x_sb[:, h, t, c * P:(c + 1) * P],
                                                           k.ident[:, :])
                            last.then_inc(turned, 1)
                        for half in range(2):
                            pe.wait_ge(copied, TT * e + HT * (half + 1) + 2)
                            for f in range(FC):
                                pe.wait_ge(relued, 2 * FC * e + FC * half + f + 1)
                                for c in range(2):
                                    last = nc.tensor.matmul(ph[f % 4][:, 0:HW], w1_sb[:, h, c, f * P:(f + 1) * P],
                                                            xt[:, c, half * HW:(half + 1) * HW], start=(c == 0), stop=(c == 1))
                                last.then_inc(h_made, 1)
                        for t in range(TT):
                            if t % HT == 0:
                                pe.wait_ge(relued, 2 * FC * e + FC * (t // HT + 1) + 4)
                            pe.wait_ge(evacuated, TT * e + t + 1)
                            for f in range(FC):
                                last = nc.tensor.matmul(py[t % 2][:, 0:D], ht[:, f, t * P:(t + 1) * P], w2_sb[:, h, f, :],
                                                        start=(f == 0), stop=(f == FC - 1))
                            last.then_inc(y_made, 1)

            @block.scalar
            def _(act):
                act.sem_inc(relued, 4)
                with nc.scalar.Fori(0, EXPERTS // 2) as i:
                    for h in range(2):
                        e = 2 * i + h
                        act.wait_ge(loaded[h], 80 * (i + 1))
                        for half in range(2):
                            for f in range(FC):
                                act.wait_ge(h_made, 2 * FC * e + FC * half + f + 1)
                                nc.scalar.activation(ht[:, f, half * HW:(half + 1) * HW], ph[f % 4][:, 0:HW], ACT.Relu,
                                                     bias=b1_sb[:, h, f:f + 1]).then_inc(relued, 1)

            @block.vector
            def _(dve):
                dve.sem_inc(copied, 2)
                dve.sem_inc(evacuated, 2)
                with nc.vector.Fori(0, EXPERTS // 2) as i:
                    for h in range(2):
                        e = 2 * i + h
                        for t in range(TT):
                            dve.wait_ge(turned, TT * e + t + 1)
                            nc.vector.tensor_copy(xt[:, :, t * P:(t + 1) * P], pt[:, t % 2, 0:D].rearrange("p (c n) -> p c n", c=2)).then_inc(copied, 1)
                        dve.wait_ge(y_free, e + 1)
                        dve.wait_ge(loaded[h], 80 * (i + 1))
                        for t in range(TT):
                            dve.wait_ge(y_made, TT * e + t + 1)
                            nc.vector.tensor_tensor(y_sb[:, h, t, :], py[t % 2][:, 0:D], b2_sb[:, h, :], ALU.add).then_inc(evacuated, 1)


def stage_combine(nc, k, name, rows, from_slot, x, prob, guard, x_out=None):
    R = 4
    with ExitStack() as ctx:
        sb, ps, sem = allocators(nc, ctx, name)
        got = sb("got", [P, R, D])
        bad = sb("bad", [P, 2, D], i32)
        most = sb("most", [P, D])
        least = sb("least", [P, D])
        nought = sb("nought", [P, D])
        gathered = [sem(f"gathered{j}") for j in range(R)]
        done, v, stored, turn = sem("done"), sem("v"), sem("stored"), sem("turn")
        FULL = NB // R

        with nc.Block() as block:
            @block.gpsimd
            def _(pool):
                for b in range(NB):
                    if b >= R:
                        pool.wait_ge(done, b - R + 1)
                    nc.gpsimd.indirect_dma_start(out=got[:, b % R, :], out_offset=None, in_=rows,
                                                 in_offset=bass.IndirectOffsetOnAxis(ap=from_slot[:, b:b + 1], axis=0),
                                                 ).then_inc(gathered[b % R], 16)

            @block.vector
            def _(dve):
                if guard:
                    nc.vector.memset(most[:, :], 10000.0).then_inc(v, 1)
                    nc.vector.memset(least[:, :], -10000.0).then_inc(v, 1)
                    nc.vector.memset(nought[:, :], 0.0).then_inc(v, 1)

                def combine(b, j, use):
                    g = got[:, j, :]
                    a = x[:, bass.ds(b, 1), 0:D]
                    dve.wait_ge(gathered[j], 16 * use)
                    if not guard:
                        nc.vector.scalar_tensor_tensor(out=a, in0=got[:, j:j + 1, :], scalar=prob[:, bass.ds(b, 1)], in1=a,
                                                       op0=ALU.mult, op1=ALU.add).then_inc(done, 1)
                        return
                    w = 3 + 9 * b
                    dve.wait_ge(v, w)
                    nc.vector.tensor_scalar(g, g, prob[:, bass.ds(b, 1)], None, ALU.mult).then_inc(v, 1)
                    dve.wait_ge(v, w + 1)
                    nc.vector.tensor_scalar(bad[:, 0, :], g, FMAX, None, ALU.is_gt).then_inc(v, 1)
                    nc.vector.tensor_scalar(bad[:, 1, :], g, -FMAX, None, ALU.is_lt).then_inc(v, 1)
                    dve.wait_ge(v, w + 3)
                    dve.sem_inc(turn, 1)
                    nc.vector.copy_predicated(g, bad[:, 0, :], most[:, :]).then_inc(v, 1)
                    dve.wait_ge(v, w + 4)
                    dve.sem_inc(turn, 1)
                    nc.vector.copy_predicated(g, bad[:, 1, :], least[:, :]).then_inc(v, 1)
                    dve.wait_ge(v, w + 5)
                    nc.vector.tensor_tensor(bad[:, 0, :], g, g, ALU.not_equal).then_inc(v, 1)
                    dve.wait_ge(v, w + 6)
                    dve.sem_inc(turn, 1)
                    nc.vector.copy_predicated(g, bad[:, 0, :], nought[:, :]).then_inc(v, 1)
                    dve.wait_ge(v, w + 7)
                    nc.vector.tensor_tensor(a, a, got[:, j:j + 1, :], ALU.add).then_inc(v, 1)
                    dve.wait_ge(v, w + 8)
                    dve.sem_inc(v, 1)
                    dve.sem_inc(done, 1)

                with nc.vector.Fori(0, FULL) as i:
                    for j in range(R):
                        combine(R * i + j, j, i + 1)
                for b in range(FULL * R, NB):
                    combine(b, b % R, FULL + 1)

            @block.sync
            def _(sp):
                if x_out is not None:
                    for g in range(NG):
                        b = slice(g * CG, (g + 1) * CG)
                        sp.wait_ge(done, (g + 1) * CG)
                        sp.dma_start(in_blocks(x_out)[:, b, :], x[:, b, 0:D]).then_inc(stored, 16)
                    sp.wait_ge(stored, 16 * NG)


ECOLS = ET
EPAD = ECOLS * P
EROWS = EG * P
LOW = -1e30


class Tally:

    def __init__(self):
        self.n = 0

    def one(self):
        self.n += 1
        return 1


def stage_gat_project(nc, k, name, xn, w, w_t, a_src, a_dst, heads, acc, esd, table):
    C = D // heads
    W2 = D + 2 * heads
    with ExitStack() as ctx:
        sb, _, sem = allocators(nc, ctx, name + "_out")
        w_sb = sb("w", [P, 2, W2])
        stored = sem("stored")
        with ExitStack() as fold:
            sb, ps, sem = allocators(nc, fold, name + "a")
            wt_sb = sb("wt", [P, 2, D])
            a_sb = sb("a", [P, 2, 2 * heads])
            pa = ps("pa", [P, 2, 512])
            zeroed, loaded, folded = sem("zeroed"), sem("loaded"), sem("folded")
            pieces = 2 * heads * (C // min(C, P))
            with nc.Block() as block:
                @block.sync
                def _(sp):
                    sp.dma_start(w_sb[:, :, 0:D], w.rearrange("(c p) n -> p c n", p=P)).then_inc(loaded, 16)
                    sp.dma_start(wt_sb[:, :, :], w_t.rearrange("(c p) n -> p c n", p=P)).then_inc(loaded, 16)
                    sp.wait_ge(zeroed, 1)
                    for s, a in enumerate((a_src, a_dst)):
                        for q in range(heads):
                            for r in range(q * C, (q + 1) * C, min(C, P)):
                                n = min(C, P)
                                sp.dma_start(a_sb[r % P:r % P + n, r // P, s * heads + q:s * heads + q + 1],
                                             a[q, r - q * C:r - q * C + n].rearrange("(n a) -> n a", a=1)).then_inc(loaded, 16)

                @block.tensor
                def _(pe):
                    pe.wait_ge(loaded, 16 * (2 + pieces))
                    for m in range(2):
                        for c in range(2):
                            last = nc.tensor.matmul(pa[:, m, 0:2 * heads], wt_sb[:, c, m * P:(m + 1) * P], a_sb[:, c, :],
                                                    start=(c == 0), stop=(c == 1))
                    last.then_inc(folded, 1)

                @block.vector
                def _(dve):
                    nc.vector.memset(a_sb[:, :, :], 0.0).then_inc(zeroed, 1)
                    dve.wait_ge(folded, 1)
                    nc.vector.tensor_copy(w_sb[:, :, D:W2], pa[:, :, 0:2 * heads])

        def finish(dve, n, out, extra, step):
            nc.vector.tensor_copy(acc[:, bass.ds(n, 1), 0:D], out[:, :, 0:D])
            return nc.vector.tensor_copy(esd[:, bass.ds(n, 1), :], out[:, :, D:W2])

        def store(sp, done):
            for g in range(NG):
                b = slice(g * CG, (g + 1) * CG)
                sp.wait_ge(done, (g + 1) * CG + RING)
                sp.dma_start(in_blocks(table)[:, b, :], acc[:, b, 0:D]).then_inc(stored, 16)
            sp.wait_ge(stored, 16 * NG)
        project_rows(nc, k, name, 2, lambda c: w_sb[:, c, :], W2, finish,
                     load=lambda sp, n, staged, extra: [sp.dma_start(staged, block_rows(xn, n))], loads=1, store=store)


def stage_gat_weights(nc, k, name, heads, esd, src_flat, dst_flat, prev_flat, run_dram, node_dram, p_dram, weights, p_self):
    H = heads
    ECOLS8 = -(-ECOLS // 16) * 16
    TB = min(8, 512 // (H * NB))
    TB = 8 if TB == 8 else 2
    BANKS1 = 4 if TB < 8 else 2
    with ExitStack() as ctx:
        sb, ps, sem = allocators(nc, ctx, name)
        dst_c = sb("dst_c", [P, ECOLS], i32)
        prev_c = sb("prev_c", [P, ECOLS], i32)
        es_all = sb("es", [P, ECOLS8, H])
        es = es_all[:, 0:ECOLS, :]
        with ExitStack() as pick:
            sb1 = lambda n, s_, t=f32: pick.enter_context(nc.sbuf_tensor(f"{name}_{n}", s_, t))
            src_c = sb1("src_c", [P, ECOLS8], i32)
            src_i = sb1("src_i", [P, ECOLS8], i32)
            src_blk = sb1("src_blk", [P, ECOLS8])
            src_lane = sb1("src_lane", [P, ECOLS8])
            ident16 = sb1("ident16", [P, P], bf16)
            parts = sb1("parts", [P, 3, H, NB], bf16)
            rest = sb1("rest", [P, H, NB])
            hot = sb1("hot", [P, 2, 8, P], bf16)
            hot_t = sb1("hot_t", [P, 2, 8 * P], bf16)
            blk_hot = sb1("blk_hot", [P, 2, 8, NB])
            picked = sb1("picked", [P, 2, TB, H, NB])
            pt1 = [pick.enter_context(nc.psum_tensor(f"{name}_pt1{h}", [P, 8 * P], bf16)) for h in range(2)]
            po1 = [pick.enter_context(nc.psum_tensor(f"{name}_po1{h}", [P, 512], f32)) for h in range(BANKS1)]
            loaded, v1, hot1, turned1, copied1 = sem("loaded"), sem("v1"), sem("hot1"), sem("turned1"), sem("copied1")
            blk1, out1, masked1, reduced1, split1 = sem("blk1"), sem("out1"), sem("masked1"), sem("reduced1"), sem("split1")
            halves = lambda engine, one: in_pairs(engine, ECOLS8 // 8, one)
            with nc.Block() as block:
                @block.sync
                def _(sp):
                    sp.dma_start(src_c[:, 0:ECOLS], src_flat[0:EPAD].rearrange("(q i) -> q i", q=P)).then_inc(loaded, 16)
                    sp.dma_start(dst_c[:, :], dst_flat[0:EPAD].rearrange("(q i) -> q i", q=P)).then_inc(loaded, 16)
                    sp.dma_start(prev_c[:, :], prev_flat[0:EPAD].rearrange("(q i) -> q i", q=P)).then_inc(loaded, 16)

                @block.tensor
                def _(pe):
                    pe.sem_inc(turned1, 2)
                    pe.wait_ge(v1, 6)
                    pe.wait_ge(split1, 5)

                    def turn(n, h):
                        pe.wait_ge(hot1, n + 1)
                        pe.wait_ge(copied1, n + 1)
                        for j in range(8):
                            last = nc.tensor.transpose(pt1[h][:, j * P:(j + 1) * P], hot[:, h, j, :], ident16[:, :])
                        last.then_inc(turned1, 1)

                    def multiply(n, h):
                        pe.wait_ge(copied1, n + 3)
                        for b in range(8 // TB):
                            bank = b if TB < 8 else h
                            pe.wait_ge(masked1, 8 // TB * n + b + 1)
                            for j in range(TB):
                                for part in range(3):
                                    last = nc.tensor.matmul(po1[bank][:, j * H * NB:(j + 1) * H * NB],
                                                            hot_t[:, h, (b * TB + j) * P:(b * TB + j + 1) * P],
                                                            parts[:, part, :, :].rearrange("p h b -> p (h b)"),
                                                            start=(part == 0), stop=(part == 2))
                            last.then_inc(out1, 1)

                    turn(0, 0)
                    turn(1, 1)
                    with nc.tensor.Fori(0, ECOLS8 // 16 - 1) as i:
                        for h in range(2):
                            multiply(2 * i + h, h)
                            turn(2 * i + h + 2, h)
                    multiply(ECOLS8 // 8 - 2, 0)
                    multiply(ECOLS8 // 8 - 1, 1)

                @block.scalar
                def _(act):
                    act.sem_inc(copied1, 2)

                    def copy(n, h):
                        act.wait_ge(turned1, n + 3)
                        act.wait_ge(out1, 8 // TB * (n + 1))
                        nc.scalar.activation(hot_t[:, h, :], pt1[h][:, :], ACT.Copy).then_inc(copied1, 1)
                    halves(nc.scalar, copy)

                @block.vector
                def _(dve):
                    dve.sem_inc(out1, 16 // TB)
                    dve.sem_inc(masked1, BANKS1)
                    dve.wait_ge(loaded, 48)
                    nc.vector.tensor_single_scalar(src_i[:, 0:ECOLS], src_c[:, 0:ECOLS], 7, op=ALU.arith_shift_right).then_inc(v1, 1)
                    nc.vector.memset(src_i[:, ECOLS:], 0).then_inc(v1, 1)
                    dve.wait_ge(v1, 2)
                    nc.vector.tensor_copy(src_blk[:, :], src_i[:, :]).then_inc(v1, 1)
                    dve.wait_ge(v1, 3)
                    nc.vector.tensor_single_scalar(src_i[:, 0:ECOLS], src_c[:, 0:ECOLS], P - 1, op=ALU.bitwise_and).then_inc(v1, 1)
                    dve.wait_ge(v1, 4)
                    nc.vector.tensor_copy(src_lane[:, :], src_i[:, :]).then_inc(v1, 1)
                    nc.vector.tensor_copy(ident16[:, :], k.ident[:, :]).then_inc(v1, 1)
                    dve.wait_ge(v1, 6)
                    es_h = esd[:, :, 0:H].rearrange("p b h -> p h b")
                    nc.vector.tensor_copy(parts[:, 0, :, :], es_h).then_inc(split1, 1)
                    dve.wait_ge(split1, 1)
                    nc.vector.tensor_tensor(rest[:, :, :], es_h, parts[:, 0, :, :], ALU.subtract).then_inc(split1, 1)
                    dve.wait_ge(split1, 2)
                    nc.vector.tensor_copy(parts[:, 1, :, :], rest[:, :, :]).then_inc(split1, 1)
                    dve.wait_ge(split1, 3)
                    nc.vector.tensor_tensor(rest[:, :, :], rest[:, :, :], parts[:, 1, :, :], ALU.subtract).then_inc(split1, 1)
                    dve.wait_ge(split1, 4)
                    nc.vector.tensor_copy(parts[:, 2, :, :], rest[:, :, :]).then_inc(split1, 1)

                    def find(n, h):
                        dve.wait_ge(turned1, n + 1)
                        nc.vector.tensor_tensor(hot[:, h, :, :], k.iota[:, :].unsqueeze(1).to_broadcast([P, 8, P]),
                                                src_lane[:, bass.ds(8 * n, 8)].unsqueeze(2).to_broadcast([P, 8, P]),
                                                ALU.is_equal).then_inc(hot1, 1)

                    slot_of = lambda b, h: b % 2 if TB < 8 else h

                    def mask(n, h, b):
                        m = 8 // TB * n + b
                        dve.wait_ge(out1, 16 // TB + m + 1)
                        dve.wait_ge(reduced1, m + 1)
                        nc.vector.tensor_tensor(
                            picked[:, slot_of(b, h), :, :, :],
                            po1[b if TB < 8 else h][:, 0:TB * H * NB].rearrange("p (j h b) -> p j h b", j=TB, h=H),
                            blk_hot[:, h, b * TB:(b + 1) * TB, :].unsqueeze(2).to_broadcast([P, TB, H, NB]), ALU.mult).then_inc(masked1, 1)

                    def total(n, h, b):
                        dve.wait_ge(masked1, BANKS1 + 8 // TB * n + b + 1)
                        nc.vector.tensor_reduce(es_all[:, bass.ds(8 * n + b * TB, TB), :], picked[:, slot_of(b, h), :, :, :],
                                                AX.X, ALU.add).then_inc(reduced1, 1)

                    def take(n, h, first=False):
                        if not (isinstance(n, int) and n < 2):
                            dve.wait_ge(masked1, BANKS1 + 8 // TB * (n - 1))
                        nc.vector.tensor_tensor(blk_hot[:, h, :, :], k.iota[:, 0:NB].unsqueeze(1).to_broadcast([P, 8, NB]),
                                                src_blk[:, bass.ds(8 * n, 8)].unsqueeze(2).to_broadcast([P, 8, NB]),
                                                ALU.is_equal).then_inc(blk1, 1)
                        dve.wait_ge(blk1, n + 1)
                        for b in range(8 // TB):
                            mask(n, h, b)
                            if b:
                                total(n, h, b - 1)
                            elif not first:
                                total(n - 1, 1 - h, 8 // TB - 1)
                    dve.sem_inc(reduced1, 2)
                    find(0, 0)
                    find(1, 1)
                    find(2, 0)
                    take(0, 0, first=True)
                    with nc.vector.Fori(0, ECOLS8 // 16 - 2) as i:
                        find(2 * i + 3, 1)
                        take(2 * i + 1, 1)
                        find(2 * i + 4, 0)
                        take(2 * i + 2, 0)
                    find(ECOLS8 // 8 - 1, 1)
                    take(ECOLS8 // 8 - 3, 1)
                    take(ECOLS8 // 8 - 2, 0)
                    take(ECOLS8 // 8 - 1, 1)
                    total(ECOLS8 // 8 - 1, 1, 8 // TB - 1)

        same = sb("same", [P, ECOLS])
        pen = sb("pen", [P, ECOLS])
        run = sb("run", [P, ECOLS, 2 * H])
        node = sb("node", [P, NB, 2 * H])
        nodes = sb("nodes", [P, ECOLS, 2 * H])
        top = nodes[:, :, :].rearrange("p i h -> p (i h)")[:, 0:ECOLS * H].rearrange("p (i h) -> p i h", h=H)
        ends = sb("ends", [P, 3 * H + 2])
        ends_t = sb("ends_t", [3 * H + 2, P])
        whole = sb("whole", [P, 1])
        end_idx = sb("end_idx", [P, NB], i32)
        start_idx = sb("start_idx", [P, NB], i32)
        cnt = sb("cnt", [P, NB])
        beg = sb("beg", [P, NB])
        none = sb("none", [P, NB])
        tmp = sb("tmp", [P, NB])
        seg = sb("seg", [P, NB, H])
        rows = sb("rows", [2 * H, 4, P])
        carry = sb("carry", [P, 2 * H])
        tiles = sb("tiles", [P, SG, P * H])
        pt = ps("pt", [P, 512])
        pw = ps("pw", [P, 2, 512])

        v2, turned2, stored2, seg2 = sem("v2"), sem("turned2"), sem("stored2"), sem("seg2")
        c = Tally()
        with nc.Block() as block:
            @block.vector
            def _(dve):
                nc.vector.tensor_tensor(same[:, :], dst_c[:, :], prev_c[:, :], ALU.is_equal).then_inc(v2, c.one())
                dve.wait_ge(v2, c.n)
                nc.vector.tensor_scalar(pen[:, :], same[:, :], -LOW, LOW, ALU.mult, ALU.add).then_inc(v2, c.one())
                nc.vector.tensor_reduce(ends[:, H:H + 1], same[:, :], AX.X, ALU.min).then_inc(v2, c.one())
                dve.wait_ge(v2, c.n)
                nc.vector.tensor_copy(whole[:, :], ends[:, H:H + 1]).then_inc(v2, c.one())
                for q in range(H):
                    nc.vector.tensor_tensor_scan(top[:, :, q], pen[:, :], es[:, :, q], LOW, ALU.add, ALU.max).then_inc(v2, c.one())
                dve.wait_ge(v2, c.n)
                nc.vector.tensor_copy(ends[:, 0:H], top[:, ECOLS - 1, :]).then_inc(v2, c.one())
                dve.wait_ge(turned2, 2)
                nc.vector.tensor_copy(ends_t[0:H + 1, :], pt[0:H + 1, 0:P]).then_inc(v2, c.one())
                dve.wait_ge(turned2, 2)
                nc.vector.tensor_copy(rows[0:H, 0, :], pt[0:H, P:2 * P]).then_inc(v2, c.one())
                dve.wait_ge(v2, c.n)
                nc.vector.tensor_scalar(rows[0:H, 1, :], rows[0:H, 0, :], -LOW, LOW, ALU.mult, ALU.add).then_inc(v2, c.one())
                nc.vector.memset(rows[0:H, 3, :], LOW).then_inc(v2, c.one())
                dve.wait_ge(v2, c.n)
                nc.vector.tensor_tensor_scan(rows[0:H, 2, :], rows[0:H, 1, :], ends_t[0:H, :], LOW, ALU.add, ALU.max).then_inc(v2, c.one())
                dve.wait_ge(v2, c.n)
                nc.vector.tensor_copy(rows[0:H, 3, 1:P], rows[0:H, 2, 0:P - 1]).then_inc(v2, c.one())
                dve.wait_ge(turned2, 3)
                nc.vector.tensor_copy(carry[:, 0:H], pt[:, 2 * P:2 * P + H]).then_inc(v2, c.one())
                dve.wait_ge(v2, c.n)
                for q in range(H):
                    nc.vector.tensor_tensor_scan(top[:, :, q], pen[:, :], es[:, :, q], carry[:, q:q + 1], ALU.add, ALU.max).then_inc(v2, c.one())
                nc.vector.tensor_copy(cnt[:, :], k.row_count[:, :]).then_inc(v2, c.one())
                nc.vector.tensor_copy(beg[:, :], k.row_start[:, :]).then_inc(v2, c.one())
                dve.wait_ge(v2, c.n)
                nc.vector.tensor_scalar(none[:, :], cnt[:, :], 0.5, None, ALU.is_lt).then_inc(v2, c.one())
                nc.vector.tensor_tensor(tmp[:, :], beg[:, :], cnt[:, :], ALU.add).then_inc(v2, c.one())
                dve.wait_ge(v2, c.n)
                nc.vector.tensor_scalar(tmp[:, :], tmp[:, :], -1.0, 0.0, ALU.add, ALU.max).then_inc(v2, c.one())
                nc.vector.scalar_tensor_tensor(out=beg[:, :], in0=none[:, :], scalar=float(OUTSIDE), in1=beg[:, :],
                                               op0=ALU.mult, op1=ALU.add).then_inc(v2, c.one())
                dve.wait_ge(v2, c.n)
                nc.vector.tensor_copy(end_idx[:, :], tmp[:, :]).then_inc(v2, c.one())
                nc.vector.tensor_copy(start_idx[:, :], beg[:, :]).then_inc(v2, c.one())

            @block.tensor
            def _(pe):
                pe.wait_ge(v2, 4 + H + 1)
                nc.tensor.transpose(pt[0:H + 1, 0:P], ends[:, 0:H + 1], k.ident[:, :]).then_inc(turned2, 1)
                nc.tensor.matmul(pt[0:H, P:2 * P], whole[:, :].to_broadcast([P, H]), k.ident[:, :], start=True, stop=True).then_inc(turned2, 1)
                pe.wait_ge(v2, 4 + H + 1 + 6)
                nc.tensor.transpose(pt[:, 2 * P:2 * P + H], rows[0:H, 3, :], k.ident[0:H, 0:H]).then_inc(turned2, 1)

            @block.sync
            def _(sp):
                sp.wait_ge(v2, 4 + H + 1 + 7 + H)
                sp.dma_start(run_dram.rearrange("(q i) h -> q i h", q=P), top[:, :, :]).then_inc(stored2, 16)

            @block.gpsimd
            def _(pool):
                pool.wait_ge(v2, 4 + H + 1 + 7 + H + 8)
                pool.wait_ge(stored2, 16)
                for b in range(NB):
                    nc.gpsimd.indirect_dma_start(out=seg[:, b, :], out_offset=None, in_=run_dram,
                                                 in_offset=bass.IndirectOffsetOnAxis(ap=end_idx[:, b:b + 1], axis=0)).then_inc(seg2, 16)
                pool.wait_ge(seg2, 16 * NB)

        v3, exp3, sent3, back3 = sem("v3"), sem("exp3"), sem("sent3"), sem("back3")
        c3 = Tally()
        wide = lambda t: t[:, :].unsqueeze(2).to_broadcast([P, NB, H])
        with nc.Block() as block:
            @block.vector
            def _(dve):
                for q in range(H):
                    nc.vector.scalar_tensor_tensor(out=seg[:, :, q], in0=none[:, :], scalar=2 * LOW, in1=seg[:, :, q],
                                                   op0=ALU.mult, op1=ALU.add).then_inc(v3, c3.one())
                nc.vector.tensor_tensor(p_self[:, :, :], esd[:, :, 0:H], esd[:, :, H:2 * H], ALU.add).then_inc(v3, c3.one())
                nc.vector.tensor_copy(node[:, :, 0:H], esd[:, :, H:2 * H]).then_inc(v3, c3.one())
                dve.wait_ge(v3, c3.n)
                nc.vector.tensor_tensor(seg[:, :, :], seg[:, :, :], esd[:, :, 0:H], ALU.max).then_inc(v3, c3.one())
                nc.vector.scalar_tensor_tensor(out=p_self[:, :, :], in0=p_self[:, :, :], scalar=0.2, in1=p_self[:, :, :],
                                               op0=ALU.mult, op1=ALU.max).then_inc(v3, c3.one())
                dve.wait_ge(v3, c3.n)
                nc.vector.tensor_tensor(seg[:, :, :], seg[:, :, :], esd[:, :, H:2 * H], ALU.add).then_inc(v3, c3.one())
                dve.wait_ge(v3, c3.n)
                nc.vector.scalar_tensor_tensor(out=node[:, :, H:2 * H], in0=seg[:, :, :], scalar=0.2, in1=seg[:, :, :],
                                               op0=ALU.mult, op1=ALU.max).then_inc(v3, c3.one())
                dve.wait_ge(v3, c3.n)
                nc.vector.tensor_tensor(p_self[:, :, :], p_self[:, :, :], node[:, :, H:2 * H], ALU.subtract).then_inc(v3, c3.one())

            @block.scalar
            def _(act):
                act.wait_ge(v3, H + 7)
                nc.scalar.activation(p_self[:, :, :], p_self[:, :, :], ACT.Exp).then_inc(exp3, 1)

            @block.gpsimd
            def _(pool):
                pool.wait_ge(v3, H + 6)
                for b in range(NB):
                    nc.gpsimd.indirect_dma_start(
                        out=node_dram[:, 0:2 * H], out_offset=bass.IndirectOffsetOnAxis(ap=start_idx[:, b:b + 1], axis=0),
                        in_=node[:, b, :], in_offset=None, bounds_check=EPAD - 1, oob_is_err=False).then_inc(sent3, 16)

            @block.sync
            def _(sp):
                sp.wait_ge(sent3, 16 * NB)
                sp.dma_start(nodes[:, :, :], node_dram.rearrange("(q i) h -> q i h", q=P)).then_inc(back3, 16)
                sp.wait_ge(back3, 16)

        v4, turned4, exp4, stored4 = sem("v4"), sem("turned4"), sem("exp4"), sem("stored4")
        c4 = Tally()
        with nc.Block() as block:
            @block.vector
            def _(dve):
                for q in range(2 * H):
                    nc.vector.tensor_tensor_scan(run[:, :, q], same[:, :], nodes[:, :, q], 0.0, ALU.mult, ALU.add).then_inc(v4, c4.one())
                dve.wait_ge(v4, c4.n)
                nc.vector.tensor_copy(ends[:, 0:2 * H], run[:, ECOLS - 1, :]).then_inc(v4, c4.one())
                dve.wait_ge(turned4, 2)
                nc.vector.tensor_copy(ends_t[0:2 * H, :], pt[0:2 * H, 0:P]).then_inc(v4, c4.one())
                nc.vector.tensor_copy(rows[0:2 * H, 0, :], pt[0:2 * H, P:2 * P]).then_inc(v4, c4.one())
                nc.vector.memset(rows[0:2 * H, 3, :], 0.0).then_inc(v4, c4.one())
                dve.wait_ge(v4, c4.n)
                nc.vector.tensor_tensor_scan(rows[0:2 * H, 2, :], rows[0:2 * H, 0, :], ends_t[0:2 * H, :], 0.0, ALU.mult, ALU.add).then_inc(v4, c4.one())
                dve.wait_ge(v4, c4.n)
                nc.vector.tensor_copy(rows[0:2 * H, 3, 1:P], rows[0:2 * H, 2, 0:P - 1]).then_inc(v4, c4.one())
                dve.wait_ge(turned4, 3)
                nc.vector.tensor_copy(carry[:, :], pt[:, 2 * P:2 * P + 2 * H]).then_inc(v4, c4.one())
                dve.wait_ge(v4, c4.n)
                for q in range(2 * H):
                    nc.vector.tensor_tensor_scan(run[:, :, q], same[:, :], nodes[:, :, q], carry[:, q:q + 1], ALU.mult, ALU.add).then_inc(v4, c4.one())
                dve.wait_ge(v4, c4.n)
                nc.vector.tensor_tensor(es[:, :, :], es[:, :, :], run[:, :, 0:H], ALU.add).then_inc(v4, c4.one())
                dve.wait_ge(v4, c4.n)
                nc.vector.scalar_tensor_tensor(out=es[:, :, :], in0=es[:, :, :], scalar=0.2, in1=es[:, :, :],
                                               op0=ALU.mult, op1=ALU.max).then_inc(v4, c4.one())
                dve.wait_ge(v4, c4.n)
                nc.vector.tensor_tensor(es[:, :, :], es[:, :, :], run[:, :, H:2 * H], ALU.subtract).then_inc(v4, c4.one())

            @block.tensor
            def _(pe):
                pe.wait_ge(v4, 2 * H + 1)
                nc.tensor.transpose(pt[0:2 * H, 0:P], ends[:, 0:2 * H], k.ident[:, :]).then_inc(turned4, 1)
                nc.tensor.matmul(pt[0:2 * H, P:2 * P], whole[:, :].to_broadcast([P, 2 * H]), k.ident[:, :], start=True, stop=True).then_inc(turned4, 1)
                pe.wait_ge(v4, 2 * H + 1 + 5)
                nc.tensor.transpose(pt[:, 2 * P:2 * P + 2 * H], rows[0:2 * H, 3, :], k.ident[0:2 * H, 0:2 * H]).then_inc(turned4, 1)

            @block.scalar
            def _(act):
                act.wait_ge(v4, 4 * H + 10)
                nc.scalar.activation(es[:, :, :], es[:, :, :], ACT.Exp).then_inc(exp4, 1)

            @block.sync
            def _(sp):
                sp.wait_ge(exp4, 1)
                sp.dma_start(p_dram[0:EPAD, :].rearrange("(q i) h -> q i h", q=P), es[:, :, :]).then_inc(stored4, 16)
                sp.wait_ge(stored4, 16)

        got5, turned5, v5 = sem("got5"), sem("turned5"), sem("v5")
        by_tile = p_dram.rearrange("(t l) h -> t (l h)", l=P)
        w3 = weights[:, :].rearrange("p (s h) -> p s h", h=H)
        with nc.Block() as block:
            @block.gpsimd
            def _(pool):
                for g in range(SG):
                    nc.gpsimd.indirect_dma_start(out=tiles[:, g, :], out_offset=None, in_=by_tile,
                                                 in_offset=bass.IndirectOffsetOnAxis(ap=k.tile_idx[:, g:g + 1], axis=0)).then_inc(got5, 16)

            @block.tensor
            def _(pe):
                pe.wait_ge(got5, 16 * SG)
                for n in range(SG * H):
                    g, q = n // H, n % H
                    if n >= 2:
                        pe.wait_ge(v5, n - 1)
                    nc.tensor.transpose(pw[:, n % 2, 0:P], tiles[:, g, :].rearrange("s (l h) -> s l h", h=H)[:, :, q], k.ident[:, :]).then_inc(turned5, 1)

            @block.vector
            def _(dve):
                for n in range(SG * H):
                    g, q = n // H, n % H
                    dve.wait_ge(turned5, n + 1)
                    nc.vector.tensor_copy(w3[:, g * P:(g + 1) * P, q], pw[:, n % 2, 0:P]).then_inc(v5, 1)


def stage_gat_self(nc, k, name, heads, acc, p_self):
    C = D // heads
    with ExitStack() as ctx:
        sb, ps, sem = allocators(nc, ctx, name)
        with nc.Block() as block:
            @block.vector
            def _(dve):
                nc.vector.tensor_copy(acc[:, :, D:D + heads], p_self[:, :, :])
                with nc.vector.Fori(0, NB) as n:
                    a = acc[:, bass.ds(n, 1), 0:D].rearrange("p a (h c) -> p (a h) c", c=C)
                    nc.vector.tensor_tensor(a, a, p_self[:, bass.ds(n, 1), :].rearrange("p a h -> p (a h)").unsqueeze(2)
                                            .to_broadcast([P, heads, C]), ALU.mult)


HEADS1, DH1 = 4, 32
INNER1 = HEADS1 * DH1
MEM = 4
assert INNER1 == P


def sum_squares(nc, dve, v, c, x, sq, ss):
    for g in range(NG):
        b = slice(g * CG, (g + 1) * CG)
        if c.n:
            dve.wait_ge(v, c.n)
        nc.vector.tensor_tensor(sq[:, :, :], x[:, b, 0:D], x[:, b, 0:D], ALU.mult).then_inc(v, c.one())
        dve.wait_ge(v, c.n)
        nc.vector.tensor_reduce(ss[:, b], sq[:, :, :], AX.X, ALU.add).then_inc(v, c.one())


def inverse_norm(nc, dve, v, c, rooted, ss, dev, rn, t):
    dve.wait_ge(v, c.n)
    nc.vector.tensor_scalar(ss[:, :], ss[:, :], 1e-24, None, ALU.max).then_inc(v, c.one())
    at = c.n
    dve.wait_ge(rooted, 1)
    nc.vector.reciprocal(rn[:, :], dev[:, :]).then_inc(v, c.one())
    dve.wait_ge(v, c.n)
    sharpen_inverse_root(nc, dve, v, c.n, ss[:, :], rn[:, :], t[:, :])
    c.n += 4
    return at


def stage_mix1(nc, k, xn, acc, w_qkv, g_pre, mem_k, mem_k_t, mem_v_t, w_out, b_out, g_out, x_out):
    with ExitStack() as ctx:
        sb, ps, sem = allocators(nc, ctx, "mix1")
        kv = sb("kv", [P, NB, D + 1])
        q = sb("q", [P, NB, INNER1])
        w_sb = sb("w", [P, 2, 3 * INNER1])
        gp = sb("gp", [P, 2])
        wo = sb("wo", [P, D])
        bo = sb("bo", [P, D])
        go = sb("go", [P, D])
        mk = sb("mk", [P, MEM])
        mkt = sb("mkt", [MEM, INNER1])
        mvt = sb("mvt", [MEM, INNER1 + 1])
        sq = q[:, 0:2 * CG, :].rearrange("p (g b) c -> p g (b c)", b=D // INNER1)
        ss = sb("ss", [P, NB])
        dev = sb("dev", [P, NB])
        rn = sb("rn", [P, NB])
        t = sb("t", [P, NB])
        real = k.before[:, LASTROWS:LASTROWS + 1]
        heads = lambda a: a.rearrange("p b (h d) -> p (b h) d", d=DH1)

        loaded, v0, root0 = sem("loaded"), sem("v0"), sem("root0")
        c0 = Tally()
        at0 = []
        with nc.Block() as block:
            @block.sync
            def _(sp):
                for to, src in ((w_sb[:, :, :], w_qkv.rearrange("(c p) n -> p c n", p=P)), (gp[:, :], g_pre), (wo[:, :], w_out),
                                (bo[:, :], on_all(b_out)), (go[:, :], on_all(g_out)), (mk[:, :], mem_k), (mkt[:, :], mem_k_t),
                                (mvt[:, 0:INNER1], mem_v_t)):
                    sp.dma_start(to, src).then_inc(loaded, 16)

            @block.vector
            def _(dve):
                sum_squares(nc, dve, v0, c0, xn, sq, ss)
                at0.append(inverse_norm(nc, dve, v0, c0, root0, ss, dev, rn, t))
                nc.vector.memset(kv[:, :, D:D + 1], 1.0)
                nc.vector.memset(mvt[:, INNER1:], 1.0)
                dve.wait_ge(loaded, 16 * 8)
                for c in range(2):
                    nc.vector.tensor_scalar(w_sb[:, c, :], w_sb[:, c, :], gp[:, c:c + 1], float(D) ** 0.5, ALU.mult, ALU.mult)
                nc.vector.tensor_scalar(go[:, :], go[:, :], float(D) ** 0.5, None, ALU.mult)

            @block.scalar
            def _(act):
                act.wait_ge(v0, at0[0])
                nc.scalar.activation(dev[:, :], ss[:, :], ACT.Sqrt).then_inc(root0, 1)

        def scale(n, out):
            return nc.vector.tensor_scalar(out.unsqueeze(1), xn[:, bass.ds(n, 1), :], rn[:, bass.ds(n, 1)], None, ALU.mult)

        def finish(dve, n, out, extra, step):
            nc.vector.tensor_copy(kv[:, bass.ds(n, 1), 0:D], out[:, :, INNER1:3 * INNER1])
            return nc.vector.tensor_copy(q[:, bass.ds(n, 1), :], out[:, :, 0:INNER1])
        project_rows(nc, k, "qkv1", 2, lambda c: w_sb[:, c, :], 3 * INNER1, finish, scale=scale)

        e_k = sb("e_k", [P, 2, INNER1])
        top = sb("top", [P, INNER1])
        most = sb("most", [P, 2])
        low = sb("low", [P, 1])
        diag = sb("diag", [P, P])
        tops = sb("tops", [P, INNER1])
        qm = sb("qm", [P, NB * HEADS1])
        rz = sb("rz", [P, 1])
        mix = sb("mix", [P, D])
        att, att_t = top, diag
        middle = ctx.enter_context(ExitStack())
        pt = middle.enter_context(nc.psum_tensor("mix1_pt", [P, 2, 512], f32))
        po = middle.enter_context(nc.psum_tensor("mix1_po", [P, 2, 512], f32))
        pc = middle.enter_context(nc.psum_tensor("mix1_pc", [P, 512], f32))
        v1, turned1, exp1 = sem("v1"), sem("turned1"), sem("exp1")
        c1 = Tally()
        with nc.Block() as block:
            @block.vector
            def _(dve):
                nc.vector.tensor_scalar(low[:, :], real, -LOW, LOW, ALU.mult, ALU.add).then_inc(v1, c1.one())
                dve.wait_ge(v1, c1.n)
                last = kv[:, NB - 1, 0:INNER1]
                nc.vector.tensor_scalar(last, last, real, low[:, :], ALU.mult, ALU.add).then_inc(v1, c1.one())
                dve.wait_ge(v1, c1.n)
                nc.vector.tensor_reduce(top[:, :], kv[:, :, 0:INNER1].rearrange("p b c -> p c b"), AX.X, ALU.max).then_inc(v1, c1.one())
                nc.vector.tensor_reduce(most[:, 1:2], mk[:, :], AX.X, ALU.max).then_inc(v1, c1.one())
                nc.vector.tensor_reduce(qm[:, :], heads(q[:, :, :]), AX.X, ALU.max).then_inc(v1, c1.one())
                dve.wait_ge(v1, c1.n)
                nc.vector.tensor_tensor(heads(q[:, :, :]), heads(q[:, :, :]), qm[:, :].unsqueeze(2).to_broadcast([P, NB * HEADS1, DH1]),
                                        ALU.subtract).then_inc(v1, c1.one())
                dve.wait_ge(turned1, 1)
                nc.vector.tensor_reduce(most[:, 0:1], pt[:, 0, 0:P], AX.X, ALU.max).then_inc(v1, c1.one())
                dve.wait_ge(v1, c1.n)
                nc.vector.tensor_tensor(most[:, 0:1], most[:, 0:1], most[:, 1:2], ALU.max).then_inc(v1, c1.one())
                dve.wait_ge(v1, c1.n)
                nc.vector.tensor_scalar(diag[:, :], k.ident[:, :], most[:, 0:1], None, ALU.mult).then_inc(v1, c1.one())
                dve.wait_ge(turned1, 2)
                nc.vector.tensor_copy(tops[:, :], pt[:, 1, 0:P]).then_inc(v1, c1.one())
                dve.wait_ge(v1, c1.n)
                nc.vector.tensor_tensor(mkt[:, :], mkt[:, :], tops[0:MEM, :], ALU.subtract).then_inc(v1, c1.one())
                nc.vector.tensor_tensor(kv[:, :, 0:INNER1], kv[:, :, 0:INNER1], tops[:, :].unsqueeze(1).to_broadcast([P, NB, INNER1]),
                                        ALU.subtract).then_inc(v1, c1.one())
                dve.wait_ge(exp1, 1)
                nc.vector.tensor_reduce(qm[:, :], heads(q[:, :, :]), AX.X, ALU.add).then_inc(v1, c1.one())
                dve.wait_ge(v1, c1.n)
                nc.vector.reciprocal(qm[:, :], qm[:, :])

            @block.tensor
            def _(pe):
                pe.wait_ge(v1, 3)
                nc.tensor.transpose(pt[:, 0, 0:P], top[:, :], k.ident[:, :]).then_inc(turned1, 1)
                pe.wait_ge(v1, 9)
                nc.tensor.matmul(pt[:, 1, 0:P], k.ones[:, :], diag[:, :], start=True, stop=True).then_inc(turned1, 1)

            @block.scalar
            def _(act):
                act.wait_ge(v1, 6)
                nc.scalar.activation(q[:, :, :], q[:, :, :], ACT.Exp).then_inc(exp1, 1)
                act.wait_ge(v1, 11)
                nc.scalar.activation(mkt[:, :], mkt[:, :], ACT.Exp).then_inc(exp1, 1)

        e_ready, e_used, seen2 = sem("e_ready"), sem("e_used"), sem("seen2")
        with nc.Block() as block:
            @block.scalar
            def _(act):
                def exponentiate(n, h):
                    act.wait_ge(e_used, n + 1)
                    act.sem_inc(seen2, 1)
                    nc.scalar.activation(e_k[:, h:h + 1, :], kv[:, bass.ds(n, 1), 0:INNER1], ACT.Exp).then_inc(e_ready, 1)
                paired(nc.scalar, exponentiate)

            @block.tensor
            def _(pe):
                pe.sem_inc(e_used, 2)
                nc.tensor.matmul(pc[:, 0:INNER1 + 1], mkt[:, :], mvt[:, :], start=True, stop=False)

                def multiply(n, h):
                    pe.wait_ge(e_ready, n + 1)
                    nc.tensor.matmul(pc[:, 0:INNER1 + 1], e_k[:, h, :], kv[:, bass.ds(n, 1), INNER1:D + 1].rearrange("p a d -> p (a d)"),
                                     start=False, stop=isinstance(n, int)).then_inc(e_used, 1)
                paired(nc.tensor, multiply)

        v2, made2 = sem("v2"), sem("made2")
        with nc.Block() as block:
            @block.vector
            def _(dve):
                nc.vector.memset(att[:, :], 0.0).then_inc(v2, 1)
                nc.vector.reciprocal(rz[:, :], pc[:, INNER1:INNER1 + 1]).then_inc(v2, 1)
                dve.wait_ge(v2, 2)
                nc.vector.tensor_scalar(rz[:, :], rz[:, :], DH1 ** -0.5, None, ALU.mult).then_inc(v2, 1)
                dve.wait_ge(v2, 3)
                for h in range(HEADS1):
                    s = slice(h * DH1, (h + 1) * DH1)
                    nc.vector.tensor_scalar(att[s, s], pc[s, s], rz[s, :], None, ALU.mult).then_inc(v2, 1)
                dve.wait_ge(made2, 1)
                nc.vector.tensor_copy(att_t[:, :], pt[:, 0, 0:P]).then_inc(v2, 1)
                dve.wait_ge(made2, 2)
                nc.vector.tensor_copy(mix[:, :], po[:, 0, 0:D])

            @block.tensor
            def _(pe):
                pe.wait_ge(v2, 3 + HEADS1)
                nc.tensor.transpose(pt[:, 0, 0:P], att[:, :], k.ident[:, :]).then_inc(made2, 1)
                pe.wait_ge(v2, 4 + HEADS1)
                nc.tensor.matmul(po[:, 0, 0:D], att_t[:, :], wo[:, :], start=True, stop=True).then_inc(made2, 1)

        middle.close()

        def scale_q(n, out):
            return nc.vector.tensor_tensor(out.rearrange("p (h d) -> p h d", d=DH1),
                                           q[:, bass.ds(n, 1), :].rearrange("p a (h d) -> p (a h) d", d=DH1),
                                           qm[:, bass.ds(n * HEADS1, HEADS1)].unsqueeze(2).to_broadcast([P, HEADS1, DH1]), ALU.mult)

        def finish_out(dve, n, out, extra, step):
            return nc.vector.tensor_tensor(kv[:, bass.ds(n, 1), 0:D], out, bo[:, :].unsqueeze(1), ALU.add)
        project_rows(nc, k, "out1", 1, lambda c: mix[:, :], D, finish_out, scale=scale_q)

        v4, root4, added4, stored4 = sem("v4"), sem("root4"), sem("added4"), sem("stored4")
        c4 = Tally()
        at4 = []
        with nc.Block() as block:
            @block.vector
            def _(dve):
                sum_squares(nc, dve, v4, c4, kv, sq, ss)
                at4.append(inverse_norm(nc, dve, v4, c4, root4, ss, dev, rn, t))
                for b in range(NB):
                    nc.vector.scalar_tensor_tensor(out=kv[:, b, 0:D], in0=kv[:, b, 0:D], scalar=rn[:, b:b + 1], in1=go[:, :],
                                                   op0=ALU.mult, op1=ALU.mult).then_inc(v4, c4.one())
                for g in range(NG):
                    b = slice(g * CG, (g + 1) * CG)
                    nc.vector.tensor_tensor(acc[:, b, 0:D], acc[:, b, 0:D], xn[:, b, :], ALU.add).then_inc(v4, c4.one())
                for g in range(NG):
                    b = slice(g * CG, (g + 1) * CG)
                    dve.wait_ge(v4, c4.n)
                    nc.vector.tensor_tensor(acc[:, b, 0:D], acc[:, b, 0:D], kv[:, b, 0:D], ALU.add).then_inc(added4, 1)

            @block.scalar
            def _(act):
                act.wait_ge(v4, at4[0])
                nc.scalar.activation(dev[:, :], ss[:, :], ACT.Sqrt).then_inc(root4, 1)

            @block.sync
            def _(sp):
                for g in range(NG):
                    b = slice(g * CG, (g + 1) * CG)
                    sp.wait_ge(added4, g + 1)
                    sp.dma_start(in_blocks(x_out)[:, b, :], acc[:, b, 0:D]).then_inc(stored4, 16)
                sp.wait_ge(stored4, 16 * NG)


def divide_sums(nc, dve, v, c, acc, rz, bias, heads):
    nc.vector.reciprocal(rz[:, :, :], acc[:, :, D:D + heads]).then_inc(v, c.one())
    dve.wait_ge(v, c.n)
    for q in range(heads):
        s = slice(q * (D // heads), (q + 1) * (D // heads))
        nc.vector.tensor_tensor(acc[:, :, s], acc[:, :, s], rz[:, :, q:q + 1].to_broadcast([P, NB, D // heads]), ALU.mult).then_inc(v, c.one())
    dve.wait_ge(v, c.n)
    nc.vector.tensor_tensor(acc[:, :, 0:D], acc[:, :, 0:D], bias[:, :].unsqueeze(1).to_broadcast([P, NB, D]), ALU.add).then_inc(v, c.one())
    dve.wait_ge(v, c.n)


def stage_gat_norm(nc, k, acc, xn, bias, gamma, beta):
    with ExitStack() as ctx:
        sb, ps, sem = allocators(nc, ctx, "gnorm")
        rz = sb("rz", [P, NB, HEADS1])
        bi, ga, be = sb("bi", [P, D]), sb("ga", [P, D]), sb("be", [P, D])
        part = sb("part", [P, D])
        mean = sb("mean", [P, D])
        var, dev, rstd, t = sb("var", [P, D]), sb("dev", [P, D]), sb("rstd", [P, D]), sb("t", [P, D])
        pm = ps("pm", [P, 2, 512])
        loaded, v, squared, summed, rooted, exped = (sem(n) for n in ("loaded", "v", "squared", "summed", "rooted", "exped"))
        real = k.before[:, LASTROWS:LASTROWS + 1]
        c = Tally()
        at = {}
        a = acc[:, :, 0:D]
        wide = lambda r: r[:, :].unsqueeze(1).to_broadcast([P, NB, D])
        with nc.Block() as block:
            @block.sync
            def _(sp):
                for to, src in ((bi, bias), (ga, gamma), (be, beta)):
                    sp.dma_start(to[:, :], on_all(src)).then_inc(loaded, 16)

            @block.vector
            def _(dve):
                dve.wait_ge(loaded, 48)
                divide_sums(nc, dve, v, c, acc, rz, bi, HEADS1)

                def clear_padding():
                    nc.vector.tensor_scalar(acc[:, NB - 1, 0:D], acc[:, NB - 1, 0:D], real, None, ALU.mult).then_inc(v, c.one())
                    dve.wait_ge(v, c.n)
                clear_padding()
                nc.vector.tensor_reduce(part[:, :], a.rearrange("p b d -> p d b"), AX.X, ALU.add).then_inc(v, c.one())
                at["sum"] = c.n
                dve.wait_ge(summed, 1)
                nc.vector.tensor_scalar(mean[:, :], pm[:, 0, 0:D], 1.0 / NODES, None, ALU.mult).then_inc(v, c.one())
                dve.wait_ge(v, c.n)
                nc.vector.tensor_tensor(a, a, wide(mean), ALU.subtract).then_inc(v, c.one())
                dve.wait_ge(v, c.n)
                clear_padding()
                at["square"] = c.n
                dve.wait_ge(squared, 1)
                nc.vector.tensor_reduce(part[:, :], xn[:, :, :].rearrange("p b d -> p d b"), AX.X, ALU.add).then_inc(v, c.one())
                at["sum2"] = c.n
                dve.wait_ge(summed, 2)
                nc.vector.tensor_scalar(var[:, :], pm[:, 1, 0:D], 1.0 / NODES, 1e-5, ALU.mult, ALU.add).then_inc(v, c.one())
                at["root"] = c.n
                dve.wait_ge(rooted, 1)
                nc.vector.reciprocal(rstd[:, :], dev[:, :]).then_inc(v, c.one())
                dve.wait_ge(v, c.n)
                sharpen_inverse_root(nc, dve, v, c.n, var[:, :], rstd[:, :], t[:, :])
                c.n += 4
                nc.vector.tensor_tensor(rstd[:, :], rstd[:, :], ga[:, :], ALU.mult).then_inc(v, c.one())
                dve.wait_ge(v, c.n)
                nc.vector.tensor_tensor(a, a, wide(rstd), ALU.mult).then_inc(v, c.one())
                dve.wait_ge(v, c.n)
                nc.vector.tensor_tensor(a, a, wide(be), ALU.add).then_inc(v, c.one())
                dve.wait_ge(v, c.n)
                nc.vector.tensor_scalar(xn[:, :, :], a, 0.0, None, ALU.min).then_inc(v, c.one())
                at["exp"] = c.n
                nc.vector.tensor_scalar(a, a, 0.0, None, ALU.max).then_inc(v, c.one())
                dve.wait_ge(v, c.n)
                dve.wait_ge(exped, 1)
                nc.vector.scalar_tensor_tensor(out=xn[:, :, :], in0=xn[:, :, :], scalar=-1.0, in1=a, op0=ALU.add, op1=ALU.add)

            @block.tensor
            def _(pe):
                pe.wait_ge(v, at["sum"])
                nc.tensor.matmul(pm[:, 0, 0:D], k.ones[:, :], part[:, :], start=True, stop=True).then_inc(summed, 1)
                pe.wait_ge(v, at["sum2"])
                nc.tensor.matmul(pm[:, 1, 0:D], k.ones[:, :], part[:, :], start=True, stop=True).then_inc(summed, 1)

            @block.scalar
            def _(act):
                act.wait_ge(v, at["square"])
                nc.scalar.activation(xn[:, :, :], a, ACT.Square).then_inc(squared, 1)
                act.wait_ge(v, at["root"])
                nc.scalar.activation(dev[:, :], var[:, :], ACT.Sqrt).then_inc(rooted, 1)
                act.wait_ge(v, at["exp"])
                nc.scalar.activation(xn[:, :, :], xn[:, :, :], ACT.Exp).then_inc(exped, 1)


def stage_gat_out(nc, k, acc, bias, x_in, xin):
    with ExitStack() as ctx:
        sb, ps, sem = allocators(nc, ctx, "gout")
        rz = sb("rz", [P, NB, 1])
        bi = sb("bi", [P, D])
        sq = sb("sq", [P, CG, D])
        ss, dev, rn, t = sb("ss", [P, NB]), sb("dev", [P, NB]), sb("rn", [P, NB]), sb("t", [P, NB])
        loaded, v, rooted = sem("loaded"), sem("v"), sem("rooted")
        c = Tally()
        at = []
        with nc.Block() as block:
            @block.sync
            def _(sp):
                sp.dma_start(bi[:, :], on_all(bias)).then_inc(loaded, 16)
                sp.dma_start(xin[:, :, :], in_blocks(x_in)).then_inc(loaded, 16)

            @block.vector
            def _(dve):
                dve.wait_ge(loaded, 32)
                divide_sums(nc, dve, v, c, acc, rz, bi, 1)
                sum_squares(nc, dve, v, c, acc, sq, ss)
                at.append(inverse_norm(nc, dve, v, c, rooted, ss, dev, rn, t))
                for b in range(NB):
                    nc.vector.scalar_tensor_tensor(out=acc[:, b, 0:D], in0=acc[:, b, 0:D], scalar=rn[:, b:b + 1], in1=xin[:, b, :],
                                                   op0=ALU.mult, op1=ALU.add)

            @block.scalar
            def _(act):
                act.wait_ge(v, at[0])
                nc.scalar.activation(dev[:, :], ss[:, :], ACT.Sqrt).then_inc(rooted, 1)


GB = 7
HALFTOK = GB * P // 2
SLOT_BLOCKS = NB + EXPERTS - 1
SLOT_GROUPS = -(-SLOT_BLOCKS // GB)
assert SLOT_GROUPS * GB * P <= EXPERTS * CAPPAD


def stage_ffn1(nc, k, name, groups, rows, w1, b1, wg=None, bg=None, logits=None,
               wd=None, bd=None, block_expert=None, out=None):
    WIDTH = EXPERTS if wg is not None else D
    with ExitStack() as ctx:
        sb, ps, sem = allocators(nc, ctx, name)
        w1_sb = sb("w1", [P, 2, HID])
        b1_sb = sb("b1", [P, FC])
        x_sb = sb("x", [P, 2, GB, D])
        xt = sb("xt", [P, 2, GB * P])
        ht = sb("ht", [P, FC, GB * P])
        if wg is not None:
            wg_sb = sb("wg", [P, FC, EXPERTS])
            bg_sb = sb("bg", [P, EXPERTS])
        else:
            wd_sb = sb("wd", [P, EXPERTS, FC * D])
            bd_sb = sb("bd", [P, EXPERTS, D])
            y_sb = sb("y", [P, GB, D])
        pt = ps("pt", [P, 2, 512])
        ph = [ps(f"ph{j}", [P, 512]) for j in range(4)]
        py = [ps(f"py{j}", [P, 512]) for j in range(2)]
        wloaded = sem("wloaded")
        dloaded = sem("dloaded")
        loaded = [sem("loaded0"), sem("loaded1")]
        stored = sem("stored")
        turned = sem("turned")
        copied = sem("copied")
        h_made = sem("h_made")
        active = sem("active")
        y_made = sem("y_made")
        evacuated = sem("evacuated")
        y_free = sem("y_free")
        DLOADS = 2 if wg is not None else 1 + EXPERTS

        with nc.Block() as block:
            @block.sync
            def _(sp):
                sp.dma_start(w1_sb[:, :, :], w1.rearrange("(c p) n -> p c n", p=P)).then_inc(wloaded, 16)
                sp.dma_start(b1_sb[:, :], b1).then_inc(wloaded, 16)

                def load(n, h):
                    sp.wait_ge(turned, GB * n + GB)
                    sp.dma_start(x_sb[:, h, :, :], rows[:, bass.ds(GB * n, GB), :]).then_inc(loaded[h], 16)
                in_pairs(nc.sync, groups, load)

            @block.gpsimd
            def _(pool):
                if wg is not None:
                    pool.dma_start(wg_sb[:, :, :], wg.rearrange("(f p) e -> p f e", p=P)).then_inc(dloaded, 16)
                    pool.dma_start(bg_sb[:, :], on_all(bg)).then_inc(dloaded, 16)
                    return
                pool.dma_start(bd_sb[:, :, :], bd.rearrange("e (a n) -> a e n", a=1).to_broadcast([P, EXPERTS, D])).then_inc(dloaded, 16)
                for e in range(EXPERTS):
                    pool.dma_start(wd_sb[:, e, :].rearrange("p (f n) -> p f n", n=D),
                                   wd[e].rearrange("(f p) n -> p f n", p=P)).then_inc(dloaded, 16)

                pool.sem_inc(y_free, 1)

                def store(n, h):
                    pool.wait_ge(evacuated, GB * n + GB + 2)
                    pool.dma_start(out[:, bass.ds(GB * n, GB), :], y_sb[:, :, :]).then_inc(stored, 16)
                    pool.wait_ge(stored, 16 * n + 16)
                    pool.sem_inc(y_free, 1)
                in_pairs(nc.gpsimd, groups, store)

            @block.tensor
            def _(pe):
                pe.sem_inc(turned, 2 * GB)
                pe.wait_ge(wloaded, 32)
                pe.wait_ge(dloaded, 16 * DLOADS)

                def group(n, h):
                    pe.wait_ge(loaded[h], 16 * half_index(n, h))
                    for t in range(GB):
                        pe.wait_ge(copied, GB * n + t + 1)
                        for c in range(2):
                            last = nc.tensor.transpose(pt[:, (t + h) % 2, c * P:(c + 1) * P],
                                                       x_sb[:, h, t, c * P:(c + 1) * P], k.ident[:, :])
                        last.then_inc(turned, 1)
                    if wd is not None:
                        _, experts = nc.values_load_multi_w_load_instructions(
                            block_expert[0:1, bass.ds(GB * n, GB)], engines=(mybir.EngineType.PE,), min_val=0, max_val=EXPERTS - 1,
                            skip_runtime_bounds_check_because="a block's expert counts experts before the last")
                    for half in range(2):
                        pe.wait_ge(copied, GB * n + (GB + 1) // 2 * (1 - half) + GB * half + 2)
                        for f in range(FC):
                            pe.wait_ge(active, 2 * FC * n + FC * half + f + 1)
                            for c in range(2):
                                last = nc.tensor.matmul(ph[f % 4][:, 0:HALFTOK], w1_sb[:, c, f * P:(f + 1) * P],
                                                        xt[:, c, half * HALFTOK:(half + 1) * HALFTOK], start=(c == 0), stop=(c == 1))
                            last.then_inc(h_made, 1)
                    for t in range(GB):
                        if t == 0:
                            pe.wait_ge(active, 2 * FC * n + FC + 4)
                        if t == GB // 2:
                            pe.wait_ge(active, 2 * FC * n + 2 * FC + 4)
                        pe.wait_ge(evacuated, GB * n + t + 1)
                        for f in range(FC):
                            rhs = wg_sb[:, f, :] if wg is not None else \
                                wd_sb[:, bass.ds(experts[t], 1), f * D:(f + 1) * D].rearrange("p a d -> p (a d)")
                            last = nc.tensor.matmul(py[(t + h) % 2][:, 0:WIDTH], ht[:, f, t * P:(t + 1) * P], rhs,
                                                    start=(f == 0), stop=(f == FC - 1))
                        last.then_inc(y_made, 1)
                in_pairs(nc.tensor, groups, group)

            @block.scalar
            def _(act):
                act.sem_inc(active, 4)
                act.wait_ge(wloaded, 32)

                def activate(n, h):
                    for half in range(2):
                        for f in range(FC):
                            act.wait_ge(h_made, 2 * FC * n + FC * half + f + 1)
                            nc.scalar.activation(ht[:, f, half * HALFTOK:(half + 1) * HALFTOK], ph[f % 4][:, 0:HALFTOK], ACT.Gelu,
                                                 bias=b1_sb[:, f:f + 1]).then_inc(active, 1)
                in_pairs(nc.scalar, groups, activate)

            @block.vector
            def _(dve):
                dve.sem_inc(copied, 2)
                dve.sem_inc(evacuated, 2)
                dve.wait_ge(dloaded, 16 * DLOADS)

                def group(n, h):
                    if wd is not None:
                        _, experts = nc.values_load_multi_w_load_instructions(
                            block_expert[0:1, bass.ds(GB * n, GB)], engines=(mybir.EngineType.DVE,), min_val=0, max_val=EXPERTS - 1,
                            skip_runtime_bounds_check_because="a block's expert counts experts before the last")
                    for t in range(GB):
                        dve.wait_ge(turned, GB * n + 2 * GB + t + 1)
                        nc.vector.tensor_copy(xt[:, :, t * P:(t + 1) * P],
                                              pt[:, (t + h) % 2, 0:D].rearrange("p (c n) -> p c n", c=2)).then_inc(copied, 1)
                    if wd is not None:
                        dve.wait_ge(y_free, n + 1)
                    for t in range(GB):
                        dve.wait_ge(y_made, GB * n + t + 1)
                        y = py[(t + h) % 2]
                        if wd is not None:
                            nc.vector.tensor_tensor(y_sb[:, t:t + 1, :], y[:, 0:D].unsqueeze(1), bd_sb[:, bass.ds(experts[t], 1), :],
                                                    ALU.add).then_inc(evacuated, 1)
                        else:
                            nc.vector.tensor_tensor(logits[:, bass.ds(GB * n + t, 1), :], y[:, 0:EXPERTS].unsqueeze(1),
                                                    bg_sb[:, :].unsqueeze(1), ALU.add).then_inc(evacuated, 1)
                in_pairs(nc.vector, groups, group)


def stage_clear(nc, k, tables):
    WIDE = max(t.shape[0] * t.shape[1] // P for t in tables)
    with ExitStack() as ctx:
        sb, ps, sem = allocators(nc, ctx, "clear")
        zeros = sb("zeros", [P, WIDE])
        zeroed, stored = sem("zeroed"), sem("stored")
        with nc.Block() as block:
            @block.vector
            def _(dve):
                nc.vector.memset(zeros[:, :], 0.0).then_inc(zeroed, 1)
                nc.vector.memset(k.dots[:, :, :], 0.0)

            @block.sync
            def _(sp):
                sp.wait_ge(zeroed, 1)
                for t in tables:
                    sp.dma_start(t.rearrange("(p a) d -> p (a d)", p=P), zeros[:, 0:t.shape[0] * t.shape[1] // P]).then_inc(stored, 16)
                sp.wait_ge(stored, 16 * len(tables))


def gps_two_layers(nc, a, out):
    dram = lambda n, s: nc.dram_tensor(n, s, f32).ap()
    table = [dram(f"table{j}", [NPAD, D]) for j in range(4)]
    slots = dram("slots", [EXPERTS * CAPPAD, D])
    expert_out = dram("expert_out", [EXPERTS * CAPPAD, D])
    x2 = dram("x2", [NPAD, D])
    gat = [(dram(f"run{j}", [EPAD, h]), dram(f"node{j}", [EPAD, 2 * h]), dram(f"p{j}", [EROWS * P, h]))
           for j, h in enumerate((HEADS1, 1))]
    edge_rows = lambda flat: flat.rearrange("(r l) -> r l", l=P)

    with ExitStack() as ctx:
        sb = lambda c, n, s, t=f32: c.enter_context(nc.sbuf_tensor(n, s, t))
        k = Kept(nc, ctx)
        stage_prepare(nc, k, edge_rows(a["src"]), edge_rows(a["dst"]), edge_rows(a["edge_weight"]))
        acc = sb(ctx, "acc", [P, NB, D + HEADS1])
        esd = [sb(ctx, f"esd{j}", [P, NB, 2 * h]) for j, h in enumerate((HEADS1, 1))]

        with ExitStack() as c:
            xn = sb(c, "xn", [P, NB, D])
            with ExitStack() as c0:
                k.dots = sb(c0, "dots", [P, 4, P])
                k.mix = sb(c0, "mix", [P, 2, D])
                with ExitStack() as cc:
                    stage_clear(nc, k, [slots[e * CAPPAD:(e + 1) * CAPPAD, :] for e in range(EXPERTS)] +
                                [g[1] for g in gat] + [g[2][EPAD:, :] for g in gat])
                stage_layernorm(nc, k, "norm0", acc, xn, a["x"])
                stage_scale_store(nc, k, "self0", xn, k.dinv, acc, table[0])
                stage_aggregate(nc, k, "conv0", table[0], acc, D, k.weight, side=Mix0Side(xn, a["L0_mix_Wqkv_t"][:, INNER0:3 * INNER0]))
                stage_mix0_fold(nc, k, a["L0_mix_Wqkv"][0:INNER0, :], a["L0_mix_Wout_t"])
                stage_gcn_dense(nc, k, "dense0", acc, a["L0_gnn_W1"], a["L0_gnn_b1"], table=table[1])
                stage_aggregate(nc, k, "conv1", table[1], acc, D, k.weight)
                stage_gcn_dense(nc, k, "dense1", acc, a["L0_gnn_W2"], a["L0_gnn_b2"], xn=xn, x_in=a["x"], bias2=a["L0_mix_bout"])
            with ExitStack() as c1:
                logits = sb(c1, "logits0", [P, NB, EXPERTS])
                prob = sb(c1, "prob0", [P, NB])
                to_slot, from_slot = sb(c1, "to_slot0", [P, NB], i32), sb(c1, "from_slot0", [P, NB], i32)
                stage_layernorm(nc, k, "norm1", acc, xn)
                stage_gate(nc, k, xn, a["L0_ffn_gate_w"], a["L0_ffn_gate_b"], logits)
                stage_route(nc, k, "route0", logits, prob, to_slot, from_slot, capacity=CAP)
                stage_dispatch(nc, k, "send0", xn, to_slot, slots)
                stage_experts0(nc, k, slots, a["L0_ffn_w1"], a["L0_ffn_b1"], a["L0_ffn_w2"], a["L0_ffn_b2"], expert_out, xn)
                stage_combine(nc, k, "combine0", expert_out, from_slot, acc, prob, True)
            stage_layernorm(nc, k, "norm2", acc, xn)
            stage_mix1(nc, k, xn, acc, a["L1_mix_w_qkv"], a["L1_mix_g_pre"], a["mem_k"], a["mem_k_t"], a["mem_v_t"],
                       a["L1_mix_w_out"], a["L1_mix_b_out"], a["L1_mix_g_out"], x2)
            stage_gat_project(nc, k, "project0", xn, a["L1_gnn_W0"], a["L1_gnn_W0_t"], a["L1_gnn_a_src0"], a["L1_gnn_a_dst0"],
                              HEADS1, acc, esd[0], table[2])

        def attend(j, heads):
            with ExitStack() as c:
                weights = sb(c, f"weights{j}", [P, SPAD * heads])
                p_self = sb(c, f"p_self{j}", [P, NB, heads])
                stage_gat_weights(nc, k, f"soft{j}", heads, esd[j], a["src"], a["dst"], a["last_dst"], *gat[j], weights, p_self)
                stage_gat_self(nc, k, f"own{j}", heads, acc, p_self)
                stage_aggregate(nc, k, f"attend{j}", table[2 + j], acc, D + heads, weights, heads=heads if heads > 1 else 0)
        attend(0, HEADS1)
        with ExitStack() as c:
            xn = sb(c, "h1", [P, NB, D])
            stage_gat_norm(nc, k, acc, xn, a["L1_gnn_b0"], a["L1_gnn_gamma0"], a["L1_gnn_beta0"])
            stage_gat_project(nc, k, "project1", xn, a["L1_gnn_W1"], a["L1_gnn_W1_t"], a["L1_gnn_a_src1"], a["L1_gnn_a_dst1"],
                              1, acc, esd[1], table[3])
        attend(1, 1)

        prob = sb(ctx, "prob1", [P, NB])
        from_slot = sb(ctx, "from_slot1", [P, NB], i32)
        block_expert = sb(ctx, "block_expert", [1, P], i32)
        with ExitStack() as c:
            xn = sb(c, "xn1", [P, NB, D])
            logits = sb(c, "logits1", [P, NB, EXPERTS])
            to_slot = sb(c, "to_slot1", [P, NB], i32)
            stage_gat_out(nc, k, acc, a["L1_gnn_b1"], x2, xn)
            stage_layernorm(nc, k, "norm3", acc, xn)
            stage_ffn1(nc, k, "gate1", NG, xn, a["L1_ffn_W1"], a["L1_ffn_b1"], wg=a["L1_ffn_Wg"], bg=a["L1_ffn_bg"], logits=logits)
            stage_route(nc, k, "route1", logits, prob, to_slot, from_slot, block_expert=block_expert)
            stage_dispatch(nc, k, "send1", xn, to_slot, slots)
        stage_ffn1(nc, k, "experts1", SLOT_GROUPS, in_blocks(slots), a["L1_ffn_W1"], a["L1_ffn_b1"],
                   wd=a["L1_ffn_Wd"], bd=a["L1_ffn_bd"], block_expert=block_expert, out=in_blocks(expert_out))
        stage_combine(nc, k, "combine1", expert_out, from_slot, acc, prob, False, x_out=out)


def kernel(**inputs):
    import concourse.bacc as _bacc
    from concourse.bass_utils import run_bass_kernel_spmd as _run

    arr = {n: np.ascontiguousarray(v) for n, v in inputs.items() if n != "L1_mix_t"}
    turned = lambda v: np.ascontiguousarray(v.T)
    mem = arr.pop("L1_mix_mem_kv")
    dst = arr.pop("dst").astype(np.int32, copy=False)
    src = arr.pop("src").astype(np.int32, copy=False)
    tail = EROWS * P - EDGES
    arr["x"] = np.concatenate([arr["x"], np.zeros((NPAD - NODES, D), arr["x"].dtype)])
    arr["src"] = np.concatenate([src, np.zeros(tail, np.int32)])
    arr["dst"] = np.concatenate([dst, np.full(tail, NODES, np.int32)])
    arr["last_dst"] = np.concatenate([np.full(1, -1, np.int32), arr["dst"][:-1]])
    arr["edge_weight"] = np.concatenate([arr["edge_weight"], np.zeros(tail, arr["edge_weight"].dtype)])
    for n in ("L0_mix_Wqkv", "L1_gnn_W0", "L1_gnn_W1"):
        arr[n + "_t"] = turned(arr[n])
    arr["L0_mix_Wout_t"] = turned(arr.pop("L0_mix_Wout"))
    arr["L0_ffn_b1"] = np.ascontiguousarray(arr["L0_ffn_b1"].reshape(EXPERTS, FC, P).transpose(0, 2, 1))
    arr["L1_ffn_b1"] = turned(arr["L1_ffn_b1"].reshape(FC, P))
    arr["L1_mix_g_pre"] = turned(arr["L1_mix_g_pre"].reshape(2, P))
    arr["mem_k"] = np.ascontiguousarray(mem[0].reshape(INNER1, MEM))
    arr["mem_k_t"] = turned(arr["mem_k"])
    arr["mem_v_t"] = turned(mem[1].reshape(INNER1, MEM))

    nc = _bacc.Bacc("TRN2", target_bir_lowering=False, num_devices=1)
    aps = {n: nc.dram_tensor("in_" + n, v.shape, mybir.dt.from_np(v.dtype), kind="ExternalInput").ap() for n, v in arr.items()}
    out = nc.dram_tensor("out", (NPAD, D), f32, kind="ExternalOutput").ap()
    gps_two_layers(nc, aps, out)
    r = _run(nc, [{"in_" + n: v for n, v in arr.items()}], core_ids=[0])
    return r.results[0]["out"][:NODES]
```

```python
import numpy as np
from contextlib import ExitStack
import concourse.bass as bass
from concourse import mybir

f32 = mybir.dt.float32
i32 = mybir.dt.int32
bf16 = mybir.dt.bfloat16
ALU = mybir.AluOpType
ACT = mybir.ActivationFunctionType
AX = mybir.AxisListType

P = 128
NODES = 6250
D = 256
NB = -(-NODES // P)
NPAD = NB * P
LASTROWS = NODES - (NB - 1) * P
EDGES = 100000
ET = -(-EDGES // P)
EG = -(-ET // P)
STEPS = ET + NB - 1
SG = -(-STEPS // P)
SPAD = SG * P
CG = 7
NG = NB // CG


class Kept:

    def __init__(self, nc, ctx):
        sb = lambda n, s, t=f32: ctx.enter_context(nc.sbuf_tensor(n, s, t))
        self.ident = sb("ident", [P, P])
        self.before = sb("before", [P, P])
        self.ones = sb("ones", [P, P])
        self.iota = sb("iota", [P, P])
        self.row_start = sb("row_start", [P, NB], i32)
        self.row_count = sb("row_count", [P, NB], i32)
        self.dinv = sb("dinv", [P, NB])
        self.src_idx = sb("src_idx", [P, SPAD], i32)
        self.lane = sb("lane", [P, SPAD])
        self.weight = sb("weight", [P, SPAD])
        self.step_blk = sb("step_blk", [P, SPAD], i32)
        self.tile_idx = sb("tile_idx", [P, SG], i32)


class Tally:

    def __init__(self):
        self.n = 0

    def one(self):
        self.n += 1
        return 1


def allocators(nc, ctx, stage):
    sems = []

    def clear():
        nc.clear_and_free_semaphores(sems)
        nc.all_engine_barrier()

    def sem(n):
        sems.append(nc.alloc_semaphore(name=f"{stage}_{n}"))
        return sems[-1]

    ctx.callback(clear)
    sb = lambda n, s, t=f32: ctx.enter_context(nc.sbuf_tensor(f"{stage}_{n}", s, t))
    ps = lambda n, s, t=f32: ctx.enter_context(nc.psum_tensor(f"{stage}_{n}", s, t))
    return sb, ps, sem


def stage_prepare(nc, k, src_rows, dst_rows, w_rows, more_loads=None):
    T = 17
    assert ET % (2 * T) == 0
    with ExitStack() as ctx:
        sb, ps, sem = allocators(nc, ctx, "prep")
        iota_i = sb("iota_i", [P, P], i32)
        iota_sf = sb("iota_sf", [P, SPAD])
        iota_si = sb("iota_si", [P, SPAD], i32)
        tile_i = sb("tile_i", [P, EG], i32)
        tile_f = sb("tile_f", [P, EG])
        dst_r = sb("dst_r", [P, EG, P], i32)
        w_r = sb("w_r", [P, EG, P])
        dst_rf = sb("dst_rf", [P, EG, P])
        last_i = sb("last_i", [P, EG], i32)
        last_f = sb("last_f", [P, EG])
        key = sb("key", [P, EG])
        dst_t = sb("dst_t", [P, EG * P], i32)
        blk_ti = sb("blk_ti", [P, EG * P], i32)
        lane_ti = sb("lane_ti", [P, EG * P], i32)
        blk_t = sb("blk_t", [P, EG * P])
        lane_t = sb("lane_t", [P, EG * P])
        w_t = sb("w_t", [P, EG * P])
        lane_hot = sb("lane_hot", [P, 2, T, P])
        blk_hot = sb("blk_hot", [P, 2, T, 2, NB])
        cmp = sb("cmp", [P, 2, SPAD])
        counts = sb("counts", [P, 2 * NB])
        deg = sb("deg", [P, NB])
        pos = sb("pos", [P, NB])
        rdeg = sb("rdeg", [P, NB])
        totals = sb("totals", [P, NB])
        base = sb("base", [P, NB])
        zero = sb("zero", [P, NB])
        start_f = sb("start_f", [P, NB])
        step_tile = sb("step_tile", [P, SPAD])
        step_blk = sb("step_blk", [P, SPAD])
        diag = sb("diag", [P, SG, P])
        tile_col = sb("tile_col", [P, SG])
        got_src = sb("got_src", [P, SG, P], i32)
        got_dst = sb("got_dst", [P, SG, P], i32)
        got_w = sb("got_w", [P, SG, P])
        got_srcf = sb("got_srcf", [P, SG, P])
        got_dstf = sb("got_dstf", [P, SG, P])
        psA = ps("psA", [P, 2, 512])
        psB = ps("psB", [P, 2, 512])
        psC = ps("psC", [P, 512])
        psD = ps("psD", [P, 2, 512])
        loaded = sem("loaded")
        pool_done = sem("pool_done")
        v = sem("v_prep")
        turned = sem("turned")
        hot = sem("hot")
        hot_a = sem("hot_a")
        hot_prep = sem("hot_prep")
        counted = sem("counted")
        totalled = sem("totalled")
        compared = sem("compared")
        stepped = sem("stepped")
        gathered = sem("gathered")
        turned2 = sem("turned2")

        with nc.Block() as block:
            @block.sync
            def _(sp):
                sp.dma_start(dst_r[:, :, :], dst_rows.rearrange("(g r) l -> r g l", r=P)).then_inc(loaded, 16)
                sp.dma_start(w_r[:, :, :], w_rows.rearrange("(g r) l -> r g l", r=P)).then_inc(loaded, 16)
                if more_loads:
                    more_loads(sp)

            @block.gpsimd
            def _(pool):
                nc.gpsimd.iota(iota_i[:, :], pattern=[[1, P]], base=0, channel_multiplier=0).then_inc(pool_done, 1)
                nc.gpsimd.iota(iota_si[:, :], pattern=[[1, SPAD]], base=0, channel_multiplier=0).then_inc(pool_done, 1)
                nc.gpsimd.iota(tile_i[:, :], pattern=[[P, EG]], base=0, channel_multiplier=1).then_inc(pool_done, 1)
                nc.gpsimd.memset(k.ones[:, :], 1.0).then_inc(pool_done, 1)
                nc.gpsimd.memset(k.ident[:, :], 0.0).then_inc(pool_done, 1)
                pool.wait_ge(pool_done, 5)
                nc.gpsimd.affine_select(out=k.ident[:, :], in_=k.ident[:, :], compare_op=ALU.not_equal, fill=1.0,
                                        base=0, pattern=[[-1, P]], channel_multiplier=1).then_inc(pool_done, 1)
                nc.gpsimd.affine_select(out=k.before[:, :], in_=k.ones[:, :], compare_op=ALU.is_gt, fill=0.0,
                                        base=0, pattern=[[1, P]], channel_multiplier=-1).then_inc(pool_done, 1)
                pool.wait_ge(stepped, 1)
                for g in range(SG):
                    idx = bass.IndirectOffsetOnAxis(ap=k.tile_idx[:, g:g + 1], axis=0)
                    for to, rows in ((got_src, src_rows), (got_dst, dst_rows), (got_w, w_rows)):
                        nc.gpsimd.indirect_dma_start(out=to[:, g, :], out_offset=None, in_=rows,
                                                     in_offset=idx).then_inc(gathered, 16)
                pool.wait_ge(gathered, 16 * 3 * SG)

            @block.tensor
            def _(pe):
                pe.wait_ge(pool_done, 7)
                pe.wait_ge(loaded, 32)
                pe.wait_ge(v, 4)
                for g in range(EG):
                    nc.tensor.transpose(psA[:, g // 4, g % 4 * P:(g % 4 + 1) * P], dst_rf[:, g, :], k.ident[:, :])
                    last = nc.tensor.transpose(psB[:, g // 4, g % 4 * P:(g % 4 + 1) * P], w_r[:, g, :], k.ident[:, :])
                last.then_inc(turned, 1)
                pe.wait_ge(v, 8)
                nc.tensor.matmul(psC[:, 0:2 * NB], k.ident[:, :], counts[:, :], start=True, stop=False)
                with nc.tensor.Fori(0, ET // T // 2) as i:
                    for h in range(2):
                        pe.wait_ge(hot, 2 * i + h + 1)
                        for t in range(T):
                            last = nc.tensor.matmul(psC[:, 0:2 * NB], lane_hot[:, h, t, :],
                                                    blk_hot[:, h, t, :, :].rearrange("p a b -> p (a b)"),
                                                    start=False, stop=False)
                        last.then_inc(counted, 1)
                nc.tensor.matmul(psC[:, 0:2 * NB], k.ident[:, :], counts[:, :], start=False, stop=True).then_inc(counted, 1)
                pe.wait_ge(v, 9)
                nc.tensor.matmul(psA[:, 0, 0:NB], k.before[:, :], counts[:, 0:NB], start=True, stop=True)
                nc.tensor.matmul(psA[:, 1, 0:NB], k.ones[:, :], counts[:, 0:NB], start=True, stop=True).then_inc(totalled, 1)
                for g in range(EG):
                    pe.wait_ge(compared, g + 1)
                    for h in range(2):
                        last = nc.tensor.matmul(psD[:, h, 0:SPAD // 2], k.ones[:, :],
                                                cmp[:, g % 2, h * (SPAD // 2):(h + 1) * (SPAD // 2)],
                                                start=(g == 0), stop=(g == EG - 1))
                    last.then_inc(totalled, 1)
                pe.wait_ge(turned2, 1)
                for g in range(SG):
                    nc.tensor.transpose(psA[:, g // 4, g % 4 * P:(g % 4 + 1) * P], got_srcf[:, g, :], k.ident[:, :])
                    nc.tensor.transpose(psB[:, g // 4, g % 4 * P:(g % 4 + 1) * P], got_dstf[:, g, :], k.ident[:, :])
                    last = nc.tensor.transpose(psD[:, g // 4, g % 4 * P:(g % 4 + 1) * P], got_w[:, g, :], k.ident[:, :])
                last.then_inc(turned2, 1)

            @block.vector
            def _(dve):
                dve.wait_ge(pool_done, 3)
                dve.wait_ge(loaded, 32)
                nc.vector.tensor_copy(k.iota[:, :], iota_i[:, :]).then_inc(v, 1)
                nc.vector.tensor_copy(iota_sf[:, :], iota_si[:, :]).then_inc(v, 1)
                nc.vector.tensor_copy(tile_f[:, :], tile_i[:, :]).then_inc(v, 1)
                nc.vector.tensor_copy(dst_rf[:, :, :], dst_r[:, :, :]).then_inc(v, 1)
                nc.vector.tensor_single_scalar(last_i[:, :], dst_r[:, :, P - 1], 7, op=ALU.arith_shift_right).then_inc(v, 1)
                nc.vector.memset(counts[:, :], 0.0).then_inc(v, 1)
                dve.wait_ge(v, 5)
                nc.vector.tensor_copy(last_f[:, :], last_i[:, :]).then_inc(v, 1)
                dve.wait_ge(v, 7)
                nc.vector.tensor_tensor(key[:, :], last_f[:, :], tile_f[:, :], ALU.add).then_inc(v, 1)
                dve.wait_ge(turned, 1)
                for h in range(2):
                    w = 512 if h == 0 else EG * P - 512
                    nc.vector.tensor_copy(dst_t[:, h * 512:h * 512 + w], psA[:, h, 0:w]).then_inc(hot_prep, 1)
                    nc.vector.tensor_copy(w_t[:, h * 512:h * 512 + w], psB[:, h, 0:w]).then_inc(hot_prep, 1)
                dve.wait_ge(hot_prep, 4)
                nc.vector.tensor_single_scalar(blk_ti[:, :], dst_t[:, :], 7, op=ALU.arith_shift_right).then_inc(hot_prep, 1)
                nc.vector.tensor_single_scalar(lane_ti[:, :], dst_t[:, :], P - 1, op=ALU.bitwise_and).then_inc(hot_prep, 1)
                dve.wait_ge(hot_prep, 6)
                nc.vector.tensor_copy(blk_t[:, :], blk_ti[:, :]).then_inc(hot_prep, 1)
                nc.vector.tensor_copy(lane_t[:, :], lane_ti[:, :]).then_inc(hot_prep, 1)
                dve.wait_ge(hot_prep, 8)

                def make_hot(t0, h):
                    nc.vector.tensor_tensor(lane_hot[:, h, :, :], k.iota[:, :].unsqueeze(1).to_broadcast([P, T, P]),
                                            lane_t[:, bass.ds(t0, T)].unsqueeze(2).to_broadcast([P, T, P]), ALU.is_equal).then_inc(hot_a, 1)
                    nc.vector.tensor_tensor(blk_hot[:, h, :, 0, :], k.iota[:, 0:NB].unsqueeze(1).to_broadcast([P, T, NB]),
                                            blk_t[:, bass.ds(t0, T)].unsqueeze(2).to_broadcast([P, T, NB]), ALU.is_equal).then_inc(hot_a, 1)

                def weigh_hot(t0, h):
                    nc.vector.tensor_tensor(blk_hot[:, h, :, 1, :], blk_hot[:, h, :, 0, :],
                                            w_t[:, bass.ds(t0, T)].unsqueeze(2).to_broadcast([P, T, NB]), ALU.mult).then_inc(hot, 1)

                make_hot(0, 0)
                make_hot(T, 1)
                dve.wait_ge(hot_a, 2)
                weigh_hot(0, 0)
                dve.wait_ge(hot_a, 4)
                weigh_hot(T, 1)
                with nc.vector.Fori(1, ET // T // 2) as i:
                    for h in range(2):
                        dve.wait_ge(counted, 2 * i + h - 1)
                        make_hot((2 * i + h) * T, h)
                        dve.wait_ge(hot_a, 4 * i + 2 * h + 2)
                        weigh_hot((2 * i + h) * T, h)
                dve.wait_ge(counted, ET // T + 1)
                nc.vector.tensor_copy(counts[:, :], psC[:, 0:2 * NB]).then_inc(v, 1)
                dve.wait_ge(v, 9)
                nc.vector.tensor_scalar(deg[:, :], counts[:, NB:2 * NB], 1.0, None, ALU.add).then_inc(v, 1)
                nc.vector.memset(zero[:, :], 0.0).then_inc(v, 1)
                dve.wait_ge(v, 11)
                nc.vector.tensor_scalar(pos[:, :], deg[:, :], 0.0, None, ALU.is_gt).then_inc(v, 1)
                nc.vector.tensor_scalar(deg[:, :], deg[:, :], 1e-30, None, ALU.max).then_inc(v, 1)
                dve.wait_ge(v, 13)
                nc.vector.reciprocal(rdeg[:, :], deg[:, :]).then_inc(v, 1)
                dve.wait_ge(totalled, 1)
                nc.vector.tensor_copy(totals[:, :], psA[:, 1, 0:NB]).then_inc(v, 1)
                dve.wait_ge(v, 15)
                nc.vector.tensor_tensor_scan(base[:, :], totals[:, :], zero[:, :], 0.0, ALU.add, ALU.add).then_inc(v, 1)
                dve.wait_ge(v, 16)
                nc.vector.tensor_tensor(base[:, :], base[:, :], totals[:, :], ALU.subtract).then_inc(v, 1)
                dve.wait_ge(v, 17)
                nc.vector.tensor_tensor(start_f[:, :], base[:, :], psA[:, 0, 0:NB], ALU.add).then_inc(v, 1)
                dve.wait_ge(v, 18)
                nc.vector.tensor_copy(k.row_start[:, :], start_f[:, :]).then_inc(v, 1)
                nc.vector.tensor_copy(k.row_count[:, :], counts[:, 0:NB]).then_inc(v, 1)
                for g in range(EG):
                    if g >= 2:
                        dve.wait_ge(totalled, g)
                    nc.vector.tensor_scalar(cmp[:, g % 2, :], iota_sf[:, :], key[:, g:g + 1], None, ALU.is_gt).then_inc(compared, 1)
                dve.wait_ge(totalled, EG + 1)
                for h in range(2):
                    nc.vector.tensor_copy(step_tile[:, h * (SPAD // 2):(h + 1) * (SPAD // 2)], psD[:, h, 0:SPAD // 2]).then_inc(v, 1)
                dve.wait_ge(v, 22)
                nc.vector.tensor_tensor(step_blk[:, :], iota_sf[:, :], step_tile[:, :], ALU.subtract).then_inc(v, 1)
                nc.vector.tensor_tensor(diag[:, :, :], step_tile[:, :].rearrange("p (g l) -> p g l", l=P),
                                        k.ident[:, :].unsqueeze(1).to_broadcast([P, SG, P]), ALU.mult).then_inc(v, 1)
                dve.wait_ge(v, 24)
                nc.vector.tensor_reduce(tile_col[:, :], diag[:, :, :], AX.X, ALU.add).then_inc(v, 1)
                nc.vector.tensor_copy(k.step_blk[:, :], step_blk[:, :]).then_inc(v, 1)
                dve.wait_ge(v, 25)
                nc.vector.tensor_copy(k.tile_idx[:, :], tile_col[:, :]).then_inc(stepped, 1)
                dve.wait_ge(gathered, 16 * 3 * SG)
                nc.vector.tensor_copy(got_srcf[:, :, :], got_src[:, :, :]).then_inc(v, 1)
                nc.vector.tensor_copy(got_dstf[:, :, :], got_dst[:, :, :]).then_inc(turned2, 1)
                dve.wait_ge(turned2, 2)
                for h in range(2):
                    w = 512 if h == 0 else SPAD - 512
                    c = slice(h * 512, h * 512 + w)
                    nc.vector.tensor_copy(k.src_idx[:, c], psA[:, h, 0:w]).then_inc(v, 1)
                    nc.vector.scalar_tensor_tensor(out=k.lane[:, c], in0=step_blk[:, c], scalar=-float(P), in1=psB[:, h, 0:w],
                                                   op0=ALU.mult, op1=ALU.add).then_inc(v, 1)
                    nc.vector.tensor_copy(k.weight[:, c], psD[:, h, 0:w]).then_inc(v, 1)

            @block.scalar
            def _(act):
                act.wait_ge(v, 14)
                nc.scalar.activation(rdeg[:, :], rdeg[:, :], ACT.Sqrt).then_inc(turned, 1)

        with nc.Block() as block:
            @block.vector
            def _(dve):
                nc.vector.tensor_tensor(k.dinv[:, :], rdeg[:, :], pos[:, :], ALU.mult).then_inc(v, 1)


HALF = 8
PASSES = -(-STEPS // (2 * HALF))
BANKS = 4
assert PASSES * 2 * HALF <= SPAD


def stage_aggregate(nc, k, name, table, acc, width, weights, heads=0, side=None):
    with ExitStack() as ctx:
        sb, ps, sem = allocators(nc, ctx, name)
        rows = sb("rows", [P, 2, HALF, width])
        scaled = sb("scaled", [P, 2, HALF, width]) if heads else rows
        hot = sb("hot", [P, 2, HALF, P])
        idx = sb("idx", [P, 2, HALF], i32)
        part = [ps(f"part{j}", [P, 512]) for j in range(BANKS)]
        gathered = [sem(f"gathered{j}") for j in range(2 * HALF)]
        idx_ready = sem("idx_ready")
        hot_ready = sem("hot_ready")
        scaled_ready = sem("scaled_ready")
        multiplied = sem("multiplied")
        added = sem("added")
        slot_free = sem("slot_free")
        row_seen = sem("row_seen")
        ones_ready = sem("ones_ready")
        state = side.open(nc, k, ctx) if side else None
        SIDE = NB if side else 0

        with nc.Block() as block:
            @block.sync
            def _(sp):
                if side:
                    side.sync(sp, state)

            @block.gpsimd
            def _(pool):
                if width > D and not heads:
                    nc.gpsimd.memset(rows[:, :, :, D:width], 1.0).then_inc(ones_ready, 1)

                def gather(i, first):
                    for h in range(2):
                        pool.wait_ge(idx_ready, 2 * i + h + 1)
                        pool.sem_inc(slot_free, 1)
                        for j in range(HALF):
                            if not first:
                                pool.wait_ge(multiplied, 2 * HALF * (i - 1) + HALF * h + j + 1)
                                pool.sem_inc(slot_free, 1)
                            nc.gpsimd.indirect_dma_start(
                                out=rows[:, h, j, 0:D], out_offset=None, in_=table,
                                in_offset=bass.IndirectOffsetOnAxis(ap=idx[:, h, j:j + 1], axis=0),
                            ).then_inc(gathered[h * HALF + j], 16)

                gather(0, True)
                with nc.gpsimd.Fori(1, PASSES) as i:
                    gather(i, False)

            @block.scalar
            def _(act):
                if side:
                    side.act_start(act, state)

                def scale_rows(i):
                    for h in range(2):
                        for j in range(HALF):
                            act.wait_ge(gathered[h * HALF + j], 16 * (i + 1))
                            act.sem_inc(row_seen, 1)
                            for q in range(heads):
                                c = slice(q * (D // heads), (q + 1) * (D // heads))
                                nc.scalar.activation(
                                    scaled[:, h, j, c], rows[:, h, j, c], ACT.Copy,
                                    scale=weights[:, bass.ds((2 * HALF * i + HALF * h + j) * heads + q, 1)],
                                ).then_inc(scaled_ready, 1)

                with nc.scalar.Fori(0, PASSES) if not SIDE else nc.scalar.Fori(0, SIDE) as i:
                    if heads:
                        scale_rows(i)
                    if side:
                        side.act(act, state, i)
                if side:
                    if heads:
                        with nc.scalar.Fori(SIDE, PASSES) as i:
                            scale_rows(i)
                    side.act_end(act, state)

            @block.tensor
            def _(pe):
                if side:
                    side.pe_start(pe, state)
                if width > D and not heads:
                    pe.wait_ge(ones_ready, 1)

                def products(i, first, with_side):
                    for h in range(2):
                        pe.wait_ge(hot_ready, 2 * i + h + 1)
                        for j in range(HALF):
                            s = 2 * HALF * i + HALF * h + j
                            if heads:
                                pe.wait_ge(scaled_ready, heads * s + heads)
                            else:
                                pe.wait_ge(gathered[h * HALF + j], 16 * (i + 1))
                            if not first or h * HALF + j >= BANKS:
                                pe.wait_ge(added, s - BANKS + 1)
                            nc.tensor.matmul(part[j % BANKS][:, 0:width], hot[:, h, j, :], scaled[:, h, j, :],
                                             start=True, stop=True).then_inc(multiplied, 1)
                        if with_side:
                            side.pe(pe, state, i, h)

                products(0, True, side)
                with nc.tensor.Fori(1, SIDE or PASSES) as i:
                    products(i, False, side)
                if side:
                    with nc.tensor.Fori(SIDE, PASSES) as i:
                        products(i, False, False)
                    side.pe_end(pe, state)

            @block.vector
            def _(dve):
                if side:
                    side.dve_start(dve, state)

                def make_hot(n, h):
                    s = HALF * n
                    nc.vector.tensor_copy(idx[:, h, :], k.src_idx[:, bass.ds(s, HALF)]).then_inc(idx_ready, 1)
                    if heads:
                        nc.vector.tensor_copy(
                            scaled[:, h, :, D:D + heads],
                            weights[:, bass.ds(s * heads, HALF * heads)].rearrange("p (j q) -> p j q", q=heads))
                    for j in range(HALF):
                        last = nc.vector.tensor_scalar(
                            hot[:, h, j, :], k.iota[:, :], k.lane[:, bass.ds(s + j, 1)],
                            None if heads else weights[:, bass.ds(s + j, 1)],
                            ALU.is_equal, *(() if heads else (ALU.mult,)))
                    last.then_inc(hot_ready, 1)

                def add_parts(n, h):
                    s = HALF * n
                    _, blocks = nc.values_load_multi_w_load_instructions(
                        k.step_blk[0:1, bass.ds(s, HALF)], engines=(mybir.EngineType.DVE,), min_val=0, max_val=NB - 1,
                        skip_runtime_bounds_check_because="a step's block lies in the blocks of its edge tile")
                    for j in range(HALF):
                        dve.wait_ge(multiplied, s + j + 1)
                        dve.wait_ge(added, s + j)
                        a = acc[:, bass.ds(blocks[j], 1), 0:width]
                        nc.vector.tensor_tensor(a, a, part[j % BANKS][:, 0:width].unsqueeze(1), ALU.add).then_inc(added, 1)

                make_hot(0, 0)
                make_hot(1, 1)

                def one_pass(i, with_side):
                    for h in range(2):
                        add_parts(2 * i + h, h)
                        if with_side and h:
                            side.vary(dve, state, i)
                        make_hot(2 * i + h + 2, h)
                        if with_side and h:
                            side.scale(dve, state, i)

                one_pass(0, side)
                if side:
                    with nc.vector.Fori(1, SIDE) as i:
                        one_pass(i, True)
                with nc.vector.Fori(SIDE or 1, PASSES - 1) as i:
                    one_pass(i, False)
                for h in range(2):
                    add_parts(2 * (PASSES - 1) + h, h)
                if side:
                    side.dve_end(dve, state)


def sharpen_inverse_root(nc, dve, v, at, s, y, t):
    nc.vector.tensor_tensor(t, y, y, ALU.mult).then_inc(v, 1)
    dve.wait_ge(v, at + 1)
    nc.vector.tensor_tensor(t, t, s, ALU.mult).then_inc(v, 1)
    dve.wait_ge(v, at + 2)
    nc.vector.tensor_scalar(t, t, -0.5, 1.5, ALU.mult, ALU.add).then_inc(v, 1)
    dve.wait_ge(v, at + 3)
    nc.vector.tensor_tensor(y, y, t, ALU.mult).then_inc(v, 1)
    dve.wait_ge(v, at + 4)


def stage_layernorm(nc, k, name, x, xn, x_there=None):
    with ExitStack() as ctx:
        sb, ps, sem = allocators(nc, ctx, name)
        stats = sb("stats", [P, NB, 6])
        mean = sb("mean", [P, NB])
        apart = sb("apart", [P, NB])
        var = sb("var", [P, NB])
        dev = sb("dev", [P, NB])
        rstd = sb("rstd", [P, NB])
        summed = sem("summed")
        v = sem("v")
        root = sem("root")
        with nc.Block() as block:
            @block.vector
            def _(dve):
                if x_there:
                    dve.wait_ge(*x_there)
                with nc.vector.Fori(0, NG) as g:
                    for j in range(CG):
                        nc.vector.bn_stats(stats[:, bass.ds(g * CG + j, 1), :], x[:, bass.ds(g * CG + j, 1), 0:D]).then_inc(summed, 1)
                dve.wait_ge(summed, NB)
                even, odd = stats[:, :, 1], stats[:, :, 4]
                nc.vector.tensor_tensor(mean[:, :], even, odd, ALU.add).then_inc(v, 1)
                nc.vector.tensor_tensor(apart[:, :], even, odd, ALU.subtract).then_inc(v, 1)
                nc.vector.tensor_tensor(var[:, :], stats[:, :, 2], stats[:, :, 5], ALU.add).then_inc(v, 1)
                dve.wait_ge(v, 3)
                nc.vector.tensor_scalar(mean[:, :], mean[:, :], 0.5, None, ALU.mult).then_inc(v, 1)
                nc.vector.tensor_tensor(apart[:, :], apart[:, :], apart[:, :], ALU.mult).then_inc(v, 1)
                nc.vector.tensor_scalar(var[:, :], var[:, :], 1.0 / D, 1e-5, ALU.mult, ALU.add).then_inc(v, 1)
                dve.wait_ge(v, 6)
                nc.vector.scalar_tensor_tensor(out=var[:, :], in0=apart[:, :], scalar=0.25, in1=var[:, :],
                                               op0=ALU.mult, op1=ALU.add).then_inc(v, 1)
                dve.wait_ge(root, 1)
                nc.vector.reciprocal(rstd[:, :], dev[:, :]).then_inc(v, 1)
                dve.wait_ge(v, 8)
                sharpen_inverse_root(nc, dve, v, 8, var[:, :], rstd[:, :], apart[:, :])
                with nc.vector.Fori(0, NG) as g:
                    for j in range(CG):
                        n = g * CG + j
                        nc.vector.tensor_scalar(xn[:, bass.ds(n, 1), :], x[:, bass.ds(n, 1), 0:D],
                                                mean[:, bass.ds(n, 1)], rstd[:, bass.ds(n, 1)],
                                                ALU.subtract, ALU.mult)

            @block.scalar
            def _(act):
                act.wait_ge(v, 7)
                nc.scalar.activation(dev[:, :], var[:, :], ACT.Sqrt).then_inc(root, 1)


def stage_scale_store(nc, k, name, x, scale, acc, table):
    with ExitStack() as ctx:
        sb, ps, sem = allocators(nc, ctx, name)
        v = sem("v")
        stored = sem("stored")
        t = table.rearrange("(b l) d -> l b d", l=P)
        with nc.Block() as block:
            @block.vector
            def _(dve):
                with nc.vector.Fori(0, NG) as g:
                    for j in range(CG):
                        n = g * CG + j
                        nc.vector.tensor_scalar(acc[:, bass.ds(n, 1), 0:D], x[:, bass.ds(n, 1), 0:D],
                                                scale[:, bass.ds(n, 1)], None, ALU.mult).then_inc(v, 1)

            @block.sync
            def _(sp):
                for g in range(NG):
                    b = slice(g * CG, (g + 1) * CG)
                    sp.wait_ge(v, (g + 1) * CG)
                    sp.dma_start(t[:, b, :], acc[:, b, 0:D]).then_inc(stored, 16)
                sp.wait_ge(stored, 16 * NG)


HEADS0, DH0 = 8, 64
INNER0 = HEADS0 * DH0


class Mix0Side:

    def __init__(self, xn, wkv_t):
        self.xn, self.wkv_t = xn, wkv_t

    def open(self, nc, k, ctx):
        self.nc, self.k = nc, k
        sb, ps, sem = allocators(nc, ctx, "mix0")
        self.w = sb("w", [P, 2, 2 * INNER0])
        self.mean = sb("mean", [P, 2, 2 * HEADS0])
        self.xt = sb("xt", [P, D])
        self.staged = sb("staged", [P, D])
        self.stage_ready = sem("stage_ready")
        self.sq = sb("sq", [P, 2 * HEADS0, DH0])
        self.kc = sb("kc", [P, INNER0])
        self.vs = sb("vs", [P, INNER0])
        self.var = sb("var", [P, 2 * HEADS0])
        self.var2 = sb("var2", [P, 2 * HEADS0])
        self.dev = sb("dev", [P, HEADS0])
        self.pt = ps("pt", [P, 512])
        self.kv = ps("kv", [P, 2, 512])
        self.dots = ps("dots", [P, 512])
        self.loaded, self.centred, self.zeroed, self.turned = sem("loaded"), sem("centred"), sem("zeroed"), sem("turned")
        self.copied, self.projected, self.squared, self.varied = sem("copied"), sem("projected"), sem("squared"), sem("varied")
        self.rooted, self.weighed, self.scaled, self.dotted = sem("rooted"), sem("weighed"), sem("scaled"), sem("dotted")
        self.closed, self.cleared = sem("closed"), sem("cleared")
        return self

    def sync(self, sp, s):
        sp.dma_start(s.w[:, :, :], s.wkv_t.rearrange("(c p) f -> p c f", p=P)).then_inc(s.loaded, 16)
        sp.sem_inc(s.turned, 1)
        with self.nc.sync.Fori(0, NB) as i:
            sp.wait_ge(s.turned, i + 1)
            sp.dma_start(s.staged[:, :], s.xn[:, bass.ds(i, 1), :].rearrange("p a d -> p (a d)")).then_inc(s.stage_ready, 16)

    def dve_start(self, dve, s):
        v = self.nc.vector
        v.memset(s.xt[:, :], 0.0).then_inc(s.zeroed, 1)
        v.memset(s.kc[:, :], 0.0).then_inc(s.zeroed, 1)
        v.memset(s.vs[:, :], 0.0).then_inc(s.zeroed, 1)
        v.memset(self.k.dots[:, :, :], 0.0).then_inc(s.zeroed, 1)
        dve.wait_ge(s.loaded, 16)
        w = s.w[:, :, :].rearrange("p c (h d) -> p (c h) d", d=DH0)
        mean = s.mean[:, :, :].rearrange("p c h -> p (c h)")
        v.tensor_reduce(mean, w, AX.X, ALU.add).then_inc(s.centred, 1)
        dve.wait_ge(s.centred, 1)
        v.tensor_scalar(mean, mean, -1.0 / DH0, None, ALU.mult).then_inc(s.centred, 1)
        dve.wait_ge(s.centred, 2)
        v.tensor_tensor(w, w, mean.unsqueeze(2).to_broadcast([P, 4 * HEADS0, DH0]), ALU.add).then_inc(s.centred, 1)

    def pe_start(self, pe, s):
        t = self.nc.tensor
        pe.wait_ge(s.zeroed, 4)
        pe.wait_ge(s.centred, 3)
        t.matmul(s.dots[:, :], self.k.ident[:, :], s.kc[:, :], start=True, stop=False)

    def products(self, pe, s):
        for g in range(HEADS0 // 2):
            c = slice(g * P, (g + 1) * P)
            last = self.nc.tensor.matmul(s.dots[:, c], s.vs[:, c], s.kc[:, c], start=False, stop=False)
        last.then_inc(s.dotted, 1)

    def project(self, pe, s):
        for h in range(2):
            for c in range(2):
                last = self.nc.tensor.matmul(s.kv[:, h, :], s.xt[:, c * P:(c + 1) * P], s.w[:, c, h * 512:(h + 1) * 512],
                                             start=(c == 0), stop=(c == 1))
        last.then_inc(s.projected, 1)

    def pe(self, pe, s, i, h):
        first = isinstance(i, int)
        if h == 0:
            if not first:
                pe.wait_ge(s.scaled, i)
                pe.wait_ge(s.squared, 2 * i)
                pe.wait_ge(s.copied, i)
            self.products(pe, s)
            self.project(pe, s)
            return
        pe.wait_ge(s.stage_ready, 16 * i + 16)
        for c in range(2):
            last = self.nc.tensor.transpose(s.pt[:, c * P:(c + 1) * P], s.staged[:, c * P:(c + 1) * P], self.k.ident[:, :])
        last.then_inc(s.turned, 1)

    def pe_end(self, pe, s):
        for n in range(2):
            pe.wait_ge(s.scaled, NB + n)
            pe.wait_ge(s.squared, 2 * (NB + n))
            pe.wait_ge(s.copied, NB)
            self.products(pe, s)
            if n == 0:
                self.project(pe, s)
        pe.wait_ge(s.cleared, 1)
        self.nc.tensor.matmul(s.dots[:, :], self.k.ident[:, :], s.kc[:, :], start=False, stop=True).then_inc(s.closed, 1)

    def act_start(self, act, s):
        act.wait_ge(s.zeroed, 4)

    def evacuate(self, act, s, i):
        a = self.nc.scalar
        act.wait_ge(s.projected, i + 1)
        for h in range(2 * HEADS0):
            last = a.activation(s.sq[:, h, :], s.kv[:, h // HEADS0, h % HEADS0 * DH0:(h % HEADS0 + 1) * DH0],
                                ACT.Square, accum_out=s.var[:, h:h + 1])
        last.then_inc(s.squared, 1)
        a.activation(s.kc[:, :], s.kv[:, 0, :], ACT.Copy).then_inc(s.squared, 1)
        act.wait_ge(s.varied, 2 * i + 2)
        a.activation(s.dev[:, :], s.dev[:, :], ACT.Sqrt).then_inc(s.rooted, 1)

    def act(self, act, s, i):
        self.evacuate(act, s, i)
        act.wait_ge(s.turned, i + 2)
        self.nc.scalar.activation(s.xt[:, :], s.pt[:, 0:D], ACT.Copy).then_inc(s.copied, 1)
        self.divide(act, s, i)

    def divide(self, act, s, i):
        act.wait_ge(s.weighed, i + 1)
        for h in range(HEADS0):
            c = slice(h * DH0, (h + 1) * DH0)
            last = self.nc.scalar.activation(s.vs[:, c], s.kv[:, 1, c], ACT.Copy, scale=s.dev[:, h:h + 1])
        last.then_inc(s.scaled, 1)

    def act_end(self, act, s):
        self.evacuate(act, s, NB)
        self.divide(act, s, NB)

    def vary(self, dve, s, i):
        v = self.nc.vector
        dve.wait_ge(s.squared, 2 * i + 1)
        v.tensor_scalar(s.var2[:, :], s.var[:, :], 1.0 / DH0, 1e-5, ALU.mult, ALU.add).then_inc(s.varied, 1)
        dve.wait_ge(s.varied, 2 * i + 1)
        v.tensor_tensor(s.dev[:, :], s.var2[:, 0:HEADS0], s.var2[:, HEADS0:], ALU.mult).then_inc(s.varied, 1)

    def scale(self, dve, s, i):
        v = self.nc.vector
        dve.wait_ge(s.rooted, i + 1)
        v.reciprocal(s.dev[:, :], s.dev[:, :]).then_inc(s.weighed, 1)

    def dve_end(self, dve, s):
        self.vary(dve, s, NB)
        self.scale(dve, s, NB)
        v = self.nc.vector
        dve.wait_ge(s.dotted, NB + 2)
        v.memset(s.kc[:, :], 0.0).then_inc(s.cleared, 1)
        dve.wait_ge(s.closed, 1)
        for g in range(HEADS0 // 2):
            for a in range(2):
                r, c = slice(a * DH0, (a + 1) * DH0), g * P + a * DH0
                v.tensor_scalar(self.k.dots[r, g, a * DH0:(a + 1) * DH0], s.dots[r, c:c + DH0], 1.0 / NODES, None, ALU.mult)


def stage_mix0_fold(nc, k, wq, wout_t):
    with ExitStack() as ctx:
        sb, ps, sem = allocators(nc, ctx, "fold0")
        wq_sb = sb("wq", [P, 4, D])
        wo_sb = sb("wo", [P, 4, D])
        a1 = sb("a1", [P, 4, D])
        pa = ps("pa", [P, 4, D])
        pm = ps("pm", [P, 2, D])
        loaded, made, copied, folded = sem("loaded"), sem("made"), sem("copied"), sem("folded")
        with nc.Block() as block:
            @block.sync
            def _(sp):
                sp.dma_start(wq_sb[:, :, :], wq.rearrange("(g p) c -> p g c", p=P)).then_inc(loaded, 16)
                sp.dma_start(wo_sb[:, :, :], wout_t.rearrange("(g p) c -> p g c", p=P)).then_inc(loaded, 16)

            @block.tensor
            def _(pe):
                pe.wait_ge(loaded, 32)
                for g in range(4):
                    nc.tensor.matmul(pa[:, g, :], k.dots[:, g, :], wo_sb[:, g, :], start=True, stop=True).then_inc(made, 1)
                pe.wait_ge(copied, 1)
                for c in range(2):
                    for g in range(4):
                        last = nc.tensor.matmul(pm[:, c, :], wq_sb[:, g, c * P:(c + 1) * P], a1[:, g, :],
                                                start=(g == 0), stop=(g == 3))
                last.then_inc(folded, 1)

            @block.vector
            def _(dve):
                dve.wait_ge(made, 4)
                nc.vector.tensor_copy(a1[:, :, :], pa[:, :, :]).then_inc(copied, 1)
                dve.wait_ge(folded, 1)
                nc.vector.tensor_copy(k.mix[:, :, :], pm[:, :, :])


RING = 4


def led(engine, lead, ahead, one):
    for n in range(lead):
        ahead(n, n % RING)
    full = (NB - lead) // RING
    with engine.Fori(0, full) as i:
        for h in range(RING):
            if lead:
                ahead(RING * i + h + lead, (h + lead) % RING)
            one(RING * i + h, h)
    for n in range(full * RING, NB):
        if lead and n + lead < NB:
            ahead(n + lead, (n + lead) % RING)
        one(n, n % RING)


def project_rows(nc, k, name, chunks, rhs, width, finish, load=None, loads=0, scale=None, columns=None, store=None, late=False):
    columns = columns or chunks * P
    with ExitStack() as ctx:
        sb, ps, sem = allocators(nc, ctx, name)
        staged = sb("staged", [P, RING, columns])
        extra = sb("extra", [P, RING, D]) if loads > 1 or (loads and scale) else None
        xt = sb("xt", [P, RING, chunks * P])
        pt = ps("pt", [P, RING, 512])
        po = ps("po", [P, RING, 512])
        loaded = [sem(f"loaded{h}") for h in range(RING)]
        scaled = sem("scaled")
        step = sem("step")
        turned, copied, multiplied, done = sem("turned"), sem("copied"), sem("multiplied"), sem("done")
        uses = lambda n, h: (n - h) // RING + 1

        with nc.Block() as block:
            @block.sync
            def _(sp):
                if load:
                    def bring(n, h):
                        if not late:
                            sp.wait_ge(turned, n + 1)
                        if extra is not None:
                            sp.wait_ge(done, n + 1)
                        for dma in load(sp, n, staged[:, h, :], extra[:, h:h + 1, :] if extra is not None else None):
                            dma.then_inc(loaded[h], 16)
                    led(nc.sync, 0, None, bring)
                if store:
                    store(sp, done)

            @block.tensor
            def _(pe):
                pe.sem_inc(turned, RING)
                pe.sem_inc(multiplied, RING)

                def turn(n, h):
                    pe.wait_ge(copied, n + 1)
                    if load and not late:
                        pe.wait_ge(loaded[h], 16 * loads * uses(n, h))
                    if scale:
                        pe.wait_ge(scaled, n + 1)
                    for c in range(chunks):
                        last = nc.tensor.transpose(pt[:, h, c * P:(c + 1) * P], staged[:, h, c * P:(c + 1) * P], k.ident[:, :])
                    last.then_inc(turned, 1)

                def multiply(n, h):
                    pe.wait_ge(copied, n + RING + 1)
                    pe.wait_ge(done, n + 1)
                    for c in range(chunks):
                        last = nc.tensor.matmul(po[:, h, 0:width], xt[:, h, c * P:(c + 1) * P], rhs(c),
                                                start=(c == 0), stop=(c == chunks - 1))
                    last.then_inc(multiplied, 1)
                led(nc.tensor, 2, turn, multiply)

            @block.scalar
            def _(act):
                act.sem_inc(copied, RING)

                def copy(n, h):
                    act.wait_ge(turned, n + RING + 1)
                    act.wait_ge(multiplied, n + 1)
                    nc.scalar.activation(xt[:, h, :], pt[:, h, 0:chunks * P], ACT.Copy).then_inc(copied, 1)
                led(nc.scalar, 0, None, copy)

            @block.vector
            def _(dve):
                dve.sem_inc(done, RING)

                def make(n, h):
                    dve.wait_ge(turned, n + 1)
                    scale(n, staged[:, h, :]).then_inc(scaled, 1)

                def end(n, h):
                    dve.wait_ge(multiplied, n + RING + 1)
                    if extra is not None:
                        dve.wait_ge(loaded[h], 16 * loads * uses(n, h))
                    finish(dve, n, po[:, h:h + 1, 0:width], extra[:, h:h + 1, :] if extra is not None else None, step).then_inc(done, 1)
                if scale:
                    led(nc.vector, 3, make, end)
                else:
                    led(nc.vector, 0, None, end)


def in_blocks(ap):
    return ap.rearrange("(b l) d -> l b d", l=P)


def on_all(ap):
    return ap.rearrange("(a n) -> a n", a=1).to_broadcast([P, ap.shape[0]])


def block_rows(t, n):
    return t[:, bass.ds(n, 1), 0:D].rearrange("p a d -> p (a d)")


def load_weights(nc, ctx, name, loads):
    sem = allocators(nc, ctx, name)[2]
    loaded = sem("loaded")
    with nc.Block() as block:
        @block.sync
        def _(sp):
            for to, source in loads:
                sp.dma_start(to, source).then_inc(loaded, 16)
            sp.wait_ge(loaded, 16 * len(loads))


def stage_gcn_dense(nc, k, name, acc, w, bias, table=None, xn=None, x_in=None, bias2=None):
    with ExitStack() as ctx:
        sb, _, sem = allocators(nc, ctx, name + "_out")
        w_sb = sb("w", [P, 2, D])
        b_sb = sb("b", [P, 2, D])
        stored = sem("stored")
        load_weights(nc, ctx, name + "w", [(w_sb[:, :, :], w.rearrange("(c p) n -> p c n", p=P)), (b_sb[:, 0, :], on_all(bias))] +
                     ([] if table is not None else [(b_sb[:, 1, :], on_all(bias2))]))

        def scale(n, staged):
            return nc.vector.tensor_scalar(staged[:, 0:D].unsqueeze(1), acc[:, bass.ds(n, 1), 0:D], k.dinv[:, bass.ds(n, 1)], None, ALU.mult)

        if table is not None:
            def finish(dve, n, out, extra, step):
                a = acc[:, bass.ds(n, 1), 0:D]
                nc.vector.tensor_tensor(a, out, b_sb[:, 0:1, :], ALU.add).then_inc(step, 1)
                dve.wait_ge(step, n + 1)
                return nc.vector.tensor_scalar(a, a, 0.0, k.dinv[:, bass.ds(n, 1)], ALU.max, ALU.mult)

            def store(sp, done):
                for g in range(NG):
                    b = slice(g * CG, (g + 1) * CG)
                    sp.wait_ge(done, (g + 1) * CG + RING)
                    sp.dma_start(in_blocks(table)[:, b, :], acc[:, b, 0:D]).then_inc(stored, 16)
                sp.wait_ge(stored, 16 * NG)
            project_rows(nc, k, name, 2, lambda c: w_sb[:, c, :], D, finish, scale=scale, store=store)
            return

        def load(sp, n, staged, extra):
            return [sp.dma_start(extra, in_blocks(x_in)[:, bass.ds(n, 1), :])]

        def scale_both(n, staged):
            scale(n, staged)
            return nc.vector.tensor_copy(staged[:, D:2 * D].unsqueeze(1), xn[:, bass.ds(n, 1), :])

        def finish(dve, n, out, extra, step):
            a = acc[:, bass.ds(n, 1), 0:D]
            nc.vector.tensor_tensor(a, out, extra, ALU.add).then_inc(step, 1)
            dve.wait_ge(step, 2 * n + 1)
            nc.vector.tensor_tensor(a, a, b_sb[:, 0:1, :], ALU.add).then_inc(step, 1)
            dve.wait_ge(step, 2 * n + 2)
            return nc.vector.tensor_tensor(a, a, b_sb[:, 1:2, :], ALU.add)
        project_rows(nc, k, name, 4, lambda c: w_sb[:, c, :] if c < 2 else k.mix[:, c - 2, :], D, finish,
                     load=load, loads=1, scale=scale_both, late=True)


EXPERTS = 8
HID = 1024
FC = HID // P
CAP = -(-(5 * NODES) // (4 * EXPERTS))
CAPPAD = -(-CAP // P) * P
TT = CAPPAD // P
OUTSIDE = 1 << 20
FMAX = 3.4028234e38


def half_index(n, h):
    return (n - h) // 2 + 1


def paired(engine, one):
    with engine.Fori(0, NB // 2) as i:
        for h in range(2):
            one(2 * i + h, h)
    one(NB - 1, 0)


def in_pairs(engine, count, one):
    with engine.Fori(0, count // 2) as i:
        for h in range(2):
            one(2 * i + h, h)
    if count % 2:
        one(count - 1, 0)


def stage_gate(nc, k, xn, gate_w, gate_b, logits):
    with ExitStack() as ctx:
        w_sb = ctx.enter_context(nc.sbuf_tensor("gate_w", [P, 2, EXPERTS], f32))
        b_sb = ctx.enter_context(nc.sbuf_tensor("gate_b", [P, EXPERTS], f32))
        load_weights(nc, ctx, "gatew", [(w_sb[:, :, :], gate_w.rearrange("(c p) n -> p c n", p=P)), (b_sb[:, :], on_all(gate_b))])
        project_rows(nc, k, "gate", 2, lambda c: w_sb[:, c, :], EXPERTS,
                     lambda dve, n, out, extra, step: nc.vector.tensor_tensor(logits[:, bass.ds(n, 1), :], out, b_sb[:, :].unsqueeze(1), ALU.add),
                     load=lambda sp, n, staged, extra: [sp.dma_start(staged, block_rows(xn, n))], loads=1)


def stage_route(nc, k, name, logits, prob, to_slot, from_slot, capacity=None, block_expert=None):
    SLOTS = EXPERTS * NB
    with ExitStack() as ctx:
        sb, ps, sem = allocators(nc, ctx, name)
        best = sb("best", [P, NB])
        hot = sb("hot", [P, NB, EXPERTS])
        exps = sb("exps", [P, NB, EXPERTS])
        code = sb("code", [P, EXPERTS])
        codes = sb("codes", [P, NB, EXPERTS])
        first = sb("first", [P, NB])
        tot = sb("tot", [P, NB, EXPERTS])
        run = sb("run", [P, NB, EXPERTS])
        zero = sb("zero", [P, NB])
        pos = sb("pos", [P, NB])
        slot = sb("slot", [P, NB])
        kept = sb("kept", [P, NB])
        away = sb("away", [P, NB])
        last_slot = sb("last_slot", [P, NB])
        size = sb("size", [P, EXPERTS])
        size_i = sb("size_i", [P, EXPERTS], i32)
        ends = sb("ends", [P, EXPERTS])
        below = sb("below", [P, P])
        owner = sb("owner", [P, P])
        p_in = ps("p_in", [P, 512])
        p_tot = ps("p_tot", [P, 512])
        v, exped, counted = sem("v"), sem("exped"), sem("counted")
        flat = lambda t: t[:, :, :].rearrange("p b e -> p (b e)")
        wide = lambda t: t[:, :].unsqueeze(2).to_broadcast([P, NB, EXPERTS])
        with nc.Block() as block:
            @block.tensor
            def _(pe):
                pe.wait_ge(v, 8)
                nc.tensor.matmul(p_in[:, 0:SLOTS], k.before[:, :], flat(hot), start=True, stop=True)
                nc.tensor.matmul(p_tot[:, 0:SLOTS], k.ones[:, :], flat(hot), start=True, stop=True).then_inc(counted, 1)

            @block.scalar
            def _(act):
                act.wait_ge(v, 3)
                nc.scalar.activation(flat(exps), flat(exps), ACT.Exp).then_inc(exped, 1)

            @block.vector
            def _(dve):
                nc.vector.tensor_reduce(best[:, :], logits[:, :, :], AX.X, ALU.max).then_inc(v, 1)
                nc.vector.tensor_scalar(code[:, :], k.iota[:, 0:EXPERTS], -float(EXPERTS), None, ALU.add).then_inc(v, 1)
                dve.wait_ge(v, 2)
                nc.vector.tensor_tensor(exps[:, :, :], logits[:, :, :], wide(best), ALU.subtract).then_inc(v, 1)
                nc.vector.tensor_tensor(hot[:, :, :], logits[:, :, :], wide(best), ALU.is_equal).then_inc(v, 1)
                dve.wait_ge(v, 4)
                nc.vector.tensor_tensor(codes[:, :, :], hot[:, :, :], code[:, :].unsqueeze(1).to_broadcast([P, NB, EXPERTS]),
                                        ALU.mult).then_inc(v, 1)
                dve.wait_ge(v, 5)
                nc.vector.tensor_reduce(first[:, :], codes[:, :, :], AX.X, ALU.min).then_inc(v, 1)
                dve.wait_ge(v, 6)
                nc.vector.tensor_tensor(hot[:, :, :], code[:, :].unsqueeze(1).to_broadcast([P, NB, EXPERTS]), wide(first),
                                        ALU.is_equal).then_inc(v, 1)
                nc.vector.memset(zero[:, :], 0.0).then_inc(v, 1)
                dve.wait_ge(exped, 1)
                nc.vector.tensor_reduce(prob[:, :], exps[:, :, :], AX.X, ALU.add).then_inc(v, 1)
                dve.wait_ge(v, 9)
                nc.vector.reciprocal(prob[:, :], prob[:, :]).then_inc(v, 1)
                dve.wait_ge(counted, 1)
                nc.vector.tensor_copy(flat(tot), p_tot[:, 0:SLOTS]).then_inc(v, 1)
                dve.wait_ge(v, 11)
                for e in range(EXPERTS):
                    nc.vector.tensor_tensor_scan(run[:, :, e], tot[:, :, e], zero[:, :], 0.0, ALU.add, ALU.add).then_inc(v, 1)
                dve.wait_ge(v, 19)
                nc.vector.tensor_copy(size[:, :], run[:, NB - 1, :]).then_inc(v, 1)
                dve.wait_ge(v, 20)
                nc.vector.tensor_tensor(run[:, :, :], run[:, :, :], tot[:, :, :], ALU.subtract).then_inc(v, 1)
                dve.wait_ge(v, 21)
                nc.vector.tensor_tensor(flat(run), flat(run), p_in[:, 0:SLOTS], ALU.add).then_inc(v, 1)
                if capacity is None:
                    nc.vector.tensor_scalar(size[:, :], size[:, :], float(P - 1), None, ALU.add).then_inc(v, 1)
                    dve.wait_ge(v, 23)
                    nc.vector.tensor_copy(size_i[:, :], size[:, :]).then_inc(v, 1)
                    dve.wait_ge(v, 24)
                    nc.vector.tensor_single_scalar(size_i[:, :], size_i[:, :], 7, op=ALU.arith_shift_right).then_inc(v, 1)
                    dve.wait_ge(v, 25)
                    nc.vector.tensor_copy(size[:, :], size_i[:, :]).then_inc(v, 1)
                    dve.wait_ge(v, 26)
                    nc.vector.tensor_tensor_scan(ends[:, :], size[:, :], zero[:, 0:EXPERTS], 0.0, ALU.add, ALU.add).then_inc(v, 1)
                    dve.wait_ge(v, 27)
                    nc.vector.memset(owner[:, :], 0.0).then_inc(v, 1)
                    for e in range(EXPERTS - 1):
                        dve.wait_ge(v, 28 + 2 * e)
                        nc.vector.tensor_scalar(below[:, :], k.iota[:, :], ends[:, e:e + 1], None, ALU.is_ge).then_inc(v, 1)
                        dve.wait_ge(v, 29 + 2 * e)
                        nc.vector.tensor_tensor(owner[:, :], owner[:, :], below[:, :], ALU.add).then_inc(v, 1)
                    dve.wait_ge(v, 42)
                    nc.vector.tensor_copy(block_expert[:, :], owner[0:1, :]).then_inc(v, 1)
                    nc.vector.tensor_tensor(ends[:, :], ends[:, :], size[:, :], ALU.subtract).then_inc(v, 1)
                    dve.wait_ge(v, 44)
                    nc.vector.tensor_scalar(ends[:, :], ends[:, :], float(P), None, ALU.mult).then_inc(v, 1)
                    dve.wait_ge(v, 45)
                    nc.vector.tensor_tensor(run[:, :, :], run[:, :, :], ends[:, :].unsqueeze(1).to_broadcast([P, NB, EXPERTS]),
                                            ALU.add).then_inc(v, 1)
                    at = 46
                else:
                    at = 22
                dve.wait_ge(v, at)
                nc.vector.tensor_tensor(run[:, :, :], run[:, :, :], hot[:, :, :], ALU.mult).then_inc(v, 1)
                dve.wait_ge(v, at + 1)
                nc.vector.tensor_reduce(pos[:, :], run[:, :, :], AX.X, ALU.add).then_inc(v, 1)
                dve.wait_ge(v, at + 2)
                if capacity is None:
                    nc.vector.tensor_copy(to_slot[:, :], pos[:, :]).then_inc(v, 1)
                    nc.vector.tensor_copy(from_slot[:, :], pos[:, :]).then_inc(v, 1)
                else:
                    nc.vector.tensor_scalar(kept[:, :], pos[:, :], float(capacity), None, ALU.is_lt).then_inc(v, 1)
                    nc.vector.tensor_scalar(slot[:, :], first[:, :], float(EXPERTS), float(CAPPAD), ALU.add, ALU.mult).then_inc(v, 1)
                    nc.vector.tensor_scalar(last_slot[:, :], pos[:, :], float(capacity - 1), None, ALU.min).then_inc(v, 1)
                    dve.wait_ge(v, at + 5)
                    nc.vector.tensor_tensor(last_slot[:, :], last_slot[:, :], slot[:, :], ALU.add).then_inc(v, 1)
                    nc.vector.tensor_tensor(slot[:, :], slot[:, :], pos[:, :], ALU.add).then_inc(v, 1)
                    nc.vector.tensor_tensor(prob[:, :], prob[:, :], kept[:, :], ALU.mult).then_inc(v, 1)
                    nc.vector.tensor_scalar(away[:, :], kept[:, :], -float(OUTSIDE), float(OUTSIDE), ALU.mult, ALU.add).then_inc(v, 1)
                    dve.wait_ge(v, at + 9)
                    nc.vector.tensor_copy(from_slot[:, :], last_slot[:, :]).then_inc(v, 1)
                    nc.vector.tensor_tensor(slot[:, :], slot[:, :], away[:, :], ALU.add).then_inc(v, 1)
                    dve.wait_ge(v, at + 11)
                    nc.vector.tensor_copy(to_slot[:, :], slot[:, :]).then_inc(v, 1)


def stage_dispatch(nc, k, name, xn, to_slot, slots):
    with ExitStack() as ctx:
        sb, ps, sem = allocators(nc, ctx, name)
        sent = sem("sent")
        with nc.Block() as block:
            @block.gpsimd
            def _(pool):
                for b in range(NB):
                    nc.gpsimd.indirect_dma_start(
                        out=slots, out_offset=bass.IndirectOffsetOnAxis(ap=to_slot[:, b:b + 1], axis=0),
                        in_=xn[:, b, :], in_offset=None, bounds_check=EXPERTS * CAPPAD - 1, oob_is_err=False,
                    ).then_inc(sent, 16)
                pool.wait_ge(sent, 16 * NB)


def stage_experts0(nc, k, slots, w1, b1, w2, b2, out, scratch):
    HT = TT // 2
    HW = HT * P
    with ExitStack() as ctx:
        sb, ps, sem = allocators(nc, ctx, "experts0")
        w1_sb = sb("w1", [P, 2, 2, HID])
        w2_sb = sb("w2", [P, 2, FC, D])
        b1_sb = sb("b1", [P, 2, FC])
        b2_sb = sb("b2", [P, 2, D])
        x_sb = sb("x", [P, 2, TT, D])
        xt = sb("xt", [P, 2, TT * P])
        ht = scratch[:, 0:FC * TT * P // D, :].rearrange("p b d -> p (b d)").rearrange("p (f n) -> p f n", f=FC)
        y_sb = sb("y", [P, 2, TT, D])
        pt = ps("pt", [P, 2, 512])
        ph = [ps(f"ph{j}", [P, 512]) for j in range(4)]
        py = [ps(f"py{j}", [P, 512]) for j in range(2)]
        loaded = [sem("loaded0"), sem("loaded1")]
        stored = [sem("stored0"), sem("stored1")]
        turned, copied = sem("turned"), sem("copied")
        h_made, relued = sem("h_made"), sem("relued")
        y_made, evacuated, y_free = sem("y_made"), sem("evacuated"), sem("y_free")
        with nc.Block() as block:
            @block.sync
            def _(sp):
                sp.sem_inc(y_free, 2)

                def load(e, h):
                    d = bass.ds(e, 1)
                    sp.dma_start(x_sb[:, h, :, :], slots.rearrange("(e t l) d -> l e t d", l=P, t=TT)[:, d, :, :]
                                 .rearrange("l a t d -> l (a t) d")).then_inc(loaded[h], 16)
                    sp.dma_start(w1_sb[:, h, :, :], w1[d, :, :].rearrange("a (c p) f -> p (a c) f", p=P)).then_inc(loaded[h], 16)
                    sp.dma_start(w2_sb[:, h, :, :], w2[d, :, :].rearrange("a (c p) n -> p (a c) n", p=P)).then_inc(loaded[h], 16)
                    sp.dma_start(b2_sb[:, h, :], b2[d, :].to_broadcast([P, D])).then_inc(loaded[h], 16)
                    sp.dma_start(b1_sb[:, h, :], b1[d, :, :].rearrange("a p f -> p (a f)")).then_inc(loaded[h], 16)

                def store(e, h):
                    sp.wait_ge(evacuated, TT * (e + 1) + 2)
                    sp.dma_start(out.rearrange("(e t l) d -> l e t d", l=P, t=TT)[:, bass.ds(e, 1), :, :]
                                 .rearrange("l a t d -> l (a t) d"), y_sb[:, h, :, :]).then_inc(stored[h], 16)

                load(0, 0)
                load(1, 1)
                with nc.sync.Fori(0, EXPERTS // 2 - 1) as i:
                    for h in range(2):
                        e = 2 * i + h
                        store(e, h)
                        load(e + 2, h)
                        sp.wait_ge(stored[h], 16 * (i + 1))
                        sp.sem_inc(y_free, 1)
                for h in range(2):
                    store(EXPERTS - 2 + h, h)
                for h in range(2):
                    sp.wait_ge(stored[h], 16 * (EXPERTS // 2))

            @block.tensor
            def _(pe):
                def turn(e, h):
                    pe.wait_ge(loaded[h], 80 * half_index(e, h))
                    for t in range(TT):
                        pe.wait_ge(copied, TT * e + t + 1)
                        for c in range(2):
                            last = nc.tensor.transpose(pt[:, t % 2, c * P:(c + 1) * P], x_sb[:, h, t, c * P:(c + 1) * P],
                                                       k.ident[:, :])
                        last.then_inc(turned, 1)

                def first(e, h):
                    for half in range(2):
                        pe.wait_ge(copied, TT * e + HT * (half + 1) + 2)
                        for f in range(FC):
                            pe.wait_ge(relued, 2 * FC * e + FC * half + f + 1)
                            for c in range(2):
                                last = nc.tensor.matmul(ph[f % 4][:, 0:HW], w1_sb[:, h, c, f * P:(f + 1) * P],
                                                        xt[:, c, half * HW:(half + 1) * HW], start=(c == 0), stop=(c == 1))
                            last.then_inc(h_made, 1)

                def second(e, h):
                    for t in range(TT):
                        if t % HT == 0:
                            pe.wait_ge(relued, 2 * FC * e + FC * (t // HT + 1) + 4)
                        pe.wait_ge(evacuated, TT * e + t + 1)
                        for f in range(FC):
                            last = nc.tensor.matmul(py[t % 2][:, 0:D], ht[:, f, t * P:(t + 1) * P], w2_sb[:, h, f, :],
                                                    start=(f == 0), stop=(f == FC - 1))
                        last.then_inc(y_made, 1)

                turn(0, 0)
                with nc.tensor.Fori(0, EXPERTS // 2 - 1) as i:
                    for h in range(2):
                        first(2 * i + h, h)
                        turn(2 * i + h + 1, 1 - h)
                        second(2 * i + h, h)
                first(EXPERTS - 2, 0)
                turn(EXPERTS - 1, 1)
                second(EXPERTS - 2, 0)
                first(EXPERTS - 1, 1)
                second(EXPERTS - 1, 1)

            @block.scalar
            def _(act):
                act.sem_inc(relued, 4)
                with nc.scalar.Fori(0, EXPERTS // 2) as i:
                    for h in range(2):
                        e = 2 * i + h
                        act.wait_ge(loaded[h], 80 * (i + 1))
                        for half in range(2):
                            for f in range(FC):
                                act.wait_ge(h_made, 2 * FC * e + FC * half + f + 2)
                                nc.scalar.activation(ht[:, f, half * HW:(half + 1) * HW], ph[f % 4][:, 0:HW], ACT.Relu,
                                                     bias=b1_sb[:, h, f:f + 1]).then_inc(relued, 1)

            @block.vector
            def _(dve):
                dve.sem_inc(copied, 2)
                dve.sem_inc(evacuated, 2)
                dve.sem_inc(h_made, 1)

                def copy(e, h):
                    dve.wait_ge(h_made, 2 * FC * e + 1)
                    for t in range(TT):
                        dve.wait_ge(turned, TT * e + t + 1)
                        nc.vector.tensor_copy(xt[:, :, t * P:(t + 1) * P],
                                              pt[:, t % 2, 0:D].rearrange("p (c n) -> p c n", c=2)).then_inc(copied, 1)

                def end(e, h):
                    dve.wait_ge(y_free, e + 1)
                    dve.wait_ge(loaded[h], 80 * half_index(e, h))
                    for t in range(TT):
                        dve.wait_ge(y_made, TT * e + t + 1)
                        nc.vector.tensor_tensor(y_sb[:, h, t, :], py[t % 2][:, 0:D], b2_sb[:, h, :], ALU.add).then_inc(evacuated, 1)

                copy(0, 0)
                with nc.vector.Fori(0, EXPERTS // 2 - 1) as i:
                    for h in range(2):
                        copy(2 * i + h + 1, 1 - h)
                        end(2 * i + h, h)
                copy(EXPERTS - 1, 1)
                end(EXPERTS - 2, 0)
                end(EXPERTS - 1, 1)


def stage_combine(nc, k, name, rows, from_slot, x, prob, guard, x_out=None):
    with ExitStack() as ctx:
        sb, ps, sem = allocators(nc, ctx, name)
        got = sb("got", [P, 2, CG, D])
        if guard:
            bad = sb("bad", [P, 2, CG * D], i32)
            most = sb("most", [P, CG * D])
            least = sb("least", [P, CG * D])
            nought = sb("nought", [P, CG * D])
        gathered = [sem("gathered0"), sem("gathered1")]
        done, v, stored, weighed = sem("done"), sem("v"), sem("stored"), sem("weighed")

        with nc.Block() as block:
            @block.gpsimd
            def _(pool):
                for g in range(NG):
                    if g >= 2:
                        pool.wait_ge(done, g - 1)
                    for j in range(CG):
                        nc.gpsimd.indirect_dma_start(
                            out=got[:, g % 2, j, :], out_offset=None, in_=rows,
                            in_offset=bass.IndirectOffsetOnAxis(ap=from_slot[:, g * CG + j:g * CG + j + 1], axis=0),
                        ).then_inc(gathered[g % 2], 16)

            @block.scalar
            def _(act):
                for g in range(NG):
                    act.wait_ge(gathered[g % 2], 16 * CG * (g // 2 + 1))
                    for j in range(CG):
                        last = nc.scalar.activation(got[:, g % 2, j, :], got[:, g % 2, j, :], ACT.Copy,
                                                    scale=prob[:, g * CG + j:g * CG + j + 1])
                    last.then_inc(weighed, 1)

            @block.vector
            def _(dve):
                c = Tally()
                if guard:
                    nc.vector.memset(most[:, :], 10000.0).then_inc(v, c.one())
                    nc.vector.memset(least[:, :], -10000.0).then_inc(v, c.one())
                    nc.vector.memset(nought[:, :], 0.0).then_inc(v, c.one())
                for g in range(NG):
                    a = x[:, g * CG:(g + 1) * CG, 0:D]
                    y = got[:, g % 2, :, :].rearrange("p b d -> p (b d)")
                    dve.wait_ge(weighed, g + 1)
                    if guard:
                        dve.wait_ge(v, c.n)
                        nc.vector.tensor_scalar(bad[:, 0, :], y, FMAX, None, ALU.is_gt).then_inc(v, c.one())
                        nc.vector.tensor_scalar(bad[:, 1, :], y, -FMAX, None, ALU.is_lt).then_inc(v, c.one())
                        dve.wait_ge(v, c.n)
                        nc.vector.copy_predicated(y, bad[:, 0, :], most[:, :]).then_inc(v, c.one())
                        dve.wait_ge(v, c.n)
                        nc.vector.copy_predicated(y, bad[:, 1, :], least[:, :]).then_inc(v, c.one())
                        dve.wait_ge(v, c.n)
                        nc.vector.tensor_tensor(bad[:, 0, :], y, y, ALU.not_equal).then_inc(v, c.one())
                        dve.wait_ge(v, c.n)
                        nc.vector.copy_predicated(y, bad[:, 0, :], nought[:, :]).then_inc(v, c.one())
                        dve.wait_ge(v, c.n)
                    nc.vector.tensor_tensor(a, a, got[:, g % 2, :, :], ALU.add).then_inc(done, 1)

            @block.sync
            def _(sp):
                if x_out is not None:
                    for g in range(NG):
                        b = slice(g * CG, (g + 1) * CG)
                        sp.wait_ge(done, g + 1)
                        sp.dma_start(in_blocks(x_out)[:, b, :], x[:, b, 0:D]).then_inc(stored, 16)
                    sp.wait_ge(stored, 16 * NG)


ECOLS = ET
EPAD = ECOLS * P
EROWS = EG * P
LOW = -1e30


def stage_gat_project(nc, k, name, xn, w, w_t, a_cols, heads, acc, esd, table, es_table):
    W2 = D + 2 * heads
    with ExitStack() as ctx:
        sb, _, sem = allocators(nc, ctx, name + "_out")
        w_sb = sb("w", [P, 2, W2])
        stored = sem("stored")
        with ExitStack() as fold:
            sb, ps, sem = allocators(nc, fold, name + "a")
            wt_sb = sb("wt", [P, 2, D])
            a_sb = sb("a", [P, 2, 2 * heads])
            pa = ps("pa", [P, 2, 512])
            loaded, folded = sem("loaded"), sem("folded")
            with nc.Block() as block:
                @block.sync
                def _(sp):
                    sp.dma_start(w_sb[:, :, 0:D], w.rearrange("(c p) n -> p c n", p=P)).then_inc(loaded, 16)
                    sp.dma_start(wt_sb[:, :, :], w_t.rearrange("(c p) n -> p c n", p=P)).then_inc(loaded, 16)
                    sp.dma_start(a_sb[:, :, :], a_cols.rearrange("(c p) n -> p c n", p=P)).then_inc(loaded, 16)

                @block.tensor
                def _(pe):
                    pe.wait_ge(loaded, 48)
                    for m in range(2):
                        for c in range(2):
                            last = nc.tensor.matmul(pa[:, m, 0:2 * heads], wt_sb[:, c, m * P:(m + 1) * P], a_sb[:, c, :],
                                                    start=(c == 0), stop=(c == 1))
                    last.then_inc(folded, 1)

                @block.vector
                def _(dve):
                    dve.wait_ge(folded, 1)
                    nc.vector.tensor_copy(w_sb[:, :, D:W2], pa[:, :, 0:2 * heads])

        def finish(dve, n, out, extra, step):
            nc.vector.tensor_copy(acc[:, bass.ds(n, 1), 0:D], out[:, :, 0:D])
            return nc.vector.tensor_copy(esd[:, bass.ds(n, 1), :], out[:, :, D:W2])

        def store(sp, done):
            for g in range(NG):
                b = slice(g * CG, (g + 1) * CG)
                sp.wait_ge(done, (g + 1) * CG + RING)
                sp.dma_start(in_blocks(table)[:, b, :], acc[:, b, 0:D]).then_inc(stored, 16)
            sp.dma_start(in_blocks(es_table), esd[:, :, :]).then_inc(stored, 16)
            sp.wait_ge(stored, 16 * (NG + 1))
        project_rows(nc, k, name, 2, lambda c: w_sb[:, c, :], W2, finish,
                     load=lambda sp, n, staged, extra: [sp.dma_start(staged, block_rows(xn, n))], loads=1, store=store)


def stage_gat_weights(nc, k, name, heads, es_table, esd, src_flat, dst_flat, prev_flat, run_dram, node_dram, p_dram, weights, p_self, acc):
    H = heads
    ECOLS8 = -(-ECOLS // 16) * 16
    TB = min(8, 512 // (H * NB))
    TB = 8 if TB == 8 else 2
    BANKS1 = 4 if TB < 8 else 2
    PICKED = 480 if TB < 8 else 624
    GATHERED = ECOLS8 - PICKED
    assert PICKED % 16 == 0 and GATHERED % 16 == 0
    with ExitStack() as ctx:
        sb, ps, sem = allocators(nc, ctx, name)
        dst_c = sb("dst_c", [P, ECOLS], i32)
        prev_c = sb("prev_c", [P, ECOLS], i32)
        es_all = sb("es", [P, ECOLS8, H])
        es = es_all[:, 0:ECOLS, :]
        with ExitStack() as pick:
            sb1 = lambda n, s_, t=f32: pick.enter_context(nc.sbuf_tensor(f"{name}_{n}", s_, t))
            src_c = sb1("src_c", [P, ECOLS8], i32)
            src_i = sb1("src_i", [P, ECOLS8], i32)
            idx = sb1("idx", [P, 2, 8], i32)
            got = sb1("got", [P, 2, 8, 2 * H])
            src_blk = sb1("src_blk", [P, ECOLS8])
            src_lane = sb1("src_lane", [P, ECOLS8])
            ident16 = sb1("ident16", [P, P], bf16)
            parts = sb1("parts", [P, 3, H, NB], bf16)
            rest = sb1("rest", [P, H, NB])
            hot = sb1("hot", [P, 2, 8, P], bf16)
            hot_t = sb1("hot_t", [P, 2, 8 * P], bf16)
            blk_hot = sb1("blk_hot", [P, 2, 8, NB])
            picked = sb1("picked", [P, 2, TB, H, NB])
            pt1 = [pick.enter_context(nc.psum_tensor(f"{name}_pt1{h}", [P, 8 * P], bf16)) for h in range(2)]
            po1 = [pick.enter_context(nc.psum_tensor(f"{name}_po1{h}", [P, 512], f32)) for h in range(BANKS1)]
            loaded, v1, hot1, turned1, copied1 = sem("loaded"), sem("v1"), sem("hot1"), sem("turned1"), sem("copied1")
            given, took, kept1 = sem("given"), sem("took"), sem("kept1")
            arrived = [sem("arrived0"), sem("arrived1")]
            blk1, out1, masked1, reduced1, split1 = sem("blk1"), sem("out1"), sem("masked1"), sem("reduced1"), sem("split1")
            halves = lambda engine, one: in_pairs(engine, PICKED // 8, one)
            with nc.Block() as block:
                @block.sync
                def _(sp):
                    sp.dma_start(src_c[:, 0:ECOLS], src_flat[0:EPAD].rearrange("(q i) -> q i", q=P)).then_inc(loaded, 16)
                    sp.dma_start(dst_c[:, :], dst_flat[0:EPAD].rearrange("(q i) -> q i", q=P)).then_inc(loaded, 16)
                    sp.dma_start(prev_c[:, :], prev_flat[0:EPAD].rearrange("(q i) -> q i", q=P)).then_inc(loaded, 16)

                @block.gpsimd
                def _(pool):
                    pool.wait_ge(loaded, 48)

                    def send(n, h):
                        nc.gpsimd.tensor_copy(idx[:, h, :], src_c[:, bass.ds(PICKED + 8 * n, 8)]).then_inc(given, 1)
                        pool.wait_ge(given, n + 1)
                        pool.sem_inc(took, 1)
                        for j in range(8):
                            nc.gpsimd.indirect_dma_start(
                                out=got[:, h, j, :], out_offset=None, in_=es_table,
                                in_offset=bass.IndirectOffsetOnAxis(ap=idx[:, h, j:j + 1], axis=0)).then_inc(arrived[h], 16)

                    def keep(n, h):
                        pool.wait_ge(arrived[h], 16 * 8 * half_index(n, h))
                        nc.gpsimd.tensor_copy(es_all[:, bass.ds(PICKED + 8 * n, 8), :], got[:, h, :, 0:H]).then_inc(kept1, 1)
                        pool.wait_ge(kept1, n + 1)
                    pool.wait_ge(v1, 7)
                    send(0, 0)
                    send(1, 1)
                    with nc.gpsimd.Fori(0, GATHERED // 16 - 1) as i:
                        for h in range(2):
                            keep(2 * i + h, h)
                            send(2 * i + h + 2, h)
                    keep(GATHERED // 8 - 2, 0)
                    keep(GATHERED // 8 - 1, 1)

                @block.tensor
                def _(pe):
                    pe.sem_inc(turned1, 2)
                    pe.wait_ge(v1, 6)
                    pe.wait_ge(split1, 5)

                    def turn(n, h):
                        pe.wait_ge(hot1, n + 1)
                        pe.wait_ge(copied1, n + 1)
                        for j in range(8):
                            last = nc.tensor.transpose(pt1[h][:, j * P:(j + 1) * P], hot[:, h, j, :], ident16[:, :])
                        last.then_inc(turned1, 1)

                    def multiply(n, h):
                        pe.wait_ge(copied1, n + 3)
                        for b in range(8 // TB):
                            bank = b if TB < 8 else h
                            pe.wait_ge(masked1, 8 // TB * n + b + 1)
                            for j in range(TB):
                                for part in range(3):
                                    last = nc.tensor.matmul(po1[bank][:, j * H * NB:(j + 1) * H * NB],
                                                            hot_t[:, h, (b * TB + j) * P:(b * TB + j + 1) * P],
                                                            parts[:, part, :, :].rearrange("p h b -> p (h b)"),
                                                            start=(part == 0), stop=(part == 2))
                            last.then_inc(out1, 1)

                    turn(0, 0)
                    turn(1, 1)
                    with nc.tensor.Fori(0, PICKED // 16 - 1) as i:
                        for h in range(2):
                            multiply(2 * i + h, h)
                            turn(2 * i + h + 2, h)
                    multiply(PICKED // 8 - 2, 0)
                    multiply(PICKED // 8 - 1, 1)

                @block.scalar
                def _(act):
                    act.sem_inc(copied1, 2)

                    def copy(n, h):
                        act.wait_ge(turned1, n + 3)
                        act.wait_ge(out1, 8 // TB * (n + 1))
                        nc.scalar.activation(hot_t[:, h, :], pt1[h][:, :], ACT.Copy).then_inc(copied1, 1)
                    halves(nc.scalar, copy)

                @block.vector
                def _(dve):
                    dve.sem_inc(out1, 16 // TB)
                    dve.sem_inc(masked1, BANKS1)
                    dve.wait_ge(loaded, 48)
                    nc.vector.tensor_single_scalar(src_i[:, 0:ECOLS], src_c[:, 0:ECOLS], 7, op=ALU.arith_shift_right).then_inc(v1, 1)
                    nc.vector.memset(src_i[:, ECOLS:], 0).then_inc(v1, 1)
                    dve.wait_ge(v1, 2)
                    nc.vector.tensor_copy(src_blk[:, :], src_i[:, :]).then_inc(v1, 1)
                    dve.wait_ge(v1, 3)
                    nc.vector.tensor_single_scalar(src_i[:, 0:ECOLS], src_c[:, 0:ECOLS], P - 1, op=ALU.bitwise_and).then_inc(v1, 1)
                    dve.wait_ge(v1, 4)
                    nc.vector.tensor_copy(src_lane[:, :], src_i[:, :]).then_inc(v1, 1)
                    nc.vector.tensor_copy(ident16[:, :], k.ident[:, :]).then_inc(v1, 1)
                    nc.vector.memset(src_c[:, ECOLS:], 0).then_inc(v1, 1)
                    dve.wait_ge(v1, 7)
                    es_h = esd[:, :, 0:H].rearrange("p b h -> p h b")
                    nc.vector.tensor_copy(parts[:, 0, :, :], es_h).then_inc(split1, 1)
                    dve.wait_ge(split1, 1)
                    nc.vector.tensor_tensor(rest[:, :, :], es_h, parts[:, 0, :, :], ALU.subtract).then_inc(split1, 1)
                    dve.wait_ge(split1, 2)
                    nc.vector.tensor_copy(parts[:, 1, :, :], rest[:, :, :]).then_inc(split1, 1)
                    dve.wait_ge(split1, 3)
                    nc.vector.tensor_tensor(rest[:, :, :], rest[:, :, :], parts[:, 1, :, :], ALU.subtract).then_inc(split1, 1)
                    dve.wait_ge(split1, 4)
                    nc.vector.tensor_copy(parts[:, 2, :, :], rest[:, :, :]).then_inc(split1, 1)

                    def find(n, h):
                        dve.wait_ge(turned1, n + 1)
                        nc.vector.tensor_tensor(hot[:, h, :, :], k.iota[:, :].unsqueeze(1).to_broadcast([P, 8, P]),
                                                src_lane[:, bass.ds(8 * n, 8)].unsqueeze(2).to_broadcast([P, 8, P]),
                                                ALU.is_equal).then_inc(hot1, 1)

                    slot_of = lambda b, h: b % 2 if TB < 8 else h

                    def mask(n, h, b):
                        m = 8 // TB * n + b
                        dve.wait_ge(out1, 16 // TB + m + 1)
                        dve.wait_ge(reduced1, m + 1)
                        nc.vector.tensor_tensor(
                            picked[:, slot_of(b, h), :, :, :],
                            po1[b if TB < 8 else h][:, 0:TB * H * NB].rearrange("p (j h b) -> p j h b", j=TB, h=H),
                            blk_hot[:, h, b * TB:(b + 1) * TB, :].unsqueeze(2).to_broadcast([P, TB, H, NB]), ALU.mult).then_inc(masked1, 1)

                    def total(n, h, b):
                        dve.wait_ge(masked1, BANKS1 + 8 // TB * n + b + 1)
                        nc.vector.tensor_reduce(es_all[:, bass.ds(8 * n + b * TB, TB), :], picked[:, slot_of(b, h), :, :, :],
                                                AX.X, ALU.add).then_inc(reduced1, 1)

                    def take(n, h, first=False):
                        if not (isinstance(n, int) and n < 2):
                            dve.wait_ge(masked1, BANKS1 + 8 // TB * (n - 1))
                        nc.vector.tensor_tensor(blk_hot[:, h, :, :], k.iota[:, 0:NB].unsqueeze(1).to_broadcast([P, 8, NB]),
                                                src_blk[:, bass.ds(8 * n, 8)].unsqueeze(2).to_broadcast([P, 8, NB]),
                                                ALU.is_equal).then_inc(blk1, 1)
                        dve.wait_ge(blk1, n + 1)
                        for b in range(8 // TB):
                            mask(n, h, b)
                            if b:
                                total(n, h, b - 1)
                            elif not first:
                                total(n - 1, 1 - h, 8 // TB - 1)
                    dve.sem_inc(reduced1, 2)
                    find(0, 0)
                    find(1, 1)
                    find(2, 0)
                    take(0, 0, first=True)
                    with nc.vector.Fori(0, PICKED // 16 - 2) as i:
                        find(2 * i + 3, 1)
                        take(2 * i + 1, 1)
                        find(2 * i + 4, 0)
                        take(2 * i + 2, 0)
                    find(PICKED // 8 - 1, 1)
                    take(PICKED // 8 - 3, 1)
                    take(PICKED // 8 - 2, 0)
                    take(PICKED // 8 - 1, 1)
                    total(PICKED // 8 - 1, 1, 8 // TB - 1)

        same = sb("same", [P, ECOLS])
        pen = sb("pen", [P, ECOLS])
        run = sb("run", [P, ECOLS, 2 * H])
        node = sb("node", [P, NB, 2 * H])
        nodes = sb("nodes", [P, ECOLS, 2 * H])
        top = nodes[:, :, :].rearrange("p i h -> p (i h)")[:, 0:ECOLS * H].rearrange("p (i h) -> p i h", h=H)
        ends = sb("ends", [P, 3 * H + 2])
        ends_t = sb("ends_t", [3 * H + 2, P])
        whole = sb("whole", [P, 1])
        end_idx = sb("end_idx", [P, NB], i32)
        start_idx = sb("start_idx", [P, NB], i32)
        cnt = sb("cnt", [P, NB])
        beg = sb("beg", [P, NB])
        none = sb("none", [P, NB])
        tmp = sb("tmp", [P, NB])
        seg = sb("seg", [P, NB, H])
        rows = sb("rows", [2 * H, 4, P])
        carry = sb("carry", [P, 2 * H])
        tiles = sb("tiles", [P, SG, P * H])
        pt = ps("pt", [P, 512])
        pw = ps("pw", [P, 2, 512])

        v2, turned2, stored2, seg2 = sem("v2"), sem("turned2"), sem("stored2"), sem("seg2")
        c = Tally()
        with nc.Block() as block:
            @block.vector
            def _(dve):
                nc.vector.tensor_tensor(same[:, :], dst_c[:, :], prev_c[:, :], ALU.is_equal).then_inc(v2, c.one())
                dve.wait_ge(v2, c.n)
                nc.vector.tensor_scalar(pen[:, :], same[:, :], -LOW, LOW, ALU.mult, ALU.add).then_inc(v2, c.one())
                nc.vector.tensor_reduce(ends[:, H:H + 1], same[:, :], AX.X, ALU.min).then_inc(v2, c.one())
                dve.wait_ge(v2, c.n)
                nc.vector.tensor_copy(whole[:, :], ends[:, H:H + 1]).then_inc(v2, c.one())
                for q in range(H):
                    nc.vector.tensor_tensor_scan(top[:, :, q], pen[:, :], es[:, :, q], LOW, ALU.add, ALU.max).then_inc(v2, c.one())
                dve.wait_ge(v2, c.n)
                nc.vector.tensor_copy(ends[:, 0:H], top[:, ECOLS - 1, :]).then_inc(v2, c.one())
                dve.wait_ge(turned2, 2)
                nc.vector.tensor_copy(ends_t[0:H + 1, :], pt[0:H + 1, 0:P]).then_inc(v2, c.one())
                dve.wait_ge(turned2, 2)
                nc.vector.tensor_copy(rows[0:H, 0, :], pt[0:H, P:2 * P]).then_inc(v2, c.one())
                dve.wait_ge(v2, c.n)
                nc.vector.tensor_scalar(rows[0:H, 1, :], rows[0:H, 0, :], -LOW, LOW, ALU.mult, ALU.add).then_inc(v2, c.one())
                nc.vector.memset(rows[0:H, 3, :], LOW).then_inc(v2, c.one())
                dve.wait_ge(v2, c.n)
                nc.vector.tensor_tensor_scan(rows[0:H, 2, :], rows[0:H, 1, :], ends_t[0:H, :], LOW, ALU.add, ALU.max).then_inc(v2, c.one())
                dve.wait_ge(v2, c.n)
                nc.vector.tensor_copy(rows[0:H, 3, 1:P], rows[0:H, 2, 0:P - 1]).then_inc(v2, c.one())
                dve.wait_ge(turned2, 3)
                nc.vector.tensor_copy(carry[:, 0:H], pt[:, 2 * P:2 * P + H]).then_inc(v2, c.one())
                dve.wait_ge(v2, c.n)
                for q in range(H):
                    nc.vector.tensor_tensor_scan(top[:, :, q], pen[:, :], es[:, :, q], carry[:, q:q + 1], ALU.add, ALU.max).then_inc(v2, c.one())
                nc.vector.tensor_copy(cnt[:, :], k.row_count[:, :]).then_inc(v2, c.one())
                nc.vector.tensor_copy(beg[:, :], k.row_start[:, :]).then_inc(v2, c.one())
                dve.wait_ge(v2, c.n)
                nc.vector.tensor_scalar(none[:, :], cnt[:, :], 0.5, None, ALU.is_lt).then_inc(v2, c.one())
                nc.vector.tensor_tensor(tmp[:, :], beg[:, :], cnt[:, :], ALU.add).then_inc(v2, c.one())
                dve.wait_ge(v2, c.n)
                nc.vector.tensor_scalar(tmp[:, :], tmp[:, :], -1.0, 0.0, ALU.add, ALU.max).then_inc(v2, c.one())
                nc.vector.scalar_tensor_tensor(out=beg[:, :], in0=none[:, :], scalar=float(OUTSIDE), in1=beg[:, :],
                                               op0=ALU.mult, op1=ALU.add).then_inc(v2, c.one())
                dve.wait_ge(v2, c.n)
                nc.vector.tensor_copy(end_idx[:, :], tmp[:, :]).then_inc(v2, c.one())
                nc.vector.tensor_copy(start_idx[:, :], beg[:, :]).then_inc(v2, c.one())

            @block.tensor
            def _(pe):
                pe.wait_ge(v2, 4 + H + 1)
                nc.tensor.transpose(pt[0:H + 1, 0:P], ends[:, 0:H + 1], k.ident[:, :]).then_inc(turned2, 1)
                nc.tensor.matmul(pt[0:H, P:2 * P], whole[:, :].to_broadcast([P, H]), k.ident[:, :], start=True, stop=True).then_inc(turned2, 1)
                pe.wait_ge(v2, 4 + H + 1 + 6)
                nc.tensor.transpose(pt[:, 2 * P:2 * P + H], rows[0:H, 3, :], k.ident[0:H, 0:H]).then_inc(turned2, 1)

            @block.sync
            def _(sp):
                sp.wait_ge(v2, 4 + H + 1 + 7 + H)
                sp.dma_start(run_dram.rearrange("(q i) h -> q i h", q=P), top[:, :, :]).then_inc(stored2, 16)

            @block.gpsimd
            def _(pool):
                pool.wait_ge(v2, 4 + H + 1 + 7 + H + 8)
                pool.wait_ge(stored2, 16)
                for b in range(NB):
                    nc.gpsimd.indirect_dma_start(out=seg[:, b, :], out_offset=None, in_=run_dram,
                                                 in_offset=bass.IndirectOffsetOnAxis(ap=end_idx[:, b:b + 1], axis=0)).then_inc(seg2, 16)
                pool.wait_ge(seg2, 16 * NB)

        v3, exp3, sent3, back3 = sem("v3"), sem("exp3"), sem("sent3"), sem("back3")
        c3 = Tally()
        wide = lambda t: t[:, :].unsqueeze(2).to_broadcast([P, NB, H])
        with nc.Block() as block:
            @block.vector
            def _(dve):
                for q in range(H):
                    nc.vector.scalar_tensor_tensor(out=seg[:, :, q], in0=none[:, :], scalar=2 * LOW, in1=seg[:, :, q],
                                                   op0=ALU.mult, op1=ALU.add).then_inc(v3, c3.one())
                nc.vector.tensor_tensor(p_self[:, :, :], esd[:, :, 0:H], esd[:, :, H:2 * H], ALU.add).then_inc(v3, c3.one())
                nc.vector.tensor_copy(node[:, :, 0:H], esd[:, :, H:2 * H]).then_inc(v3, c3.one())
                dve.wait_ge(v3, c3.n)
                nc.vector.tensor_tensor(seg[:, :, :], seg[:, :, :], esd[:, :, 0:H], ALU.max).then_inc(v3, c3.one())
                nc.vector.scalar_tensor_tensor(out=p_self[:, :, :], in0=p_self[:, :, :], scalar=0.2, in1=p_self[:, :, :],
                                               op0=ALU.mult, op1=ALU.max).then_inc(v3, c3.one())
                dve.wait_ge(v3, c3.n)
                nc.vector.tensor_tensor(seg[:, :, :], seg[:, :, :], esd[:, :, H:2 * H], ALU.add).then_inc(v3, c3.one())
                dve.wait_ge(v3, c3.n)
                nc.vector.scalar_tensor_tensor(out=node[:, :, H:2 * H], in0=seg[:, :, :], scalar=0.2, in1=seg[:, :, :],
                                               op0=ALU.mult, op1=ALU.max).then_inc(v3, c3.one())
                dve.wait_ge(v3, c3.n)
                nc.vector.tensor_tensor(p_self[:, :, :], p_self[:, :, :], node[:, :, H:2 * H], ALU.subtract).then_inc(v3, c3.one())

            @block.scalar
            def _(act):
                act.wait_ge(v3, H + 7)
                nc.scalar.activation(p_self[:, :, :], p_self[:, :, :], ACT.Exp).then_inc(exp3, 1)
                act.wait_ge(exp3, 1)
                nc.scalar.activation(acc[:, :, D:D + H], p_self[:, :, :], ACT.Copy)
                with nc.scalar.Fori(0, NB) as n:
                    for q in range(H):
                        a = acc[:, bass.ds(n, 1), q * (D // H):(q + 1) * (D // H)]
                        nc.scalar.activation(a, a, ACT.Copy, scale=p_self[:, bass.ds(n, 1), q:q + 1].rearrange("p a h -> p (a h)"))

            @block.gpsimd
            def _(pool):
                pool.wait_ge(v3, H + 6)
                for b in range(NB):
                    nc.gpsimd.indirect_dma_start(
                        out=node_dram[:, 0:2 * H], out_offset=bass.IndirectOffsetOnAxis(ap=start_idx[:, b:b + 1], axis=0),
                        in_=node[:, b, :], in_offset=None, bounds_check=EPAD - 1, oob_is_err=False).then_inc(sent3, 16)

            @block.sync
            def _(sp):
                sp.wait_ge(sent3, 16 * NB)
                sp.dma_start(nodes[:, :, :], node_dram.rearrange("(q i) h -> q i h", q=P)).then_inc(back3, 16)
                sp.wait_ge(back3, 16)

        v4, turned4, exp4, stored4 = sem("v4"), sem("turned4"), sem("exp4"), sem("stored4")
        c4 = Tally()
        with nc.Block() as block:
            @block.vector
            def _(dve):
                for q in range(2 * H):
                    nc.vector.tensor_tensor_scan(run[:, :, q], same[:, :], nodes[:, :, q], 0.0, ALU.mult, ALU.add).then_inc(v4, c4.one())
                dve.wait_ge(v4, c4.n)
                nc.vector.tensor_copy(ends[:, 0:2 * H], run[:, ECOLS - 1, :]).then_inc(v4, c4.one())
                dve.wait_ge(turned4, 2)
                nc.vector.tensor_copy(ends_t[0:2 * H, :], pt[0:2 * H, 0:P]).then_inc(v4, c4.one())
                nc.vector.tensor_copy(rows[0:2 * H, 0, :], pt[0:2 * H, P:2 * P]).then_inc(v4, c4.one())
                nc.vector.memset(rows[0:2 * H, 3, :], 0.0).then_inc(v4, c4.one())
                dve.wait_ge(v4, c4.n)
                nc.vector.tensor_tensor_scan(rows[0:2 * H, 2, :], rows[0:2 * H, 0, :], ends_t[0:2 * H, :], 0.0, ALU.mult, ALU.add).then_inc(v4, c4.one())
                dve.wait_ge(v4, c4.n)
                nc.vector.tensor_copy(rows[0:2 * H, 3, 1:P], rows[0:2 * H, 2, 0:P - 1]).then_inc(v4, c4.one())
                dve.wait_ge(turned4, 3)
                nc.vector.tensor_copy(carry[:, :], pt[:, 2 * P:2 * P + 2 * H]).then_inc(v4, c4.one())
                dve.wait_ge(v4, c4.n)
                for q in range(2 * H):
                    nc.vector.tensor_tensor_scan(run[:, :, q], same[:, :], nodes[:, :, q], carry[:, q:q + 1], ALU.mult, ALU.add).then_inc(v4, c4.one())
                dve.wait_ge(v4, c4.n)
                nc.vector.tensor_tensor(es[:, :, :], es[:, :, :], run[:, :, 0:H], ALU.add).then_inc(v4, c4.one())
                dve.wait_ge(v4, c4.n)
                nc.vector.scalar_tensor_tensor(out=es[:, :, :], in0=es[:, :, :], scalar=0.2, in1=es[:, :, :],
                                               op0=ALU.mult, op1=ALU.max).then_inc(v4, c4.one())
                dve.wait_ge(v4, c4.n)
                nc.vector.tensor_tensor(es[:, :, :], es[:, :, :], run[:, :, H:2 * H], ALU.subtract).then_inc(v4, c4.one())

            @block.tensor
            def _(pe):
                pe.wait_ge(v4, 2 * H + 1)
                nc.tensor.transpose(pt[0:2 * H, 0:P], ends[:, 0:2 * H], k.ident[:, :]).then_inc(turned4, 1)
                nc.tensor.matmul(pt[0:2 * H, P:2 * P], whole[:, :].to_broadcast([P, 2 * H]), k.ident[:, :], start=True, stop=True).then_inc(turned4, 1)
                pe.wait_ge(v4, 2 * H + 1 + 5)
                nc.tensor.transpose(pt[:, 2 * P:2 * P + 2 * H], rows[0:2 * H, 3, :], k.ident[0:2 * H, 0:2 * H]).then_inc(turned4, 1)

            @block.scalar
            def _(act):
                act.wait_ge(v4, 4 * H + 10)
                nc.scalar.activation(es[:, :, :], es[:, :, :], ACT.Exp).then_inc(exp4, 1)

            @block.sync
            def _(sp):
                sp.wait_ge(exp4, 1)
                sp.dma_start(p_dram[0:EPAD, :].rearrange("(q i) h -> q i h", q=P), es[:, :, :]).then_inc(stored4, 16)
                sp.wait_ge(stored4, 16)

        got5, turned5, v5 = sem("got5"), sem("turned5"), sem("v5")
        by_tile = p_dram.rearrange("(t l) h -> t (l h)", l=P)
        w3 = weights[:, :].rearrange("p (s h) -> p s h", h=H)
        with nc.Block() as block:
            @block.gpsimd
            def _(pool):
                for g in range(SG):
                    nc.gpsimd.indirect_dma_start(out=tiles[:, g, :], out_offset=None, in_=by_tile,
                                                 in_offset=bass.IndirectOffsetOnAxis(ap=k.tile_idx[:, g:g + 1], axis=0)).then_inc(got5, 16)

            @block.tensor
            def _(pe):
                pe.wait_ge(got5, 16 * SG)
                for n in range(SG * H):
                    g, q = n // H, n % H
                    if n >= 2:
                        pe.wait_ge(v5, n - 1)
                    nc.tensor.transpose(pw[:, n % 2, 0:P], tiles[:, g, :].rearrange("s (l h) -> s l h", h=H)[:, :, q], k.ident[:, :]).then_inc(turned5, 1)

            @block.vector
            def _(dve):
                for n in range(SG * H):
                    g, q = n // H, n % H
                    dve.wait_ge(turned5, n + 1)
                    nc.vector.tensor_copy(w3[:, g * P:(g + 1) * P, q], pw[:, n % 2, 0:P]).then_inc(v5, 1)


HEADS1, DH1 = 4, 32
INNER1 = HEADS1 * DH1
MEM = 4
assert INNER1 == P


def sum_squares(nc, act, x, sq, ss, summed, turn):
    act.sem_inc(summed, CG)
    with nc.scalar.Fori(0, NG) as g:
        act.wait_ge(summed, CG * (g + 1))
        act.sem_inc(turn, 1)
        for j in range(CG):
            n = g * CG + j
            nc.scalar.activation(sq[:, j:j + 1, :], x[:, bass.ds(n, 1), 0:D], ACT.Square,
                                 accum_out=ss[:, bass.ds(n, 1)]).then_inc(summed, 1)


def inverse_norm(nc, dve, v, c, rooted, ss, dev, rn, t):
    dve.wait_ge(v, c.n)
    nc.vector.tensor_scalar(ss[:, :], ss[:, :], 1e-24, None, ALU.max).then_inc(v, c.one())
    at = c.n
    dve.wait_ge(rooted, 1)
    nc.vector.reciprocal(rn[:, :], dev[:, :]).then_inc(v, c.one())
    dve.wait_ge(v, c.n)
    sharpen_inverse_root(nc, dve, v, c.n, ss[:, :], rn[:, :], t[:, :])
    c.n += 4
    return at


def stage_mix1(nc, k, xn, acc, w_qkv, g_pre, mem_k, mem_k_t, mem_v_t, w_out, b_out, g_out, x_out):
    with ExitStack() as ctx:
        sb, ps, sem = allocators(nc, ctx, "mix1")
        kv = sb("kv", [P, NB, D + 1])
        q = sb("q", [P, NB, INNER1])
        w_sb = sb("w", [P, 2, 3 * INNER1])
        gp = sb("gp", [P, 2])
        wo = sb("wo", [P, D])
        bo = sb("bo", [P, D])
        go = sb("go", [P, D])
        mk = sb("mk", [P, MEM])
        mkt = sb("mkt", [MEM, INNER1])
        mvt = sb("mvt", [MEM, INNER1 + 1])
        sq = q[:, 0:2 * CG, :].rearrange("p (g b) c -> p g (b c)", b=D // INNER1)
        ss = sb("ss", [P, NB])
        dev = sb("dev", [P, NB])
        rn = sb("rn", [P, NB])
        t = sb("t", [P, NB])
        real = k.before[:, LASTROWS:LASTROWS + 1]
        heads = lambda a: a.rearrange("p b (h d) -> p (b h) d", d=DH1)

        loaded, v0, root0, summed0 = sem("loaded"), sem("v0"), sem("root0"), sem("summed0")
        turn0, turn4 = sem("turn0"), sem("turn4")
        c0 = Tally()
        at0 = []
        with nc.Block() as block:
            @block.sync
            def _(sp):
                for to, src in ((w_sb[:, :, :], w_qkv.rearrange("(c p) n -> p c n", p=P)), (gp[:, :], g_pre), (wo[:, :], w_out),
                                (bo[:, :], on_all(b_out)), (go[:, :], on_all(g_out)), (mk[:, :], mem_k), (mkt[:, :], mem_k_t),
                                (mvt[:, 0:INNER1], mem_v_t)):
                    sp.dma_start(to, src).then_inc(loaded, 16)

            @block.vector
            def _(dve):
                dve.wait_ge(summed0, NB + CG)
                at0.append(inverse_norm(nc, dve, v0, c0, root0, ss, dev, rn, t))
                nc.vector.memset(kv[:, :, D:D + 1], 1.0)
                nc.vector.memset(mvt[:, INNER1:], 1.0)
                dve.wait_ge(loaded, 16 * 8)
                for c in range(2):
                    nc.vector.tensor_scalar(w_sb[:, c, :], w_sb[:, c, :], gp[:, c:c + 1], float(D) ** 0.5, ALU.mult, ALU.mult)
                nc.vector.tensor_scalar(go[:, :], go[:, :], float(D) ** 0.5, None, ALU.mult)

            @block.scalar
            def _(act):
                sum_squares(nc, act, xn, sq, ss, summed0, turn0)
                act.wait_ge(v0, at0[0])
                nc.scalar.activation(dev[:, :], ss[:, :], ACT.Sqrt).then_inc(root0, 1)

        def scale(n, out):
            return nc.vector.tensor_scalar(out.unsqueeze(1), xn[:, bass.ds(n, 1), :], rn[:, bass.ds(n, 1)], None, ALU.mult)

        def finish(dve, n, out, extra, step):
            nc.vector.tensor_copy(kv[:, bass.ds(n, 1), 0:D], out[:, :, INNER1:3 * INNER1])
            return nc.vector.tensor_copy(q[:, bass.ds(n, 1), :], out[:, :, 0:INNER1])
        project_rows(nc, k, "qkv1", 2, lambda c: w_sb[:, c, :], 3 * INNER1, finish, scale=scale)

        e_k = sb("e_k", [P, 2, INNER1])
        top = sb("top", [P, INNER1])
        most = sb("most", [P, 2])
        low = sb("low", [P, 1])
        diag = sb("diag", [P, P])
        tops = sb("tops", [P, INNER1])
        qm = sb("qm", [P, NB * HEADS1])
        rz = sb("rz", [P, 1])
        mix = sb("mix", [P, D])
        att, att_t = top, diag
        middle = ctx.enter_context(ExitStack())
        pt = middle.enter_context(nc.psum_tensor("mix1_pt", [P, 2, 512], f32))
        po = middle.enter_context(nc.psum_tensor("mix1_po", [P, 2, 512], f32))
        pc = middle.enter_context(nc.psum_tensor("mix1_pc", [P, 512], f32))
        v1, turned1, exp1 = sem("v1"), sem("turned1"), sem("exp1")
        c1 = Tally()
        with nc.Block() as block:
            @block.vector
            def _(dve):
                nc.vector.tensor_scalar(low[:, :], real, -LOW, LOW, ALU.mult, ALU.add).then_inc(v1, c1.one())
                dve.wait_ge(v1, c1.n)
                last = kv[:, NB - 1, 0:INNER1]
                nc.vector.tensor_scalar(last, last, real, low[:, :], ALU.mult, ALU.add).then_inc(v1, c1.one())
                dve.wait_ge(v1, c1.n)
                nc.vector.tensor_reduce(top[:, :], kv[:, :, 0:INNER1].rearrange("p b c -> p c b"), AX.X, ALU.max).then_inc(v1, c1.one())
                nc.vector.tensor_reduce(most[:, 1:2], mk[:, :], AX.X, ALU.max).then_inc(v1, c1.one())
                nc.vector.tensor_reduce(qm[:, :], heads(q[:, :, :]), AX.X, ALU.max).then_inc(v1, c1.one())
                dve.wait_ge(v1, c1.n)
                nc.vector.tensor_tensor(heads(q[:, :, :]), heads(q[:, :, :]), qm[:, :].unsqueeze(2).to_broadcast([P, NB * HEADS1, DH1]),
                                        ALU.subtract).then_inc(v1, c1.one())
                dve.wait_ge(turned1, 1)
                nc.vector.tensor_reduce(most[:, 0:1], pt[:, 0, 0:P], AX.X, ALU.max).then_inc(v1, c1.one())
                dve.wait_ge(v1, c1.n)
                nc.vector.tensor_tensor(most[:, 0:1], most[:, 0:1], most[:, 1:2], ALU.max).then_inc(v1, c1.one())
                dve.wait_ge(v1, c1.n)
                nc.vector.tensor_scalar(diag[:, :], k.ident[:, :], most[:, 0:1], None, ALU.mult).then_inc(v1, c1.one())
                dve.wait_ge(turned1, 2)
                nc.vector.tensor_copy(tops[:, :], pt[:, 1, 0:P]).then_inc(v1, c1.one())
                dve.wait_ge(v1, c1.n)
                nc.vector.tensor_tensor(mkt[:, :], mkt[:, :], tops[0:MEM, :], ALU.subtract).then_inc(v1, c1.one())
                nc.vector.tensor_tensor(kv[:, :, 0:INNER1], kv[:, :, 0:INNER1], tops[:, :].unsqueeze(1).to_broadcast([P, NB, INNER1]),
                                        ALU.subtract).then_inc(v1, c1.one())
                dve.wait_ge(exp1, 1)
                nc.vector.tensor_reduce(qm[:, :], heads(q[:, :, :]), AX.X, ALU.add).then_inc(v1, c1.one())
                dve.wait_ge(v1, c1.n)
                nc.vector.reciprocal(qm[:, :], qm[:, :])

            @block.tensor
            def _(pe):
                pe.wait_ge(v1, 3)
                nc.tensor.transpose(pt[:, 0, 0:P], top[:, :], k.ident[:, :]).then_inc(turned1, 1)
                pe.wait_ge(v1, 9)
                nc.tensor.matmul(pt[:, 1, 0:P], k.ones[:, :], diag[:, :], start=True, stop=True).then_inc(turned1, 1)

            @block.scalar
            def _(act):
                act.wait_ge(v1, 6)
                nc.scalar.activation(q[:, :, :], q[:, :, :], ACT.Exp).then_inc(exp1, 1)
                act.wait_ge(v1, 11)
                nc.scalar.activation(mkt[:, :], mkt[:, :], ACT.Exp).then_inc(exp1, 1)

        e_ready, e_used, seen2 = sem("e_ready"), sem("e_used"), sem("seen2")
        with nc.Block() as block:
            @block.scalar
            def _(act):
                def exponentiate(n, h):
                    act.wait_ge(e_used, n + 1)
                    act.sem_inc(seen2, 1)
                    nc.scalar.activation(e_k[:, h:h + 1, :], kv[:, bass.ds(n, 1), 0:INNER1], ACT.Exp).then_inc(e_ready, 1)
                paired(nc.scalar, exponentiate)

            @block.tensor
            def _(pe):
                pe.sem_inc(e_used, 2)
                nc.tensor.matmul(pc[:, 0:INNER1 + 1], mkt[:, :], mvt[:, :], start=True, stop=False)

                def multiply(n, h):
                    pe.wait_ge(e_ready, n + 1)
                    nc.tensor.matmul(pc[:, 0:INNER1 + 1], e_k[:, h, :], kv[:, bass.ds(n, 1), INNER1:D + 1].rearrange("p a d -> p (a d)"),
                                     start=False, stop=isinstance(n, int)).then_inc(e_used, 1)
                paired(nc.tensor, multiply)

        v2, made2 = sem("v2"), sem("made2")
        with nc.Block() as block:
            @block.vector
            def _(dve):
                nc.vector.memset(att[:, :], 0.0).then_inc(v2, 1)
                nc.vector.reciprocal(rz[:, :], pc[:, INNER1:INNER1 + 1]).then_inc(v2, 1)
                dve.wait_ge(v2, 2)
                nc.vector.tensor_scalar(rz[:, :], rz[:, :], DH1 ** -0.5, None, ALU.mult).then_inc(v2, 1)
                dve.wait_ge(v2, 3)
                for h in range(HEADS1):
                    s = slice(h * DH1, (h + 1) * DH1)
                    nc.vector.tensor_scalar(att[s, s], pc[s, s], rz[s, :], None, ALU.mult).then_inc(v2, 1)
                dve.wait_ge(made2, 1)
                nc.vector.tensor_copy(att_t[:, :], pt[:, 0, 0:P]).then_inc(v2, 1)
                dve.wait_ge(made2, 2)
                nc.vector.tensor_copy(mix[:, :], po[:, 0, 0:D])

            @block.tensor
            def _(pe):
                pe.wait_ge(v2, 3 + HEADS1)
                nc.tensor.transpose(pt[:, 0, 0:P], att[:, :], k.ident[:, :]).then_inc(made2, 1)
                pe.wait_ge(v2, 4 + HEADS1)
                nc.tensor.matmul(po[:, 0, 0:D], att_t[:, :], wo[:, :], start=True, stop=True).then_inc(made2, 1)

        middle.close()

        def scale_q(n, out):
            return nc.vector.tensor_tensor(out.rearrange("p (h d) -> p h d", d=DH1),
                                           q[:, bass.ds(n, 1), :].rearrange("p a (h d) -> p (a h) d", d=DH1),
                                           qm[:, bass.ds(n * HEADS1, HEADS1)].unsqueeze(2).to_broadcast([P, HEADS1, DH1]), ALU.mult)

        def finish_out(dve, n, out, extra, step):
            return nc.vector.tensor_tensor(kv[:, bass.ds(n, 1), 0:D], out, bo[:, :].unsqueeze(1), ALU.add)
        project_rows(nc, k, "out1", 1, lambda c: mix[:, :], D, finish_out, scale=scale_q)

        v4, root4, added4, stored4, summed4 = sem("v4"), sem("root4"), sem("added4"), sem("stored4"), sem("summed4")
        c4 = Tally()
        at4 = []
        with nc.Block() as block:
            @block.vector
            def _(dve):
                for g in range(NG):
                    b = slice(g * CG, (g + 1) * CG)
                    nc.vector.tensor_tensor(acc[:, b, 0:D], acc[:, b, 0:D], xn[:, b, :], ALU.add).then_inc(v4, c4.one())
                dve.wait_ge(summed4, NB + CG)
                at4.append(inverse_norm(nc, dve, v4, c4, root4, ss, dev, rn, t))
                for b in range(NB):
                    nc.vector.scalar_tensor_tensor(out=kv[:, b, 0:D], in0=kv[:, b, 0:D], scalar=rn[:, b:b + 1], in1=go[:, :],
                                                   op0=ALU.mult, op1=ALU.mult).then_inc(v4, c4.one())
                for g in range(NG):
                    b = slice(g * CG, (g + 1) * CG)
                    dve.wait_ge(v4, c4.n)
                    nc.vector.tensor_tensor(acc[:, b, 0:D], acc[:, b, 0:D], kv[:, b, 0:D], ALU.add).then_inc(added4, 1)

            @block.scalar
            def _(act):
                sum_squares(nc, act, kv, sq, ss, summed4, turn4)
                act.wait_ge(v4, at4[0])
                nc.scalar.activation(dev[:, :], ss[:, :], ACT.Sqrt).then_inc(root4, 1)

            @block.sync
            def _(sp):
                for g in range(NG):
                    b = slice(g * CG, (g + 1) * CG)
                    sp.wait_ge(added4, g + 1)
                    sp.dma_start(in_blocks(x_out)[:, b, :], acc[:, b, 0:D]).then_inc(stored4, 16)
                sp.wait_ge(stored4, 16 * NG)


def divide_sums(nc, dve, v, c, acc, rz, bias, heads):
    nc.vector.reciprocal(rz[:, :, :], acc[:, :, D:D + heads]).then_inc(v, c.one())
    dve.wait_ge(v, c.n)
    for q in range(heads):
        s = slice(q * (D // heads), (q + 1) * (D // heads))
        nc.vector.tensor_tensor(acc[:, :, s], acc[:, :, s], rz[:, :, q:q + 1].to_broadcast([P, NB, D // heads]), ALU.mult).then_inc(v, c.one())
    dve.wait_ge(v, c.n)
    nc.vector.tensor_tensor(acc[:, :, 0:D], acc[:, :, 0:D], bias[:, :].unsqueeze(1).to_broadcast([P, NB, D]), ALU.add).then_inc(v, c.one())
    dve.wait_ge(v, c.n)


def stage_gat_norm(nc, k, acc, xn, bias, gamma, beta):
    with ExitStack() as ctx:
        sb, ps, sem = allocators(nc, ctx, "gnorm")
        rz = sb("rz", [P, NB, HEADS1])
        bi, ga, be = sb("bi", [P, D]), sb("ga", [P, D]), sb("be", [P, D])
        part = sb("part", [P, D])
        mean = sb("mean", [P, D])
        var, dev, rstd, t = sb("var", [P, D]), sb("dev", [P, D]), sb("rstd", [P, D]), sb("t", [P, D])
        pm = ps("pm", [P, 2, 512])
        loaded, v, squared, summed, rooted, exped = (sem(n) for n in ("loaded", "v", "squared", "summed", "rooted", "exped"))
        real = k.before[:, LASTROWS:LASTROWS + 1]
        c = Tally()
        at = {}
        a = acc[:, :, 0:D]
        wide = lambda r: r[:, :].unsqueeze(1).to_broadcast([P, NB, D])
        with nc.Block() as block:
            @block.sync
            def _(sp):
                for to, src in ((bi, bias), (ga, gamma), (be, beta)):
                    sp.dma_start(to[:, :], on_all(src)).then_inc(loaded, 16)

            @block.vector
            def _(dve):
                dve.wait_ge(loaded, 48)
                divide_sums(nc, dve, v, c, acc, rz, bi, HEADS1)

                def clear_padding():
                    nc.vector.tensor_scalar(acc[:, NB - 1, 0:D], acc[:, NB - 1, 0:D], real, None, ALU.mult).then_inc(v, c.one())
                    dve.wait_ge(v, c.n)
                clear_padding()
                nc.vector.tensor_reduce(part[:, :], a.rearrange("p b d -> p d b"), AX.X, ALU.add).then_inc(v, c.one())
                at["sum"] = c.n
                dve.wait_ge(summed, 1)
                nc.vector.tensor_scalar(mean[:, :], pm[:, 0, 0:D], 1.0 / NODES, None, ALU.mult).then_inc(v, c.one())
                dve.wait_ge(v, c.n)
                nc.vector.tensor_tensor(a, a, wide(mean), ALU.subtract).then_inc(v, c.one())
                dve.wait_ge(v, c.n)
                clear_padding()
                at["square"] = c.n
                dve.wait_ge(squared, 1)
                nc.vector.tensor_reduce(part[:, :], xn[:, :, :].rearrange("p b d -> p d b"), AX.X, ALU.add).then_inc(v, c.one())
                at["sum2"] = c.n
                dve.wait_ge(summed, 2)
                nc.vector.tensor_scalar(var[:, :], pm[:, 1, 0:D], 1.0 / NODES, 1e-5, ALU.mult, ALU.add).then_inc(v, c.one())
                at["root"] = c.n
                dve.wait_ge(rooted, 1)
                nc.vector.reciprocal(rstd[:, :], dev[:, :]).then_inc(v, c.one())
                dve.wait_ge(v, c.n)
                sharpen_inverse_root(nc, dve, v, c.n, var[:, :], rstd[:, :], t[:, :])
                c.n += 4
                nc.vector.tensor_tensor(rstd[:, :], rstd[:, :], ga[:, :], ALU.mult).then_inc(v, c.one())
                dve.wait_ge(v, c.n)
                nc.vector.tensor_tensor(a, a, wide(rstd), ALU.mult).then_inc(v, c.one())
                dve.wait_ge(v, c.n)
                nc.vector.tensor_tensor(a, a, wide(be), ALU.add).then_inc(v, c.one())
                dve.wait_ge(v, c.n)
                nc.vector.tensor_scalar(xn[:, :, :], a, 0.0, None, ALU.min).then_inc(v, c.one())
                at["exp"] = c.n
                nc.vector.tensor_scalar(a, a, 0.0, None, ALU.max).then_inc(v, c.one())
                dve.wait_ge(v, c.n)
                dve.wait_ge(exped, 1)
                nc.vector.scalar_tensor_tensor(out=xn[:, :, :], in0=xn[:, :, :], scalar=-1.0, in1=a, op0=ALU.add, op1=ALU.add)

            @block.tensor
            def _(pe):
                pe.wait_ge(v, at["sum"])
                nc.tensor.matmul(pm[:, 0, 0:D], k.ones[:, :], part[:, :], start=True, stop=True).then_inc(summed, 1)
                pe.wait_ge(v, at["sum2"])
                nc.tensor.matmul(pm[:, 1, 0:D], k.ones[:, :], part[:, :], start=True, stop=True).then_inc(summed, 1)

            @block.scalar
            def _(act):
                act.wait_ge(v, at["square"])
                nc.scalar.activation(xn[:, :, :], a, ACT.Square).then_inc(squared, 1)
                act.wait_ge(v, at["root"])
                nc.scalar.activation(dev[:, :], var[:, :], ACT.Sqrt).then_inc(rooted, 1)
                act.wait_ge(v, at["exp"])
                nc.scalar.activation(xn[:, :, :], xn[:, :, :], ACT.Exp).then_inc(exped, 1)


def stage_gat_out(nc, k, acc, bias, x_in, xin):
    with ExitStack() as ctx:
        sb, ps, sem = allocators(nc, ctx, "gout")
        rz = sb("rz", [P, NB, 1])
        bi = sb("bi", [P, D])
        sq = sb("sq", [P, CG, D])
        ss, dev, rn, t = sb("ss", [P, NB]), sb("dev", [P, NB]), sb("rn", [P, NB]), sb("t", [P, NB])
        loaded, v, rooted, summed = sem("loaded"), sem("v"), sem("rooted"), sem("summed")
        loaded_bias, turn = sem("loaded_bias"), sem("turn")
        c = Tally()
        at, at_sums = [], []
        with nc.Block() as block:
            @block.sync
            def _(sp):
                sp.dma_start(bi[:, :], on_all(bias)).then_inc(loaded_bias, 16)
                sp.dma_start(xin[:, :, :], in_blocks(x_in)).then_inc(loaded, 16)

            @block.vector
            def _(dve):
                dve.wait_ge(loaded_bias, 16)
                divide_sums(nc, dve, v, c, acc, rz, bi, 1)
                at_sums.append(c.n)
                dve.wait_ge(summed, NB + CG)
                at.append(inverse_norm(nc, dve, v, c, rooted, ss, dev, rn, t))
                dve.wait_ge(loaded, 16)
                for b in range(NB):
                    nc.vector.scalar_tensor_tensor(out=acc[:, b, 0:D], in0=acc[:, b, 0:D], scalar=rn[:, b:b + 1], in1=xin[:, b, :],
                                                   op0=ALU.mult, op1=ALU.add)

            @block.scalar
            def _(act):
                act.wait_ge(v, at_sums[0])
                sum_squares(nc, act, acc, sq, ss, summed, turn)
                act.wait_ge(v, at[0])
                nc.scalar.activation(dev[:, :], ss[:, :], ACT.Sqrt).then_inc(rooted, 1)


GB = 7
HALFTOK = GB * P // 2
SLOT_BLOCKS = NB + EXPERTS - 1
SLOT_GROUPS = -(-SLOT_BLOCKS // GB)
assert SLOT_GROUPS * GB * P <= EXPERTS * CAPPAD


def staggered(engine, count, one):
    loops = (count - 1) // 2
    with engine.Fori(0, loops) as i:
        for h in range(2):
            one(2 * i + h, h)
    for n in range(2 * loops, count):
        one(n, n % 2, n == count - 1)


def stage_ffn1(nc, k, name, groups, rows, w1, b1, wg=None, bg=None, logits=None,
               wd=None, bd=None, block_expert=None, out=None):
    with ExitStack() as ctx:
        sb, ps, sem = allocators(nc, ctx, name)
        w1_sb = sb("w1", [P, 2, HID])
        b1_sb = sb("b1", [P, FC])
        x_sb = sb("x", [P, 2, GB, D])
        xt = sb("xt", [P, 2, GB * P])
        ht = sb("ht", [P, FC, GB * P])
        if wg is not None:
            wg_sb = sb("wg", [P, FC, EXPERTS])
            bg_sb = sb("bg", [EXPERTS, 1])
            turned_logits = sb("turned_logits", [EXPERTS, groups * GB * P])
        else:
            wd_sb = sb("wd", [P, EXPERTS, FC * D])
            bd_sb = sb("bd", [P, EXPERTS, D])
            y_sb = sb("y", [P, GB, D])
        pt = ps("pt", [P, 2, 512])
        ph = [ps(f"ph{j}", [P, 512]) for j in range(4)]
        py = [ps(f"py{j}", [P, 512]) for j in range(2)]
        wloaded = sem("wloaded")
        dloaded = sem("dloaded")
        loaded = [sem("loaded0"), sem("loaded1")]
        stored = sem("stored")
        turned = sem("turned")
        copied = sem("copied")
        h_made = sem("h_made")
        active = sem("active")
        y_made = sem("y_made")
        evacuated = sem("evacuated")
        y_free = sem("y_free")
        DLOADS = 2 if wg is not None else 1 + EXPERTS

        with nc.Block() as block:
            @block.sync
            def _(sp):
                sp.dma_start(w1_sb[:, :, :], w1.rearrange("(c p) n -> p c n", p=P)).then_inc(wloaded, 16)
                sp.dma_start(b1_sb[:, :], b1).then_inc(wloaded, 16)

                def load(n, h):
                    sp.wait_ge(turned, GB * n + GB)
                    sp.dma_start(x_sb[:, h, :, :], rows[:, bass.ds(GB * n, GB), :]).then_inc(loaded[h], 16)
                in_pairs(nc.sync, groups, load)

            @block.gpsimd
            def _(pool):
                if wg is not None:
                    pool.dma_start(wg_sb[:, :, :], wg.rearrange("(f p) e -> p f e", p=P)).then_inc(dloaded, 16)
                    pool.dma_start(bg_sb[:, :], bg.rearrange("(n a) -> n a", a=1)).then_inc(dloaded, 16)
                    return
                pool.dma_start(bd_sb[:, :, :], bd.rearrange("e (a n) -> a e n", a=1).to_broadcast([P, EXPERTS, D])).then_inc(dloaded, 16)
                for e in range(EXPERTS):
                    pool.dma_start(wd_sb[:, e, :].rearrange("p (f n) -> p f n", n=D),
                                   wd[e].rearrange("(f p) n -> p f n", p=P)).then_inc(dloaded, 16)

                pool.sem_inc(y_free, 1)

                def store(n, h):
                    pool.wait_ge(evacuated, GB * n + GB + 2)
                    pool.dma_start(out[:, bass.ds(GB * n, GB), :], y_sb[:, :, :]).then_inc(stored, 16)
                    pool.wait_ge(stored, 16 * n + 16)
                    pool.sem_inc(y_free, 1)
                in_pairs(nc.gpsimd, groups, store)

            @block.tensor
            def _(pe):
                pe.sem_inc(turned, 2 * GB)
                pe.wait_ge(wloaded, 32)
                pe.wait_ge(dloaded, 16 * DLOADS)

                def turn(n, h):
                    pe.wait_ge(loaded[h], 16 * half_index(n, h))
                    for t in range(GB):
                        pe.wait_ge(copied, GB * n + t + 1)
                        for c in range(2):
                            last = nc.tensor.transpose(pt[:, (t + h) % 2, c * P:(c + 1) * P], x_sb[:, h, t, c * P:(c + 1) * P],
                                                       k.ident[:, :])
                        last.then_inc(turned, 1)

                def first(n, h):
                    for half in range(2):
                        pe.wait_ge(copied, GB * n + (GB + 1) // 2 * (1 - half) + GB * half + 2)
                        for f in range(FC):
                            pe.wait_ge(active, 2 * FC * n + FC * half + f + 1)
                            for c in range(2):
                                last = nc.tensor.matmul(ph[f % 4][:, 0:HALFTOK], w1_sb[:, c, f * P:(f + 1) * P],
                                                        xt[:, c, half * HALFTOK:(half + 1) * HALFTOK], start=(c == 0), stop=(c == 1))
                            last.then_inc(h_made, 1)

                def second(n, h):
                    if wg is not None:
                        for half in range(2):
                            pe.wait_ge(active, 2 * FC * n + FC * (half + 1) + 4)
                            pe.wait_ge(evacuated, 2 * n + half + 1)
                            for f in range(FC):
                                last = nc.tensor.matmul(py[half][0:EXPERTS, 0:HALFTOK], wg_sb[:, f, :],
                                                        ht[:, f, half * HALFTOK:(half + 1) * HALFTOK],
                                                        start=(f == 0), stop=(f == FC - 1))
                            last.then_inc(y_made, 1)
                        return
                    _, experts = nc.values_load_multi_w_load_instructions(
                        block_expert[0:1, bass.ds(GB * n, GB)], engines=(mybir.EngineType.PE,), min_val=0, max_val=EXPERTS - 1,
                        skip_runtime_bounds_check_because="a block's expert counts experts before the last")
                    for t in range(GB):
                        if t == 0:
                            pe.wait_ge(active, 2 * FC * n + FC + 4)
                        if t == GB // 2:
                            pe.wait_ge(active, 2 * FC * n + 2 * FC + 4)
                        pe.wait_ge(evacuated, GB * n + t + 1)
                        for f in range(FC):
                            last = nc.tensor.matmul(py[(t + h) % 2][:, 0:D], ht[:, f, t * P:(t + 1) * P],
                                                    wd_sb[:, bass.ds(experts[t], 1), f * D:(f + 1) * D].rearrange("p a d -> p (a d)"),
                                                    start=(f == 0), stop=(f == FC - 1))
                        last.then_inc(y_made, 1)

                turn(0, 0)

                def group(n, h, last=False):
                    first(n, h)
                    if not last:
                        turn(n + 1, 1 - h)
                    second(n, h)
                staggered(nc.tensor, groups, group)

            @block.scalar
            def _(act):
                act.sem_inc(active, 4)
                act.wait_ge(wloaded, 32)

                def activate(n, h):
                    for half in range(2):
                        for f in range(FC):
                            act.wait_ge(h_made, 2 * FC * n + FC * half + f + 2)
                            nc.scalar.activation(ht[:, f, half * HALFTOK:(half + 1) * HALFTOK], ph[f % 4][:, 0:HALFTOK], ACT.Gelu,
                                                 bias=b1_sb[:, f:f + 1]).then_inc(active, 1)
                in_pairs(nc.scalar, groups, activate)

            @block.vector
            def _(dve):
                dve.sem_inc(copied, 2)
                dve.sem_inc(evacuated, 2)
                dve.sem_inc(h_made, 1)
                dve.wait_ge(dloaded, 16 * DLOADS)

                def copy(n, h):
                    dve.wait_ge(h_made, 2 * FC * n + 1)
                    for t in range(GB):
                        dve.wait_ge(turned, GB * n + 2 * GB + t + 1)
                        nc.vector.tensor_copy(xt[:, :, t * P:(t + 1) * P],
                                              pt[:, (t + h) % 2, 0:D].rearrange("p (c n) -> p c n", c=2)).then_inc(copied, 1)

                def end(n, h):
                    if wg is not None:
                        for half in range(2):
                            dve.wait_ge(y_made, 2 * n + half + 1)
                            nc.vector.tensor_scalar(turned_logits[:, bass.ds(GB * P * n + HALFTOK * half, HALFTOK)],
                                                    py[half][0:EXPERTS, 0:HALFTOK], bg_sb[:, :], None, ALU.add).then_inc(evacuated, 1)
                        return
                    _, experts = nc.values_load_multi_w_load_instructions(
                        block_expert[0:1, bass.ds(GB * n, GB)], engines=(mybir.EngineType.DVE,), min_val=0, max_val=EXPERTS - 1,
                        skip_runtime_bounds_check_because="a block's expert counts experts before the last")
                    dve.wait_ge(y_free, n + 1)
                    for t in range(GB):
                        dve.wait_ge(y_made, GB * n + t + 1)
                        nc.vector.tensor_tensor(y_sb[:, t:t + 1, :], py[(t + h) % 2][:, 0:D].unsqueeze(1),
                                                bd_sb[:, bass.ds(experts[t], 1), :], ALU.add).then_inc(evacuated, 1)

                copy(0, 0)

                def group(n, h, last=False):
                    if not last:
                        copy(n + 1, 1 - h)
                    end(n, h)
                staggered(nc.vector, groups, group)

        if wg is not None:
            laned = sem("laned")
            with nc.Block() as block:
                @block.tensor
                def _(pe):
                    for b in range(groups * GB):
                        last = nc.tensor.transpose(py[0][:, b * EXPERTS:(b + 1) * EXPERTS], turned_logits[:, b * P:(b + 1) * P],
                                                   k.ident[0:EXPERTS, 0:EXPERTS])
                    last.then_inc(laned, 1)

                @block.vector
                def _(dve):
                    dve.wait_ge(laned, 1)
                    nc.vector.tensor_copy(logits[:, :, :].rearrange("p b e -> p (b e)"), py[0][:, 0:groups * GB * EXPERTS])


ZEROS = 2048


def stage_zeros(nc, zeros):
    with ExitStack() as ctx:
        with nc.Block() as block:
            @block.vector
            def _(dve):
                nc.vector.memset(zeros[:, :], 0.0)


def begin_loads(sp, x, acc, x_there, tables, zeros, cleared):
    sp.dma_start(acc[:, :, 0:D], in_blocks(x)).then_inc(x_there, 16)
    for t in tables:
        rows = t.rearrange("(p a) d -> p (a d)", p=P)
        for at in range(0, rows.shape[1], ZEROS):
            n = min(ZEROS, rows.shape[1] - at)
            sp.dma_start(rows[:, at:at + n], zeros[:, 0:n]).then_inc(cleared, 16)


def zero_loads(tables):
    return sum(-(-t.shape[0] * t.shape[1] // P // ZEROS) for t in tables)


def gps_two_layers(nc, a, out):
    dram = lambda n, s: nc.dram_tensor(n, s, f32).ap()
    table = [dram(f"table{j}", [NPAD, D]) for j in range(4)]
    slots = dram("slots", [EXPERTS * CAPPAD, D])
    expert_out = dram("expert_out", [EXPERTS * CAPPAD, D])
    x2 = dram("x2", [NPAD, D])
    gat = [(dram(f"run{j}", [EPAD, h]), dram(f"node{j}", [EPAD, 2 * h]), dram(f"p{j}", [EROWS * P, h]))
           for j, h in enumerate((HEADS1, 1))]
    es_table = [dram(f"es{j}", [NPAD, 2 * h]) for j, h in enumerate((HEADS1, 1))]
    edge_rows = lambda flat: flat.rearrange("(r l) -> r l", l=P)

    with ExitStack() as ctx:
        sb = lambda c, n, s, t=f32: c.enter_context(nc.sbuf_tensor(n, s, t))
        k = Kept(nc, ctx)
        acc = sb(ctx, "acc", [P, NB, D + HEADS1])
        x_there = nc.alloc_semaphore(name="x_there")
        cleared = nc.alloc_semaphore(name="cleared")
        begin = ExitStack()
        zeros = sb(begin, "zeros", [P, ZEROS])
        to_clear = [slots[e * CAPPAD:(e + 1) * CAPPAD, :] for e in range(EXPERTS)] + [g[1] for g in gat] + [g[2][EPAD:, :] for g in gat]
        stage_zeros(nc, zeros)
        stage_prepare(nc, k, edge_rows(a["src"]), edge_rows(a["dst"]), edge_rows(a["edge_weight"]),
                      more_loads=lambda sp: begin_loads(sp, a["x"], acc, x_there, to_clear, zeros, cleared))
        with nc.Block() as block:
            @block.sync
            def _(sp):
                sp.wait_ge(cleared, 16 * zero_loads(to_clear))
        begin.close()
        esd = [sb(ctx, f"esd{j}", [P, NB, 2 * h]) for j, h in enumerate((HEADS1, 1))]

        with ExitStack() as c:
            xn = sb(c, "xn", [P, NB, D])
            with ExitStack() as c0:
                k.dots = sb(c0, "dots", [P, 4, P])
                k.mix = sb(c0, "mix", [P, 2, D])
                stage_layernorm(nc, k, "norm0", acc, xn, x_there=(x_there, 16))
                stage_scale_store(nc, k, "self0", xn, k.dinv, acc, table[0])
                stage_aggregate(nc, k, "conv0", table[0], acc, D, k.weight, side=Mix0Side(xn, a["L0_mix_Wqkv_t"][:, INNER0:3 * INNER0]))
                stage_mix0_fold(nc, k, a["L0_mix_Wqkv"][0:INNER0, :], a["L0_mix_Wout_t"])
                stage_gcn_dense(nc, k, "dense0", acc, a["L0_gnn_W1"], a["L0_gnn_b1"], table=table[1])
                stage_aggregate(nc, k, "conv1", table[1], acc, D, k.weight)
                stage_gcn_dense(nc, k, "dense1", acc, a["L0_gnn_W2"], a["L0_gnn_b2"], xn=xn, x_in=a["x"], bias2=a["L0_mix_bout"])
            with ExitStack() as c1:
                logits = sb(c1, "logits0", [P, NB, EXPERTS])
                prob = sb(c1, "prob0", [P, NB])
                to_slot, from_slot = sb(c1, "to_slot0", [P, NB], i32), sb(c1, "from_slot0", [P, NB], i32)
                stage_layernorm(nc, k, "norm1", acc, xn)
                stage_gate(nc, k, xn, a["L0_ffn_gate_w"], a["L0_ffn_gate_b"], logits)
                stage_route(nc, k, "route0", logits, prob, to_slot, from_slot, capacity=CAP)
                stage_dispatch(nc, k, "send0", xn, to_slot, slots)
                stage_experts0(nc, k, slots, a["L0_ffn_w1"], a["L0_ffn_b1"], a["L0_ffn_w2"], a["L0_ffn_b2"], expert_out, xn)
                stage_combine(nc, k, "combine0", expert_out, from_slot, acc, prob, True)
            stage_layernorm(nc, k, "norm2", acc, xn)
            stage_mix1(nc, k, xn, acc, a["L1_mix_w_qkv"], a["L1_mix_g_pre"], a["mem_k"], a["mem_k_t"], a["mem_v_t"],
                       a["L1_mix_w_out"], a["L1_mix_b_out"], a["L1_mix_g_out"], x2)
            stage_gat_project(nc, k, "project0", xn, a["L1_gnn_W0"], a["L1_gnn_W0_t"], a["a_cols0"],
                              HEADS1, acc, esd[0], table[2], es_table[0])

        def attend(j, heads):
            with ExitStack() as c:
                weights = sb(c, f"weights{j}", [P, SPAD * heads])
                p_self = sb(c, f"p_self{j}", [P, NB, heads])
                stage_gat_weights(nc, k, f"soft{j}", heads, es_table[j], esd[j], a["src"], a["dst"], a["last_dst"], *gat[j], weights, p_self, acc)
                stage_aggregate(nc, k, f"attend{j}", table[2 + j], acc, D + heads, weights, heads=heads if heads > 1 else 0)
        attend(0, HEADS1)
        with ExitStack() as c:
            xn = sb(c, "h1", [P, NB, D])
            stage_gat_norm(nc, k, acc, xn, a["L1_gnn_b0"], a["L1_gnn_gamma0"], a["L1_gnn_beta0"])
            stage_gat_project(nc, k, "project1", xn, a["L1_gnn_W1"], a["L1_gnn_W1_t"], a["a_cols1"],
                              1, acc, esd[1], table[3], es_table[1])
        attend(1, 1)

        prob = sb(ctx, "prob1", [P, NB])
        from_slot = sb(ctx, "from_slot1", [P, NB], i32)
        block_expert = sb(ctx, "block_expert", [1, P], i32)
        with ExitStack() as c:
            xn = sb(c, "xn1", [P, NB, D])
            logits = sb(c, "logits1", [P, NB, EXPERTS])
            to_slot = sb(c, "to_slot1", [P, NB], i32)
            stage_gat_out(nc, k, acc, a["L1_gnn_b1"], x2, xn)
            stage_layernorm(nc, k, "norm3", acc, xn)
            stage_ffn1(nc, k, "gate1", NG, xn, a["L1_ffn_W1"], a["L1_ffn_b1"], wg=a["L1_ffn_Wg"], bg=a["L1_ffn_bg"], logits=logits)
            stage_route(nc, k, "route1", logits, prob, to_slot, from_slot, block_expert=block_expert)
            stage_dispatch(nc, k, "send1", xn, to_slot, slots)
        stage_ffn1(nc, k, "experts1", SLOT_GROUPS, in_blocks(slots), a["L1_ffn_W1"], a["L1_ffn_b1"],
                   wd=a["L1_ffn_Wd"], bd=a["L1_ffn_bd"], block_expert=block_expert, out=in_blocks(expert_out))
        stage_combine(nc, k, "combine1", expert_out, from_slot, acc, prob, False, x_out=out)


def kernel(**inputs):
    import concourse.bacc as _bacc
    from concourse.bass_utils import run_bass_kernel_spmd as _run

    arr = {n: np.ascontiguousarray(v) for n, v in inputs.items() if n != "L1_mix_t"}
    turned = lambda v: np.ascontiguousarray(v.T)
    mem = arr.pop("L1_mix_mem_kv")
    dst = arr.pop("dst").astype(np.int32, copy=False)
    src = arr.pop("src").astype(np.int32, copy=False)
    tail = EROWS * P - EDGES
    arr["x"] = np.concatenate([arr["x"], np.zeros((NPAD - NODES, D), arr["x"].dtype)])
    arr["src"] = np.concatenate([src, np.zeros(tail, np.int32)])
    arr["dst"] = np.concatenate([dst, np.full(tail, NODES, np.int32)])
    arr["last_dst"] = np.concatenate([np.full(1, -1, np.int32), arr["dst"][:-1]])
    arr["edge_weight"] = np.concatenate([arr["edge_weight"], np.zeros(tail, arr["edge_weight"].dtype)])
    for j, heads in ((0, HEADS1), (1, 1)):
        cols = np.zeros((D, 2 * heads), np.float32)
        for s, a in enumerate((arr.pop(f"L1_gnn_a_src{j}"), arr.pop(f"L1_gnn_a_dst{j}"))):
            for q in range(heads):
                cols[q * (D // heads):(q + 1) * (D // heads), s * heads + q] = a[q]
        arr[f"a_cols{j}"] = cols
    for n in ("L0_mix_Wqkv", "L1_gnn_W0", "L1_gnn_W1"):
        arr[n + "_t"] = turned(arr[n])
    arr["L0_mix_Wout_t"] = turned(arr.pop("L0_mix_Wout"))
    arr["L0_ffn_b1"] = np.ascontiguousarray(arr["L0_ffn_b1"].reshape(EXPERTS, FC, P).transpose(0, 2, 1))
    arr["L1_ffn_b1"] = turned(arr["L1_ffn_b1"].reshape(FC, P))
    arr["L1_mix_g_pre"] = turned(arr["L1_mix_g_pre"].reshape(2, P))
    arr["mem_k"] = np.ascontiguousarray(mem[0].reshape(INNER1, MEM))
    arr["mem_k_t"] = turned(arr["mem_k"])
    arr["mem_v_t"] = turned(mem[1].reshape(INNER1, MEM))

    nc = _bacc.Bacc("TRN2", target_bir_lowering=False, num_devices=1)
    aps = {n: nc.dram_tensor("in_" + n, v.shape, mybir.dt.from_np(v.dtype), kind="ExternalInput").ap() for n, v in arr.items()}
    out = nc.dram_tensor("out", (NPAD, D), f32, kind="ExternalOutput").ap()
    gps_two_layers(nc, aps, out)
    r = _run(nc, [{"in_" + n: v for n, v in arr.items()}], core_ids=[0])
    return r.results[0]["out"][:NODES]
```
